# Optimizing a Trainium2 kernel written in Bass

```python
import numpy as np
import jax
import jax.numpy as jnp

def _softmax(x, axis=-1):
    return jax.nn.softmax(x, axis=axis)

def _gelu(x):
    return jax.nn.gelu(x, approximate=True)

def _silu(x):
    return jax.nn.silu(x)

def _sigmoid(x):
    return jax.nn.sigmoid(x)

def _layernorm(x, axis=-1, eps=1e-05):
    m = jnp.mean(x, axis=axis, keepdims=True)
    v = jnp.var(x, axis=axis, keepdims=True)
    return (x - m) / jnp.sqrt(v + eps)

def _scatter_add(tgt, idx, src, axis=0):
    return tgt.at[idx].add(src)

def _segment_sum(src, seg, n):
    return jax.ops.segment_sum(src, seg, n)
kernel_name = 'mk_decoder_preln_d4_seqx_r8_e74a7a'

def setup_inputs(seed: int=0):
    np.random.seed(seed)
    _w = jnp.asarray

    def _rec_inputs():
        import jax
        import jax.numpy as jnp
        _rk = jax.random.key(seed)
        x = -0.0005207 + 1.001 * jax.random.normal(jax.random.fold_in(_rk, 1), (4, 512, 128), jnp.float32)
        _lenS = 512 - jax.random.randint(jax.random.fold_in(_rk, 7), (4,), 0, max(1, 512 // 4) + 1, jnp.int32)
        _lenS2 = 32 - jax.random.randint(jax.random.fold_in(_rk, 8), (4,), 0, max(1, 32 // 4) + 1, jnp.int32)
        _ctx_1024P = jax.random.normal(jax.random.fold_in(_rk, 11), (4, 16, 128), jnp.float32)
        _ctx_1024c = jax.random.dirichlet(jax.random.fold_in(_rk, 511), 0.3 * jnp.ones((16,), jnp.float32), (4, 32))
        _ctx_1024t = jnp.einsum('bsk,bkd->bsd', _ctx_1024c, _ctx_1024P)
        _ctx_1024t = _ctx_1024t * jax.lax.rsqrt(jnp.mean(jnp.square(_ctx_1024t)) + 1e-12) * 0.953939
        ctx_1024 = 4.13588e-05 + 0.999923 * (_ctx_1024t + 0.3 * jax.random.normal(jax.random.fold_in(_rk, 611), (4, 32, 128), jnp.float32))
        _validS = jnp.arange(512)[None, :] < _lenS[:, None]
        _validS2 = jnp.arange(32)[None, :] < _lenS2[:, None]
        _causal = jnp.tril(jnp.ones((512, 512), dtype=bool))
        mask_BxSxS2_bk0 = jnp.logical_not(jnp.broadcast_to(_validS2[:, None, :], (4, 512, 32)))
        mask_SxS2_ik1 = jnp.where(jnp.broadcast_to(_validS2[0:1, :], (512, 32)), 1, 0).astype(jnp.int32)
        return (x, ctx_1024, mask_BxSxS2_bk0, mask_SxS2_ik1)
    x, ctx_1024, mask_BxSxS2_bk0, mask_SxS2_ik1 = _rec_inputs()

    def _L0_attn_setup():
        import jax, jax.numpy as jnp
        import numpy as np
        D_MODEL, N_HEADS, D_FF = (128, 16, 512)
        SCALE = 0.1
        NUM_BITS = 8
        LEVELS = 1 << NUM_BITS
        HALF = LEVELS // 2
        MAX_EXP = 4
        EPS = 1e-05

        def pow2_weight(key, shape, max_exp=MAX_EXP):
            k1, k2 = jax.random.split(key)
            sign = jax.random.randint(k1, shape, -1, 2).astype(jnp.float32)
            e = jax.random.randint(k2, shape, max_exp, max_exp + 4).astype(jnp.float32)
            return sign * jnp.exp2(-e)

        def _layernorm(x, g, b):
            mu = jnp.mean(x, axis=-1, keepdims=True)
            var = jnp.var(x, axis=-1, keepdims=True)
            return (x - mu) * jax.lax.rsqrt(var + EPS) * g + b

        def _lookup_act(x):
            grid = (jnp.arange(LEVELS, dtype=jnp.float32) - HALF) * SCALE
            table = jax.nn.gelu(grid)
            idx = jnp.clip(jnp.round(x / SCALE).astype(jnp.int32) + HALF, 0, LEVELS - 1)
            return table[idx]

        def _linear_attention(x, wq, wk, wv, wo):
            B, S, D = x.shape
            H, Dh = (N_HEADS, D // N_HEADS)
            q = (x @ wq).reshape(B, S, H, Dh)
            k = (x @ wk).reshape(B, S, H, Dh)
            v = (x @ wv).reshape(B, S, H, Dh)
            phi_q = jax.nn.elu(q) + 1.0
            phi_k = jax.nn.elu(k) + 1.0
            kv = jnp.einsum('bshd,bshe->bhde', phi_k, v)
            z = jnp.sum(phi_k, axis=1)
            num = jnp.einsum('bshd,bhde->bshe', phi_q, kv)
            den = jnp.einsum('bshd,bhd->bsh', phi_q, z)[..., None] + 1e-06
            out = (num / den).reshape(B, S, D)
            return out @ wo
        key = jax.random.key(seed)
        ks = jax.random.split(key, 8)
        x = jax.random.normal(ks[0], (4, 256, D_MODEL), dtype=jnp.float32)
        return {'x': x, 'ln1_g': jnp.ones((D_MODEL,), jnp.float32), 'ln1_b': jnp.zeros((D_MODEL,), jnp.float32), 'wq': pow2_weight(ks[1], (D_MODEL, D_MODEL)), 'wk': pow2_weight(ks[2], (D_MODEL, D_MODEL)), 'wv': pow2_weight(ks[3], (D_MODEL, D_MODEL)), 'wo': pow2_weight(ks[4], (D_MODEL, D_MODEL)), 'ln2_g': jnp.ones((D_MODEL,), jnp.float32), 'ln2_b': jnp.zeros((D_MODEL,), jnp.float32), 'w1': pow2_weight(ks[5], (D_MODEL, D_FF)), 'w2': pow2_weight(ks[6], (D_FF, D_MODEL))}
    _L0_attn_all = _L0_attn_setup()
    _L0_attn_in = {k: v for k, v in _L0_attn_all.items() if k in ('ln1_g', 'ln1_b', 'wq', 'wk', 'wv', 'wo', 'ln2_g', 'ln2_b', 'w1', 'w2')}
    del _L0_attn_all

    def _L0_xattn_setup():
        import jax, jax.numpy as jnp
        import numpy as np
        NUM_HEADS = 16

        def softmax1(attn):
            padded = jnp.pad(attn, ((0, 0), (0, 0), (0, 0), (0, 1)))
            return jax.nn.softmax(padded, axis=-1)[..., :-1]
        key = jax.random.key(seed)
        ks = jax.random.split(key, 7)
        B, N, M, C = (2, 128, 512, 128)
        x = jax.random.normal(ks[0], (B, N, C), dtype=jnp.float32)
        context = jax.random.normal(ks[1], (B, M, C), dtype=jnp.float32)
        mask = jax.random.randint(ks[2], (B, N, M), 0, 2) > 0
        s = 1.0 / np.sqrt(C)
        Wq = jax.random.normal(ks[3], (C, C), dtype=jnp.float32) * s
        Wkv = jax.random.normal(ks[4], (C, 2 * C), dtype=jnp.float32) * s
        Wproj = jax.random.normal(ks[5], (C, C), dtype=jnp.float32) * s
        bproj = jnp.zeros((C,), dtype=jnp.float32)
        return {'x': x, 'context': context, 'mask': mask, 'Wq': Wq, 'Wkv': Wkv, 'Wproj': Wproj, 'bproj': bproj}
    _L0_xattn_all = _L0_xattn_setup()
    _L0_xattn_in = {k: v for k, v in _L0_xattn_all.items() if k in ('Wq', 'Wkv', 'Wproj', 'bproj')}
    del _L0_xattn_all

    def _L0_ffn_setup():
        import jax, jax.numpy as jnp
        import numpy as np
        D_MODEL = 128
        NUM_EXPERTS = 8
        TOP_K = 2
        B, S = (1, 256)
        key = jax.random.key(seed)
        ks = jax.random.split(key, 8)
        sd = 1.0 / np.sqrt(D_MODEL)
        x = jax.random.normal(ks[0], (B, S, D_MODEL), dtype=jnp.float32)
        gate_w = jax.random.normal(ks[1], (D_MODEL, NUM_EXPERTS), dtype=jnp.float32) * sd
        gate_b = jnp.zeros((NUM_EXPERTS,), dtype=jnp.float32)
        w1 = jax.random.normal(ks[2], (NUM_EXPERTS, D_MODEL, 8 * D_MODEL), dtype=jnp.float32) * sd
        b1 = jnp.zeros((NUM_EXPERTS, 8 * D_MODEL), dtype=jnp.float32)
        w2 = jax.random.normal(ks[3], (NUM_EXPERTS, 4 * D_MODEL, D_MODEL), dtype=jnp.float32) * (1.0 / np.sqrt(4 * D_MODEL))
        b2 = jnp.zeros((NUM_EXPERTS, D_MODEL), dtype=jnp.float32)
        return {'x': x, 'gate_w': gate_w, 'gate_b': gate_b, 'w1': w1, 'b1': b1, 'w2': w2, 'b2': b2}
    _L0_ffn_all = _L0_ffn_setup()
    _L0_ffn_in = {k: v for k, v in _L0_ffn_all.items() if k in ('gate_w', 'gate_b', 'w1', 'b1', 'w2', 'b2')}
    del _L0_ffn_all

    def _L1_attn_setup():
        import jax, jax.numpy as jnp
        import numpy as np
        B, L, D, N = (4, 512, 128, 128)
        EPS = 1e-05

        def _gated_scan(A, b):

            def combine(c1, c2):
                a1, u1 = c1
                a2, u2 = c2
                return (a1 * a2, a2 * u1 + u2)
            _, h = jax.lax.associative_scan(combine, (A, b), axis=1)
            return h
        key = jax.random.key(seed)
        ks = jax.random.split(key, 8)
        s = 0.02
        return {'x': jax.random.normal(ks[0], (B, L, D), jnp.float32), 'rms_weight': jnp.ones((D,), jnp.float32), 'w_A': jax.random.normal(ks[1], (D, N), jnp.float32) * s, 'b_A': jnp.zeros((N,), jnp.float32), 'w_x': jax.random.normal(ks[2], (D, N), jnp.float32) * s, 'w_sidegate': jax.random.normal(ks[3], (D, N), jnp.float32) * s, 'w_output': jax.random.normal(ks[4], (D, N), jnp.float32) * s, 'w_o': jax.random.normal(ks[5], (N, D), jnp.float32) * s}
    _L1_attn_all = _L1_attn_setup()
    _L1_attn_in = {k: v for k, v in _L1_attn_all.items() if k in ('rms_weight', 'w_A', 'b_A', 'w_x', 'w_sidegate', 'w_output', 'w_o')}
    del _L1_attn_all

    def _L1_xattn_setup():
        import jax, jax.numpy as jnp
        import numpy as np
        DIM = 128
        key = jax.random.key(seed)
        k1, k2, k3, k4, k5 = jax.random.split(key, 5)
        B, Sq, Skv = (8, 256, 256)
        x = jax.random.normal(k1, (B, Sq, DIM), dtype=jnp.float32)
        context = jax.random.normal(k2, (B, Skv, DIM), dtype=jnp.float32)
        s = DIM ** (-0.5)
        Wq = jax.random.normal(k3, (DIM, DIM), dtype=jnp.float32) * s
        Wk = jax.random.normal(k4, (DIM, DIM), dtype=jnp.float32) * s
        Wv = jax.random.normal(k5, (DIM, DIM), dtype=jnp.float32) * s
        return {'x': x, 'context': context, 'Wq': Wq, 'Wk': Wk, 'Wv': Wv}
    _L1_xattn_all = _L1_xattn_setup()
    _L1_xattn_in = {k: v for k, v in _L1_xattn_all.items() if k in ('Wq', 'Wk', 'Wv')}
    del _L1_xattn_all

    def _L1_ffn_setup():
        import jax, jax.numpy as jnp
        import numpy as np
        EPS_NORM = 1e-08
        EPS_Q = 1e-05

        def rmsnorm(x, w):
            v = jnp.mean(jnp.square(x.astype(jnp.float32)), axis=-1, keepdims=True)
            x_hat = x * jax.lax.rsqrt(v + EPS_NORM)
            return (x_hat * w).astype(x.dtype)

        def activation_quant(x):
            scale = 127.0 / jnp.clip(jnp.max(jnp.abs(x), axis=-1, keepdims=True), EPS_Q, None)
            return jnp.clip(jnp.round(x * scale), -128, 127) / scale

        def weight_quant(w):
            scale = 1.0 / jnp.clip(jnp.mean(jnp.abs(w)), EPS_Q, None)
            return jnp.clip(jnp.round(w * scale), -1, 1) / scale

        def bitlinear(x, norm_w, w):
            x_norm = rmsnorm(x, norm_w)
            x_q = x_norm + jax.lax.stop_gradient(activation_quant(x_norm) - x_norm)
            w_q = w + jax.lax.stop_gradient(weight_quant(w) - w)
            return jnp.einsum('bsd,hd->bsh', x_q, w_q)
        key = jax.random.key(seed)
        k1, k2, k3 = jax.random.split(key, 3)
        dim, hidden = (128, 512)
        return {'x': jax.random.normal(k1, (4, 256, dim), dtype=jnp.float32), 'norm1_w': jnp.ones((dim,), jnp.float32), 'w1': jax.random.normal(k2, (hidden, dim), jnp.float32) * 0.02, 'act_scale': jnp.ones((1,), jnp.float32), 'act_bias': jnp.zeros((1,), jnp.float32), 'norm2_w': jnp.ones((hidden,), jnp.float32), 'w2': jax.random.normal(k3, (dim, hidden), jnp.float32) * 0.02}
    _L1_ffn_all = _L1_ffn_setup()
    _L1_ffn_in = {k: v for k, v in _L1_ffn_all.items() if k in ('norm1_w', 'w1', 'act_scale', 'act_bias', 'norm2_w', 'w2')}
    del _L1_ffn_all

    def _L2_attn_setup():
        import jax, jax.numpy as jnp
        import numpy as np
        from jax import lax
        B, T, HID = (4, 128, 128)
        H, DK, DV = (8, 128, 128)
        KCONV = 4
        EPS = 1e-06
        KEY_DIM = H * DK
        VAL_DIM = H * DV
        CONV_DIM = 2 * KEY_DIM + VAL_DIM
        key = jax.random.key(seed)
        ks = jax.random.split(key, 11)
        s = 0.02
        return {'hidden_states': jax.random.normal(ks[0], (B, T, HID), jnp.float32), 'qkv_w': jax.random.normal(ks[1], (CONV_DIM, HID), jnp.float32) * s, 'z_w': jax.random.normal(ks[2], (VAL_DIM, HID), jnp.float32) * s, 'b_w': jax.random.normal(ks[3], (H, HID), jnp.float32) * s, 'a_w': jax.random.normal(ks[4], (H, HID), jnp.float32) * s, 'conv_w': jax.random.normal(ks[5], (CONV_DIM, 1, KCONV), jnp.float32) * 0.2, 'dt_bias': jnp.ones((H,), jnp.float32), 'A_log': jnp.log(jax.random.uniform(ks[6], (H,), jnp.float32, 0.001, 16.0)), 'norm_w': jnp.ones((DV,), jnp.float32), 'out_w': jax.random.normal(ks[7], (HID, VAL_DIM), jnp.float32) * s}
    _L2_attn_all = _L2_attn_setup()
    _L2_attn_in = {k: v for k, v in _L2_attn_all.items() if k in ('qkv_w', 'z_w', 'b_w', 'a_w', 'conv_w', 'dt_bias', 'A_log', 'norm_w', 'out_w')}
    del _L2_attn_all

    def _L2_xattn_setup():
        import jax, jax.numpy as jnp
        import numpy as np
        B, T, S, E, H = (2, 256, 256, 128, 16)
        HD = E // H
        key = jax.random.key(seed)
        ks = jax.random.split(key, 13)
        sc = 1.0 / np.sqrt(E)
        inp = {'q': jax.random.normal(ks[0], (B, T, E), jnp.float32), 'k': jax.random.normal(ks[1], (B, S, E), jnp.float32), 'v': jax.random.normal(ks[2], (B, S, E), jnp.float32), 'attn_mask': jax.random.randint(ks[3], (T, S), 0, 2, jnp.int32), 'Wq': jax.random.normal(ks[4], (E, E), jnp.float32) * sc, 'bq': jax.random.normal(ks[5], (E,), jnp.float32) * 0.01, 'Wk': jax.random.normal(ks[6], (E, E), jnp.float32) * sc, 'bk': jax.random.normal(ks[7], (E,), jnp.float32) * 0.01, 'Wv': jax.random.normal(ks[8], (E, E), jnp.float32) * sc, 'bv': jax.random.normal(ks[9], (E,), jnp.float32) * 0.01, 'Wo': jax.random.normal(ks[10], (E, E), jnp.float32) * sc, 'bo': jax.random.normal(ks[11], (E,), jnp.float32) * 0.01}
        return inp
    _L2_xattn_all = _L2_xattn_setup()
    _L2_xattn_in = {k: v for k, v in _L2_xattn_all.items() if k in ('Wq', 'bq', 'Wk', 'bk', 'Wv', 'bv', 'Wo', 'bo')}
    del _L2_xattn_all

    def _L2_ffn_setup():
        import jax, jax.numpy as jnp
        import numpy as np
        TOP_K = 8
        key = jax.random.key(seed)
        k1, k2, k3, k4, k5 = jax.random.split(key, 5)
        B, S, D, F, E = (2, 256, 128, 96, 64)
        return {'hidden_states': jax.random.normal(k1, (B, S, D), dtype=jnp.float32), 'gate_w': jax.random.normal(k2, (E, D), dtype=jnp.float32) * 0.02, 'w_gate': jax.random.normal(k3, (E, F, D), dtype=jnp.float32) * 0.02, 'w_up': jax.random.normal(k4, (E, F, D), dtype=jnp.float32) * 0.02, 'w_down': jax.random.normal(k5, (E, D, F), dtype=jnp.float32) * 0.02}
    _L2_ffn_all = _L2_ffn_setup()
    _L2_ffn_in = {k: v for k, v in _L2_ffn_all.items() if k in ('gate_w', 'w_gate', 'w_up', 'w_down')}
    del _L2_ffn_all

    def _L3_attn_setup():
        import jax, jax.numpy as jnp
        import numpy as np
        import math
        H = 16
        N_EMBD = 128
        EPS = 1e-05
        key = jax.random.key(seed)
        ks = jax.random.split(key, 6)
        B, T, C = (2, 256, 128)
        x = jax.random.normal(ks[0], (B, T, C), dtype=jnp.float32)
        s = 0.02
        Wq = jax.random.normal(ks[1], (C, N_EMBD), dtype=jnp.float32) * s
        Wk = jax.random.normal(ks[2], (C, N_EMBD), dtype=jnp.float32) * s
        Wv = jax.random.normal(ks[3], (C, N_EMBD), dtype=jnp.float32) * s
        Wo = jax.random.normal(ks[4], (N_EMBD, C), dtype=jnp.float32) * s
        return {'x': x, 'Wq': Wq, 'bq': jnp.zeros((N_EMBD,), jnp.float32), 'Wk': Wk, 'bk': jnp.zeros((N_EMBD,), jnp.float32), 'Wv': Wv, 'bv': jnp.zeros((N_EMBD,), jnp.float32), 'Wo': Wo, 'bo': jnp.zeros((C,), jnp.float32), 'gamma': jnp.ones((C,), jnp.float32), 'beta': jnp.zeros((C,), jnp.float32)}
    _L3_attn_all = _L3_attn_setup()
    _L3_attn_in = {k: v for k, v in _L3_attn_all.items() if k in ('Wq', 'bq', 'Wk', 'bk', 'Wv', 'bv', 'Wo', 'bo', 'gamma', 'beta')}
    del _L3_attn_all

    def _L3_xattn_setup():
        import jax, jax.numpy as jnp
        import numpy as np
        EMB = 128
        HEADS = 16
        HEAD_DIM = EMB // HEADS
        B, S = (2, 256)
        key = jax.random.key(seed)
        ks = jax.random.split(key, 11)
        scale = 1.0 / np.sqrt(EMB)
        inp = {'query': jax.random.normal(ks[0], (B, S, EMB), jnp.float32), 'key': jax.random.normal(ks[1], (B, S, EMB), jnp.float32), 'value': jax.random.normal(ks[2], (B, S, EMB), jnp.float32), 'Wq': jax.random.normal(ks[3], (EMB, EMB), jnp.float32) * scale, 'bq': jnp.zeros((EMB,), jnp.float32), 'Wk': jax.random.normal(ks[4], (EMB, EMB), jnp.float32) * scale, 'bk': jnp.zeros((EMB,), jnp.float32), 'Wv': jax.random.normal(ks[5], (EMB, EMB), jnp.float32) * scale, 'bv': jnp.zeros((EMB,), jnp.float32), 'Wo': jax.random.normal(ks[6], (EMB, EMB), jnp.float32) * scale, 'bo': jnp.zeros((EMB,), jnp.float32)}
        return inp
    _L3_xattn_all = _L3_xattn_setup()
    _L3_xattn_in = {k: v for k, v in _L3_xattn_all.items() if k in ('Wq', 'bq', 'Wk', 'bk', 'Wv', 'bv', 'Wo', 'bo')}
    del _L3_xattn_all

    def _L3_ffn_setup():
        import jax, jax.numpy as jnp
        import numpy as np
        N_EMBD = 128
        ITER_SIZE = 4 * N_EMBD
        FULL_SIZE = 3 * ITER_SIZE
        R = 0.7

        def _topk_mask(ck, k):
            probs = jax.nn.softmax(ck, axis=-1)
            _, idx = jax.lax.top_k(probs, k)
            b = jnp.arange(probs.shape[0])[:, None]
            return jnp.zeros_like(probs).at[b, idx].set(1.0)

        def _forward(x, Wm, Wp, Wc1, Wc2):
            B = x.shape[0]
            base = jnp.zeros((B, FULL_SIZE), x.dtype).at[:, :ITER_SIZE].set(1.0)

            def step(carry, _):
                xc, active, history, done = carry
                h = jnp.einsum('btc,fc->btf', xc, Wm) * active[:, None, :]
                h = jax.nn.relu(h)
                x_new = jnp.einsum('btf,cf->btc', h, Wp)
                pooled = x_new.mean(axis=1)
                ck = jnp.einsum('bd,fd->bf', jax.nn.relu(jnp.einsum('bc,dc->bd', pooled, Wc1)), Wc2)
                new_mask = _topk_mask(ck, ITER_SIZE)
                combined = jnp.clip(history + new_mask, 0.0, 1.0)
                novelty = (combined - history).sum(axis=1).mean() / ITER_SIZE
                done_next = jnp.logical_or(done, novelty < R)
                x_out = jnp.where(done, xc, x_new)
                active_out = jnp.where(done, active, new_mask)
                history_out = jnp.where(done, history, combined)
                return ((x_out, active_out, history_out, done_next), None)
            init = (x, base, base, jnp.array(False))
            (x_fin, _, _, _), _ = jax.lax.scan(step, init, None, length=3)
            return x_fin
        key = jax.random.key(seed)
        ks = jax.random.split(key, 5)
        B, T = (8, 128)
        s = 0.02
        return {'x': jax.random.normal(ks[0], (B, T, N_EMBD), jnp.float32), 'Wm': jax.random.normal(ks[1], (FULL_SIZE, N_EMBD), jnp.float32) * s, 'Wp': jax.random.normal(ks[2], (N_EMBD, FULL_SIZE), jnp.float32) * s, 'Wc1': jax.random.normal(ks[3], (N_EMBD // 4, N_EMBD), jnp.float32) * s, 'Wc2': jax.random.normal(ks[4], (FULL_SIZE, N_EMBD // 4), jnp.float32) * s}
    _L3_ffn_all = _L3_ffn_setup()
    _L3_ffn_in = {k: v for k, v in _L3_ffn_all.items() if k in ('Wm', 'Wp', 'Wc1', 'Wc2')}
    del _L3_ffn_all
    return {'x': x, 'ctx_1024': ctx_1024, 'mask_BxSxS2_bk0': mask_BxSxS2_bk0, 'mask_SxS2_ik1': mask_SxS2_ik1, 'L0_attn_ln1_g': _L0_attn_in['ln1_g'], 'L0_attn_ln1_b': _L0_attn_in['ln1_b'], 'L0_attn_wq': _L0_attn_in['wq'], 'L0_attn_wk': _L0_attn_in['wk'], 'L0_attn_wv': _L0_attn_in['wv'], 'L0_attn_wo': _L0_attn_in['wo'], 'L0_attn_ln2_g': _L0_attn_in['ln2_g'], 'L0_attn_ln2_b': _L0_attn_in['ln2_b'], 'L0_attn_w1': _L0_attn_in['w1'], 'L0_attn_w2': _L0_attn_in['w2'], 'L0_xattn_Wq': _L0_xattn_in['Wq'], 'L0_xattn_Wkv': _L0_xattn_in['Wkv'], 'L0_xattn_Wproj': _L0_xattn_in['Wproj'], 'L0_xattn_bproj': _L0_xattn_in['bproj'], 'L0_ffn_gate_w': _L0_ffn_in['gate_w'], 'L0_ffn_gate_b': _L0_ffn_in['gate_b'], 'L0_ffn_w1': _L0_ffn_in['w1'], 'L0_ffn_b1': _L0_ffn_in['b1'], 'L0_ffn_w2': _L0_ffn_in['w2'], 'L0_ffn_b2': _L0_ffn_in['b2'], 'L1_attn_rms_weight': _L1_attn_in['rms_weight'], 'L1_attn_w_A': _L1_attn_in['w_A'], 'L1_attn_b_A': _L1_attn_in['b_A'], 'L1_attn_w_x': _L1_attn_in['w_x'], 'L1_attn_w_sidegate': _L1_attn_in['w_sidegate'], 'L1_attn_w_output': _L1_attn_in['w_output'], 'L1_attn_w_o': _L1_attn_in['w_o'], 'L1_xattn_Wq': _L1_xattn_in['Wq'], 'L1_xattn_Wk': _L1_xattn_in['Wk'], 'L1_xattn_Wv': _L1_xattn_in['Wv'], 'L1_ffn_norm1_w': _L1_ffn_in['norm1_w'], 'L1_ffn_w1': _L1_ffn_in['w1'], 'L1_ffn_act_scale': _L1_ffn_in['act_scale'], 'L1_ffn_act_bias': _L1_ffn_in['act_bias'], 'L1_ffn_norm2_w': _L1_ffn_in['norm2_w'], 'L1_ffn_w2': _L1_ffn_in['w2'], 'L2_attn_qkv_w': _L2_attn_in['qkv_w'], 'L2_attn_z_w': _L2_attn_in['z_w'], 'L2_attn_b_w': _L2_attn_in['b_w'], 'L2_attn_a_w': _L2_attn_in['a_w'], 'L2_attn_conv_w': _L2_attn_in['conv_w'], 'L2_attn_dt_bias': _L2_attn_in['dt_bias'], 'L2_attn_A_log': _L2_attn_in['A_log'], 'L2_attn_norm_w': _L2_attn_in['norm_w'], 'L2_attn_out_w': _L2_attn_in['out_w'], 'L2_xattn_Wq': _L2_xattn_in['Wq'], 'L2_xattn_bq': _L2_xattn_in['bq'], 'L2_xattn_Wk': _L2_xattn_in['Wk'], 'L2_xattn_bk': _L2_xattn_in['bk'], 'L2_xattn_Wv': _L2_xattn_in['Wv'], 'L2_xattn_bv': _L2_xattn_in['bv'], 'L2_xattn_Wo': _L2_xattn_in['Wo'], 'L2_xattn_bo': _L2_xattn_in['bo'], 'L2_ffn_gate_w': _L2_ffn_in['gate_w'], 'L2_ffn_w_gate': _L2_ffn_in['w_gate'], 'L2_ffn_w_up': _L2_ffn_in['w_up'], 'L2_ffn_w_down': _L2_ffn_in['w_down'], 'L3_attn_Wq': _L3_attn_in['Wq'], 'L3_attn_bq': _L3_attn_in['bq'], 'L3_attn_Wk': _L3_attn_in['Wk'], 'L3_attn_bk': _L3_attn_in['bk'], 'L3_attn_Wv': _L3_attn_in['Wv'], 'L3_attn_bv': _L3_attn_in['bv'], 'L3_attn_Wo': _L3_attn_in['Wo'], 'L3_attn_bo': _L3_attn_in['bo'], 'L3_attn_gamma': _L3_attn_in['gamma'], 'L3_attn_beta': _L3_attn_in['beta'], 'L3_xattn_Wq': _L3_xattn_in['Wq'], 'L3_xattn_bq': _L3_xattn_in['bq'], 'L3_xattn_Wk': _L3_xattn_in['Wk'], 'L3_xattn_bk': _L3_xattn_in['bk'], 'L3_xattn_Wv': _L3_xattn_in['Wv'], 'L3_xattn_bv': _L3_xattn_in['bv'], 'L3_xattn_Wo': _L3_xattn_in['Wo'], 'L3_xattn_bo': _L3_xattn_in['bo'], 'L3_ffn_Wm': _L3_ffn_in['Wm'], 'L3_ffn_Wp': _L3_ffn_in['Wp'], 'L3_ffn_Wc1': _L3_ffn_in['Wc1'], 'L3_ffn_Wc2': _L3_ffn_in['Wc2']}

def reference(x, ctx_1024, mask_BxSxS2_bk0, mask_SxS2_ik1, L0_attn_ln1_g, L0_attn_ln1_b, L0_attn_wq, L0_attn_wk, L0_attn_wv, L0_attn_wo, L0_attn_ln2_g, L0_attn_ln2_b, L0_attn_w1, L0_attn_w2, L0_xattn_Wq, L0_xattn_Wkv, L0_xattn_Wproj, L0_xattn_bproj, L0_ffn_gate_w, L0_ffn_gate_b, L0_ffn_w1, L0_ffn_b1, L0_ffn_w2, L0_ffn_b2, L1_attn_rms_weight, L1_attn_w_A, L1_attn_b_A, L1_attn_w_x, L1_attn_w_sidegate, L1_attn_w_output, L1_attn_w_o, L1_xattn_Wq, L1_xattn_Wk, L1_xattn_Wv, L1_ffn_norm1_w, L1_ffn_w1, L1_ffn_act_scale, L1_ffn_act_bias, L1_ffn_norm2_w, L1_ffn_w2, L2_attn_qkv_w, L2_attn_z_w, L2_attn_b_w, L2_attn_a_w, L2_attn_conv_w, L2_attn_dt_bias, L2_attn_A_log, L2_attn_norm_w, L2_attn_out_w, L2_xattn_Wq, L2_xattn_bq, L2_xattn_Wk, L2_xattn_bk, L2_xattn_Wv, L2_xattn_bv, L2_xattn_Wo, L2_xattn_bo, L2_ffn_gate_w, L2_ffn_w_gate, L2_ffn_w_up, L2_ffn_w_down, L3_attn_Wq, L3_attn_bq, L3_attn_Wk, L3_attn_bk, L3_attn_Wv, L3_attn_bv, L3_attn_Wo, L3_attn_bo, L3_attn_gamma, L3_attn_beta, L3_xattn_Wq, L3_xattn_bq, L3_xattn_Wk, L3_xattn_bk, L3_xattn_Wv, L3_xattn_bv, L3_xattn_Wo, L3_xattn_bo, L3_ffn_Wm, L3_ffn_Wp, L3_ffn_Wc1, L3_ffn_Wc2):
    import jax
    import jax.numpy as jnp

    def _L0_attn_ref(x, ln1_g, ln1_b, wq, wk, wv, wo, ln2_g, ln2_b, w1, w2):
        import jax, jax.numpy as jnp
        import numpy as np
        D_MODEL, N_HEADS, D_FF = (128, 16, 512)
        SCALE = 0.1
        NUM_BITS = 8
        LEVELS = 1 << NUM_BITS
        HALF = LEVELS // 2
        MAX_EXP = 4
        EPS = 1e-05

        def pow2_weight(key, shape, max_exp=MAX_EXP):
            k1, k2 = jax.random.split(key)
            sign = jax.random.randint(k1, shape, -1, 2).astype(jnp.float32)
            e = jax.random.randint(k2, shape, max_exp, max_exp + 4).astype(jnp.float32)
            return sign * jnp.exp2(-e)

        def _layernorm(x, g, b):
            mu = jnp.mean(x, axis=-1, keepdims=True)
            var = jnp.var(x, axis=-1, keepdims=True)
            return (x - mu) * jax.lax.rsqrt(var + EPS) * g + b

        def _lookup_act(x):
            grid = (jnp.arange(LEVELS, dtype=jnp.float32) - HALF) * SCALE
            table = jax.nn.gelu(grid)
            idx = jnp.clip(jnp.round(x / SCALE).astype(jnp.int32) + HALF, 0, LEVELS - 1)
            return table[idx]

        def _linear_attention(x, wq, wk, wv, wo):
            B, S, D = x.shape
            H, Dh = (N_HEADS, D // N_HEADS)
            q = (x @ wq).reshape(B, S, H, Dh)
            k = (x @ wk).reshape(B, S, H, Dh)
            v = (x @ wv).reshape(B, S, H, Dh)
            phi_q = jax.nn.elu(q) + 1.0
            phi_k = jax.nn.elu(k) + 1.0
            kv = jnp.einsum('bshd,bshe->bhde', phi_k, v)
            z = jnp.sum(phi_k, axis=1)
            num = jnp.einsum('bshd,bhde->bshe', phi_q, kv)
            den = jnp.einsum('bshd,bhd->bsh', phi_q, z)[..., None] + 1e-06
            out = (num / den).reshape(B, S, D)
            return out @ wo
        x = x + _linear_attention(_layernorm(x, ln1_g, ln1_b), wq, wk, wv, wo)
        h = _layernorm(x, ln2_g, ln2_b)
        x = x + _lookup_act(h @ w1) @ w2
        return x

    def _L0_xattn_ref(x, context, mask, Wq, Wkv, Wproj, bproj):
        import jax, jax.numpy as jnp
        import numpy as np
        NUM_HEADS = 16

        def softmax1(attn):
            padded = jnp.pad(attn, ((0, 0), (0, 0), (0, 0), (0, 1)))
            return jax.nn.softmax(padded, axis=-1)[..., :-1]
        B, N, C = x.shape
        M = context.shape[1]
        H = NUM_HEADS
        d = C // H
        scale = d ** (-0.5)
        q = (x @ Wq).reshape(B, N, H, d).transpose(0, 2, 1, 3)
        kv = (context @ Wkv).reshape(B, M, 2, H, d)
        k = kv[:, :, 0].transpose(0, 2, 1, 3)
        v = kv[:, :, 1].transpose(0, 2, 1, 3)
        attn = jnp.einsum('bhnd,bhmd->bhnm', q, k) * scale
        neg = -jnp.finfo(attn.dtype).max
        attn = jnp.where(mask[:, None, :, :], neg, attn)
        attn = softmax1(attn)
        out = jnp.einsum('bhnm,bhmd->bhnd', attn, v)
        out = out.transpose(0, 2, 1, 3).reshape(B, N, C)
        return out @ Wproj + bproj

    def _L0_ffn_ref(x, gate_w, gate_b, w1, b1, w2, b2):
        import jax, jax.numpy as jnp
        import numpy as np
        D_MODEL = 128
        NUM_EXPERTS = 8
        TOP_K = 2
        B, S = (1, 256)
        gate_logits = jnp.einsum('bsd,de->bse', x, gate_w) + gate_b
        weights, indices = jax.lax.top_k(gate_logits, TOP_K)
        weights = jax.nn.softmax(weights, axis=-1)
        h = jnp.einsum('bsd,edh->ebsh', x, w1) + b1[:, None, None, :]
        xh, gh = jnp.split(h, 2, axis=-1)
        act = jax.nn.silu(gh) * xh
        out_e = jnp.einsum('ebsf,efd->ebsd', act, w2) + b2[:, None, None, :]
        out_e = jnp.transpose(out_e, (1, 2, 0, 3))
        sel = jnp.take_along_axis(out_e, indices[..., None], axis=2)
        return jnp.sum(sel * weights[..., None], axis=2)

    def _L1_attn_ref(x, rms_weight, w_A, b_A, w_x, w_sidegate, w_output, w_o):
        import jax, jax.numpy as jnp
        import numpy as np
        B, L, D, N = (4, 512, 128, 128)
        EPS = 1e-05

        def _gated_scan(A, b):

            def combine(c1, c2):
                a1, u1 = c1
                a2, u2 = c2
                return (a1 * a2, a2 * u1 + u2)
            _, h = jax.lax.associative_scan(combine, (A, b), axis=1)
            return h
        residual = x
        norm = jnp.sqrt(jnp.mean(x * x, axis=-1, keepdims=True) + EPS)
        xn = x * (rms_weight / norm)
        A = jax.nn.sigmoid(jnp.einsum('bld,dn->bln', xn, w_A) + b_A)
        x_el = jnp.einsum('bld,dn->bln', xn, w_x)
        sidegate = jax.nn.sigmoid(jnp.einsum('bld,dn->bln', xn, w_output))
        gate = jax.nn.sigmoid(jnp.einsum('bld,dn->bln', xn, w_sidegate))
        h = _gated_scan(A, x_el * sidegate)
        y = gate * h
        return jnp.einsum('bln,nd->bld', y, w_o) + residual

    def _L1_xattn_ref(x, context, Wq, Wk, Wv):
        import jax, jax.numpy as jnp
        import numpy as np
        DIM = 128
        q = jnp.einsum('bsd,ed->bse', x, Wq)
        k = jnp.einsum('btd,ed->bte', context, Wk)
        v = jnp.einsum('btd,ed->bte', context, Wv)
        scale = Wq.shape[0] ** (-0.5)
        dots = jnp.einsum('bse,bte->bst', q, k) * scale
        attn = jax.nn.softmax(dots, axis=-1)
        out = jnp.einsum('bst,bte->bse', attn, v)
        return out

    def _L1_ffn_ref(x, norm1_w, w1, act_scale, act_bias, norm2_w, w2):
        import jax, jax.numpy as jnp
        import numpy as np
        EPS_NORM = 1e-08
        EPS_Q = 1e-05

        def rmsnorm(x, w):
            v = jnp.mean(jnp.square(x.astype(jnp.float32)), axis=-1, keepdims=True)
            x_hat = x * jax.lax.rsqrt(v + EPS_NORM)
            return (x_hat * w).astype(x.dtype)

        def activation_quant(x):
            scale = 127.0 / jnp.clip(jnp.max(jnp.abs(x), axis=-1, keepdims=True), EPS_Q, None)
            return jnp.clip(jnp.round(x * scale), -128, 127) / scale

        def weight_quant(w):
            scale = 1.0 / jnp.clip(jnp.mean(jnp.abs(w)), EPS_Q, None)
            return jnp.clip(jnp.round(w * scale), -1, 1) / scale

        def bitlinear(x, norm_w, w):
            x_norm = rmsnorm(x, norm_w)
            x_q = x_norm + jax.lax.stop_gradient(activation_quant(x_norm) - x_norm)
            w_q = w + jax.lax.stop_gradient(weight_quant(w) - w)
            return jnp.einsum('bsd,hd->bsh', x_q, w_q)
        h = bitlinear(x, norm1_w, w1)
        h = act_scale * jnp.square(jax.nn.relu(h)) + act_bias
        y = bitlinear(h, norm2_w, w2)
        return y

    def _L2_attn_ref(hidden_states, qkv_w, z_w, b_w, a_w, conv_w, dt_bias, A_log, norm_w, out_w):
        import jax, jax.numpy as jnp
        import numpy as np
        from jax import lax
        B, T, HID = (4, 128, 128)
        H, DK, DV = (8, 128, 128)
        KCONV = 4
        EPS = 1e-06
        KEY_DIM = H * DK
        VAL_DIM = H * DV
        CONV_DIM = 2 * KEY_DIM + VAL_DIM
        b_, t_, _ = hidden_states.shape
        mixed = jnp.einsum('bth,ch->btc', hidden_states, qkv_w)
        x = mixed.transpose(0, 2, 1)
        x = lax.conv_general_dilated(x, conv_w, window_strides=(1,), padding=[(KCONV - 1, 0)], feature_group_count=CONV_DIM, dimension_numbers=('NCH', 'OIH', 'NCH'))
        mixed = x.transpose(0, 2, 1)
        z = jnp.einsum('bth,vh->btv', hidden_states, z_w).reshape(b_, t_, H, DV)
        bb = jnp.einsum('bth,nh->btn', hidden_states, b_w)
        aa = jnp.einsum('bth,nh->btn', hidden_states, a_w)
        q, k, v = jnp.split(mixed, 3, axis=-1)
        q = q.reshape(b_, t_, H, DK)
        k = k.reshape(b_, t_, H, DK)
        v = v.reshape(b_, t_, H, DV)
        beta = jax.nn.sigmoid(bb)
        g = -jnp.exp(A_log) * jax.nn.softplus(aa + dt_bias)
        alpha = jnp.exp(g)

        def step(S, inp):
            q_t, k_t, v_t, beta_t, alpha_t = inp
            S = S * alpha_t[..., None, None]
            kv = jnp.einsum('bhk,bhkv->bhv', k_t, S)
            S = S + jnp.einsum('bhk,bhv->bhkv', k_t, (v_t - kv) * beta_t[..., None])
            o_t = jnp.einsum('bhk,bhkv->bhv', q_t, S)
            return (S, o_t)
        qt = q.transpose(1, 0, 2, 3)
        kt = k.transpose(1, 0, 2, 3)
        vt = v.transpose(1, 0, 2, 3)
        bt = beta.transpose(1, 0, 2)
        at = alpha.transpose(1, 0, 2)
        S0 = jnp.zeros((b_, H, DK, DV), hidden_states.dtype)
        _, o = lax.scan(step, S0, (qt, kt, vt, bt, at))
        o = o.transpose(1, 0, 2, 3)
        var = jnp.mean(jnp.square(o), axis=-1, keepdims=True)
        o = o * lax.rsqrt(var + EPS) * norm_w
        o = o * (z * jax.nn.sigmoid(z))
        out = jnp.einsum('btv,hv->bth', o.reshape(b_, t_, VAL_DIM), out_w)
        return out

    def _L2_xattn_ref(q, k, v, attn_mask, Wq, bq, Wk, bk, Wv, bv, Wo, bo):
        import jax, jax.numpy as jnp
        import numpy as np
        B, T, S, E, H = (2, 256, 256, 128, 16)
        HD = E // H
        bsz, tgt_len, embed_dim = q.shape
        src_len = k.shape[1]
        qh = (q @ Wq.T + bq).reshape(bsz, tgt_len, H, HD).transpose(0, 2, 1, 3)
        kh = (k @ Wk.T + bk).reshape(bsz, src_len, H, HD).transpose(0, 2, 1, 3)
        vh = (v @ Wv.T + bv).reshape(bsz, src_len, H, HD).transpose(0, 2, 1, 3)
        scale = 1.0 / jnp.sqrt(jnp.asarray(HD, qh.dtype))
        attn = jnp.einsum('bhtd,bhsd->bhts', qh, kh) * scale
        attn = jnp.where(attn_mask != 0, jnp.asarray(-10000.0, attn.dtype), attn)
        attn = jax.nn.softmax(attn, axis=-1)
        out = jnp.einsum('bhts,bhsd->bhtd', attn, vh)
        out = out.transpose(0, 2, 1, 3).reshape(bsz, tgt_len, embed_dim)
        return out @ Wo.T + bo

    def _L2_ffn_ref(hidden_states, gate_w, w_gate, w_up, w_down):
        import jax, jax.numpy as jnp
        import numpy as np
        TOP_K = 8
        B, S, D = hidden_states.shape
        E = gate_w.shape[0]
        x = hidden_states.reshape(-1, D)
        logits = x.astype(jnp.float32) @ gate_w.astype(jnp.float32).T
        scores = jax.nn.softmax(logits, axis=-1)
        topk_w, topk_ids = jax.lax.top_k(scores, TOP_K)
        topk_w = topk_w / (topk_w.sum(axis=-1, keepdims=True) + 1e-20)
        flat_ids = topk_ids.reshape(-1)
        sort_idx = jnp.argsort(flat_ids)
        sorted_tokens = x[sort_idx // TOP_K]
        group_sizes = jnp.zeros((E,), jnp.int32).at[flat_ids].add(1)
        g = jax.lax.ragged_dot(sorted_tokens, jnp.swapaxes(w_gate, 1, 2), group_sizes)
        u = jax.lax.ragged_dot(sorted_tokens, jnp.swapaxes(w_up, 1, 2), group_sizes)
        h = jax.nn.silu(g) * u
        out = jax.lax.ragged_dot(h, jnp.swapaxes(w_down, 1, 2), group_sizes)
        unsorted = jnp.zeros_like(out).at[sort_idx].set(out)
        y = (unsorted.reshape(B * S, TOP_K, D) * topk_w[..., None]).sum(axis=1)
        return y.reshape(B, S, D)

    def _L3_attn_ref(x, Wq, bq, Wk, bk, Wv, bv, Wo, bo, gamma, beta):
        import jax, jax.numpy as jnp
        import numpy as np
        import math
        H = 16
        N_EMBD = 128
        EPS = 1e-05
        B, T, _ = x.shape
        Dh = N_EMBD // H

        def split_heads(y):
            return y.reshape(B, T, H, Dh).transpose(0, 2, 1, 3)
        q = split_heads(x @ Wq + bq)
        k = split_heads(x @ Wk + bk)
        v = split_heads(x @ Wv + bv)
        att = jnp.einsum('bhtd,bhsd->bhts', q, k) * (1.0 / math.sqrt(Dh))
        causal = jnp.tril(jnp.ones((T, T), dtype=bool))
        att = jnp.where(causal[None, None], att, -jnp.inf)
        att = jax.nn.softmax(att, axis=-1)
        o = jnp.einsum('bhts,bhsd->bhtd', att, v)
        o = o.transpose(0, 2, 1, 3).reshape(B, T, N_EMBD)
        y = o @ Wo + bo
        mu = jnp.mean(y, axis=-1, keepdims=True)
        var = jnp.var(y, axis=-1, keepdims=True)
        return (y - mu) * jax.lax.rsqrt(var + EPS) * gamma + beta

    def _L3_xattn_ref(query, key, value, Wq, bq, Wk, bk, Wv, bv, Wo, bo):
        import jax, jax.numpy as jnp
        import numpy as np
        EMB = 128
        HEADS = 16
        HEAD_DIM = EMB // HEADS
        B, S = (2, 256)
        b = query.shape[0]

        def proj(x, W, bias):
            y = jnp.einsum('bse,ef->bsf', x, W) + bias
            return y.reshape(b, -1, HEADS, HEAD_DIM).transpose(0, 2, 1, 3)
        Q = proj(query, Wq, bq)
        K = proj(key, Wk, bk)
        V = proj(value, Wv, bv)
        scores = jnp.einsum('bhqd,bhkd->bhqk', Q, K) / np.sqrt(HEAD_DIM).astype(np.float32)
        weights = jax.nn.softmax(scores, axis=-1)
        ctx = jnp.einsum('bhqk,bhkd->bhqd', weights, V)
        ctx = ctx.transpose(0, 2, 1, 3).reshape(b, -1, EMB)
        return jnp.einsum('bse,ef->bsf', ctx, Wo) + bo

    def _L3_ffn_ref(x, Wm, Wp, Wc1, Wc2):
        import jax, jax.numpy as jnp
        import numpy as np
        N_EMBD = 128
        ITER_SIZE = 4 * N_EMBD
        FULL_SIZE = 3 * ITER_SIZE
        R = 0.7

        def _topk_mask(ck, k):
            probs = jax.nn.softmax(ck, axis=-1)
            _, idx = jax.lax.top_k(probs, k)
            b = jnp.arange(probs.shape[0])[:, None]
            return jnp.zeros_like(probs).at[b, idx].set(1.0)

        def _forward(x, Wm, Wp, Wc1, Wc2):
            B = x.shape[0]
            base = jnp.zeros((B, FULL_SIZE), x.dtype).at[:, :ITER_SIZE].set(1.0)

            def step(carry, _):
                xc, active, history, done = carry
                h = jnp.einsum('btc,fc->btf', xc, Wm) * active[:, None, :]
                h = jax.nn.relu(h)
                x_new = jnp.einsum('btf,cf->btc', h, Wp)
                pooled = x_new.mean(axis=1)
                ck = jnp.einsum('bd,fd->bf', jax.nn.relu(jnp.einsum('bc,dc->bd', pooled, Wc1)), Wc2)
                new_mask = _topk_mask(ck, ITER_SIZE)
                combined = jnp.clip(history + new_mask, 0.0, 1.0)
                novelty = (combined - history).sum(axis=1).mean() / ITER_SIZE
                done_next = jnp.logical_or(done, novelty < R)
                x_out = jnp.where(done, xc, x_new)
                active_out = jnp.where(done, active, new_mask)
                history_out = jnp.where(done, history, combined)
                return ((x_out, active_out, history_out, done_next), None)
            init = (x, base, base, jnp.array(False))
            (x_fin, _, _, _), _ = jax.lax.scan(step, init, None, length=3)
            return x_fin
        return _forward(x, Wm, Wp, Wc1, Wc2)
    x = x + _L0_attn_ref(_layernorm(x, axis=-1), L0_attn_ln1_g, L0_attn_ln1_b, L0_attn_wq, L0_attn_wk, L0_attn_wv, L0_attn_wo, L0_attn_ln2_g, L0_attn_ln2_b, L0_attn_w1, L0_attn_w2)
    x = x + _L0_xattn_ref(_layernorm(x, axis=-1), ctx_1024, mask_BxSxS2_bk0, L0_xattn_Wq, L0_xattn_Wkv, L0_xattn_Wproj, L0_xattn_bproj)
    x = x + _L0_ffn_ref(_layernorm(x, axis=-1), L0_ffn_gate_w, L0_ffn_gate_b, L0_ffn_w1, L0_ffn_b1, L0_ffn_w2, L0_ffn_b2)
    x = x + _L1_attn_ref(_layernorm(x, axis=-1), L1_attn_rms_weight, L1_attn_w_A, L1_attn_b_A, L1_attn_w_x, L1_attn_w_sidegate, L1_attn_w_output, L1_attn_w_o)
    x = x + _L1_xattn_ref(_layernorm(x, axis=-1), ctx_1024, L1_xattn_Wq, L1_xattn_Wk, L1_xattn_Wv)
    x = x + _L1_ffn_ref(_layernorm(x, axis=-1), L1_ffn_norm1_w, L1_ffn_w1, L1_ffn_act_scale, L1_ffn_act_bias, L1_ffn_norm2_w, L1_ffn_w2)
    x = x + _L2_attn_ref(_layernorm(x, axis=-1), L2_attn_qkv_w, L2_attn_z_w, L2_attn_b_w, L2_attn_a_w, L2_attn_conv_w, L2_attn_dt_bias, L2_attn_A_log, L2_attn_norm_w, L2_attn_out_w)
    x = x + _L2_xattn_ref(_layernorm(x, axis=-1), ctx_1024, ctx_1024, mask_SxS2_ik1, L2_xattn_Wq, L2_xattn_bq, L2_xattn_Wk, L2_xattn_bk, L2_xattn_Wv, L2_xattn_bv, L2_xattn_Wo, L2_xattn_bo)
    x = x + _L2_ffn_ref(_layernorm(x, axis=-1), L2_ffn_gate_w, L2_ffn_w_gate, L2_ffn_w_up, L2_ffn_w_down)
    x = x + _L3_attn_ref(_layernorm(x, axis=-1), L3_attn_Wq, L3_attn_bq, L3_attn_Wk, L3_attn_bk, L3_attn_Wv, L3_attn_bv, L3_attn_Wo, L3_attn_bo, L3_attn_gamma, L3_attn_beta)
    x = x + _L3_xattn_ref(_layernorm(x, axis=-1), ctx_1024, ctx_1024, L3_xattn_Wq, L3_xattn_bq, L3_xattn_Wk, L3_xattn_bk, L3_xattn_Wv, L3_xattn_bv, L3_xattn_Wo, L3_xattn_bo)
    x = x + _L3_ffn_ref(_layernorm(x, axis=-1), L3_ffn_Wm, L3_ffn_Wp, L3_ffn_Wc1, L3_ffn_Wc2)
    return x

_drawn_inputs = setup_inputs


def setup_inputs(seed=0):
    import zlib

    import numpy as np

    out = dict(_drawn_inputs(seed))
    spreads = {'L0_attn_ln1_g': (1.0, 0.6),
     'L0_attn_ln1_b': (0.0, 0.618),
     'L0_attn_ln2_g': (1.0, 0.6),
     'L0_attn_ln2_b': (0.0, 0.473),
     'L0_xattn_bproj': (0.0, 0.1),
     'L0_ffn_gate_b': (0.0, 0.1),
     'L0_ffn_b1': (0.0, 0.29),
     'L0_ffn_b2': (0.0, 0.1),
     'L1_attn_rms_weight': (1.0, 0.6),
     'L1_attn_b_A': (0.0, 0.8),
     'L1_ffn_norm1_w': (1.0, 0.6),
     'L1_ffn_norm2_w': (1.0, 0.6),
     'L2_attn_dt_bias': (1.0, 0.6),
     'L2_attn_norm_w': (1.0, 0.6),
     'L3_attn_bq': (0.0, 2.0),
     'L3_attn_bk': (0.0, 2.0),
     'L3_attn_bv': (0.0, 0.341),
     'L3_attn_bo': (0.0, 0.1),
     'L3_attn_gamma': (1.0, 0.6),
     'L3_attn_beta': (0.0, 0.27),
     'L3_xattn_bq': (0.0, 2.0),
     'L3_xattn_bk': (0.0, 2.0),
     'L3_xattn_bv': (0.0, 0.304),
     'L3_xattn_bo': (0.0, 0.272)}
    factors = {'L0_attn_wq': 8.0,
     'L0_attn_wk': 8.0,
     'L0_attn_wv': 5.471,
     'L0_attn_wo': 4.94,
     'L1_attn_w_A': 8.0,
     'L1_attn_w_x': 8.0,
     'L1_attn_w_sidegate': 8.0,
     'L1_attn_w_output': 8.0,
     'L1_attn_w_o': 8.0,
     'L2_attn_qkv_w': 2.958,
     'L2_attn_z_w': 2.991,
     'L2_attn_b_w': 64.0,
     'L2_attn_a_w': 8.0,
     'L2_attn_conv_w': 2.955,
     'L2_attn_A_log': 8.0,
     'L2_attn_out_w': 2.959,
     'L2_xattn_bv': 34.061,
     'L2_xattn_bo': 35.897,
     'L2_ffn_gate_w': 8.0,
     'L2_ffn_w_gate': 8.0,
     'L2_ffn_w_up': 8.0,
     'L2_ffn_w_down': 8.0,
     'L3_attn_Wq': 21.466,
     'L3_attn_Wk': 8.0,
     'L3_ffn_Wm': 3.149}
    for name, (base, spread) in spreads.items():
        noise = np.random.default_rng([zlib.crc32(name.encode()), seed]).standard_normal(out[name].shape)
        drawn = base * np.exp(spread * noise) if base else spread * noise
        out[name] = jnp.asarray(drawn.astype(out[name].dtype))
    for name, factor in factors.items():
        out[name] = (out[name] * factor).astype(out[name].dtype)
    return out
```

```python
from contextlib import ExitStack, contextmanager

import numpy as np
import concourse.bass as bass
from concourse import mybir

ALU = mybir.AluOpType
ACT = mybir.ActivationFunctionType
AX = mybir.AxisListType
F32 = mybir.dt.float32
BF16 = mybir.dt.bfloat16
I32 = mybir.dt.int32

B, S, D, M = 4, 512, 128, 32
T = B * S
P = 128
NT, TB = T // P, S // P
H, HD = 16, 8
LN_EXP = "natural_log_exp_and_others"
MAGIC = 12582912.0


class Kit:
    pass


@contextmanager
def stage(nc, names):
    sems = {n: nc.alloc_semaphore(f"{n}_{nc.next_id()}") for n in names.split()}
    with nc.Block() as block:
        yield block, sems
    nc.clear_and_free_semaphores(list(sems.values()))
    nc.all_engine_barrier()


def after(eng, sem, n):
    if n > 0:
        eng.wait_ge(sem, n)


class Chain:

    def __init__(self, eng, sem):
        self.eng, self.sem, self.n = eng, sem, 0

    def __call__(self, ins):
        self.n += 1
        ins.then_inc(self.sem, 1)
        self.eng.wait_ge(self.sem, self.n)


def sl(i, n=S):
    return slice(i * n, (i + 1) * n)


def norm(nc, k, src, dst, eps, inner=None):
    with ExitStack() as mem, stage(nc, "mean centred squared var ln inv used ratio ln2 inv2 chain") as (block, s):
        sb = lambda n, w: mem.enter_context(nc.sbuf_tensor(f"{n}_{nc.next_id()}", [P, w], F32))
        xc, sq, rs = sb("xc", T), sb("sq", 2 * S), sb("rs", 2 * S)
        tt = sb("tt", 2 * S) if inner else None

        @block.tensor
        def _(pe):
            for b in range(B + 1):
                if b < B:
                    after(pe, s["centred"], b - 1)
                    nc.tensor.matmul(k.ps[b % 2][:, :], k.mean, src[:, sl(b)], start=True, stop=True).then_inc(s["mean"], 1)
                if b:
                    pe.wait_ge(s["squared"], b)
                    after(pe, s["used"], b - 2)
                    nc.tensor.matmul(k.ps[2 + (b - 1) % 2][:, :], k.mean, sq[:, sl((b - 1) % 2)], start=True, stop=True).then_inc(s["var"], 1)

        @block.scalar
        def _(act):
            nc.scalar.preload_act_table_set(LN_EXP)
            for b in range(B + 1):
                if b < B:
                    act.wait_ge(s["centred"], b + 1)
                    after(act, s["var"], b - 1)
                    nc.scalar.activation(sq[:, sl(b % 2)], xc[:, sl(b)], ACT.Square).then_inc(s["squared"], 1)
                if b:
                    c = b - 1
                    r = rs[:, sl(c % 2)]
                    act.wait_ge(s["var"], c + 1)
                    after(act, s["used"], c - 1)
                    nc.scalar.activation(r, k.ps[2 + c % 2][:, :], ACT.Ln, bias=k.eps[eps]).then_inc(s["ln"], 1)
                    act.wait_ge(s["ln"], c + 1)
                    nc.scalar.activation(r, r, ACT.Exp, scale=-0.5).then_inc(s["inv"], 1)
                    if inner:
                        t = tt[:, sl(c % 2)]
                        act.wait_ge(s["ratio"], c + 1)
                        nc.scalar.activation(t, t, ACT.Ln, bias=k.eps[inner[0]]).then_inc(s["ln2"], 1)
                        act.wait_ge(s["ln2"], c + 1)
                        nc.scalar.activation(t, t, ACT.Exp, scale=-0.5).then_inc(s["inv2"], 1)

        @block.vector
        def _(dve):
            link = Chain(dve, s["chain"])
            for b in range(B + 1):
                if b < B:
                    dve.wait_ge(s["mean"], b + 1)
                    nc.vector.tensor_tensor(xc[:, sl(b)], src[:, sl(b)], k.ps[b % 2][:, :], ALU.subtract).then_inc(s["centred"], 1)
                if b:
                    c = b - 1
                    r, t = rs[:, sl(c % 2)], tt[:, sl(c % 2)] if inner else None
                    dve.wait_ge(s["inv"], c + 1)
                    dve.wait_ge(s["centred"], c + 1)
                    out = nc.vector.tensor_tensor(dst[:, sl(c)], xc[:, sl(c)], r, ALU.mult)
                    if not inner:
                        out.then_inc(s["used"], 1)
                        continue
                    _, gain, bias, dst2 = inner
                    link(out)
                    link(nc.vector.tensor_tensor(t, r, r, ALU.mult))
                    nc.vector.tensor_tensor(t, t, k.ps[2 + c % 2][:, :], ALU.mult).then_inc(s["ratio"], 1)
                    dve.wait_ge(s["inv2"], c + 1)
                    if bias is None:
                        nc.vector.scalar_tensor_tensor(out=dst2[:, sl(c)], in0=dst[:, sl(c)], scalar=gain, in1=t, op0=ALU.mult, op1=ALU.mult).then_inc(s["used"], 1)
                    else:
                        link(nc.vector.tensor_tensor(t, dst[:, sl(c)], t, ALU.mult))
                        nc.vector.tensor_scalar(dst2[:, sl(c)], t, gain, bias, ALU.mult, ALU.add).then_inc(s["used"], 1)


def l0_attention(nc, k, y, a, res):
    names = ("k_tok v_tok q_feat kv z_sum num den proj k_min k_exp k_phi v_copy q_min q_exp q_phi "
             "kv_mask recip o_ready done chain")
    with ExitStack() as mem, stage(nc, names) as (block, s):
        sb = lambda n, w: mem.enter_context(nc.sbuf_tensor(f"{n}_{nc.next_id()}", [P, w], F32))
        km, ke, vt, qm, qe, o, rec, kvm, zm = (sb(n, w) for n, w in (("km", S), ("ke", S), ("vt", S), ("qm", S),
                                               ("qe", S), ("o", S), ("rec", S), ("kvm", P), ("zm", P)))
        pk, pv, pq, pkv, pn, pd, po = k.ps[:7]

        @block.tensor
        def _(pe):
            for b in range(B):
                after(pe, s["q_phi"], b)
                after(pe, s["v_copy"], b)
                for ps, w, sem in ((pk, "wk", s["k_tok"]), (pv, "wv", s["v_tok"])):
                    for t in range(TB):
                        mm = nc.tensor.matmul(ps[:, sl(t, P)], a[:, sl(b * TB + t, P)], k.w["L0_attn_" + w], start=True, stop=True)
                    mm.then_inc(sem, 1)
                nc.tensor.matmul(pq[:, :], k.w["L0_attn_wq"], a[:, sl(b)], start=True, stop=True).then_inc(s["q_feat"], 1)
                pe.wait_ge(s["k_phi"], b + 1)
                pe.wait_ge(s["v_copy"], b + 1)
                after(pe, s["kv_mask"], b)
                for t in range(TB):
                    nc.tensor.matmul(pkv[:, 0:P], ke[:, sl(t, P)], vt[:, sl(t, P)], start=t == 0, stop=t == TB - 1)
                for t in range(TB):
                    mm = nc.tensor.matmul(pkv[:, P:P + 1], ke[:, sl(t, P)], k.ones[:, 0:1], start=t == 0, stop=t == TB - 1)
                mm.then_inc(s["kv"], 1)
                pe.wait_ge(s["kv_mask"], b + 1)
                pe.wait_ge(s["q_phi"], b + 1)
                after(pe, s["o_ready"], b)
                nc.tensor.matmul(pn[:, :], kvm[:, :], qe[:, :], start=True, stop=True).then_inc(s["num"], 1)
                nc.tensor.matmul(pd[:, :], zm[:, :], qe[:, :], start=True, stop=True).then_inc(s["den"], 1)
                pe.wait_ge(s["o_ready"], b + 1)
                after(pe, s["done"], b)
                nc.tensor.matmul(po[:, :], k.w["L0_attn_wo"], o[:, :], start=True, stop=True).then_inc(s["proj"], 1)

        @block.scalar
        def _(act):
            for b in range(B):
                act.wait_ge(s["v_tok"], b + 1)
                after(act, s["kv"], b)
                nc.scalar.activation(vt[:, :], pv[:, :], ACT.Copy).then_inc(s["v_copy"], 1)
                act.wait_ge(s["k_min"], b + 1)
                nc.scalar.activation(ke[:, :], km[:, :], ACT.Exp).then_inc(s["k_exp"], 1)
                act.wait_ge(s["q_min"], b + 1)
                nc.scalar.activation(qe[:, :], qm[:, :], ACT.Exp).then_inc(s["q_exp"], 1)

        @block.vector
        def _(dve):
            link = Chain(dve, s["chain"])
            for b in range(B):
                dve.wait_ge(s["k_tok"], b + 1)
                after(dve, s["kv"], b)
                nc.vector.tensor_scalar(km[:, :], pk[:, :], 0.0, None, ALU.min).then_inc(s["k_min"], 1)
                dve.wait_ge(s["q_feat"], b + 1)
                after(dve, s["den"], b)
                nc.vector.tensor_scalar(qm[:, :], pq[:, :], 0.0, None, ALU.min).then_inc(s["q_min"], 1)
                dve.wait_ge(s["k_exp"], b + 1)
                nc.vector.scalar_tensor_tensor(out=ke[:, :], in0=pk[:, :], scalar=0.0, in1=ke[:, :], op0=ALU.max, op1=ALU.add).then_inc(s["k_phi"], 1)
                dve.wait_ge(s["q_exp"], b + 1)
                nc.vector.scalar_tensor_tensor(out=qe[:, :], in0=pq[:, :], scalar=0.0, in1=qe[:, :], op0=ALU.max, op1=ALU.add).then_inc(s["q_phi"], 1)
                dve.wait_ge(s["kv"], b + 1)
                after(dve, s["den"], b)
                nc.vector.tensor_tensor(kvm[:, :], k.heads, pkv[:, 0:P], ALU.mult)
                nc.vector.tensor_scalar(zm[:, :], k.heads, pkv[:, P:P + 1], None, ALU.mult).then_inc(s["kv_mask"], 1)
                dve.wait_ge(s["den"], b + 1)
                link(nc.vector.tensor_scalar(rec[:, :], pd[:, :], 1e-6, None, ALU.add))
                link(nc.vector.reciprocal(rec[:, :], rec[:, :]))
                after(dve, s["proj"], b)
                nc.vector.tensor_tensor(o[:, :], rec[:, :], pn[:, :], ALU.mult).then_inc(s["o_ready"], 1)
                dve.wait_ge(s["proj"], b + 1)
                nc.vector.tensor_tensor(res[:, sl(b)], y[:, sl(b)], po[:, :], ALU.add).then_inc(s["done"], 1)


def l0_lookup_mlp(nc, k, h, y, x):
    C = 4
    with ExitStack() as mem, stage(nc, "up rounded grid act down chain done") as (block, s):
        sb = lambda n, w: mem.enter_context(nc.sbuf_tensor(f"{n}_{nc.next_id()}", [P, w], F32))
        r, g = sb("r", 2 * S), sb("g", 2 * S)
        w1, w2 = k.w["L0_attn_w1"], k.w["L0_attn_w2"]

        @block.tensor
        def _(pe):
            def down(i):
                b, c = divmod(i, C)
                pe.wait_ge(s["act"], i + 1)
                if c == 0:
                    after(pe, s["done"], b)
                nc.tensor.matmul(k.ps[4][:, :], w2[:, sl(c, P)], g[:, sl(i % 2)], start=c == 0, stop=c == C - 1).then_inc(s["down"], 1)

            for i in range(B * C):
                after(pe, s["grid"], i - 3)
                nc.tensor.matmul(k.ps[i % 4][:, :], w1[:, sl(i % C, P)], h[:, sl(i // C)], start=True, stop=True).then_inc(s["up"], 1)
                if i:
                    down(i - 1)
            down(B * C - 1)

        def finish(dve, link, b):
            dve.wait_ge(s["down"], C * (b + 1))
            link(nc.vector.tensor_tensor(y[:, sl(b)], y[:, sl(b)], k.ps[4][:, :], ALU.add))
            nc.vector.tensor_tensor(x[:, sl(b)], x[:, sl(b)], y[:, sl(b)], ALU.add).then_inc(s["done"], 1)

        @block.vector
        def _(dve):
            link = Chain(dve, s["chain"])
            for i in range(B * C):
                b, c = divmod(i, C)
                rr = r[:, sl(i % 2)]
                dve.wait_ge(s["up"], i + 1)
                after(dve, s["act"], i - 1)
                link(nc.vector.tensor_scalar(rr, k.ps[i % 4][:, :], 10.0, MAGIC, ALU.mult, ALU.add))
                link(nc.vector.tensor_scalar(rr, rr, MAGIC, -128.0, ALU.subtract, ALU.max))
                nc.vector.tensor_scalar(rr, rr, 127.0, 0.1, ALU.min, ALU.mult).then_inc(s["grid"], 1)
                if c == 0 and b:
                    finish(dve, link, b - 1)
            finish(dve, link, B - 1)

        @block.scalar
        def _(act):
            for i in range(B * C):
                act.wait_ge(s["grid"], i + 1)
                after(act, s["down"], i - 1)
                nc.scalar.activation(g[:, sl(i % 2)], r[:, sl(i % 2)], ACT.Gelu_apprx_tanh).then_inc(s["act"], 1)


def project(nc, k, jobs):
    with stage(nc, "product copied") as (block, s):
        steps = [(w, src, dst, bias, scale, slice(c, min(c + S, n)))
                 for w, src, n, dst, bias, scale in jobs for c in range(0, n, S)]

        @block.tensor
        def _(pe):
            for i, (w, src, dst, bias, scale, c) in enumerate(steps):
                after(pe, s["copied"], i - 3)
                nc.tensor.matmul(k.ps[i % 4][0:w.shape[-1], 0:c.stop - c.start], w, src[:, c], start=True, stop=True).then_inc(s["product"], 1)

        @block.vector
        def _(dve):
            for i, (w, src, dst, bias, scale, c) in enumerate(steps):
                dve.wait_ge(s["product"], i + 1)
                nc.vector.tensor_scalar(dst[:, c], k.ps[i % 4][0:w.shape[-1], 0:c.stop - c.start],
                                        0.0 if bias is None else bias, scale, ALU.add, ALU.mult).then_inc(s["copied"], 1)


def cross_attention(nc, k, xn, x, q, pre, names, scale, biased, mask=None, fill=0.0, spare=False):
    wq, wk, wv, wo = (k.w[pre + n] for n in names)
    bq, bk, bo = (k.w[pre + n] if biased else None for n in ("bq", "bk", "bo"))
    bo = k.w[pre + "bproj"] if bo is None else bo
    with ExitStack() as mem:
        sb = lambda n, w, p=P: mem.enter_context(nc.sbuf_tensor(f"{n}_{nc.next_id()}", [p, w], F32))
        kt, kbig, vbig = sb("kt", B * M), xn, sb("vbig", B * S)
        crep = sb("crep", B * P)
        project(nc, k, [(wk, k.ctx, B * M, kt, bk, 1.0), (wq, xn, T, q, bq, scale)])
        with stage(nc, "repeated rows added spread") as (block, s):
            @block.vector
            def _(dve):
                for b in range(B):
                    nc.vector.tensor_copy(crep[:, sl(b, P)].rearrange("p (r m) -> p r m", r=4),
                                          k.ctx[:, sl(b, M)].unsqueeze(1).broadcast_to([P, 4, M])).then_inc(s["repeated"], 1)
                for b in range(B):
                    nc.vector.tensor_tensor(kbig[:, sl(b)].rearrange("p (h m) -> p h m", h=H),
                                            kt[:, sl(b, M)].unsqueeze(1).broadcast_to([P, H, M]),
                                            k.w["head_cols"].unsqueeze(2).broadcast_to([P, H, M]), ALU.mult).then_inc(s["spread"], 1)
                for b in range(B):
                    v = k.ps[b][:, 0:P]
                    dve.wait_ge(s["rows"], b + 1)
                    if biased:
                        nc.vector.tensor_tensor(crep[:, sl(b, P)], v, k.w[pre + "bv"], ALU.add).then_inc(s["added"], 1)
                        dve.wait_ge(s["added"], b + 1)
                        v = crep[:, sl(b, P)]
                    nc.vector.tensor_tensor(vbig[:, sl(b)].rearrange("p (c e) -> p c e", c=4),
                                            v.unsqueeze(1).broadcast_to([P, 4, P]),
                                            k.w["head_rows"].rearrange("p (c e) -> p c e", c=4), ALU.mult).then_inc(s["spread"], 1)
                dve.wait_ge(s["spread"], 2 * B)

            @block.tensor
            def _(pe):
                for b in range(B):
                    pe.wait_ge(s["repeated"], b + 1)
                    nc.tensor.matmul(k.ps[b][:, 0:P], crep[:, sl(b, P)], wv, start=True, stop=True).then_inc(s["rows"], 1)

        E = S + H
        keep, neg = (mask, sb("neg", mask.shape[1])) if mask is not None else (None, None)
        d, p, pt = sb("d", 2 * E), sb("p", 2 * E), sb("pt", 2 * 4 * S)
        spt, rmax, o, rec = sb("spt", 2 * S, H), sb("rmax", NT * H), sb("o", S), sb("rec", S)
        sems = "scores max_ready centred weights turned copied values log inv normed proj done chain"
        with stage(nc, sems) as (block, s):
            turned = k.ps[2:4]

            @block.tensor
            def _(pe):
                def attend(b):
                    pe.wait_ge(s["copied"], TB * (b + 1))
                    after(pe, s["normed"], b)
                    for c in range(4):
                        nc.tensor.matmul(k.ps[4][:, :], vbig[:, sl(4 * b + c, P)], pt[:, sl(4 * (b % 2) + c)], start=c == 0, stop=c == 3)
                    for c in range(4):
                        mm = nc.tensor.matmul(k.ps[5][:, :], k.w["head_rows"][:, sl(c, P)], pt[:, sl(4 * (b % 2) + c)],
                                              start=c == 0, stop=c == 3 and not spare)
                    if spare:
                        mm = nc.tensor.matmul(k.ps[5][:, :], k.w["head_of"][0:H, :], spt[:, sl(b % 2)], start=False, stop=True)
                    mm.then_inc(s["values"], 1)

                def out(b):
                    pe.wait_ge(s["normed"], b + 1)
                    after(pe, s["done"], b)
                    nc.tensor.matmul(k.ps[6][:, :], wo, o[:, :], start=True, stop=True).then_inc(s["proj"], 1)

                def turn(i):
                    pe.wait_ge(s["weights"], i + 1)
                    after(pe, s["copied"], i - 1)
                    for c in range(4):
                        mm = nc.tensor.transpose(turned[i % 2][:, sl(c, P)], p[:, (i % 2) * E + c * P:(i % 2) * E + (c + 1) * P], k.ident)
                    if spare:
                        after(pe, s["copied"], i)
                        mm = nc.tensor.transpose(k.ps[7][0:H, 0:P], p[:, (i % 2) * E + S:(i % 2 + 1) * E], k.ident)
                    mm.then_inc(s["turned"], 1)

                for i in range(NT + 1):
                    if i < NT:
                        b = i // TB
                        after(pe, s["centred"], i - 1)
                        nc.tensor.matmul(k.ps[i % 2][:, :], q[:, sl(i, P)], kbig[:, sl(b)], start=True, stop=True).then_inc(s["scores"], 1)
                    if i:
                        turn(i - 1)
                    if i % TB == 1 and i > TB:
                        attend(i // TB - 1)
                    if i % TB == 2 and i > TB:
                        out(i // TB - 1)
                attend(B - 1)
                out(B - 1)

            @block.vector
            def _(dve):
                link = Chain(dve, s["chain"])
                if mask is not None:
                    link(nc.vector.tensor_scalar(neg[:, :], mask, fill, None, ALU.mult))
                    link(nc.vector.tensor_scalar(keep, mask, -1.0, 1.0, ALU.mult, ALU.add))

                def normalise(b):
                    dve.wait_ge(s["inv"], b + 1)
                    after(dve, s["proj"], b)
                    nc.vector.tensor_tensor(o[:, :], rec[:, :], k.ps[4][:, :], ALU.mult).then_inc(s["normed"], 1)

                def finish(b):
                    dve.wait_ge(s["proj"], b + 1)
                    nc.vector.scalar_tensor_tensor(out=x[:, sl(b)], in0=k.ps[6][:, :], scalar=bo, in1=x[:, sl(b)],
                                                   op0=ALU.add, op1=ALU.add).then_inc(s["done"], 1)

                for i in range(NT):
                    heads = lambda a: a.rearrange("p (h m) -> p h m", h=H)
                    dd = d[:, (i % 2) * E:(i % 2) * E + S]
                    mx = rmax[:, sl(i, H)]
                    dve.wait_ge(s["scores"], i + 1)
                    after(dve, s["weights"], i - 1)
                    sc = k.ps[i % 2][:, :]
                    if mask is not None:
                        span = lambda a: a[:, sl(i % (mask.shape[1] // M), M)].unsqueeze(1).broadcast_to([P, H, M])
                        link(nc.vector.tensor_tensor(heads(dd), heads(sc), span(keep), ALU.mult))
                        link(nc.vector.tensor_tensor(heads(dd), heads(dd), span(neg), ALU.add))
                        sc = dd
                    link(nc.vector.tensor_reduce(mx, heads(sc), AX.X, ALU.max))
                    if spare:
                        link(nc.vector.tensor_scalar(mx, mx, 0.0, None, ALU.max))
                        nc.vector.tensor_scalar(d[:, (i % 2) * E + S:(i % 2 + 1) * E], mx, -1.0, None, ALU.mult)
                    nc.vector.tensor_tensor(heads(dd), heads(sc), mx.unsqueeze(2).broadcast_to([P, H, M]), ALU.subtract).then_inc(s["centred"], 1)
                    if i % TB == 2 and i > TB:
                        normalise(i // TB - 1)
                    if i % TB == 3 and i > TB:
                        finish(i // TB - 1)
                normalise(B - 1)
                finish(B - 1)

            @block.scalar
            def _(act):
                nc.scalar.preload_act_table_set(LN_EXP)

                def copy(i):
                    b, t = divmod(i, TB)
                    act.wait_ge(s["turned"], i + 1)
                    after(act, s["values"], b - 1)
                    dst = pt[:, (b % 2) * 4 * S:(b % 2 + 1) * 4 * S].rearrange("p (c t) -> p c t", c=4)[:, :, sl(t, P)]
                    ins = nc.scalar.activation(dst, turned[i % 2][:, :].rearrange("p (c t) -> p c t", c=4), ACT.Copy)
                    if spare:
                        ins = nc.scalar.activation(spt[:, (b % 2) * S + t * P:(b % 2) * S + (t + 1) * P], k.ps[7][0:H, 0:P], ACT.Copy)
                    ins.then_inc(s["copied"], 1)

                def invert(b):
                    act.wait_ge(s["values"], b + 1)
                    after(act, s["normed"], b)
                    nc.scalar.activation(rec[:, :], k.ps[5][:, :], ACT.Ln).then_inc(s["log"], 1)
                    act.wait_ge(s["log"], b + 1)
                    nc.scalar.activation(rec[:, :], rec[:, :], ACT.Exp, scale=-1.0).then_inc(s["inv"], 1)

                for i in range(NT + 1):
                    if i < NT:
                        w = S + (H if spare else 0)
                        act.wait_ge(s["centred"], i + 1)
                        after(act, s["turned"], i - 1)
                        nc.scalar.activation(p[:, (i % 2) * E:(i % 2) * E + w], d[:, (i % 2) * E:(i % 2) * E + w], ACT.Exp).then_inc(s["weights"], 1)
                    if i:
                        copy(i - 1)
                    if i % TB == 1 and i > TB:
                        invert(i // TB - 1)
                invert(B - 1)


def load_big(nc, k, name):
    with nc.Block() as block:
        @block.sync
        def _(sp):
            sp.dma_start(k.big[:, 0:k.ap[name].shape[1]], k.ap[name]).then_inc(k.big_loaded, 16)


def layer1(nc, k, x, y, a):
    norm(nc, k, x, y, 1e-5)
    cross_attention(nc, k, y, x, a, "L0_xattn_", ("Wq", "Wk", "Wv", "Wproj"), HD ** -0.5, False,
                    mask=k.mask0[:, :], fill=-1e30, spare=True)


def layer7(nc, k, x, y, a):
    norm(nc, k, x, y, 1e-5)
    cross_attention(nc, k, y, x, a, "L2_xattn_", ("Wq", "Wk", "Wv", "Wo"), HD ** -0.5, True,
                    mask=k.mask2[:, :], fill=-10000.0)


def layer10(nc, k, x, y, a):
    load_big(nc, k, "big3")
    norm(nc, k, x, y, 1e-5)
    cross_attention(nc, k, y, x, a, "L3_xattn_", ("Wq", "Wk", "Wv", "Wo"), HD ** -0.5, True)


def top2_weights(nc, k, xn, w):
    G = 8
    with ExitStack() as mem, stage(nc, "logits shifted exps done chain") as (block, s):
        sb = lambda n, w_: mem.enter_context(nc.sbuf_tensor(f"{n}_{nc.next_id()}", [P, w_], F32))
        lg, d, gt, eq, rank, mx, tot = (sb(n, c) for n, c in (("lg", NT * G), ("d", NT * G), ("gt", NT * G * G), ("eq", NT * G * G),
                                        ("rank", NT * G), ("mx", NT), ("tot", NT)))

        @block.tensor
        def _(pe):
            for i in range(NT):
                mm = nc.tensor.matmul(k.ps[0][:, sl(i, G)], xn[:, sl(i, P)], k.w["L0_ffn_gate_w"], start=True, stop=True)
            mm.then_inc(s["logits"], 1)

        @block.scalar
        def _(act):
            act.wait_ge(s["shifted"], 1)
            nc.scalar.activation(d[:, :], d[:, :], ACT.Exp).then_inc(s["exps"], 1)

        @block.vector
        def _(dve):
            link = Chain(dve, s["chain"])
            tile = lambda a: a.rearrange("p (t i) -> p t i", i=G)
            pair = lambda a: a[:, :].rearrange("p (t i j) -> p t i j", i=G, j=G)
            full = [P, NT, G, G]
            this = tile(lg[:, :]).unsqueeze(3).broadcast_to(full)
            other = tile(lg[:, :]).unsqueeze(2).broadcast_to(full)
            before = k.w["before8"].rearrange("p (i j) -> p i j", j=G).unsqueeze(1).broadcast_to(full)
            dve.wait_ge(s["logits"], 1)
            link(nc.vector.tensor_tensor(tile(lg[:, :]), tile(k.ps[0][:, 0:NT * G]),
                                         k.w["L0_ffn_gate_b"].unsqueeze(1).broadcast_to([P, NT, G]), ALU.add))
            link(nc.vector.tensor_reduce(mx[:, :], tile(lg[:, :]), AX.X, ALU.max))
            nc.vector.tensor_tensor(tile(d[:, :]), tile(lg[:, :]), mx[:, :].unsqueeze(2).broadcast_to([P, NT, G]), ALU.subtract).then_inc(s["shifted"], 1)
            nc.vector.tensor_tensor(pair(gt), other, this, ALU.is_gt)
            link(nc.vector.tensor_tensor(pair(eq), other, this, ALU.is_equal))
            link(nc.vector.tensor_tensor(pair(eq), pair(eq), before, ALU.mult))
            link(nc.vector.tensor_tensor(gt[:, :], gt[:, :], eq[:, :], ALU.add))
            link(nc.vector.tensor_reduce(rank[:, :], gt[:, :].rearrange("p (a j) -> p a j", j=G), AX.X, ALU.add))
            dve.wait_ge(s["exps"], 1)
            link(nc.vector.scalar_tensor_tensor(out=w[:, :], in0=rank[:, :], scalar=2.0, in1=d[:, :], op0=ALU.is_lt, op1=ALU.mult))
            link(nc.vector.tensor_reduce(tot[:, :], tile(w[:, :]), AX.X, ALU.add))
            link(nc.vector.reciprocal(tot[:, :], tot[:, :]))
            nc.vector.tensor_tensor(tile(w[:, :]), tile(w[:, :]), tot[:, :].unsqueeze(2).broadcast_to([P, NT, G]), ALU.mult).then_inc(s["done"], 1)
            dve.wait_ge(s["done"], 1)


def add_turned(nc, k, acc, x):
    with stage(nc, "turned added") as (block, s):
        @block.tensor
        def _(pe):
            for b in range(B):
                for t in range(TB):
                    mm = nc.tensor.transpose(k.ps[b][:, sl(t, P)], acc[:, sl(b * TB + t, P)], k.ident)
                mm.then_inc(s["turned"], 1)

        @block.vector
        def _(dve):
            for b in range(B):
                dve.wait_ge(s["turned"], b + 1)
                nc.vector.tensor_tensor(x[:, sl(b)], x[:, sl(b)], k.ps[b][:, :], ALU.add).then_inc(s["added"], 1)
            dve.wait_ge(s["added"], B)


def layer2(nc, k, x, y, a):
    G, C = 8, 4
    norm(nc, k, x, y, 1e-5)
    with ExitStack() as mem:
        sb = lambda n, w_, p=P: mem.enter_context(nc.sbuf_tensor(f"{n}_{nc.next_id()}", [p, w_], F32))
        w, wt, sg, act_ = sb("w", NT * G), sb("wt", T, G), sb("sg", 2 * S), sb("act", 2 * C * S)
        acc = a
        top2_weights(nc, k, y, w)
        with stage(nc, "turned copied bias done") as (block, s):
            @block.tensor
            def _(pe):
                for b in range(B):
                    for t in range(TB):
                        mm = nc.tensor.transpose(k.ps[b][0:G, sl(t, P)], w[:, sl(b * TB + t, G)], k.ident)
                    mm.then_inc(s["turned"], 1)
                for b in range(B):
                    pe.wait_ge(s["copied"], b + 1)
                    for t in range(TB):
                        mm = nc.tensor.matmul(k.ps[4 + b][:, sl(t, P)], wt[:, sl(b * TB + t, P)], k.w["L0_ffn_b2"][0:G, :], start=True, stop=True)
                    mm.then_inc(s["bias"], 1)

            @block.vector
            def _(dve):
                for b in range(B):
                    dve.wait_ge(s["turned"], b + 1)
                    nc.vector.tensor_copy(wt[:, sl(b)], k.ps[b][0:G, :]).then_inc(s["copied"], 1)
                for b in range(B):
                    dve.wait_ge(s["bias"], b + 1)
                    nc.vector.tensor_copy(acc[:, sl(b)], k.ps[4 + b][:, :]).then_inc(s["done"], 1)
                dve.wait_ge(s["done"], B)

        N = G * B
        with stage(nc, "up_x up_g gated act down added") as (block, s):
            pairs = [(k.ps[2 * j], k.ps[2 * j + 1]) for j in range(3)]

            @block.tensor
            def _(pe):
                def down(n):
                    pe.wait_ge(s["act"], C * (n + 1))
                    after(pe, s["added"], n - 1)
                    w2 = k.big[:, 8192 + (n // B) * 512:8192 + (n // B + 1) * 512]
                    for t in range(TB):
                        for c in range(C):
                            mm = nc.tensor.matmul(k.ps[6 + n % 2][:, sl(t, P)], act_[:, (n % 2) * C * S + c * S + t * P:][:, 0:P],
                                                  w2[:, sl(c, P)], start=c == 0, stop=c == C - 1)
                    mm.then_inc(s["down"], 1)

                pe.wait_ge(k.big_loaded, 16)
                for n in range(N):
                    e, b = divmod(n, B)
                    w1 = k.big[:, e * 1024:(e + 1) * 1024]
                    for c in range(C):
                        j = n * C + c
                        px, pg = pairs[j % 3]
                        after(pe, s["act"], j - 2)
                        nc.tensor.matmul(pg[:, :], w1[:, sl(C + c, P)], y[:, sl(b)], start=True, stop=True).then_inc(s["up_g"], 1)
                        nc.tensor.matmul(px[:, :], w1[:, sl(c, P)], y[:, sl(b)], start=True, stop=True).then_inc(s["up_x"], 1)
                    if n:
                        down(n - 1)
                down(N - 1)

            @block.scalar
            def _(act):
                for j in range(N * C):
                    e, c = j // (B * C), j % C
                    act.wait_ge(s["up_g"], j + 1)
                    after(act, s["act"], j - 1)
                    nc.scalar.activation(sg[:, sl(j % 2)], pairs[j % 3][1][:, :], ACT.Silu,
                                         bias=k.w["L0_ffn_b1"][:, 8 * e + C + c:8 * e + C + c + 1]).then_inc(s["gated"], 1)

            @block.vector
            def _(dve):
                def add(n):
                    e, b = divmod(n, B)
                    dve.wait_ge(s["down"], n + 1)
                    after(dve, s["added"], n - B + 1)
                    for t in range(TB):
                        i = b * TB + t
                        ins = nc.vector.scalar_tensor_tensor(out=acc[:, sl(i, P)], in0=k.ps[6 + n % 2][:, sl(t, P)], scalar=w[:, i * G + e:i * G + e + 1],
                                                             in1=acc[:, sl(i, P)], op0=ALU.mult, op1=ALU.add)
                    ins.then_inc(s["added"], 1)

                for j in range(N * C):
                    n, c = divmod(j, C)
                    e = n // B
                    dve.wait_ge(s["up_x"], j + 1)
                    dve.wait_ge(s["gated"], j + 1)
                    if c == 0:
                        after(dve, s["down"], n - 1)
                    nc.vector.scalar_tensor_tensor(out=act_[:, (n % 2) * C * S + c * S:][:, 0:S], in0=pairs[j % 3][0][:, :],
                                                   scalar=k.w["L0_ffn_b1"][:, 8 * e + c:8 * e + c + 1], in1=sg[:, sl(j % 2)],
                                                   op0=ALU.add, op1=ALU.mult).then_inc(s["act"], 1)
                    if c == 1 and n:
                        add(n - 1)
                add(N - 1)
        add_turned(nc, k, acc, x)


def layer3(nc, k, x, y, a):
    norm(nc, k, x, y, 1e-5, inner=(1e-5, k.w["L1_attn_rms_weight"], None, a))
    with ExitStack() as mem, stage(nc, "forget value side gate sig driven scanned gated proj done chain") as (block, s):
        sb = lambda n, w_: mem.enter_context(nc.sbuf_tensor(f"{n}_{nc.next_id()}", [P, w_], F32))
        fg, sd, gt, h = sb("fg", 2 * S), sb("sd", 2 * S), sb("gt", 2 * S), sb("h", 2 * S)

        @block.tensor
        def _(pe):
            def out(b):
                pe.wait_ge(s["gated"], b + 1)
                nc.tensor.matmul(k.ps[4 + b][:, :], k.w["L1_attn_w_o"], h[:, sl(b % 2)], start=True, stop=True).then_inc(s["proj"], 1)

            for b in range(B):
                after(pe, s["driven"], b)
                for j, (n, sem) in enumerate((("w_A", s["forget"]), ("w_output", s["side"]), ("w_sidegate", s["gate"]), ("w_x", s["value"]))):
                    nc.tensor.matmul(k.ps[j][:, :], k.w["L1_attn_" + n], a[:, sl(b)], start=True, stop=True).then_inc(sem, 1)
                if b:
                    out(b - 1)
            out(B - 1)

        @block.scalar
        def _(act):
            for b in range(B):
                after(act, s["gated"], b - 1)
                for j, (sem, dst, bias) in enumerate(((s["forget"], fg, k.w["L1_attn_b_A"]), (s["side"], sd, 0.0), (s["gate"], gt, 0.0))):
                    act.wait_ge(sem, b + 1)
                    nc.scalar.activation(dst[:, sl(b % 2)], k.ps[j][:, :], ACT.Sigmoid, bias=bias).then_inc(s["sig"], 1)

        @block.vector
        def _(dve):
            link = Chain(dve, s["chain"])
            for b in range(B):
                cur = sl(b % 2)
                dve.wait_ge(s["value"], b + 1)
                dve.wait_ge(s["sig"], 3 * b + 3)
                nc.vector.tensor_tensor(sd[:, cur], sd[:, cur], k.ps[3][:, :], ALU.mult).then_inc(s["driven"], 1)
                dve.wait_ge(s["driven"], b + 1)
                after(dve, s["proj"], b - 1)
                link(nc.vector.tensor_tensor_scan(h[:, cur], fg[:, cur], sd[:, cur], 0.0, ALU.mult, ALU.add))
                nc.vector.tensor_tensor(h[:, cur], h[:, cur], gt[:, cur], ALU.mult).then_inc(s["gated"], 1)
            for b in range(B):
                dve.wait_ge(s["proj"], b + 1)
                link(nc.vector.tensor_tensor(y[:, sl(b)], y[:, sl(b)], k.ps[4 + b][:, :], ALU.add))
                link(nc.vector.tensor_tensor(x[:, sl(b)], x[:, sl(b)], y[:, sl(b)], ALU.add))


def layer4(nc, k, x, y, a):
    norm(nc, k, x, y, 1e-5)
    q = a
    with ExitStack() as mem:
        sb = lambda n, w_, p=P: mem.enter_context(nc.sbuf_tensor(f"{n}_{nc.next_id()}", [p, w_], F32))
        kt, v, p, pt, mx = sb("kt", B * M), sb("v", B * D, M), sb("p", NT * M), sb("pt", T, M), sb("mx", NT)
        project(nc, k, [(k.w["L1_xattn_Wk"], k.ctx, B * M, kt, None, 1.0), (k.w["L1_xattn_Wq"], y, T, q, None, D ** -0.5)])
        with stage(nc, "scores values centred exps weights turned copied out done chain vcopied") as (block, s):
            @block.tensor
            def _(pe):
                for i in range(NT):
                    mm = nc.tensor.matmul(k.ps[0][:, sl(i, M)], q[:, sl(i, P)], kt[:, sl(i // TB, M)], start=True, stop=True)
                mm.then_inc(s["scores"], 1)
                for b in range(B):
                    mm = nc.tensor.matmul(k.ps[1][0:M, sl(b, D)], k.ctx[:, sl(b, M)], k.w["L1_xattn_Wv"], start=True, stop=True)
                mm.then_inc(s["values"], 1)
                pe.wait_ge(s["weights"], 1)
                for b in range(B):
                    for t in range(TB):
                        mm = nc.tensor.transpose(k.ps[2 + b][0:M, sl(t, P)], p[:, sl(b * TB + t, M)], k.ident)
                    mm.then_inc(s["turned"], 1)
                pe.wait_ge(s["vcopied"], 1)
                for b in range(B):
                    pe.wait_ge(s["copied"], b + 1)
                    after(pe, s["done"], b - 1)
                    nc.tensor.matmul(k.ps[6 + b % 2][:, :], v[:, sl(b, D)], pt[:, sl(b)], start=True, stop=True).then_inc(s["out"], 1)

            @block.scalar
            def _(act):
                act.wait_ge(s["centred"], 1)
                nc.scalar.activation(p[:, :], p[:, :], ACT.Exp).then_inc(s["exps"], 1)
                act.wait_ge(s["values"], 1)
                nc.scalar.activation(v[:, :], k.ps[1][0:M, :], ACT.Copy).then_inc(s["vcopied"], 1)
                for b in range(B):
                    act.wait_ge(s["turned"], b + 1)
                    nc.scalar.activation(pt[:, sl(b)], k.ps[2 + b][0:M, :], ACT.Copy).then_inc(s["copied"], 1)

            @block.vector
            def _(dve):
                link = Chain(dve, s["chain"])
                tile = lambda t: t[:, :].rearrange("p (t m) -> p t m", m=M)
                wide = mx[:, :].unsqueeze(2).broadcast_to([P, NT, M])
                dve.wait_ge(s["scores"], 1)
                link(nc.vector.tensor_reduce(mx[:, :], tile(k.ps[0]), AX.X, ALU.max))
                nc.vector.tensor_tensor(tile(p), tile(k.ps[0]), wide, ALU.subtract).then_inc(s["centred"], 1)
                dve.wait_ge(s["exps"], 1)
                link(nc.vector.tensor_reduce(mx[:, :], tile(p), AX.X, ALU.add))
                link(nc.vector.reciprocal(mx[:, :], mx[:, :]))
                nc.vector.tensor_tensor(tile(p), tile(p), wide, ALU.mult).then_inc(s["weights"], 1)
                for b in range(B):
                    dve.wait_ge(s["out"], b + 1)
                    nc.vector.tensor_tensor(x[:, sl(b)], x[:, sl(b)], k.ps[6 + b % 2][:, :], ALU.add).then_inc(s["done"], 1)


def layer5(nc, k, x, y, a):
    F, C = 512, 4
    norm(nc, k, x, y, 1e-5, inner=(1e-8, k.w["L1_ffn_norm1_w"], None, a))
    w1, w2 = k.w["L1_ffn_w1"], k.w["L1_ffn_w2"]
    with ExitStack() as mem:
        sb = lambda n, w_, dt=F32: mem.enter_context(nc.sbuf_tensor(f"{n}_{nc.next_id()}", [P, w_], dt))
        q1w, q2w, tmp = sb("q1w", F, BF16), sb("q2w", F, BF16), sb("tmp", F)
        part, wmean, wscale = sb("part", 2), sb("wmean", 2), sb("wscale", 2)
        with stage(nc, "abs summed total rounded chain") as (block, s):
            @block.scalar
            def _(act):
                for j, w in enumerate((w1, w2)):
                    after(act, s["abs"], j)
                    nc.scalar.activation(tmp[:, :], w, ACT.Abs, accum_out=part[:, j:j + 1]).then_inc(s["abs"], 1)

            @block.tensor
            def _(pe):
                pe.wait_ge(s["abs"], 2)
                nc.tensor.matmul(k.ps[0][:, 0:2], k.ones, part[:, :], start=True, stop=True).then_inc(s["total"], 1)

            @block.vector
            def _(dve):
                link = Chain(dve, s["chain"])
                dve.wait_ge(s["total"], 1)
                link(nc.vector.tensor_scalar(wmean[:, :], k.ps[0][:, 0:2], 1.0 / (D * F), 1e-5, ALU.mult, ALU.max))
                link(nc.vector.reciprocal(wscale[:, :], wmean[:, :]))
                for j, (w, q) in enumerate(((w1, q1w), (w2, q2w))):
                    link(nc.vector.tensor_scalar(tmp[:, :], w, wscale[:, j:j + 1], MAGIC, ALU.mult, ALU.add))
                    link(nc.vector.tensor_scalar(tmp[:, :], tmp[:, :], MAGIC, -1.0, ALU.subtract, ALU.max))
                    link(nc.vector.tensor_scalar(q[:, :], tmp[:, :], 1.0, None, ALU.min))

        top, sc, un = sb("top", 2 * NT), sb("sc", 2 * NT), sb("un", 2 * NT)
        ss, r1 = sb("ss", NT), sb("r1", NT)
        f1, q1, q1t = sb("f1", 2 * P), sb("q1", 2 * P, BF16), sb("q1t", 2 * P, BF16)
        r, h, hn, q2, q2t, o = (sb("r", 2 * F), sb("h", 2 * F), sb("hn", 2 * F), sb("q2", 2 * F, BF16), sb("q2t", 2 * F, BF16), sb("o", 2 * P))
        p_in, p_t2, p_o = k.ps[0:2], k.ps[6], k.ps[7]
        p_q = k.ps[2][:, 0:P // 2].bitcast(BF16)
        p_h = k.ps[3:5]
        p_q2 = k.ps[5][:, 0:F // 2].bitcast(BF16)
        names = ("turned quant1 q_turned q_copied up relu hidden sq log inv quant2 q2_turned q2_copied down scaled back added chain achain")
        with stage(nc, names) as (block, s):
            col = lambda t, j, i: t[:, j * NT + i:j * NT + i + 1]

            @block.tensor
            def _(pe):
                for i in range(NT + 2):
                    if i < NT:
                        after(pe, s["quant1"], i - 1)
                        nc.tensor.transpose(p_in[i % 2][:, 0:P], a[:, sl(i, P)], k.ident).then_inc(s["turned"], 1)
                    if 1 <= i <= NT:
                        c = i - 1
                        pe.wait_ge(s["quant1"], c + 1)
                        after(pe, s["q_copied"], c)
                        nc.tensor.transpose(p_q, q1[:, sl(c % 2, P)], k.ident_bf).then_inc(s["q_turned"], 1)
                        pe.wait_ge(s["q_copied"], c + 1)
                        after(pe, s["relu"], c - 1)
                        nc.tensor.matmul(p_h[c % 2][:, :], q1t[:, sl(c % 2, P)], q1w[:, :], start=True, stop=True).then_inc(s["up"], 1)
                    if i >= 2:
                        c = i - 2
                        pe.wait_ge(s["quant2"], c + 1)
                        after(pe, s["q2_copied"], c)
                        for j in range(C):
                            mm = nc.tensor.transpose(p_q2[:, sl(j, P)], q2[:, (c % 2) * F + j * P:][:, 0:P], k.ident_bf)
                        mm.then_inc(s["q2_turned"], 1)
                        pe.wait_ge(s["q2_copied"], c + 1)
                        after(pe, s["scaled"], c)
                        for j in range(C):
                            mm = nc.tensor.matmul(p_o[:, 0:P], q2t[:, (c % 2) * F + j * P:][:, 0:P], q2w[:, sl(j, P)], start=j == 0, stop=j == C - 1)
                        mm.then_inc(s["down"], 1)
                        pe.wait_ge(s["scaled"], c + 1)
                        after(pe, s["added"], c)
                        nc.tensor.transpose(p_t2[:, 0:P], o[:, sl(c % 2, P)], k.ident).then_inc(s["back"], 1)

            @block.vector
            def _(dve):
                link = Chain(dve, s["chain"])

                def quantise(src, tmp, dst, j, i, done):
                    t, m, u = col(top, j, i), col(sc, j, i), col(un, j, i)
                    link(nc.vector.tensor_reduce(t, src, AX.X, ALU.max, apply_absolute_value=True))
                    link(nc.vector.tensor_scalar(t, t, 1e-5, None, ALU.max))
                    link(nc.vector.reciprocal(m, t))
                    link(nc.vector.tensor_scalar(m, m, 127.0, None, ALU.mult))
                    link(nc.vector.tensor_scalar(u, t, 1.0 / 127.0, wmean[:, j:j + 1], ALU.mult, ALU.mult))
                    link(nc.vector.tensor_scalar(tmp, src, m, MAGIC, ALU.mult, ALU.add))
                    link(nc.vector.tensor_scalar(tmp, tmp, MAGIC, -128.0, ALU.subtract, ALU.max))
                    nc.vector.tensor_scalar(dst, tmp, 127.0, None, ALU.min).then_inc(done, 1)

                for i in range(NT + 2):
                    if i < NT:
                        dve.wait_ge(s["turned"], i + 1)
                        after(dve, s["q_turned"], i - 1)
                        quantise(p_in[i % 2][:, 0:P], f1[:, sl(i % 2, P)], q1[:, sl(i % 2, P)], 0, i, s["quant1"])
                    if 1 <= i <= NT:
                        c = i - 1
                        cur = sl(c % 2, F)
                        dve.wait_ge(s["relu"], c + 1)
                        link(nc.vector.tensor_tensor(h[:, cur], r[:, cur], r[:, cur], ALU.mult))
                        nc.vector.tensor_scalar(h[:, cur], h[:, cur], k.w["L1_ffn_act_scale"], k.w["L1_ffn_act_bias"], ALU.mult, ALU.add).then_inc(s["hidden"], 1)
                        dve.wait_ge(s["inv"], c + 1)
                        link(nc.vector.scalar_tensor_tensor(out=hn[:, cur], in0=h[:, cur], scalar=r1[:, c:c + 1], in1=k.w["L1_ffn_norm2_w"], op0=ALU.mult, op1=ALU.mult))
                        after(dve, s["q2_turned"], c - 1)
                        quantise(hn[:, cur], hn[:, cur], q2[:, cur], 1, c, s["quant2"])
                    if i >= 2:
                        c = i - 2
                        dve.wait_ge(s["down"], c + 1)
                        after(dve, s["back"], c - 1)
                        nc.vector.tensor_scalar(o[:, sl(c % 2, P)], p_o[:, 0:P], col(un, 1, c), None, ALU.mult).then_inc(s["scaled"], 1)
                        dve.wait_ge(s["back"], c + 1)
                        nc.vector.tensor_tensor(x[:, sl(c, P)], x[:, sl(c, P)], p_t2[:, 0:P], ALU.add).then_inc(s["added"], 1)

            @block.scalar
            def _(act):
                nc.scalar.preload_act_table_set(LN_EXP)
                alink = Chain(act, s["achain"])
                for i in range(NT + 2):
                    if 1 <= i <= NT:
                        c = i - 1
                        cur = sl(c % 2, F)
                        act.wait_ge(s["q_turned"], c + 1)
                        after(act, s["up"], c - 1)
                        nc.scalar.activation(q1t[:, sl(c % 2, P)], p_q, ACT.Copy).then_inc(s["q_copied"], 1)
                        act.wait_ge(s["up"], c + 1)
                        after(act, s["hidden"], c - 1)
                        nc.scalar.activation(r[:, cur], p_h[c % 2][:, :], ACT.Relu, scale=col(un, 0, c)).then_inc(s["relu"], 1)
                        act.wait_ge(s["hidden"], c + 1)
                        after(act, s["quant2"], c - 1)
                        alink(nc.scalar.activation(hn[:, cur], h[:, cur], ACT.Square, accum_out=ss[:, c:c + 1]))
                        alink(nc.scalar.activation(ss[:, c:c + 1], ss[:, c:c + 1], ACT.Ln, scale=1.0 / F, bias=k.eps[1e-8]))
                        nc.scalar.activation(r1[:, c:c + 1], ss[:, c:c + 1], ACT.Exp, scale=-0.5).then_inc(s["inv"], 1)
                    if i >= 2:
                        c = i - 2
                        act.wait_ge(s["q2_turned"], c + 1)
                        after(act, s["down"], c - 1)
                        nc.scalar.activation(q2t[:, sl(c % 2, F)], p_q2, ACT.Copy).then_inc(s["q2_copied"], 1)


def layer8(nc, k, x, y, a):
    G, F = 64, 96
    J = G * F // P
    norm(nc, k, x, y, 1e-5)
    with ExitStack() as mem:
        sb = lambda n, w_, dt=F32, p=P: mem.enter_context(nc.sbuf_tensor(f"{n}_{nc.next_id()}", [p, w_], dt))
        ind = sb("ind", J * P, BF16)
        wt_hm, wt_lo = sb("wt_hm", T, BF16), sb("wt_lo", T, BF16, G)
        with ExitStack() as mem2, stage(nc, "loaded logits shifted exps split turned copied chain") as (block, s):
            sb2 = lambda n, w_, dt=F32: mem2.enter_context(nc.sbuf_tensor(f"{n}_{nc.next_id()}", [P, w_], dt))
            sc, sel, top, mx = sb2("sc", NT * G), sb2("sel", NT * G), sb2("top", NT * 8), sb2("mx", NT)
            hm, lo = sb2("hm", NT * 2 * G, BF16), sb2("lo", NT * G, BF16)

            @block.gpsimd
            def _(pool):
                pool.dma_start(ind[:, :], k.ap["ind"]).then_inc(s["loaded"], 16)
                pool.wait_ge(s["loaded"], 16)

            @block.tensor
            def _(pe):
                for i in range(NT):
                    mm = nc.tensor.matmul(k.ps[i // 8][:, sl(i % 8, G)], y[:, sl(i, P)], k.w["L2_ffn_gate_w"], start=True, stop=True)
                mm.then_inc(s["logits"], 1)
                pe.wait_ge(s["split"], 1)
                for b in range(B):
                    after(pe, s["copied"], 2 * b)
                    for t in range(TB):
                        i = b * TB + t
                        nc.tensor.transpose(k.ps[2][:, 0:S // 2].bitcast(BF16)[:, sl(t, P)], hm[:, sl(i, P)], k.ident_bf)
                    for t in range(TB):
                        i = b * TB + t
                        mm = nc.tensor.transpose(k.ps[3][0:G, 0:S // 2].bitcast(BF16)[:, sl(t, P)], lo[:, sl(i, G)], k.ident_bf)
                    mm.then_inc(s["turned"], 1)

            @block.scalar
            def _(act):
                act.wait_ge(s["shifted"], 1)
                nc.scalar.activation(sc[:, :], sc[:, :], ACT.Exp).then_inc(s["exps"], 1)
                for b in range(B):
                    act.wait_ge(s["turned"], b + 1)
                    nc.scalar.activation(wt_hm[:, sl(b)], k.ps[2][:, 0:S // 2].bitcast(BF16), ACT.Copy).then_inc(s["copied"], 1)
                    nc.scalar.activation(wt_lo[:, sl(b)], k.ps[3][0:G, 0:S // 2].bitcast(BF16), ACT.Copy).then_inc(s["copied"], 1)

            @block.vector
            def _(dve):
                link = Chain(dve, s["chain"])
                tile = lambda t: t[:, :].rearrange("p (t i) -> p t i", t=NT)
                wide = mx[:, :].unsqueeze(2).broadcast_to([P, NT, G])
                dve.wait_ge(s["logits"], 1)
                for j in range(2):
                    link(nc.vector.tensor_copy(sc[:, sl(j)], k.ps[j][:, :]))
                link(nc.vector.tensor_reduce(mx[:, :], tile(sc), AX.X, ALU.max))
                nc.vector.tensor_tensor(tile(sc), tile(sc), wide, ALU.subtract).then_inc(s["shifted"], 1)
                dve.wait_ge(s["exps"], 1)
                link(nc.vector.tensor_reduce(mx[:, :], tile(sc), AX.X, ALU.add))
                link(nc.vector.reciprocal(mx[:, :], mx[:, :]))
                link(nc.vector.tensor_tensor(tile(sc), tile(sc), wide, ALU.mult))
                for i in range(NT):
                    link(nc.vector.max(top[:, sl(i, 8)], sc[:, sl(i, G)]))
                    link(nc.vector.match_replace(out=sel[:, sl(i, G)], in_to_replace=top[:, sl(i, 8)], in_values=sc[:, sl(i, G)], imm_value=-1.0))
                link(nc.vector.scalar_tensor_tensor(out=sc[:, :], in0=sel[:, :], scalar=0.0, in1=sc[:, :], op0=ALU.is_lt, op1=ALU.mult))
                link(nc.vector.tensor_reduce(mx[:, :], tile(sc), AX.X, ALU.add))
                link(nc.vector.tensor_scalar(mx[:, :], mx[:, :], 1e-20, None, ALU.add))
                link(nc.vector.reciprocal(mx[:, :], mx[:, :]))
                link(nc.vector.tensor_tensor(tile(sc), tile(sc), wide, ALU.mult))
                hi, mid = tile(hm)[:, :, 0:G], tile(hm)[:, :, G:2 * G]
                link(nc.vector.tensor_copy(hi, tile(sc)))
                link(nc.vector.tensor_tensor(tile(sc), tile(sc), hi, ALU.subtract))
                link(nc.vector.tensor_copy(mid, tile(sc)))
                link(nc.vector.tensor_tensor(tile(sc), tile(sc), mid, ALU.subtract))
                nc.vector.tensor_copy(lo[:, :], sc[:, :]).then_inc(s["split"], 1)

        with ExitStack() as mem2, stage(nc, "gate up spread silu weighted act down done chain") as (block, s):
            sb2 = lambda n, w_: mem2.enter_context(nc.sbuf_tensor(f"{n}_{nc.next_id()}", [P, w_], F32))
            sg, h = sb2("sg", 2 * S), sb2("h", 2 * S)
            wg, wu, wd = (k.big[:, j * J * P:(j + 1) * J * P] for j in range(3))
            banks = [k.ps[0:3], k.ps[3:6]]
            N = B * J

            @block.tensor
            def _(pe):
                def down(n):
                    b, j = divmod(n, J)
                    pe.wait_ge(s["act"], n + 1)
                    if j == 0:
                        after(pe, s["done"], b - 1)
                    nc.tensor.matmul(k.ps[6 + b % 2][:, :], wd[:, sl(j, P)], h[:, sl(n % 2)], start=j == 0, stop=j == J - 1).then_inc(s["down"], 1)

                pe.wait_ge(k.big_loaded, 32)
                for n in range(N):
                    b, j = divmod(n, J)
                    pg, pu, pw = banks[n % 2]
                    after(pe, s["act"], n - 1)
                    nc.tensor.matmul(pg[:, :], wg[:, sl(j, P)], y[:, sl(b)], start=True, stop=True).then_inc(s["gate"], 1)
                    nc.tensor.matmul(pu[:, :], wu[:, sl(j, P)], y[:, sl(b)], start=True, stop=True).then_inc(s["up"], 1)
                    nc.tensor.matmul(pw[:, :], ind[:, sl(j, P)], wt_hm[:, sl(b)], start=True, stop=False)
                    nc.tensor.matmul(pw[:, :], ind[0:G, sl(j, P)], wt_lo[:, sl(b)], start=False, stop=True).then_inc(s["spread"], 1)
                    if n:
                        down(n - 1)
                down(N - 1)

            @block.scalar
            def _(act):
                for n in range(N):
                    act.wait_ge(s["gate"], n + 1)
                    after(act, s["act"], n - 1)
                    nc.scalar.activation(sg[:, sl(n % 2)], banks[n % 2][0][:, :], ACT.Silu).then_inc(s["silu"], 1)

            @block.vector
            def _(dve):
                def finish(b):
                    dve.wait_ge(s["down"], J * (b + 1))
                    nc.vector.tensor_tensor(x[:, sl(b)], x[:, sl(b)], k.ps[6 + b % 2][:, :], ALU.add).then_inc(s["done"], 1)

                for n in range(N):
                    b, j = divmod(n, J)
                    cur = sl(n % 2)
                    dve.wait_ge(s["up"], n + 1)
                    dve.wait_ge(s["silu"], n + 1)
                    after(dve, s["down"], n - 1)
                    nc.vector.tensor_tensor(h[:, cur], sg[:, cur], banks[n % 2][1][:, :], ALU.mult).then_inc(s["weighted"], 1)
                    dve.wait_ge(s["weighted"], n + 1)
                    dve.wait_ge(s["spread"], n + 1)
                    nc.vector.tensor_tensor(h[:, cur], h[:, cur], banks[n % 2][2][:, :], ALU.mult).then_inc(s["act"], 1)
                    if j == 2 and b:
                        finish(b - 1)
                finish(B - 1)


def layer6(nc, k, x, y, a):
    HH, GH = 8, 4
    norm(nc, k, x, y, 1e-5)
    with ExitStack() as mem:
        sb = lambda n, w_, dt=F32: mem.enter_context(nc.sbuf_tensor(f"{n}_{nc.next_id()}", [P, w_], dt))
        g, beta, nbeta, gam, ngam, rest, tot = (sb(n, NT * HH) for n in ("g", "beta", "nbeta", "gam", "ngam", "rest", "tot"))
        delta_gates(nc, k, y, g, beta, nbeta, gam, ngam, rest, tot, HH)
        q, kk, v, z = (k.big[:, j * 8 * S:(j + 1) * 8 * S] for j in range(4))
        W = GH * P
        state, free = a[:, 0:HH * P], k.big[:, 32 * S:32 * S + 4 * W]
        bufs = {n: [sb(n, W) for _ in range(2)] for n in ("ea", "at", "nn", "vv", "kt")}
        bufs["mm"] = [a[:, HH * P + j * W:][:, 0:W] for j in range(2)]
        bufs["ex"] = [free[:, sl(j, W)] for j in range(2)]
        gs = [free[:, sl(2 + j, W)] for j in range(2)]
        small = {n: sb(n, 2 * GH) for n in ("ss", "rstd")}
        for b in range(B):
            delta_project(nc, k, y, b, z)
            delta_chunks(nc, k, x, b, q, kk, v, z, state, bufs, gs, small, g, beta, nbeta, gam, ngam, rest, tot, HH, GH)
    load_big(nc, k, "big2")


def delta_gates(nc, k, y, g, beta, nbeta, gam, ngam, rest, tot, HH):
    W = NT * HH
    with ExitStack() as mem, stage(nc, "ba shifted exps lns bexp aexp g_ready sums decays chain") as (block, s):
        sb = lambda n, w_: mem.enter_context(nc.sbuf_tensor(f"{n}_{nc.next_id()}", [P, w_], F32))
        bb, aa, t1, al = sb("bb", W), sb("aa", W), sb("t1", W), sb("al", HH)

        @block.tensor
        def _(pe):
            for i in range(NT):
                mm = nc.tensor.matmul(k.ps[0][:, sl(i, 2 * HH)], y[:, sl(i, P)], k.w["L2_attn_ba"], start=True, stop=True)
            mm.then_inc(s["ba"], 1)
            pe.wait_ge(s["g_ready"], 1)
            for j, w in enumerate((k.w["upto"], k.w["after"], k.ones)):
                mm = nc.tensor.matmul(k.ps[1][:, sl(j, P)], w, g[:, :], start=True, stop=True)
            mm.then_inc(s["sums"], 1)

        @block.scalar
        def _(act):
            nc.scalar.preload_act_table_set(LN_EXP)
            nc.scalar.activation(al[:, :], k.w["L2_attn_A_log"], ACT.Exp).then_inc(s["aexp"], 1)
            act.wait_ge(s["shifted"], 1)
            nc.scalar.activation(bb[:, :], bb[:, :], ACT.Exp).then_inc(s["bexp"], 1)
            nc.scalar.activation(t1[:, :], t1[:, :], ACT.Exp).then_inc(s["exps"], 1)
            act.wait_ge(s["exps"], 1)
            nc.scalar.activation(t1[:, :], t1[:, :], ACT.Ln, bias=k.ones[:, 0:1]).then_inc(s["lns"], 1)
            act.wait_ge(s["sums"], 1)
            for j, dst in enumerate((gam, rest, tot)):
                nc.scalar.activation(dst[:, :], k.ps[1][:, sl(j, P)], ACT.Exp).then_inc(s["decays"], 1)

        @block.vector
        def _(dve):
            link = Chain(dve, s["chain"])
            tile = lambda t: t[:, :].rearrange("p (t h) -> p t h", h=HH)
            ps = k.ps[0][:, 0:2 * W].rearrange("p (t h) -> p t h", h=2 * HH)
            wide = lambda c: c.unsqueeze(1).broadcast_to([P, NT, HH])
            dve.wait_ge(s["ba"], 1)
            link(nc.vector.tensor_scalar(tile(bb), ps[:, :, 0:HH], -1.0, 80.0, ALU.mult, ALU.min))
            link(nc.vector.tensor_tensor(tile(aa), ps[:, :, HH:2 * HH], wide(k.w["L2_attn_dt_bias"]), ALU.add))
            link(nc.vector.tensor_scalar(t1[:, :], aa[:, :], -1.0, None, ALU.mult))
            nc.vector.tensor_tensor(t1[:, :], t1[:, :], aa[:, :], ALU.min).then_inc(s["shifted"], 1)
            dve.wait_ge(s["bexp"], 1)
            link(nc.vector.tensor_scalar(bb[:, :], bb[:, :], 1.0, None, ALU.add))
            link(nc.vector.reciprocal(beta[:, :], bb[:, :]))
            link(nc.vector.tensor_scalar(nbeta[:, :], beta[:, :], -1.0, None, ALU.mult))
            dve.wait_ge(s["lns"], 1)
            dve.wait_ge(s["aexp"], 1)
            link(nc.vector.tensor_scalar(al[:, :], al[:, :], 3e38, -1.0, ALU.min, ALU.mult))
            link(nc.vector.scalar_tensor_tensor(out=aa[:, :], in0=aa[:, :], scalar=0.0, in1=t1[:, :], op0=ALU.max, op1=ALU.add))
            link(nc.vector.tensor_tensor(tile(aa), tile(aa), wide(al[:, :]), ALU.mult))
            nc.vector.tensor_scalar(g[:, :], aa[:, :], -200.0, None, ALU.max).then_inc(s["g_ready"], 1)
            dve.wait_ge(s["decays"], 3)
            link(nc.vector.tensor_scalar(ngam[:, :], gam[:, :], -1.0, None, ALU.mult))


def delta_project(nc, k, y, b, z):
    TAPS = 4
    with ExitStack() as mem, stage(nc, "raw scaled conv z_ps z_done chain") as (block, s):
        chans = 24
        zmm = 2 * TB

        @block.tensor
        def _(pe):
            for n in range(zmm):
                t, j = divmod(n, 2)
                after(pe, s["z_done"], n - 1)
                nc.tensor.matmul(k.ps[6 + n % 2][:, :], y[:, sl(b * TB + t, P)], k.w["L2_attn_z_w"][:, sl(j)], start=True, stop=True).then_inc(s["z_ps"], 1)
            for m in range(chans):
                after(pe, s["conv"], m - 5)
                nc.tensor.matmul(k.ps[m % 6][:, :], k.w["L2_attn_qkv_w"][:, sl(m, P)], y[:, sl(b)], start=True, stop=True).then_inc(s["raw"], 1)

        @block.scalar
        def _(act):
            for n in range(zmm):
                act.wait_ge(s["z_ps"], n + 1)
                nc.scalar.activation(z[:, sl(n)], k.ps[6 + n % 2][:, :], ACT.Silu).then_inc(s["z_done"], 1)
            for m in range(chans):
                act.wait_ge(s["raw"], m + 1)
                nc.scalar.activation(k.big[:, sl(m)], k.ps[m % 6][:, :], ACT.Copy, scale=k.w["L2_attn_conv"][:, m * TAPS + 3:m * TAPS + 4]).then_inc(s["scaled"], 1)
            act.wait_ge(s["z_done"], zmm)

        @block.vector
        def _(dve):
            link = Chain(dve, s["chain"])
            for m in range(chans):
                dve.wait_ge(s["scaled"], m + 1)
                for back in range(1, TAPS):
                    dst = k.big[:, m * S + back:(m + 1) * S]
                    tap = m * TAPS + 3 - back
                    ins = nc.vector.scalar_tensor_tensor(out=dst, in0=k.ps[m % 6][:, 0:S - back], scalar=k.w["L2_attn_conv"][:, tap:tap + 1],
                                                         in1=dst, op0=ALU.mult, op1=ALU.add)
                    if back < TAPS - 1:
                        link(ins)
                ins.then_inc(s["conv"], 1)
            dve.wait_ge(s["conv"], chans)


def delta_chunks(nc, k, x, b, q, kk, v, z, state, bufs, gs, small, g, beta, nbeta, gam, ngam, rest, tot, HH, GH):
    LEVELS = 7
    names = ("gs pairs logs masked ed eds at apt vk_turned vk_copied ap_turned init y y_copied mn mn_new from_state r_ready "
             "qs_copied w us_ready outs o_ready s_done inv normed o_turned o_copied proj added chain achain")
    with stage(nc, names) as (block, s):
        heads4 = lambda t: t.rearrange("p (h e) -> p h e", h=GH)
        each = lambda t, c, gr: t[:, (b * TB + c) * HH + gr * GH:][:, 0:GH].unsqueeze(2).broadcast_to([P, GH, P])
        one = lambda t, c, gr, h: t[:, (b * TB + c) * HH + gr * GH + h:][:, 0:1]
        bank = lambda gr, j: k.ps[4 * gr + j]
        seg = lambda t, c, gr, h: t[:, (gr * GH + h) * S + c * P:][:, 0:P]
        head = lambda n, gr, h: bufs[n][gr][:, sl(h, P)]
        buf = lambda n, gr: bufs[n][gr][:, :]
        st = lambda gr, h: state[:, sl(gr * GH + h, P)]
        wide = lambda m: m.unsqueeze(1).broadcast_to([P, GH, P])
        hs = range(GH)
        NARROW, HALF = 2, P // 2
        side = lambda t, lv, r: t if lv < NARROW else t.rearrange("p (n r w) -> p n r w", r=2, w=1 << lv)[:, :, r, :]
        side4 = lambda t, lv, r: heads4(t) if lv < NARROW else t.rearrange("p (h n r w) -> p h n r w", h=GH, r=2, w=1 << lv)[:, :, :, r, :]
        mask4 = lambda j, lv, r: (wide(k.level_masks[:, sl(j, P)]) if lv < NARROW else
                                  side(k.level_masks[:, sl(j, P)], lv, r).unsqueeze(1).broadcast_to([P, GH, HALF >> lv, 1 << lv]))
        close4 = lambda t, lv: heads4(t) if lv < NARROW else t[:, 0:GH * HALF].rearrange("p (h n w) -> p h n w", h=GH, w=1 << lv)
        nth = lambda c, gr: 2 * c + gr + 1
        level = lambda c, gr, lv: (c * (LEVELS - 1) + lv - 1) * 2 + gr + 1
        carried = lambda c, gr: 2 * (c - 1) + gr + 1

        @block.gpsimd
        def _(pool):
            for c in range(TB):
                for gr in range(2):
                    after(pool, s["logs"], nth(c - 1, gr))
                    nc.gpsimd.tensor_tensor(heads4(gs[gr][:, :]), wide(k.w["after"]), each(g, c, gr), ALU.mult).then_inc(s["gs"], 1)
                for gr in range(2):
                    pool.wait_ge(s["ed"], nth(c, gr))
                    after(pool, s["o_turned"], nth(c - 1, gr))
                    nc.gpsimd.tensor_tensor(heads4(buf("ea", gr)), heads4(buf("ex", gr)), wide(k.w["key_later"]), ALU.mult).then_inc(s["masked"], 1)
                    pool.wait_ge(s["masked"], nth(c, gr))
                    nc.gpsimd.tensor_tensor(heads4(buf("ea", gr)), heads4(buf("ea", gr)), each(nbeta, c, gr), ALU.mult).then_inc(s["eds"], 1)

        @block.tensor
        def _(pe):
            mm4 = lambda out, left, right: [nc.tensor.matmul(out[:, sl(h, P)], left(h), right(h), start=True, stop=True) for h in hs][-1]
            def level4(out, lv, left, right):
                for h in hs:
                    mm = nc.tensor.matmul(out[:, sl(h, P if lv < NARROW else HALF)], left(h), right(h), start=True, stop=True)
                return mm
            turn4 = lambda out, src: [nc.tensor.transpose(out[:, sl(h, P)], src(h), k.ident) for h in hs][-1]
            for c in range(TB):
                for gr in range(2):
                    after(pe, s["added"], nth(c - 1, gr))
                    pe.wait_ge(s["gs"], nth(c, gr))
                    for h in hs:
                        nc.tensor.matmul(bank(gr, 2)[:, sl(h, P)], gs[gr][:, sl(h, P)], k.w["upto"], start=True, stop=False)
                        mm = nc.tensor.matmul(bank(gr, 2)[:, sl(h, P)], k.ident_bf, k.cut[:, :], start=False, stop=True)
                    mm.then_inc(s["logs"], 1)
                    mm4(bank(gr, 0), lambda h: seg(kk, c, gr, h), lambda h: seg(kk, c, gr, h))
                    mm4(bank(gr, 1), lambda h: seg(kk, c, gr, h), lambda h: seg(q, c, gr, h)).then_inc(s["pairs"], 1)
                for gr in range(2):
                    pe.wait_ge(s["ed"], nth(c, gr))
                    turn4(bank(gr, 3), lambda h: seg(v, c, gr, h))
                    turn4(bank(gr, 2), lambda h: seg(kk, c, gr, h)).then_inc(s["vk_turned"], 1)
                for gr in range(2):
                    pe.wait_ge(s["apt"], nth(c, gr))
                    turn4(bank(gr, 0), lambda h: head("ea", gr, h)).then_inc(s["ap_turned"], 1)
                for lv in range(1, LEVELS):
                    for gr in range(2):
                        if lv == 1:
                            pe.wait_ge(s["init"], nth(c, gr))
                            pe.wait_ge(s["vk_copied"], nth(c, gr))
                        else:
                            pe.wait_ge(s["mn_new"], level(c, gr, lv - 1))
                        level4(bank(gr, 1), lv, lambda h: head("ea", gr, h), lambda h: side(head("mm", gr, h), lv, 0)).then_inc(s["y"], 1)
                    for gr in range(2):
                        pe.wait_ge(s["y_copied"], level(c, gr, lv))
                        if lv < LEVELS - 1:
                            level4(bank(gr, 2), lv, lambda h: head("nn", gr, h), lambda h: side(head("ex", gr, h), lv, 0))
                        level4(bank(gr, 3), lv, lambda h: head("ex", gr, h), lambda h: side(head("nn", gr, h), lv, 1)).then_inc(s["mn"], 1)
                if c:
                    for gr in range(2):
                        pe.wait_ge(s["s_done"], nth(c - 1, gr))
                        mm4(bank(gr, 0), lambda h: seg(kk, c, gr, h), lambda h: st(gr, h))
                        mm4(bank(gr, 1), lambda h: seg(q, c, gr, h), lambda h: st(gr, h)).then_inc(s["from_state"], 1)
                for gr in range(2):
                    pe.wait_ge(s["mn_new"], level(c, gr, LEVELS - 1))
                    if c:
                        pe.wait_ge(s["r_ready"], carried(c, gr))
                    mm4(bank(gr, 2), lambda h: head("nn", gr, h), lambda h: head("vv", gr, h)).then_inc(s["w"], 1)
                for gr in range(2):
                    pe.wait_ge(s["us_ready"], nth(c, gr))
                    mm = mm4(bank(gr, 3), lambda h: head("at", gr, h), lambda h: head("mm", gr, h))
                    if c < TB - 1:
                        mm = mm4(bank(gr, 0), lambda h: head("kt", gr, h), lambda h: head("ex", gr, h))
                    mm.then_inc(s["outs"], 1)
                for gr in range(2):
                    pe.wait_ge(s["normed"], nth(c, gr))
                    turn4(bank(gr, 1), lambda h: head("ea", gr, h)).then_inc(s["o_turned"], 1)
                for gr in range(2):
                    pe.wait_ge(s["o_copied"], nth(c, gr))
                    for h in hs:
                        mm = nc.tensor.matmul(bank(gr, 2)[:, 0:P], k.w["L2_attn_out_w"][:, sl(gr * GH + h, P)], head("at", gr, h),
                                              start=h == 0, stop=h == GH - 1)
                    mm.then_inc(s["proj"], 1)

        @block.scalar
        def _(act):
            alink = Chain(act, s["achain"])
            nc.scalar.preload_act_table_set(LN_EXP)
            for c in range(TB):
                for gr in range(2):
                    act.wait_ge(s["logs"], nth(c, gr))
                    nc.scalar.activation(buf("ex", gr), bank(gr, 2)[:, :], ACT.Exp).then_inc(s["ed"], 1)
                for gr in range(2):
                    act.wait_ge(s["vk_turned"], nth(c, gr))
                    nc.scalar.activation(buf("vv", gr), bank(gr, 3)[:, :], ACT.Copy)
                    nc.scalar.activation(buf("kt", gr), bank(gr, 2)[:, :], ACT.Copy).then_inc(s["vk_copied"], 1)
                for lv in range(1, LEVELS):
                    for gr in range(2):
                        act.wait_ge(s["y"], level(c, gr, lv))
                        nc.scalar.activation(side4(buf("ex", gr), lv, 0), close4(bank(gr, 1)[:, :], lv), ACT.Copy).then_inc(s["y_copied"], 1)
                if c:
                    for gr in range(2):
                        act.wait_ge(s["from_state"], carried(c, gr))
                        act.wait_ge(s["mn"], level(c, gr, LEVELS - 1))
                        for h in hs:
                            ins = nc.scalar.activation(head("ea", gr, h), bank(gr, 1)[:, sl(h, P)], ACT.Copy, scale=one(gam, c, gr, h))
                        ins.then_inc(s["qs_copied"], 1)
                for gr in range(2):
                    act.wait_ge(s["o_ready"], nth(c, gr))
                    ss, rstd = small["ss"][:, sl(gr, GH)], small["rstd"][:, sl(gr, GH)]
                    for h in hs:
                        ins = nc.scalar.activation(head("mm", gr, h), head("ea", gr, h), ACT.Square, accum_out=ss[:, h:h + 1])
                    alink(ins)
                    alink(nc.scalar.activation(ss, ss, ACT.Ln, scale=1.0 / P, bias=k.eps[1e-6]))
                    nc.scalar.activation(rstd, ss, ACT.Exp, scale=-0.5).then_inc(s["inv"], 1)
                for gr in range(2):
                    act.wait_ge(s["o_turned"], nth(c, gr))
                    nc.scalar.activation(buf("at", gr), bank(gr, 1)[:, :], ACT.Copy).then_inc(s["o_copied"], 1)

        @block.vector
        def _(dve):
            link = Chain(dve, s["chain"])
            for c in range(TB):
                for gr in range(2):
                    dve.wait_ge(s["pairs"], nth(c, gr))
                    dve.wait_ge(s["ed"], nth(c, gr))
                    nc.vector.tensor_tensor(buf("at", gr), buf("ex", gr), bank(gr, 1)[:, :], ALU.mult).then_inc(s["at"], 1)
                    dve.wait_ge(s["eds"], nth(c, gr))
                    nc.vector.tensor_tensor(buf("ea", gr), buf("ea", gr), bank(gr, 0)[:, :], ALU.mult).then_inc(s["apt"], 1)
                for gr in range(2):
                    link(nc.vector.tensor_copy(heads4(buf("nn", gr)), wide(k.ident)))
                    link(nc.vector.tensor_copy(heads4(buf("mm", gr)), wide(k.ident)))
                    dve.wait_ge(s["apt"], nth(c, gr))
                    nc.vector.copy_predicated(heads4(buf("nn", gr)), wide(k.level_masks[:, sl(LEVELS, P)]), heads4(buf("ea", gr)))
                    dve.wait_ge(s["ap_turned"], nth(c, gr))
                    nc.vector.copy_predicated(heads4(buf("mm", gr)), wide(k.level_masks[:, sl(0, P)]), heads4(bank(gr, 0)[:, :])).then_inc(s["init"], 1)
                for lv in range(1, LEVELS):
                    for gr in range(2):
                        dve.wait_ge(s["mn"], level(c, gr, lv))
                        if lv < LEVELS - 1:
                            nc.vector.copy_predicated(side4(buf("mm", gr), lv, 0), mask4(lv, lv, 0), close4(bank(gr, 2)[:, :], lv))
                        nc.vector.copy_predicated(side4(buf("nn", gr), lv, 1), mask4(LEVELS + lv, lv, 1), close4(bank(gr, 3)[:, :], lv)).then_inc(s["mn_new"], 1)
                if c:
                    for gr in range(2):
                        dve.wait_ge(s["from_state"], carried(c, gr))
                        dve.wait_ge(s["vk_copied"], nth(c, gr))
                        for h in hs:
                            ins = nc.vector.scalar_tensor_tensor(out=head("vv", gr, h), in0=bank(gr, 0)[:, sl(h, P)], scalar=one(ngam, c, gr, h),
                                                                 in1=head("vv", gr, h), op0=ALU.mult, op1=ALU.add)
                        ins.then_inc(s["r_ready"], 1)
                for gr in range(2):
                    dve.wait_ge(s["w"], nth(c, gr))
                    link(nc.vector.tensor_tensor(heads4(buf("mm", gr)), heads4(bank(gr, 2)[:, :]), each(beta, c, gr), ALU.mult))
                    nc.vector.tensor_tensor(heads4(buf("ex", gr)), heads4(buf("mm", gr)), each(rest, c, gr), ALU.mult).then_inc(s["us_ready"], 1)
                for gr in range(2):
                    dve.wait_ge(s["outs"], nth(c, gr))
                    if c:
                        dve.wait_ge(s["qs_copied"], carried(c, gr))
                        nc.vector.tensor_tensor(buf("ea", gr), buf("ea", gr), bank(gr, 3)[:, :], ALU.add).then_inc(s["o_ready"], 1)
                    else:
                        nc.vector.tensor_copy(buf("ea", gr), bank(gr, 3)[:, :]).then_inc(s["o_ready"], 1)
                    if c == 0:
                        nc.vector.tensor_copy(state[:, gr * GH * P:(gr + 1) * GH * P], bank(gr, 0)[:, :]).then_inc(s["s_done"], 1)
                    elif c < TB - 1:
                        for h in hs:
                            ins = nc.vector.scalar_tensor_tensor(out=st(gr, h), in0=st(gr, h), scalar=one(tot, c, gr, h),
                                                                 in1=bank(gr, 0)[:, sl(h, P)], op0=ALU.mult, op1=ALU.add)
                        ins.then_inc(s["s_done"], 1)
                for gr in range(2):
                    dve.wait_ge(s["inv"], nth(c, gr))
                    rstd = small["rstd"][:, sl(gr, GH)].unsqueeze(2).broadcast_to([P, GH, P])
                    link(nc.vector.tensor_tensor(heads4(buf("ea", gr)), heads4(buf("ea", gr)), rstd, ALU.mult))
                    link(nc.vector.tensor_tensor(heads4(buf("ea", gr)), heads4(buf("ea", gr)), wide(k.w["L2_attn_norm_w"]), ALU.mult))
                    nc.vector.tensor_tensor(buf("ea", gr), buf("ea", gr), z[:, (2 * c + gr) * S:(2 * c + gr + 1) * S], ALU.mult).then_inc(s["normed"], 1)
                for gr in range(2):
                    xs = x[:, sl(b * TB + c, P)]
                    dve.wait_ge(s["proj"], nth(c, gr))
                    if gr:
                        dve.wait_ge(s["added"], nth(c, 0))
                    nc.vector.tensor_tensor(xs, xs, bank(gr, 2)[:, 0:P], ALU.add).then_inc(s["added"], 1)
            dve.wait_ge(s["added"], 2 * TB)


def layer9(nc, k, x, y, a):
    norm(nc, k, x, y, 1e-5)
    q, kk = k.big[:, 0:T], k.big[:, T:2 * T]
    qh = [k.big[:, (2 + j) * T:(3 + j) * T] for j in range(2)]
    project(nc, k, [(k.w["L3_attn_W" + n], y, T, dst, k.w["L3_attn_b" + n], scale) for n, dst, scale in (("q", q, -HD ** -0.5), ("k", kk, 1.0))])
    with ExitStack() as mem:
        sb = lambda n, w_, dt=F32: mem.enter_context(nc.sbuf_tensor(f"{n}_{nc.next_id()}", [P, w_], dt))
        v = a
        with stage(nc, "rows done") as (block, s):
            @block.tensor
            def _(pe):
                for b in range(B):
                    for t in range(TB):
                        mm = nc.tensor.matmul(k.ps[b][:, sl(t, P)], y[:, sl(b * TB + t, P)], k.w["L3_attn_Wv"], start=True, stop=True)
                    mm.then_inc(s["rows"], 1)

            @block.vector
            def _(dve):
                tiles = lambda t: t.rearrange("p (t e) -> p t e", t=TB)
                for b in range(B):
                    dve.wait_ge(s["rows"], b + 1)
                    nc.vector.tensor_tensor(tiles(v[:, sl(b)]), tiles(k.ps[b][:, :]), k.w["L3_attn_bv"].unsqueeze(1).broadcast_to([P, TB, P]),
                                            ALU.add).then_inc(s["done"], 1)
                dve.wait_ge(s["done"], B)

        o = y
        units = [(b, i, h) for b in range(B) for i in range(TB) for h in range(H)]
        N, PER = len(units), TB * H
        TURN, COPY, ATTEND, PW, PT = 3, 4, 6, 5, 4
        low, tot, pw, pt = sb("low", 8), sb("tot", 8), sb("pw", PW * S), sb("pt", PT * S)
        vs = [sb("vs", TB * H * 32) for _ in range(2)]
        with stage(nc, "zeroed spread heads scores least weights inverted scaled turned copied_a copied_v values out") as (block, s):
            width = lambda u: (units[u][1] + 1) * P
            weights = lambda u: pw[:, (u % PW) * S:(u % PW) * S + width(u)]
            turned = lambda u: pt[:, (u % PT) * S:(u % PT) * S + width(u)]
            one = lambda t, u: t[:, u % 8:u % 8 + 1]

            def copy(eng, u, sem, op):
                eng.wait_ge(s["turned"], u + 1)
                after(eng, s["values"], u - PT + 1)
                op(turned(u), k.ps[3 + u % 3][:, 0:width(u)]).then_inc(sem, 1)

            @block.tensor
            def _(pe):
                def copied(u):
                    pe.wait_ge(s["copied_v"] if u % 2 else s["copied_a"], u // 2 + 1)

                def turn(u):
                    pe.wait_ge(s["scaled"], u + 1)
                    if u >= 3:
                        copied(u - 3)
                    for c in range(units[u][1] + 1):
                        mm = nc.tensor.transpose(k.ps[3 + u % 3][:, sl(c, P)], weights(u)[:, sl(c, P)], k.ident)
                    mm.then_inc(s["turned"], 1)

                def attend(u):
                    b, i, h = units[u]
                    copied(u)
                    if h == 0:
                        after(pe, s["out"], u // H - 1)
                        pe.wait_ge(s["spread"], 4 * (b + 1))
                    g, j = divmod(h, 4)
                    for c in range(i + 1):
                        mm = nc.tensor.matmul(k.ps[6 + (u // H) % 2][sl(g, 32), 0:P], vs[b % 2][:, sl(c * H + h, 32)], turned(u)[:, sl(c, P)],
                                              start=c == 0 and j == 0, stop=c == i and j == 3)
                    mm.then_inc(s["values"], 1)

                for u in range(N + ATTEND):
                    if u < N:
                        b, i, h = units[u]
                        w = width(u)
                        if h == 0:
                            pe.wait_ge(s["heads"], u // H + 1)
                        after(pe, s["weights"], u - 2)
                        nc.tensor.matmul(k.ps[u % 3][:, 0:w], qh[(u // H) % 2][:, sl(h, P)], kk[:, b * S:][:, 0:w], start=True, stop=False)
                        nc.tensor.matmul(k.ps[u % 3][:, w - P:w], k.ident_bf, k.later[:, :], start=False, stop=True).then_inc(s["scores"], 1)
                    if TURN <= u < N + TURN:
                        turn(u - TURN)
                    if u >= ATTEND:
                        attend(u - ATTEND)

            @block.scalar
            def _(act):
                for u in range(N + COPY):
                    if u < N:
                        act.wait_ge(s["least"], u + 1)
                        after(act, s["turned"], u - PW + 1)
                        after(act, s["inverted"], u - 7)
                        nc.scalar.activation(weights(u), k.ps[u % 3][:, 0:width(u)], ACT.Exp, scale=-1.0, bias=one(low, u),
                                             accum_out=one(tot, u)).then_inc(s["weights"], 1)
                    if u >= COPY and (u - COPY) % 2 == 0:
                        copy(act, u - COPY, s["copied_a"], lambda dst, src: nc.scalar.activation(dst, src, ACT.Copy))

            @block.gpsimd
            def _(pool):
                def spread(b):
                    after(pool, s["values"], (b - 1) * PER)
                    for j in range(4):
                        dst = vs[b % 2][:, :].rearrange("p (t g j q e) -> p t g j q e", t=TB, g=4, j=4, q=4)
                        src = v[:, sl(b)].rearrange("p (t g j e) -> p t g j e", t=TB, g=4, j=4)
                        nc.gpsimd.tensor_copy(dst[:, :, :, j, j, :], src[:, :, :, j, :]).then_inc(s["spread"], 1)

                pool.wait_ge(s["zeroed"], 2)
                spread(0)
                for n in range(NT):
                    after(pool, s["scores"], (n - 1) * H)
                    nc.gpsimd.tensor_tensor(qh[n % 2].rearrange("p (h e) -> p h e", h=H), q[:, sl(n, P)].unsqueeze(1).broadcast_to([P, H, P]),
                                            k.w["head_cols"].unsqueeze(2).broadcast_to([P, H, P]), ALU.mult).then_inc(s["heads"], 1)
                    if n % TB == 2 and n // TB < B - 1:
                        spread(n // TB + 1)

            @block.vector
            def _(dve):
                for j in range(2):
                    nc.vector.memset(vs[j][:, :], 0.0).then_inc(s["zeroed"], 1)
                for u in range(N + ATTEND + 2):
                    if u < N:
                        dve.wait_ge(s["scores"], u + 1)
                        after(dve, s["weights"], u - 7)
                        nc.vector.tensor_reduce(one(low, u), k.ps[u % 3][:, 0:width(u)], AX.X, ALU.min).then_inc(s["least"], 1)
                    if 2 <= u < N + 2:
                        dve.wait_ge(s["weights"], u - 1)
                        nc.vector.reciprocal(one(tot, u - 2), one(tot, u - 2)).then_inc(s["inverted"], 1)
                        dve.wait_ge(s["inverted"], u - 1)
                        nc.vector.tensor_scalar(weights(u - 2), weights(u - 2), one(tot, u - 2), None, ALU.mult).then_inc(s["scaled"], 1)
                    if COPY <= u < N + COPY and (u - COPY) % 2 == 1:
                        copy(dve, u - COPY, s["copied_v"], lambda dst, src: nc.vector.tensor_copy(dst, src))
                    if u >= ATTEND + H and (u - ATTEND) % H == 1:
                        i = (u - ATTEND) // H - 1
                        dve.wait_ge(s["values"], (i + 1) * H)
                        nc.vector.tensor_copy(o[:, sl(i, P)], k.ps[6 + i % 2][:, 0:P]).then_inc(s["out"], 1)
                dve.wait_ge(s["out"], NT)

        with stage(nc, "proj done") as (block, s):
            @block.tensor
            def _(pe):
                for b in range(B):
                    nc.tensor.matmul(k.ps[4 + b][:, :], k.w["L3_attn_Wo"], o[:, sl(b)], start=True, stop=True).then_inc(s["proj"], 1)

            @block.scalar
            def _(act):
                for b in range(B):
                    act.wait_ge(s["proj"], b + 1)
                    nc.scalar.activation(a[:, sl(b)], k.ps[4 + b][:, :], ACT.Identity, bias=k.w["L3_attn_bo"]).then_inc(s["done"], 1)
                act.wait_ge(s["done"], B)
    norm(nc, k, a, y, 1e-5)
    with stage(nc, "chain") as (block, s):
        @block.vector
        def _(dve):
            link = Chain(dve, s["chain"])
            for b in range(B):
                link(nc.vector.tensor_scalar(y[:, sl(b)], y[:, sl(b)], k.w["L3_attn_gamma"], k.w["L3_attn_beta"], ALU.mult, ALU.add))
                link(nc.vector.tensor_tensor(x[:, sl(b)], x[:, sl(b)], y[:, sl(b)], ALU.add))


def layer11(nc, k, x, y, a):
    F, R, K, CAND, ROUNDS = 1536, 32, 512, 32, 6
    C = F // P
    norm(nc, k, x, y, 1e-5)
    wm, wp = k.big[:, 0:F], k.big[:, F:2 * F]
    per_step = "up act down out pooled r_ps r scores shifted exps counts reached turned count total decided".split()
    with ExitStack() as mem:
        sb = lambda n, w_, dt=F32, p=P: mem.enter_context(nc.sbuf_tensor(f"{n}_{nc.next_id()}", [p, w_], dt))
        active, new, history, both = (sb(n, C * B) for n in ("active", "new", "history", "both"))
        pooled, r1 = sb("pooled", B), sb("r1", P, F32, R)
        seen = sb("seen", 2)
        going = sb("going", 1, I32)
        h = sb("h", 2 * S)
        with stage(nc, "chain") as (block, s):
            @block.vector
            def _(dve):
                link = Chain(dve, s["chain"])
                for t in (active, history):
                    link(nc.vector.memset(t[:, :], 0.0))
                    link(nc.vector.memset(t[:, 0:K // P * B], 1.0))

        p, m, eq, cum = sb("p", F), sb("m", F), sb("eq", F), sb("cum", F)
        c1, c2, hit = sb("c1", 1), sb("c2", 1), sb("hit", 1)
        base, trial, digit = sb("base", 1, I32), sb("trial", 1, I32), sb("digit", 1, I32)

        def map_pe(pe, s, blocks):
            N = B * blocks

            def down(n):
                b, c = divmod(n, blocks)
                pe.wait_ge(s["act"], n + 1)
                if c == 0:
                    after(pe, s["out"], b - 1)
                nc.tensor.matmul(k.ps[4 + b % 2][:, :], wp[:, sl(c, P)], h[:, sl(n % 2)], start=c == 0, stop=c == blocks - 1).then_inc(s["down"], 1)

            for n in range(N):
                after(pe, s["act"], n - 3)
                nc.tensor.matmul(k.ps[n % 4][:, :], wm[:, sl(n % blocks, P)], y[:, sl(n // blocks)], start=True, stop=True).then_inc(s["up"], 1)
                if n:
                    down(n - 1)
            down(N - 1)

        def map_act(act, s, blocks):
            for n in range(B * blocks):
                b, c = divmod(n, blocks)
                act.wait_ge(s["up"], n + 1)
                after(act, s["down"], n - 1)
                nc.scalar.activation(h[:, sl(n % 2)], k.ps[n % 4][:, :], ACT.Relu, scale=active[:, c * B + b:c * B + b + 1]).then_inc(s["act"], 1)

        def map_dve(dve, s, link, blocks):
            for b in range(B):
                dve.wait_ge(s["down"], blocks * (b + 1))
                nc.vector.tensor_scalar(a[:, sl(b)], k.ps[4 + b % 2][:, :], 1.0, None, ALU.mult, ALU.add, accum_out=pooled[:, b:b + 1]).then_inc(s["out"], 1)
            dve.wait_ge(s["out"], B)
            nc.vector.tensor_scalar(pooled[:, :], pooled[:, :], 1.0 / S, None, ALU.mult).then_inc(s["pooled"], 1)

        def choose_pe(pe, s):
            pe.wait_ge(s["pooled"], 1)
            nc.tensor.matmul(k.ps[6][0:R, 0:B], k.w["L3_ffn_Wc1"], pooled[:, :], start=True, stop=True).then_inc(s["r_ps"], 1)
            pe.wait_ge(s["r"], 1)
            for j in range(3):
                mm = nc.tensor.matmul(k.ps[j][:, :], r1[:, :], k.big[0:R, 2 * F + j * S:2 * F + (j + 1) * S], start=True, stop=True)
            mm.then_inc(s["scores"], 1)
            for n in range(ROUNDS):
                pe.wait_ge(s["counts"], n + 1)
                nc.tensor.matmul(k.ps[7][:, 0:1], k.w["same_batch"], hit[:, :], start=True, stop=True).then_inc(s["reached"], 1)
            pe.wait_ge(s["counts"], ROUNDS + 1)
            for c in range(C):
                mm = nc.tensor.transpose(k.ps[3 + c // 4][:, sl(c % 4, P)], m[:, sl(c, P)], k.ident)
            mm.then_inc(s["turned"], 1)
            pe.wait_ge(s["count"], 1)
            nc.tensor.matmul(k.ps[0][:, 0:1], k.ones, seen[:, 0:1], start=True, stop=True).then_inc(s["total"], 1)

        def choose_act(act, s):
            act.wait_ge(s["shifted"], 1)
            nc.scalar.activation(p[:, :], p[:, :], ACT.Exp).then_inc(s["exps"], 1)

        def choose_dve(dve, s, link):
            dve.wait_ge(s["r_ps"], 1)
            nc.vector.tensor_scalar(r1[:, :].rearrange("r (b c) -> r b c", b=B), k.ps[6][0:R, 0:B].unsqueeze(2).broadcast_to([R, B, CAND]),
                                    0.0, None, ALU.max).then_inc(s["r"], 1)
            dve.wait_ge(s["scores"], 1)
            for j in range(3):
                link(nc.vector.tensor_copy(p[:, sl(j)], k.ps[j][:, :]))
            link(nc.vector.tensor_reduce(c1[:, :], p[:, :], AX.X, ALU.max))
            nc.vector.tensor_scalar(p[:, :], p[:, :], c1[:, :], None, ALU.subtract).then_inc(s["shifted"], 1)
            dve.wait_ge(s["exps"], 1)
            link(nc.vector.tensor_reduce(c1[:, :], p[:, :], AX.X, ALU.add))
            link(nc.vector.reciprocal(c1[:, :], c1[:, :]))
            link(nc.vector.tensor_scalar(p[:, :], p[:, :], c1[:, :], None, ALU.mult))
            link(nc.vector.memset(base[:, :], 0))
            for n in range(ROUNDS):
                link(nc.vector.tensor_tensor(trial[:, :], base[:, :], k.candidate[:, n:n + 1], ALU.bitwise_or))
                link(nc.vector.tensor_scalar(m[:, :], p[:, :], trial[:, :].bitcast(F32), None, ALU.is_ge, ALU.add, accum_out=c1[:, :]))
                nc.vector.tensor_scalar(hit[:, :], c1[:, :], float(K), None, ALU.is_ge).then_inc(s["counts"], 1)
                dve.wait_ge(s["reached"], n + 1)
                link(nc.vector.tensor_scalar(digit[:, :], k.ps[7][:, 0:1], 1.0, None, ALU.subtract))
                link(nc.vector.tensor_scalar(digit[:, :], digit[:, :], 25 - 5 * n, None, ALU.logical_shift_left))
                link(nc.vector.tensor_tensor(base[:, :], base[:, :], digit[:, :], ALU.bitwise_or))
            kth = base[:, :].bitcast(F32)
            link(nc.vector.tensor_scalar(m[:, :], p[:, :], kth, None, ALU.is_gt, ALU.add, accum_out=c1[:, :]))
            link(nc.vector.tensor_scalar(c2[:, :], c1[:, :], -1.0, float(K), ALU.mult, ALU.add))
            link(nc.vector.tensor_scalar(eq[:, :], p[:, :], kth, None, ALU.is_equal))
            link(nc.vector.tensor_tensor_scan(cum[:, :], k.ones[:, 0:1].broadcast_to([P, F]), eq[:, :], 0.0, ALU.mult, ALU.add))
            link(nc.vector.scalar_tensor_tensor(out=eq[:, :], in0=cum[:, :], scalar=c2[:, :], in1=eq[:, :], op0=ALU.is_le, op1=ALU.mult))
            nc.vector.tensor_tensor(m[:, :], m[:, :], eq[:, :], ALU.add).then_inc(s["counts"], 1)
            dve.wait_ge(s["turned"], 1)
            for j in range(3):
                link(nc.vector.tensor_copy(new[:, sl(j, 4 * B)].rearrange("p (c b) -> p c b", c=4),
                                           k.ps[3 + j][:, :].rearrange("p (c b r) -> p c b r", c=4, b=B)[:, :, :, 0]))
            link(nc.vector.tensor_tensor(both[:, :], history[:, :], new[:, :], ALU.max))
            link(nc.vector.tensor_tensor(history[:, :], both[:, :], history[:, :], ALU.subtract))
            link(nc.vector.tensor_reduce(seen[:, 0:1], history[:, :], AX.X, ALU.add))
            link(nc.vector.tensor_scalar(seen[:, 0:1], seen[:, 0:1], 1.0 / (B * K), None, ALU.mult))
            nc.vector.tensor_copy(history[:, :], both[:, :]).then_inc(s["count"], 1)
            link(nc.vector.tensor_copy(active[:, :], new[:, :]))
            link(nc.vector.tensor_copy(y[:, :], a[:, :]))
            dve.wait_ge(s["total"], 1)
            nc.vector.tensor_scalar(going[:, :], k.ps[0][:, 0:1], 0.7, None, ALU.is_ge).then_inc(s["decided"], 1)

        with stage(nc, " ".join(per_step) + " chain") as (block, s):
            @block.tensor
            def _(pe):
                pe.wait_ge(k.big_loaded, 48)
                map_pe(pe, s, K // P)
                choose_pe(pe, s)

            @block.scalar
            def _(act):
                map_act(act, s, K // P)
                choose_act(act, s)

            @block.vector
            def _(dve):
                link = Chain(dve, s["chain"])
                map_dve(dve, s, link, K // P)
                choose_dve(dve, s, link)
                dve.wait_ge(s["decided"], 1)

        with stage(nc, " ".join(f"{n}_{i}" for i in (2, 3) for n in per_step) + " chain") as (block, s):
            second, third = ({n: s[f"{n}_{i}"] for n in per_step} for i in (2, 3))
            flag = going[0:1, 0:1]

            @block.tensor
            def _(pe):
                with pe.If(pe.value_load(flag, min_val=0, max_val=1) == 1):
                    map_pe(pe, second, C)
                    choose_pe(pe, second)
                    pe.wait_ge(second["decided"], 1)
                    with pe.If(pe.value_load(flag, min_val=0, max_val=1) == 1):
                        map_pe(pe, third, C)

            @block.scalar
            def _(act):
                with act.If(act.value_load(flag, min_val=0, max_val=1) == 1):
                    map_act(act, second, C)
                    choose_act(act, second)
                    act.wait_ge(second["decided"], 1)
                    with act.If(act.value_load(flag, min_val=0, max_val=1) == 1):
                        map_act(act, third, C)

            @block.vector
            def _(dve):
                link = Chain(dve, s["chain"])
                with dve.If(dve.value_load(flag, min_val=0, max_val=1) == 1):
                    map_dve(dve, second, link, C)
                    choose_dve(dve, second, link)
                    dve.wait_ge(second["decided"], 1)
                    with dve.If(dve.value_load(flag, min_val=0, max_val=1) == 1):
                        map_dve(dve, third, link, C)
                        link(nc.vector.tensor_copy(y[:, :], a[:, :]))
                        dve.wait_ge(third["pooled"], 1)
    with stage(nc, "chain") as (block, s):
        @block.vector
        def _(dve):
            link = Chain(dve, s["chain"])
            link(nc.vector.tensor_tensor(x[:, :], x[:, :], y[:, :], ALU.add))


def program(nc, ap, out, cols, first, last):
    with ExitStack() as mem:
        sb = lambda n, w, dt=F32, p=P: mem.enter_context(nc.sbuf_tensor(n, [p, w], dt))
        k = Kit()
        k.w = {}
        stored = nc.alloc_semaphore("stored")
        k.ps = [mem.enter_context(nc.psum_tensor(f"bank{i}", [P, S], F32)) for i in range(8)]
        x, y, a = sb("x", T), sb("y", T), sb("a", T)
        pack = sb("pack", ap["pack"].shape[1])
        for n, (lo, w) in cols.items():
            k.w[n] = pack[:, lo:lo + w]
        k.mean, k.ones, k.heads, k.ident = k.w["mean"], k.w["ones"], k.w["head_mask"], k.w["ident"]
        k.eps = {e: k.w["eps"][:, i:i + 1] for i, e in enumerate(EPSILONS)}
        k.ap = ap
        k.big = sb("big", ap["big2"].shape[1])
        k.big_loaded = nc.alloc_semaphore("big_loaded")
        k.ctx = k.w["ctx"]
        k.mask0, k.mask2 = sb("mask0", NT * M), sb("mask2", TB * M)
        k.level_masks = sb("level_masks", ap["level_masks"].shape[1], mybir.dt.uint8)[:, :]
        masks_raw = ap["level_masks"].shape[1]
        k.cut = sb("cut", P, BF16)
        k.candidate = sb("candidate", 6, I32)
        k.later = sb("later", P, BF16)
        k.ident_bf = sb("ident_bf", P, BF16)[:, :]
        raw0, raw2 = sb("raw0", NT * M, mybir.dt.uint8), sb("raw2", TB * M, I32)
        with stage(nc, "loaded masks chain") as (block, s):
            @block.sync
            def _(sp):
                sp.dma_start(raw0[:, :], ap["mask0"]).then_inc(s["masks"], 16)
                sp.dma_start(raw2[:, :], ap["mask2"]).then_inc(s["masks"], 16)
                sp.dma_start(k.candidate[:, :], ap["candidate"]).then_inc(s["masks"], 16)
                sp.dma_start(y[:, 0:masks_raw].bitcast(I32), ap["level_masks"]).then_inc(s["masks"], 16)
                sp.dma_start(x[:, :], ap["x"]).then_inc(s["loaded"], 16)
                sp.dma_start(pack[:, :], ap["pack"]).then_inc(s["loaded"], 16)
                sp.dma_start(k.big[:, 0:ap["big0"].shape[1]], ap["big0"]).then_inc(k.big_loaded, 16)
                sp.wait_ge(s["loaded"], 32)

            @block.vector
            def _(dve):
                link = Chain(dve, s["chain"])
                dve.wait_ge(s["masks"], 64)
                link(nc.vector.tensor_copy(k.mask0[:, :], raw0[:, :]))
                link(nc.vector.tensor_copy(k.level_masks, y[:, 0:masks_raw].bitcast(I32)))
                dve.wait_ge(s["loaded"], 32)
                link(nc.vector.tensor_copy(k.ident_bf, k.ident))
                link(nc.vector.tensor_scalar(k.cut[:, :], k.w["after"], -1e30, None, ALU.mult))
                link(nc.vector.tensor_scalar(k.later[:, :], k.w["key_later"], 1e30, None, ALU.mult))
                link(nc.vector.tensor_copy(k.mask2[:, :], raw2[:, :]))
                link(nc.vector.tensor_scalar(k.mask0[:, :], k.mask0[:, :], 0.0, None, ALU.not_equal))
                link(nc.vector.tensor_scalar(k.mask2[:, :], k.mask2[:, :], 0.0, None, ALU.not_equal))
        for n in range(first, last):
            LAYERS[n](nc, k, x, y, a)
        with nc.Block() as block:
            @block.sync
            def _(sp):
                sp.dma_start(out, x[:, :]).then_inc(stored, 16)
                sp.wait_ge(stored, 16)
                sp.wait_ge(k.big_loaded, 48)


def layer0(nc, k, x, y, a):
    with nc.sbuf_tensor(f"res_{nc.next_id()}", [P, T], F32) as res:
        norm(nc, k, x, y, 1e-5, inner=(1e-5, k.w["L0_attn_ln1_g"], k.w["L0_attn_ln1_b"], a))
        l0_attention(nc, k, y, a, res)
        norm(nc, k, res, y, 1e-5)
        with nc.sbuf_tensor(f"h_{nc.next_id()}", [P, T], F32) as h:
            scale_shift(nc, k, y, h, k.w["L0_attn_ln2_g"], k.w["L0_attn_ln2_b"])
            l0_lookup_mlp(nc, k, h, res, x)


def scale_shift(nc, k, src, dst, gain, bias):
    with stage(nc, "done") as (block, s):
        @block.vector
        def _(dve):
            nc.vector.tensor_scalar(dst[:, :], src[:, :], gain, bias, ALU.mult, ALU.add).then_inc(s["done"], 1)
            dve.wait_ge(s["done"], 1)


def more_parts(parts, f, vec, kblocks, rows):
    hd = np.arange(P) // HD
    parts["head_cols"] = (hd[:, None] == np.arange(H)[None]) * 1.0
    parts["head_of"] = np.eye(P)[:, :H] @ parts["head_cols"].T
    parts["head_rows"] = np.concatenate([(4 * c + np.arange(P)[:, None] // M == hd[None]) * 1.0 for c in range(4)], axis=1)
    parts["ctx"] = f("ctx_1024").reshape(B * M, D).T
    kv = f("L0_xattn_Wkv")
    for n, w in (("Wq", f("L0_xattn_Wq")), ("Wk", kv[:, :D]), ("Wv", kv[:, D:]), ("Wproj", f("L0_xattn_Wproj")), ("bproj", vec(f("L0_xattn_bproj")))):
        parts["L0_xattn_" + n] = w
    for pre, turn in (("L2_xattn_", True), ("L3_xattn_", False)):
        for n in ("Wq", "Wk", "Wv", "Wo"):
            parts[pre + n] = f(pre + n).T if turn else f(pre + n)
        for n in ("bq", "bk", "bo"):
            parts[pre + n] = vec(f(pre + n))
        parts[pre + "bv"] = rows(f(pre + "bv"))
    parts["before8"] = rows((np.arange(8)[None] < np.arange(8)[:, None]) * 1.0)
    parts["L0_ffn_gate_w"], parts["L0_ffn_gate_b"] = f("L0_ffn_gate_w"), rows(f("L0_ffn_gate_b"))
    parts["L0_ffn_b1"] = vec(f("L0_ffn_b1").reshape(-1))
    parts["L0_ffn_b2"] = np.concatenate([f("L0_ffn_b2"), np.zeros((P - 8, D))])
    parts["L1_attn_rms_weight"], parts["L1_attn_b_A"] = vec(f("L1_attn_rms_weight")), vec(f("L1_attn_b_A"))
    for n in ("w_A", "w_x", "w_sidegate", "w_output", "w_o"):
        parts["L1_attn_" + n] = f("L1_attn_" + n)
    for n in ("Wq", "Wk", "Wv"):
        parts["L1_xattn_" + n] = f("L1_xattn_" + n).T
    parts["L1_ffn_w1"], parts["L1_ffn_w2"] = f("L1_ffn_w1").T, kblocks(f("L1_ffn_w2").T)
    parts["L1_ffn_norm1_w"], parts["L1_ffn_norm2_w"] = vec(f("L1_ffn_norm1_w")), rows(f("L1_ffn_norm2_w"))
    parts["L1_ffn_act_scale"], parts["L1_ffn_act_bias"] = rows(f("L1_ffn_act_scale")), rows(f("L1_ffn_act_bias"))
    parts["L2_ffn_gate_w"] = f("L2_ffn_gate_w").T
    parts["key_later"] = np.triu(np.ones((P, P)), 1)
    for n in "qk":
        parts["L3_attn_b" + n] = vec(f("L3_attn_b" + n))
    for n in ("Wq", "Wk", "Wv", "Wo"):
        parts["L3_attn_" + n] = f("L3_attn_" + n)
    parts["L3_attn_bv"] = rows(f("L3_attn_bv"))
    for n in ("bo", "gamma", "beta"):
        parts["L3_attn_" + n] = vec(f("L3_attn_" + n))
    parts["L3_ffn_Wc1"] = f("L3_ffn_Wc1").T
    parts["same_batch"] = (np.arange(P)[:, None] // 32 == np.arange(P)[None] // 32) * 1.0
    parts["after"], parts["upto"] = np.tril(np.ones((P, P)), -1), np.triu(np.ones((P, P)))
    parts["L2_attn_qkv_w"], parts["L2_attn_z_w"] = f("L2_attn_qkv_w").T, f("L2_attn_z_w").T
    parts["L2_attn_ba"] = np.concatenate([f("L2_attn_b_w").T, f("L2_attn_a_w").T], axis=1)
    parts["L2_attn_conv"] = f("L2_attn_conv_w").reshape(-1, P, 4).transpose(1, 0, 2).reshape(P, -1)
    for n in ("dt_bias", "A_log", "norm_w"):
        parts["L2_attn_" + n] = rows(f("L2_attn_" + n))
    parts["L2_attn_out_w"] = kblocks(f("L2_attn_out_w").T)


def more_arrays(arrays, f, kblocks):
    at = np.arange(P)
    low = [(at[:, None] >> (n + 1) == at[None] >> (n + 1)) & (at[:, None] >> n & 1 == 1) & (at[None] >> n & 1 == 0) for n in range(7)]
    arrays["level_masks"] = np.concatenate(low + [m.T for m in low], axis=1).astype(np.int32)
    arrays["big3"] = np.concatenate([f("L3_ffn_Wm").T, kblocks(f("L3_ffn_Wp").T), np.pad(f("L3_ffn_Wc2").T, ((0, P - 32), (0, 0)))], axis=1)
    arrays["candidate"] = np.array([[(p % 32) << (25 - 5 * n) for n in range(6)] for p in range(P)], np.int32)
    arrays["ind"] = np.tile((np.arange(64)[:, None] == np.arange(64 * 96)[None] // 96).astype(np.float32), (2, 1))
    w1, w2 = f("L0_ffn_w1"), f("L0_ffn_w2")
    arrays["big0"] = np.concatenate([w1.transpose(1, 0, 2).reshape(D, -1)] + [kblocks(w) for w in w2], axis=1)
    arrays["big2"] = np.concatenate([f("L2_ffn_" + n).reshape(-1, D).T for n in ("w_gate", "w_up")]
                                    + [kblocks(f("L2_ffn_w_down").transpose(0, 2, 1).reshape(-1, D))], axis=1)
    tiles = lambda m: np.ascontiguousarray(m.reshape(-1, P, M).transpose(1, 0, 2).reshape(P, -1))
    arrays["mask0"] = tiles(f("mask_BxSxS2_bk0"))
    arrays["mask2"] = tiles(f("mask_SxS2_ik1"))


FIRST, LAST = 0, 12
LAYERS = [layer0, layer1, layer2, layer3, layer4, layer5, layer6, layer7, layer8, layer9, layer10, layer11]


EPSILONS = (1e-5, 1e-8, 1e-6)


def layout(inputs):
    f = lambda n: np.asarray(inputs[n])
    parts = {}
    vec = lambda v: v.reshape(-1, P).T
    kblocks = lambda w: np.concatenate(np.split(w, w.shape[0] // P), axis=1)
    rows = lambda v: np.broadcast_to(v.reshape(1, -1), (P, v.size))
    hd = np.arange(P) // HD
    parts["mean"] = np.full((P, P), 1.0 / P)
    parts["ones"] = np.ones((P, P))
    parts["head_mask"] = (hd[:, None] == hd[None]) * 1.0
    parts["ident"] = np.eye(P)
    parts["eps"] = np.tile(np.array(EPSILONS), (P, 1))
    for n in ("wq", "wk", "wv", "wo", "w1"):
        parts["L0_attn_" + n] = f("L0_attn_" + n)
    parts["L0_attn_w2"] = kblocks(f("L0_attn_w2"))
    for n in ("ln1_g", "ln1_b", "ln2_g", "ln2_b"):
        parts["L0_attn_" + n] = vec(f("L0_attn_" + n))
    more_parts(parts, f, vec, kblocks, rows)
    cols, at = {}, 0
    for n, v in parts.items():
        cols[n] = (at, v.shape[1])
        at += v.shape[1]
    pack = np.concatenate([v.astype(np.float32) for v in parts.values()], axis=1)
    arrays = {"x": np.ascontiguousarray(f("x").reshape(T, D).T), "pack": pack}
    more_arrays(arrays, f, kblocks)
    return arrays, cols


def kernel(**inputs):
    import concourse.bacc as bacc
    from concourse.bass_utils import run_bass_kernel_spmd as run

    nc = bacc.Bacc("TRN2", target_bir_lowering=False, num_devices=1)
    arrays, cols = layout(inputs)
    ap = {n: nc.dram_tensor(f"in_{n}", v.shape, mybir.dt.from_np(v.dtype), kind="ExternalInput").ap() for n, v in arrays.items()}
    out = nc.dram_tensor("out", (P, T), F32, kind="ExternalOutput").ap()
    program(nc, ap, out, cols, FIRST, LAST)
    r = run(nc, [{f"in_{n}": v for n, v in arrays.items()}], core_ids=[0])
    return np.ascontiguousarray(np.asarray(r.results[0]["out"]).T).reshape(B, S, D)
```

```python
from contextlib import ExitStack, contextmanager

import numpy as np
import concourse.bass as bass
from concourse import mybir

ALU = mybir.AluOpType
ACT = mybir.ActivationFunctionType
AX = mybir.AxisListType
F32 = mybir.dt.float32
F32R = mybir.dt.float32r
BF16 = mybir.dt.bfloat16
I32 = mybir.dt.int32

B, S, D, M = 4, 512, 128, 32
T = B * S
P = 128
NT, TB = T // P, S // P
H, HD = 16, 8
LN_EXP = "natural_log_exp_and_others"
MAGIC = 12582912.0


class Kit:
    pass


@contextmanager
def stage(nc, names):
    sems = {n: nc.alloc_semaphore(f"{n}_{nc.next_id()}") for n in names.split()}
    with nc.Block() as block:
        yield block, sems
    nc.clear_and_free_semaphores(list(sems.values()))
    nc.all_engine_barrier()


def after(eng, sem, n):
    if n > 0:
        eng.wait_ge(sem, n)


class Chain:

    def __init__(self, eng, sem):
        self.eng, self.sem, self.n = eng, sem, 0

    def __call__(self, ins):
        self.n += 1
        ins.then_inc(self.sem, 1)
        self.eng.wait_ge(self.sem, self.n)


def sl(i, n=S):
    return slice(i * n, (i + 1) * n)


def norm(nc, k, src, dst, eps, inner=None):
    with ExitStack() as mem, stage(nc, "mean centred squared var ln inv used ratio ln2 inv2 chain") as (block, s):
        sb = lambda n, w: mem.enter_context(nc.sbuf_tensor(f"{n}_{nc.next_id()}", [P, w], F32))
        xc, sq, rs = sb("xc", T), sb("sq", 2 * S), sb("rs", 2 * S)
        tt = sb("tt", 2 * S) if inner else None

        @block.tensor
        def _(pe):
            for b in range(B + 1):
                if b < B:
                    after(pe, s["centred"], b - 1)
                    nc.tensor.matmul(k.ps[b % 2][:, :], k.mean, src[:, sl(b)], start=True, stop=True).then_inc(s["mean"], 1)
                if b:
                    pe.wait_ge(s["squared"], b)
                    after(pe, s["used"], b - 2)
                    nc.tensor.matmul(k.ps[2 + (b - 1) % 2][:, :], k.mean, sq[:, sl((b - 1) % 2)], start=True, stop=True).then_inc(s["var"], 1)

        @block.scalar
        def _(act):
            nc.scalar.preload_act_table_set(LN_EXP)
            for b in range(B + 1):
                if b < B:
                    act.wait_ge(s["centred"], b + 1)
                    after(act, s["var"], b - 1)
                    nc.scalar.activation(sq[:, sl(b % 2)], xc[:, sl(b)], ACT.Square).then_inc(s["squared"], 1)
                if b:
                    c = b - 1
                    r = rs[:, sl(c % 2)]
                    act.wait_ge(s["var"], c + 1)
                    after(act, s["used"], c - 1)
                    nc.scalar.activation(r, k.ps[2 + c % 2][:, :], ACT.Ln, bias=k.eps[eps]).then_inc(s["ln"], 1)
                    act.wait_ge(s["ln"], c + 1)
                    nc.scalar.activation(r, r, ACT.Exp, scale=-0.5).then_inc(s["inv"], 1)
                    if inner:
                        t = tt[:, sl(c % 2)]
                        act.wait_ge(s["ratio"], c + 1)
                        nc.scalar.activation(t, t, ACT.Ln, bias=k.eps[inner[0]]).then_inc(s["ln2"], 1)
                        act.wait_ge(s["ln2"], c + 1)
                        nc.scalar.activation(t, t, ACT.Exp, scale=-0.5).then_inc(s["inv2"], 1)

        @block.vector
        def _(dve):
            link = Chain(dve, s["chain"])
            for b in range(B + 1):
                if b < B:
                    dve.wait_ge(s["mean"], b + 1)
                    nc.vector.tensor_tensor(xc[:, sl(b)], src[:, sl(b)], k.ps[b % 2][:, :], ALU.subtract).then_inc(s["centred"], 1)
                if b:
                    c = b - 1
                    r, t = rs[:, sl(c % 2)], tt[:, sl(c % 2)] if inner else None
                    dve.wait_ge(s["inv"], c + 1)
                    dve.wait_ge(s["centred"], c + 1)
                    out = nc.vector.tensor_tensor(dst[:, sl(c)], xc[:, sl(c)], r, ALU.mult)
                    if not inner:
                        out.then_inc(s["used"], 1)
                        continue
                    _, gain, bias, dst2 = inner
                    link(out)
                    link(nc.vector.tensor_tensor(t, r, r, ALU.mult))
                    nc.vector.tensor_tensor(t, t, k.ps[2 + c % 2][:, :], ALU.mult).then_inc(s["ratio"], 1)
                    dve.wait_ge(s["inv2"], c + 1)
                    if bias is None:
                        nc.vector.scalar_tensor_tensor(out=dst2[:, sl(c)], in0=dst[:, sl(c)], scalar=gain, in1=t, op0=ALU.mult, op1=ALU.mult).then_inc(s["used"], 1)
                    else:
                        link(nc.vector.tensor_tensor(t, dst[:, sl(c)], t, ALU.mult))
                        nc.vector.tensor_scalar(dst2[:, sl(c)], t, gain, bias, ALU.mult, ALU.add).then_inc(s["used"], 1)


def l0_attention(nc, k, y, a, res):
    names = ("k_tok v_tok q_feat kv z_sum num den proj k_min k_exp k_phi v_copy q_min q_exp q_phi "
             "kv_mask recip o_ready done chain")
    with ExitStack() as mem, stage(nc, names) as (block, s):
        sb = lambda n, w: mem.enter_context(nc.sbuf_tensor(f"{n}_{nc.next_id()}", [P, w], F32))
        km, ke, vt, qm, qe, o, rec, kvm, zm = (sb(n, w) for n, w in (("km", S), ("ke", S), ("vt", S), ("qm", S),
                                               ("qe", S), ("o", S), ("rec", S), ("kvm", P), ("zm", P)))
        pk, pv, pq, pkv, pn, pd, po = k.ps[:7]

        @block.tensor
        def _(pe):
            for b in range(B):
                after(pe, s["q_phi"], b)
                after(pe, s["v_copy"], b)
                for ps, w, sem in ((pk, "wk", s["k_tok"]), (pv, "wv", s["v_tok"])):
                    for t in range(TB):
                        mm = nc.tensor.matmul(ps[:, sl(t, P)], a[:, sl(b * TB + t, P)], k.w["L0_attn_" + w], start=True, stop=True)
                    mm.then_inc(sem, 1)
                nc.tensor.matmul(pq[:, :], k.w["L0_attn_wq"], a[:, sl(b)], start=True, stop=True).then_inc(s["q_feat"], 1)
                pe.wait_ge(s["k_phi"], b + 1)
                pe.wait_ge(s["v_copy"], b + 1)
                after(pe, s["kv_mask"], b)
                for t in range(TB):
                    nc.tensor.matmul(pkv[:, 0:P], ke[:, sl(t, P)], vt[:, sl(t, P)], start=t == 0, stop=t == TB - 1)
                for t in range(TB):
                    mm = nc.tensor.matmul(pkv[:, P:P + 1], ke[:, sl(t, P)], k.ones[:, 0:1], start=t == 0, stop=t == TB - 1)
                mm.then_inc(s["kv"], 1)
                pe.wait_ge(s["kv_mask"], b + 1)
                pe.wait_ge(s["q_phi"], b + 1)
                after(pe, s["o_ready"], b)
                nc.tensor.matmul(pn[:, :], kvm[:, :], qe[:, :], start=True, stop=True).then_inc(s["num"], 1)
                nc.tensor.matmul(pd[:, :], zm[:, :], qe[:, :], start=True, stop=True).then_inc(s["den"], 1)
                pe.wait_ge(s["o_ready"], b + 1)
                after(pe, s["done"], b)
                nc.tensor.matmul(po[:, :], k.w["L0_attn_wo"], o[:, :], start=True, stop=True).then_inc(s["proj"], 1)

        @block.scalar
        def _(act):
            for b in range(B):
                act.wait_ge(s["v_tok"], b + 1)
                after(act, s["kv"], b)
                nc.scalar.activation(vt[:, :], pv[:, :], ACT.Copy).then_inc(s["v_copy"], 1)
                act.wait_ge(s["k_min"], b + 1)
                nc.scalar.activation(ke[:, :], km[:, :], ACT.Exp).then_inc(s["k_exp"], 1)
                act.wait_ge(s["q_min"], b + 1)
                nc.scalar.activation(qe[:, :], qm[:, :], ACT.Exp).then_inc(s["q_exp"], 1)

        @block.vector
        def _(dve):
            link = Chain(dve, s["chain"])
            for b in range(B):
                dve.wait_ge(s["k_tok"], b + 1)
                after(dve, s["kv"], b)
                nc.vector.tensor_scalar(km[:, :], pk[:, :], 0.0, None, ALU.min).then_inc(s["k_min"], 1)
                dve.wait_ge(s["q_feat"], b + 1)
                after(dve, s["den"], b)
                nc.vector.tensor_scalar(qm[:, :], pq[:, :], 0.0, None, ALU.min).then_inc(s["q_min"], 1)
                dve.wait_ge(s["k_exp"], b + 1)
                nc.vector.scalar_tensor_tensor(out=ke[:, :], in0=pk[:, :], scalar=0.0, in1=ke[:, :], op0=ALU.max, op1=ALU.add).then_inc(s["k_phi"], 1)
                dve.wait_ge(s["q_exp"], b + 1)
                nc.vector.scalar_tensor_tensor(out=qe[:, :], in0=pq[:, :], scalar=0.0, in1=qe[:, :], op0=ALU.max, op1=ALU.add).then_inc(s["q_phi"], 1)
                dve.wait_ge(s["kv"], b + 1)
                after(dve, s["den"], b)
                nc.vector.tensor_tensor(kvm[:, :], k.heads, pkv[:, 0:P], ALU.mult)
                nc.vector.tensor_scalar(zm[:, :], k.heads, pkv[:, P:P + 1], None, ALU.mult).then_inc(s["kv_mask"], 1)
                dve.wait_ge(s["den"], b + 1)
                link(nc.vector.tensor_scalar(rec[:, :], pd[:, :], 1e-6, None, ALU.add))
                link(nc.vector.reciprocal(rec[:, :], rec[:, :]))
                after(dve, s["proj"], b)
                nc.vector.tensor_tensor(o[:, :], rec[:, :], pn[:, :], ALU.mult).then_inc(s["o_ready"], 1)
                dve.wait_ge(s["proj"], b + 1)
                nc.vector.tensor_tensor(res[:, sl(b)], y[:, sl(b)], po[:, :], ALU.add).then_inc(s["done"], 1)


def l0_lookup_mlp(nc, k, h, y, x):
    C = 4
    with ExitStack() as mem, stage(nc, "up rounded grid act down chain done") as (block, s):
        sb = lambda n, w: mem.enter_context(nc.sbuf_tensor(f"{n}_{nc.next_id()}", [P, w], F32))
        r, g = sb("r", 2 * S), sb("g", 2 * S)
        w1, w2 = k.w["L0_attn_w1"], k.w["L0_attn_w2"]

        @block.tensor
        def _(pe):
            def down(i):
                b, c = divmod(i, C)
                pe.wait_ge(s["act"], i + 1)
                if c == 0:
                    after(pe, s["done"], b)
                nc.tensor.matmul(k.ps[4][:, :], w2[:, sl(c, P)], g[:, sl(i % 2)], start=c == 0, stop=c == C - 1).then_inc(s["down"], 1)

            for i in range(B * C):
                after(pe, s["grid"], i - 3)
                nc.tensor.matmul(k.ps[i % 4][:, :], w1[:, sl(i % C, P)], h[:, sl(i // C)], start=True, stop=True).then_inc(s["up"], 1)
                if i:
                    down(i - 1)
            down(B * C - 1)

        def finish(dve, link, b):
            dve.wait_ge(s["down"], C * (b + 1))
            link(nc.vector.tensor_tensor(y[:, sl(b)], y[:, sl(b)], k.ps[4][:, :], ALU.add))
            nc.vector.tensor_tensor(x[:, sl(b)], x[:, sl(b)], y[:, sl(b)], ALU.add).then_inc(s["done"], 1)

        @block.vector
        def _(dve):
            link = Chain(dve, s["chain"])
            for i in range(B * C):
                b, c = divmod(i, C)
                rr = r[:, sl(i % 2)]
                dve.wait_ge(s["up"], i + 1)
                after(dve, s["act"], i - 1)
                link(nc.vector.tensor_scalar(rr, k.ps[i % 4][:, :], 10.0, MAGIC, ALU.mult, ALU.add))
                link(nc.vector.tensor_scalar(rr, rr, MAGIC, -128.0, ALU.subtract, ALU.max))
                nc.vector.tensor_scalar(rr, rr, 127.0, 0.1, ALU.min, ALU.mult).then_inc(s["grid"], 1)
                if c == 0 and b:
                    finish(dve, link, b - 1)
            finish(dve, link, B - 1)

        @block.scalar
        def _(act):
            for i in range(B * C):
                act.wait_ge(s["grid"], i + 1)
                after(act, s["down"], i - 1)
                nc.scalar.activation(g[:, sl(i % 2)], r[:, sl(i % 2)], ACT.Gelu_apprx_tanh).then_inc(s["act"], 1)


def project(nc, k, jobs):
    with stage(nc, "product copied") as (block, s):
        steps = [(w, src, dst, bias, scale, slice(c, min(c + S, n)))
                 for w, src, n, dst, bias, scale in jobs for c in range(0, n, S)]

        @block.tensor
        def _(pe):
            for i, (w, src, dst, bias, scale, c) in enumerate(steps):
                after(pe, s["copied"], i - 3)
                nc.tensor.matmul(k.ps[i % 4][0:w.shape[-1], 0:c.stop - c.start], w, src[:, c], start=True, stop=True).then_inc(s["product"], 1)

        @block.vector
        def _(dve):
            for i, (w, src, dst, bias, scale, c) in enumerate(steps):
                dve.wait_ge(s["product"], i + 1)
                nc.vector.tensor_scalar(dst[:, c], k.ps[i % 4][0:w.shape[-1], 0:c.stop - c.start],
                                        0.0 if bias is None else bias, scale, ALU.add, ALU.mult).then_inc(s["copied"], 1)


def cross_attention(nc, k, xn, x, q, pre, names, scale, biased, mask=None, fill=0.0, spare=False):
    wq, wk, wv, wo = (k.w[pre + n] for n in names)
    bq, bk, bo = (k.w[pre + n] if biased else None for n in ("bq", "bk", "bo"))
    bo = k.w[pre + "bproj"] if bo is None else bo
    with ExitStack() as mem:
        sb = lambda n, w, p=P: mem.enter_context(nc.sbuf_tensor(f"{n}_{nc.next_id()}", [p, w], F32))
        kt, kbig, vbig = sb("kt", B * M), xn, sb("vbig", B * S)
        crep = sb("crep", B * P)
        project(nc, k, [(wk, k.ctx, B * M, kt, bk, 1.0), (wq, xn, T, q, bq, scale)])
        with stage(nc, "repeated rows added spread") as (block, s):
            @block.vector
            def _(dve):
                for b in range(B):
                    nc.vector.tensor_copy(crep[:, sl(b, P)].rearrange("p (r m) -> p r m", r=4),
                                          k.ctx[:, sl(b, M)].unsqueeze(1).broadcast_to([P, 4, M])).then_inc(s["repeated"], 1)
                for b in range(B):
                    nc.vector.tensor_tensor(kbig[:, sl(b)].rearrange("p (h m) -> p h m", h=H),
                                            kt[:, sl(b, M)].unsqueeze(1).broadcast_to([P, H, M]),
                                            k.w["head_cols"].unsqueeze(2).broadcast_to([P, H, M]), ALU.mult).then_inc(s["spread"], 1)
                for b in range(B):
                    v = k.ps[b][:, 0:P]
                    dve.wait_ge(s["rows"], b + 1)
                    if biased:
                        nc.vector.tensor_tensor(crep[:, sl(b, P)], v, k.w[pre + "bv"], ALU.add).then_inc(s["added"], 1)
                        dve.wait_ge(s["added"], b + 1)
                        v = crep[:, sl(b, P)]
                    nc.vector.tensor_tensor(vbig[:, sl(b)].rearrange("p (c e) -> p c e", c=4),
                                            v.unsqueeze(1).broadcast_to([P, 4, P]),
                                            k.w["head_rows"].rearrange("p (c e) -> p c e", c=4), ALU.mult).then_inc(s["spread"], 1)
                dve.wait_ge(s["spread"], 2 * B)

            @block.tensor
            def _(pe):
                for b in range(B):
                    pe.wait_ge(s["repeated"], b + 1)
                    nc.tensor.matmul(k.ps[b][:, 0:P], crep[:, sl(b, P)], wv, start=True, stop=True).then_inc(s["rows"], 1)

        E = S + H
        keep, neg = (mask, sb("neg", mask.shape[1])) if mask is not None else (None, None)
        d, p, pt = sb("d", 2 * E), sb("p", 2 * E), sb("pt", 2 * 4 * S)
        spt, rmax, o, rec = sb("spt", 2 * S, H), sb("rmax", NT * H), sb("o", S), sb("rec", S)
        sems = "scores max_ready centred weights turned copied values log inv normed proj done chain"
        with stage(nc, sems) as (block, s):
            turned = k.ps[2:4]

            @block.tensor
            def _(pe):
                def attend(b):
                    pe.wait_ge(s["copied"], TB * (b + 1))
                    after(pe, s["normed"], b)
                    for c in range(4):
                        nc.tensor.matmul(k.ps[4][:, :], vbig[:, sl(4 * b + c, P)], pt[:, sl(4 * (b % 2) + c)], start=c == 0, stop=c == 3)
                    for c in range(4):
                        mm = nc.tensor.matmul(k.ps[5][:, :], k.w["head_rows"][:, sl(c, P)], pt[:, sl(4 * (b % 2) + c)],
                                              start=c == 0, stop=c == 3 and not spare)
                    if spare:
                        mm = nc.tensor.matmul(k.ps[5][:, :], k.w["head_of"][0:H, :], spt[:, sl(b % 2)], start=False, stop=True)
                    mm.then_inc(s["values"], 1)

                def out(b):
                    pe.wait_ge(s["normed"], b + 1)
                    after(pe, s["done"], b)
                    nc.tensor.matmul(k.ps[6][:, :], wo, o[:, :], start=True, stop=True).then_inc(s["proj"], 1)

                def turn(i):
                    pe.wait_ge(s["weights"], i + 1)
                    after(pe, s["copied"], i - 1)
                    for c in range(4):
                        mm = nc.tensor.transpose(turned[i % 2][:, sl(c, P)], p[:, (i % 2) * E + c * P:(i % 2) * E + (c + 1) * P], k.ident)
                    if spare:
                        after(pe, s["copied"], i)
                        mm = nc.tensor.transpose(k.ps[7][0:H, 0:P], p[:, (i % 2) * E + S:(i % 2 + 1) * E], k.ident)
                    mm.then_inc(s["turned"], 1)

                for i in range(NT + 1):
                    if i < NT:
                        b = i // TB
                        after(pe, s["centred"], i - 1)
                        nc.tensor.matmul(k.ps[i % 2][:, :], q[:, sl(i, P)], kbig[:, sl(b)], start=True, stop=True).then_inc(s["scores"], 1)
                    if i:
                        turn(i - 1)
                    if i % TB == 1 and i > TB:
                        attend(i // TB - 1)
                    if i % TB == 2 and i > TB:
                        out(i // TB - 1)
                attend(B - 1)
                out(B - 1)

            @block.vector
            def _(dve):
                link = Chain(dve, s["chain"])
                if mask is not None:
                    link(nc.vector.tensor_scalar(neg[:, :], mask, fill, None, ALU.mult))
                    link(nc.vector.tensor_scalar(keep, mask, -1.0, 1.0, ALU.mult, ALU.add))

                def normalise(b):
                    dve.wait_ge(s["inv"], b + 1)
                    after(dve, s["proj"], b)
                    nc.vector.tensor_tensor(o[:, :], rec[:, :], k.ps[4][:, :], ALU.mult).then_inc(s["normed"], 1)

                def finish(b):
                    dve.wait_ge(s["proj"], b + 1)
                    nc.vector.scalar_tensor_tensor(out=x[:, sl(b)], in0=k.ps[6][:, :], scalar=bo, in1=x[:, sl(b)],
                                                   op0=ALU.add, op1=ALU.add).then_inc(s["done"], 1)

                for i in range(NT):
                    heads = lambda a: a.rearrange("p (h m) -> p h m", h=H)
                    dd = d[:, (i % 2) * E:(i % 2) * E + S]
                    mx = rmax[:, sl(i, H)]
                    dve.wait_ge(s["scores"], i + 1)
                    after(dve, s["weights"], i - 1)
                    sc = k.ps[i % 2][:, :]
                    if mask is not None:
                        span = lambda a: a[:, sl(i % (mask.shape[1] // M), M)].unsqueeze(1).broadcast_to([P, H, M])
                        link(nc.vector.tensor_tensor(heads(dd), heads(sc), span(keep), ALU.mult))
                        link(nc.vector.tensor_tensor(heads(dd), heads(dd), span(neg), ALU.add))
                        sc = dd
                    link(nc.vector.tensor_reduce(mx, heads(sc), AX.X, ALU.max))
                    if spare:
                        link(nc.vector.tensor_scalar(mx, mx, 0.0, None, ALU.max))
                        nc.vector.tensor_scalar(d[:, (i % 2) * E + S:(i % 2 + 1) * E], mx, -1.0, None, ALU.mult)
                    nc.vector.tensor_tensor(heads(dd), heads(sc), mx.unsqueeze(2).broadcast_to([P, H, M]), ALU.subtract).then_inc(s["centred"], 1)
                    if i % TB == 2 and i > TB:
                        normalise(i // TB - 1)
                    if i % TB == 3 and i > TB:
                        finish(i // TB - 1)
                normalise(B - 1)
                finish(B - 1)

            @block.scalar
            def _(act):
                nc.scalar.preload_act_table_set(LN_EXP)

                def copy(i):
                    b, t = divmod(i, TB)
                    act.wait_ge(s["turned"], i + 1)
                    after(act, s["values"], b - 1)
                    dst = pt[:, (b % 2) * 4 * S:(b % 2 + 1) * 4 * S].rearrange("p (c t) -> p c t", c=4)[:, :, sl(t, P)]
                    ins = nc.scalar.activation(dst, turned[i % 2][:, :].rearrange("p (c t) -> p c t", c=4), ACT.Copy)
                    if spare:
                        ins = nc.scalar.activation(spt[:, (b % 2) * S + t * P:(b % 2) * S + (t + 1) * P], k.ps[7][0:H, 0:P], ACT.Copy)
                    ins.then_inc(s["copied"], 1)

                def invert(b):
                    act.wait_ge(s["values"], b + 1)
                    after(act, s["normed"], b)
                    nc.scalar.activation(rec[:, :], k.ps[5][:, :], ACT.Ln).then_inc(s["log"], 1)
                    act.wait_ge(s["log"], b + 1)
                    nc.scalar.activation(rec[:, :], rec[:, :], ACT.Exp, scale=-1.0).then_inc(s["inv"], 1)

                for i in range(NT + 1):
                    if i < NT:
                        w = S + (H if spare else 0)
                        act.wait_ge(s["centred"], i + 1)
                        after(act, s["turned"], i - 1)
                        nc.scalar.activation(p[:, (i % 2) * E:(i % 2) * E + w], d[:, (i % 2) * E:(i % 2) * E + w], ACT.Exp).then_inc(s["weights"], 1)
                    if i:
                        copy(i - 1)
                    if i % TB == 1 and i > TB:
                        invert(i // TB - 1)
                invert(B - 1)


def load_big(nc, k, name):
    with nc.Block() as block:
        @block.sync
        def _(sp):
            sp.dma_start(k.big[:, 0:k.ap[name].shape[1]], k.ap[name]).then_inc(k.big_loaded, 16)


def layer1(nc, k, x, y, a):
    norm(nc, k, x, y, 1e-5)
    cross_attention(nc, k, y, x, a, "L0_xattn_", ("Wq", "Wk", "Wv", "Wproj"), HD ** -0.5, False,
                    mask=k.mask0[:, :], fill=-1e30, spare=True)


def layer7(nc, k, x, y, a):
    norm(nc, k, x, y, 1e-5)
    cross_attention(nc, k, y, x, a, "L2_xattn_", ("Wq", "Wk", "Wv", "Wo"), HD ** -0.5, True,
                    mask=k.mask2[:, :], fill=-10000.0)


def layer10(nc, k, x, y, a):
    load_big(nc, k, "big3")
    norm(nc, k, x, y, 1e-5)
    cross_attention(nc, k, y, x, a, "L3_xattn_", ("Wq", "Wk", "Wv", "Wo"), HD ** -0.5, True)


def top2_weights(nc, k, xn, w):
    G = 8
    with ExitStack() as mem, stage(nc, "logits shifted exps done chain") as (block, s):
        sb = lambda n, w_: mem.enter_context(nc.sbuf_tensor(f"{n}_{nc.next_id()}", [P, w_], F32))
        lg, d, gt, eq, rank, mx, tot = (sb(n, c) for n, c in (("lg", NT * G), ("d", NT * G), ("gt", NT * G * G), ("eq", NT * G * G),
                                        ("rank", NT * G), ("mx", NT), ("tot", NT)))

        @block.tensor
        def _(pe):
            for i in range(NT):
                mm = nc.tensor.matmul(k.ps[0][:, sl(i, G)], xn[:, sl(i, P)], k.w["L0_ffn_gate_w"], start=True, stop=True)
            mm.then_inc(s["logits"], 1)

        @block.scalar
        def _(act):
            act.wait_ge(s["shifted"], 1)
            nc.scalar.activation(d[:, :], d[:, :], ACT.Exp).then_inc(s["exps"], 1)

        @block.vector
        def _(dve):
            link = Chain(dve, s["chain"])
            tile = lambda a: a.rearrange("p (t i) -> p t i", i=G)
            pair = lambda a: a[:, :].rearrange("p (t i j) -> p t i j", i=G, j=G)
            full = [P, NT, G, G]
            this = tile(lg[:, :]).unsqueeze(3).broadcast_to(full)
            other = tile(lg[:, :]).unsqueeze(2).broadcast_to(full)
            before = k.w["before8"].rearrange("p (i j) -> p i j", j=G).unsqueeze(1).broadcast_to(full)
            dve.wait_ge(s["logits"], 1)
            link(nc.vector.tensor_tensor(tile(lg[:, :]), tile(k.ps[0][:, 0:NT * G]),
                                         k.w["L0_ffn_gate_b"].unsqueeze(1).broadcast_to([P, NT, G]), ALU.add))
            link(nc.vector.tensor_reduce(mx[:, :], tile(lg[:, :]), AX.X, ALU.max))
            nc.vector.tensor_tensor(tile(d[:, :]), tile(lg[:, :]), mx[:, :].unsqueeze(2).broadcast_to([P, NT, G]), ALU.subtract).then_inc(s["shifted"], 1)
            nc.vector.tensor_tensor(pair(gt), other, this, ALU.is_gt)
            link(nc.vector.tensor_tensor(pair(eq), other, this, ALU.is_equal))
            link(nc.vector.tensor_tensor(pair(eq), pair(eq), before, ALU.mult))
            link(nc.vector.tensor_tensor(gt[:, :], gt[:, :], eq[:, :], ALU.add))
            link(nc.vector.tensor_reduce(rank[:, :], gt[:, :].rearrange("p (a j) -> p a j", j=G), AX.X, ALU.add))
            dve.wait_ge(s["exps"], 1)
            link(nc.vector.scalar_tensor_tensor(out=w[:, :], in0=rank[:, :], scalar=2.0, in1=d[:, :], op0=ALU.is_lt, op1=ALU.mult))
            link(nc.vector.tensor_reduce(tot[:, :], tile(w[:, :]), AX.X, ALU.add))
            link(nc.vector.reciprocal(tot[:, :], tot[:, :]))
            nc.vector.tensor_tensor(tile(w[:, :]), tile(w[:, :]), tot[:, :].unsqueeze(2).broadcast_to([P, NT, G]), ALU.mult).then_inc(s["done"], 1)
            dve.wait_ge(s["done"], 1)


def experts(nc, k, x, y, a, J, loaded, spread, gate_bias=None, up_bias=None, before=None):
    names = "y_high y_low w_high w_low gate up spread silu gated h high low down done"
    with ExitStack() as mem2, stage(nc, names) as (block, s):
        sb2 = lambda n, w_, dt=F32: mem2.enter_context(nc.sbuf_tensor(f"{n}_{nc.next_id()}", [P, w_], dt))
        yh, yl = sb2("yh", 2 * S, F32R), sb2("yl", 2 * S, F32R)
        sg, h, hh, hl = a[:, 0:2 * S], a[:, 2 * S:4 * S], sb2("hh", 3 * S, F32R), sb2("hl", 3 * S, F32R)
        wh, wl = sb2("wh", 3 * 3 * P, F32R), sb2("wl", 3 * 3 * P, F32R)
        banks = [k.ps[0:3], k.ps[3:6]]
        units = [(pair, j, b) for pair in range(B // 2) for j in range(J) for b in (2 * pair, 2 * pair + 1)]
        N = len(units)
        part = lambda t, n, i: t[:, ((n // 2) % 3 * 3 + i) * P:][:, 0:P]

        @block.gpsimd
        def _(pool):
            pool.wait_ge(k.big_loaded, loaded)
            for m in range(N // 2):
                j = m % J
                src = k.big[:, 0:3 * J * P].rearrange("p (w j e) -> p w j e", w=3, j=J)[:, :, j, :]
                high, low = (t[:, (m % 3) * 3 * P:][:, 0:3 * P].rearrange("p (w e) -> p w e", w=3) for t in (wh, wl))
                after(pool, s["down"], 2 * m - 4)
                nc.gpsimd.tensor_copy(high, src).then_inc(s["w_high"], 1)
                pool.wait_ge(s["w_high"], m + 1)
                nc.gpsimd.tensor_tensor(low, src, high.bitcast(F32), ALU.subtract).then_inc(s["w_low"], 1)

        @block.tensor
        def _(pe):
            def three(out, w_, data, cur, start, stop):
                (dh, dl), (ph, pl) = data, w_
                nc.tensor.matmul(out, pl, dh[:, cur], start=start, stop=False)
                nc.tensor.matmul(out, ph, dl[:, cur], start=False, stop=False)
                return nc.tensor.matmul(out, ph, dh[:, cur], start=False, stop=stop)

            def down(n):
                pair, j, b = units[n]
                pe.wait_ge(s["low"], n + 1)
                if j == 0:
                    after(pe, s["done"], 2 * pair)
                if j == 0 and before:
                    before(k.ps[6 + b % 2][:, :], b)
                three(k.ps[6 + b % 2][:, :], (part(wh, n, 2), part(wl, n, 2)), (hh, hl), sl(n % 3), j == 0 and not before, j == J - 1).then_inc(s["down"], 1)

            for n in range(N + 2):
                if n < N:
                    pair, j, b = units[n]
                    pg, pu, pw = banks[n % 2]
                    pe.wait_ge(s["w_low"], n // 2 + 1)
                    pe.wait_ge(s["y_low"], b + 1)
                    after(pe, s["h"], n - 1)
                    three(pg[:, :], (part(wh, n, 0), part(wl, n, 0)), (yh, yl), sl(b % 2), True, True).then_inc(s["gate"], 1)
                    three(pu[:, :], (part(wh, n, 1), part(wl, n, 1)), (yh, yl), sl(b % 2), True, True).then_inc(s["up"], 1)
                    spread(pw[:, :], j, b).then_inc(s["spread"], 1)
                if n >= 2:
                    down(n - 2)

        @block.scalar
        def _(act):
            for n in range(N + 1):
                if n < N:
                    act.wait_ge(s["gate"], n + 1)
                    after(act, s["gated"], n - 1)
                    nc.scalar.activation(sg[:, sl(n % 2)], banks[n % 2][0][:, :], ACT.Silu, bias=gate_bias(units[n][1]) if gate_bias else 0.0).then_inc(s["silu"], 1)
                if n:
                    act.wait_ge(s["h"], n)
                    after(act, s["down"], n - 3)
                    nc.scalar.activation(hh[:, sl((n - 1) % 3)], h[:, sl((n - 1) % 2)], ACT.Copy).then_inc(s["high"], 1)

        @block.vector
        def _(dve):
            def finish(pair):
                dve.wait_ge(s["down"], 2 * J * (pair + 1))
                for b in (2 * pair, 2 * pair + 1):
                    nc.vector.tensor_tensor(x[:, sl(b)], x[:, sl(b)], k.ps[6 + b % 2][:, :], ALU.add).then_inc(s["done"], 1)

            def split(b):
                nc.vector.tensor_copy(yh[:, sl(b % 2)], y[:, sl(b)]).then_inc(s["y_high"], 1)
                dve.wait_ge(s["y_high"], b + 1)
                nc.vector.tensor_tensor(yl[:, sl(b % 2)], y[:, sl(b)], yh[:, sl(b % 2)].bitcast(F32), ALU.subtract).then_inc(s["y_low"], 1)

            for n in range(N + 1):
                cur = sl(n % 2)
                if n < N:
                    pair, j, b = units[n]
                    if j == 0 and b % 2 == 0:
                        after(dve, s["up"], n)
                        split(b)
                        split(b + 1)
                    dve.wait_ge(s["up"], n + 1)
                    dve.wait_ge(s["silu"], n + 1)
                    after(dve, s["low"], n - 1)
                    if up_bias:
                        ins = nc.vector.scalar_tensor_tensor(out=h[:, cur], in0=banks[n % 2][1][:, :], scalar=up_bias(j), in1=sg[:, cur],
                                                             op0=ALU.add, op1=ALU.mult)
                    else:
                        ins = nc.vector.tensor_tensor(h[:, cur], sg[:, cur], banks[n % 2][1][:, :], ALU.mult)
                    ins.then_inc(s["gated"], 1)
                    dve.wait_ge(s["gated"], n + 1)
                    dve.wait_ge(s["spread"], n + 1)
                    nc.vector.tensor_tensor(h[:, cur], h[:, cur], banks[n % 2][2][:, :], ALU.mult).then_inc(s["h"], 1)
                    if pair and j == 1 and b % 2 == 0:
                        finish(pair - 1)
                if n:
                    m = n - 1
                    dve.wait_ge(s["high"], m + 1)
                    after(dve, s["down"], m - 2)
                    nc.vector.tensor_tensor(hl[:, sl(m % 3)], h[:, sl(m % 2)], hh[:, sl(m % 3)].bitcast(F32), ALU.subtract).then_inc(s["low"], 1)
            finish(B // 2 - 1)


def layer2(nc, k, x, y, a):
    G, C = 8, 4
    norm(nc, k, x, y, 1e-5)
    with ExitStack() as mem:
        sb = lambda n, w_, dt=F32, p=P: mem.enter_context(nc.sbuf_tensor(f"{n}_{nc.next_id()}", [p, w_], dt))
        w, wt, w3, wt3, ind = (sb("w", NT * G), sb("wt", T, F32, G), sb("w3", NT * 3 * G, BF16), sb("wt3", T, BF16, 3 * G),
                               sb("ind", G * P, BF16, 3 * G))
        top2_weights(nc, k, y, w)
        with stage(nc, "loaded split turned copied chain") as (block, s):
            @block.gpsimd
            def _(pool):
                pool.dma_start(ind[:, :], k.ap["ind0"]).then_inc(s["loaded"], 16)
                pool.wait_ge(s["loaded"], 16)

            @block.tensor
            def _(pe):
                for b in range(B):
                    for t in range(TB):
                        nc.tensor.transpose(k.ps[b][0:G, sl(t, P)], w[:, sl(b * TB + t, G)], k.ident)
                pe.wait_ge(s["split"], 1)
                for b in range(B):
                    for t in range(TB):
                        mm = nc.tensor.transpose(k.ps[4 + b][0:3 * G, 0:S // 2].bitcast(BF16)[:, sl(t, P)], w3[:, sl(b * TB + t, 3 * G)], k.ident_bf)
                    mm.then_inc(s["turned"], 1)

            @block.vector
            def _(dve):
                link = Chain(dve, s["chain"])
                tile = lambda t, n: t[:, :].rearrange("p (t i) -> p t i", i=n)
                parts = [tile(w3, 3 * G)[:, :, n * G:(n + 1) * G] for n in range(3)]
                left = sb("left", NT * G)
                link(nc.vector.tensor_copy(parts[0], tile(w, G)))
                link(nc.vector.tensor_tensor(tile(left, G), tile(w, G), parts[0], ALU.subtract))
                link(nc.vector.tensor_copy(parts[1], tile(left, G)))
                link(nc.vector.tensor_tensor(tile(left, G), tile(left, G), parts[1], ALU.subtract))
                nc.vector.tensor_copy(parts[2], tile(left, G)).then_inc(s["split"], 1)
                for b in range(B):
                    dve.wait_ge(s["turned"], b + 1)
                    nc.vector.tensor_copy(wt[:, sl(b)], k.ps[b][0:G, :]).then_inc(s["copied"], 1)
                dve.wait_ge(s["copied"], 2 * B)

            @block.scalar
            def _(act):
                for b in range(B):
                    act.wait_ge(s["turned"], b + 1)
                    nc.scalar.activation(wt3[:, sl(b)], k.ps[4 + b][0:3 * G, 0:S // 2].bitcast(BF16), ACT.Copy).then_inc(s["copied"], 1)

        experts(nc, k, x, y, a, G * C, 16,
                spread=lambda bank, j, b: nc.tensor.matmul(bank, ind[:, sl(j // C, P)], wt3[:, sl(b)], start=True, stop=True),
                gate_bias=lambda j: k.w["L0_ffn_b1"][:, j // C * 2 * C + C + j % C:][:, 0:1],
                up_bias=lambda j: k.w["L0_ffn_b1"][:, j // C * 2 * C + j % C:][:, 0:1],
                before=lambda bank, b: nc.tensor.matmul(bank, k.w["L0_ffn_b2"][0:G, :], wt[:, sl(b)], start=True, stop=False))


def layer3(nc, k, x, y, a):
    norm(nc, k, x, y, 1e-5, inner=(1e-5, k.w["L1_attn_rms_weight"], None, a))
    with ExitStack() as mem, stage(nc, "forget value side gate sig driven scanned gated proj done chain") as (block, s):
        sb = lambda n, w_: mem.enter_context(nc.sbuf_tensor(f"{n}_{nc.next_id()}", [P, w_], F32))
        fg, sd, gt, h = sb("fg", 2 * S), sb("sd", 2 * S), sb("gt", 2 * S), sb("h", 2 * S)

        @block.tensor
        def _(pe):
            def out(b):
                pe.wait_ge(s["gated"], b + 1)
                nc.tensor.matmul(k.ps[4 + b][:, :], k.w["L1_attn_w_o"], h[:, sl(b % 2)], start=True, stop=True).then_inc(s["proj"], 1)

            for b in range(B):
                after(pe, s["driven"], b)
                for j, (n, sem) in enumerate((("w_A", s["forget"]), ("w_output", s["side"]), ("w_sidegate", s["gate"]), ("w_x", s["value"]))):
                    nc.tensor.matmul(k.ps[j][:, :], k.w["L1_attn_" + n], a[:, sl(b)], start=True, stop=True).then_inc(sem, 1)
                if b:
                    out(b - 1)
            out(B - 1)

        @block.scalar
        def _(act):
            for b in range(B):
                after(act, s["gated"], b - 1)
                for j, (sem, dst, bias) in enumerate(((s["forget"], fg, k.w["L1_attn_b_A"]), (s["side"], sd, 0.0), (s["gate"], gt, 0.0))):
                    act.wait_ge(sem, b + 1)
                    nc.scalar.activation(dst[:, sl(b % 2)], k.ps[j][:, :], ACT.Sigmoid, bias=bias).then_inc(s["sig"], 1)

        @block.vector
        def _(dve):
            link = Chain(dve, s["chain"])
            for b in range(B):
                cur = sl(b % 2)
                dve.wait_ge(s["value"], b + 1)
                dve.wait_ge(s["sig"], 3 * b + 3)
                nc.vector.tensor_tensor(sd[:, cur], sd[:, cur], k.ps[3][:, :], ALU.mult).then_inc(s["driven"], 1)
                dve.wait_ge(s["driven"], b + 1)
                after(dve, s["proj"], b - 1)
                link(nc.vector.tensor_tensor_scan(h[:, cur], fg[:, cur], sd[:, cur], 0.0, ALU.mult, ALU.add))
                nc.vector.tensor_tensor(h[:, cur], h[:, cur], gt[:, cur], ALU.mult).then_inc(s["gated"], 1)
            for b in range(B):
                dve.wait_ge(s["proj"], b + 1)
                link(nc.vector.tensor_tensor(y[:, sl(b)], y[:, sl(b)], k.ps[4 + b][:, :], ALU.add))
                link(nc.vector.tensor_tensor(x[:, sl(b)], x[:, sl(b)], y[:, sl(b)], ALU.add))


def layer4(nc, k, x, y, a):
    norm(nc, k, x, y, 1e-5)
    q = a
    with ExitStack() as mem:
        sb = lambda n, w_, p=P: mem.enter_context(nc.sbuf_tensor(f"{n}_{nc.next_id()}", [p, w_], F32))
        kt, v, p, pt, mx = sb("kt", B * M), sb("v", B * D, M), sb("p", NT * M), sb("pt", T, M), sb("mx", NT)
        project(nc, k, [(k.w["L1_xattn_Wk"], k.ctx, B * M, kt, None, 1.0), (k.w["L1_xattn_Wq"], y, T, q, None, D ** -0.5)])
        with stage(nc, "scores values centred exps weights turned copied out done chain vcopied") as (block, s):
            @block.tensor
            def _(pe):
                for i in range(NT):
                    mm = nc.tensor.matmul(k.ps[0][:, sl(i, M)], q[:, sl(i, P)], kt[:, sl(i // TB, M)], start=True, stop=True)
                mm.then_inc(s["scores"], 1)
                for b in range(B):
                    mm = nc.tensor.matmul(k.ps[1][0:M, sl(b, D)], k.ctx[:, sl(b, M)], k.w["L1_xattn_Wv"], start=True, stop=True)
                mm.then_inc(s["values"], 1)
                pe.wait_ge(s["weights"], 1)
                for b in range(B):
                    for t in range(TB):
                        mm = nc.tensor.transpose(k.ps[2 + b][0:M, sl(t, P)], p[:, sl(b * TB + t, M)], k.ident)
                    mm.then_inc(s["turned"], 1)
                pe.wait_ge(s["vcopied"], 1)
                for b in range(B):
                    pe.wait_ge(s["copied"], b + 1)
                    after(pe, s["done"], b - 1)
                    nc.tensor.matmul(k.ps[6 + b % 2][:, :], v[:, sl(b, D)], pt[:, sl(b)], start=True, stop=True).then_inc(s["out"], 1)

            @block.scalar
            def _(act):
                act.wait_ge(s["centred"], 1)
                nc.scalar.activation(p[:, :], p[:, :], ACT.Exp).then_inc(s["exps"], 1)
                act.wait_ge(s["values"], 1)
                nc.scalar.activation(v[:, :], k.ps[1][0:M, :], ACT.Copy).then_inc(s["vcopied"], 1)
                for b in range(B):
                    act.wait_ge(s["turned"], b + 1)
                    nc.scalar.activation(pt[:, sl(b)], k.ps[2 + b][0:M, :], ACT.Copy).then_inc(s["copied"], 1)

            @block.vector
            def _(dve):
                link = Chain(dve, s["chain"])
                tile = lambda t: t[:, :].rearrange("p (t m) -> p t m", m=M)
                wide = mx[:, :].unsqueeze(2).broadcast_to([P, NT, M])
                dve.wait_ge(s["scores"], 1)
                link(nc.vector.tensor_reduce(mx[:, :], tile(k.ps[0]), AX.X, ALU.max))
                nc.vector.tensor_tensor(tile(p), tile(k.ps[0]), wide, ALU.subtract).then_inc(s["centred"], 1)
                dve.wait_ge(s["exps"], 1)
                link(nc.vector.tensor_reduce(mx[:, :], tile(p), AX.X, ALU.add))
                link(nc.vector.reciprocal(mx[:, :], mx[:, :]))
                nc.vector.tensor_tensor(tile(p), tile(p), wide, ALU.mult).then_inc(s["weights"], 1)
                for b in range(B):
                    dve.wait_ge(s["out"], b + 1)
                    nc.vector.tensor_tensor(x[:, sl(b)], x[:, sl(b)], k.ps[6 + b % 2][:, :], ALU.add).then_inc(s["done"], 1)


def layer5(nc, k, x, y, a):
    F, C = 512, 4
    norm(nc, k, x, y, 1e-5, inner=(1e-8, k.w["L1_ffn_norm1_w"], None, a))
    w1, w2 = k.w["L1_ffn_w1"], k.w["L1_ffn_w2"]
    with ExitStack() as mem:
        sb = lambda n, w_, dt=F32: mem.enter_context(nc.sbuf_tensor(f"{n}_{nc.next_id()}", [P, w_], dt))
        q1w, q2w, tmp = sb("q1w", F, BF16), sb("q2w", F, BF16), sb("tmp", F)
        part, wmean, wscale = sb("part", 2), sb("wmean", 2), sb("wscale", 2)
        with stage(nc, "abs summed total rounded chain") as (block, s):
            @block.scalar
            def _(act):
                for j, w in enumerate((w1, w2)):
                    after(act, s["abs"], j)
                    nc.scalar.activation(tmp[:, :], w, ACT.Abs, accum_out=part[:, j:j + 1]).then_inc(s["abs"], 1)

            @block.tensor
            def _(pe):
                pe.wait_ge(s["abs"], 2)
                nc.tensor.matmul(k.ps[0][:, 0:2], k.ones, part[:, :], start=True, stop=True).then_inc(s["total"], 1)

            @block.vector
            def _(dve):
                link = Chain(dve, s["chain"])
                dve.wait_ge(s["total"], 1)
                link(nc.vector.tensor_scalar(wmean[:, :], k.ps[0][:, 0:2], 1.0 / (D * F), 1e-5, ALU.mult, ALU.max))
                link(nc.vector.reciprocal(wscale[:, :], wmean[:, :]))
                for j, (w, q) in enumerate(((w1, q1w), (w2, q2w))):
                    link(nc.vector.tensor_scalar(tmp[:, :], w, wscale[:, j:j + 1], MAGIC, ALU.mult, ALU.add))
                    link(nc.vector.tensor_scalar(tmp[:, :], tmp[:, :], MAGIC, -1.0, ALU.subtract, ALU.max))
                    link(nc.vector.tensor_scalar(q[:, :], tmp[:, :], 1.0, None, ALU.min))

        top, sc, un = sb("top", 2 * NT), sb("sc", 2 * NT), sb("un", 2 * NT)
        ss, r1 = sb("ss", NT), sb("r1", NT)
        f1, q1, q1t = sb("f1", 2 * P), sb("q1", 2 * P, BF16), sb("q1t", 2 * P, BF16)
        r, h, hn, q2, q2t, o = (sb("r", 2 * F), sb("h", 2 * F), sb("hn", 2 * F), sb("q2", 2 * F, BF16), sb("q2t", 2 * F, BF16), sb("o", 2 * P))
        p_in, p_t2, p_o = k.ps[0:2], k.ps[6], k.ps[7]
        p_q = k.ps[2][:, 0:P // 2].bitcast(BF16)
        p_h = k.ps[3:5]
        p_q2 = k.ps[5][:, 0:F // 2].bitcast(BF16)
        names = ("turned quant1 q_turned q_copied up relu hidden sq log inv quant2 q2_turned q2_copied down scaled back added chain achain")
        with stage(nc, names) as (block, s):
            col = lambda t, j, i: t[:, j * NT + i:j * NT + i + 1]

            @block.tensor
            def _(pe):
                for i in range(NT + 2):
                    if i < NT:
                        after(pe, s["quant1"], i - 1)
                        nc.tensor.transpose(p_in[i % 2][:, 0:P], a[:, sl(i, P)], k.ident).then_inc(s["turned"], 1)
                    if 1 <= i <= NT:
                        c = i - 1
                        pe.wait_ge(s["quant1"], c + 1)
                        after(pe, s["q_copied"], c)
                        nc.tensor.transpose(p_q, q1[:, sl(c % 2, P)], k.ident_bf).then_inc(s["q_turned"], 1)
                        pe.wait_ge(s["q_copied"], c + 1)
                        after(pe, s["relu"], c - 1)
                        nc.tensor.matmul(p_h[c % 2][:, :], q1t[:, sl(c % 2, P)], q1w[:, :], start=True, stop=True).then_inc(s["up"], 1)
                    if i >= 2:
                        c = i - 2
                        pe.wait_ge(s["quant2"], c + 1)
                        after(pe, s["q2_copied"], c)
                        for j in range(C):
                            mm = nc.tensor.transpose(p_q2[:, sl(j, P)], q2[:, (c % 2) * F + j * P:][:, 0:P], k.ident_bf)
                        mm.then_inc(s["q2_turned"], 1)
                        pe.wait_ge(s["q2_copied"], c + 1)
                        after(pe, s["scaled"], c)
                        for j in range(C):
                            mm = nc.tensor.matmul(p_o[:, 0:P], q2t[:, (c % 2) * F + j * P:][:, 0:P], q2w[:, sl(j, P)], start=j == 0, stop=j == C - 1)
                        mm.then_inc(s["down"], 1)
                        pe.wait_ge(s["scaled"], c + 1)
                        after(pe, s["added"], c)
                        nc.tensor.transpose(p_t2[:, 0:P], o[:, sl(c % 2, P)], k.ident).then_inc(s["back"], 1)

            @block.vector
            def _(dve):
                link = Chain(dve, s["chain"])

                def quantise(src, tmp, dst, j, i, done):
                    t, m, u = col(top, j, i), col(sc, j, i), col(un, j, i)
                    link(nc.vector.tensor_reduce(t, src, AX.X, ALU.max, apply_absolute_value=True))
                    link(nc.vector.tensor_scalar(t, t, 1e-5, None, ALU.max))
                    link(nc.vector.reciprocal(m, t))
                    link(nc.vector.tensor_scalar(m, m, 127.0, None, ALU.mult))
                    link(nc.vector.tensor_scalar(u, t, 1.0 / 127.0, wmean[:, j:j + 1], ALU.mult, ALU.mult))
                    link(nc.vector.tensor_scalar(tmp, src, m, MAGIC, ALU.mult, ALU.add))
                    link(nc.vector.tensor_scalar(tmp, tmp, MAGIC, -128.0, ALU.subtract, ALU.max))
                    nc.vector.tensor_scalar(dst, tmp, 127.0, None, ALU.min).then_inc(done, 1)

                for i in range(NT + 2):
                    if i < NT:
                        dve.wait_ge(s["turned"], i + 1)
                        after(dve, s["q_turned"], i - 1)
                        quantise(p_in[i % 2][:, 0:P], f1[:, sl(i % 2, P)], q1[:, sl(i % 2, P)], 0, i, s["quant1"])
                    if 1 <= i <= NT:
                        c = i - 1
                        cur = sl(c % 2, F)
                        dve.wait_ge(s["relu"], c + 1)
                        link(nc.vector.tensor_tensor(h[:, cur], r[:, cur], r[:, cur], ALU.mult))
                        nc.vector.tensor_scalar(h[:, cur], h[:, cur], k.w["L1_ffn_act_scale"], k.w["L1_ffn_act_bias"], ALU.mult, ALU.add).then_inc(s["hidden"], 1)
                        dve.wait_ge(s["inv"], c + 1)
                        link(nc.vector.scalar_tensor_tensor(out=hn[:, cur], in0=h[:, cur], scalar=r1[:, c:c + 1], in1=k.w["L1_ffn_norm2_w"], op0=ALU.mult, op1=ALU.mult))
                        after(dve, s["q2_turned"], c - 1)
                        quantise(hn[:, cur], hn[:, cur], q2[:, cur], 1, c, s["quant2"])
                    if i >= 2:
                        c = i - 2
                        dve.wait_ge(s["down"], c + 1)
                        after(dve, s["back"], c - 1)
                        nc.vector.tensor_scalar(o[:, sl(c % 2, P)], p_o[:, 0:P], col(un, 1, c), None, ALU.mult).then_inc(s["scaled"], 1)
                        dve.wait_ge(s["back"], c + 1)
                        nc.vector.tensor_tensor(x[:, sl(c, P)], x[:, sl(c, P)], p_t2[:, 0:P], ALU.add).then_inc(s["added"], 1)

            @block.scalar
            def _(act):
                nc.scalar.preload_act_table_set(LN_EXP)
                alink = Chain(act, s["achain"])
                for i in range(NT + 2):
                    if 1 <= i <= NT:
                        c = i - 1
                        cur = sl(c % 2, F)
                        act.wait_ge(s["q_turned"], c + 1)
                        after(act, s["up"], c - 1)
                        nc.scalar.activation(q1t[:, sl(c % 2, P)], p_q, ACT.Copy).then_inc(s["q_copied"], 1)
                        act.wait_ge(s["up"], c + 1)
                        after(act, s["hidden"], c - 1)
                        nc.scalar.activation(r[:, cur], p_h[c % 2][:, :], ACT.Relu, scale=col(un, 0, c)).then_inc(s["relu"], 1)
                        act.wait_ge(s["hidden"], c + 1)
                        after(act, s["quant2"], c - 1)
                        alink(nc.scalar.activation(hn[:, cur], h[:, cur], ACT.Square, accum_out=ss[:, c:c + 1]))
                        alink(nc.scalar.activation(ss[:, c:c + 1], ss[:, c:c + 1], ACT.Ln, scale=1.0 / F, bias=k.eps[1e-8]))
                        nc.scalar.activation(r1[:, c:c + 1], ss[:, c:c + 1], ACT.Exp, scale=-0.5).then_inc(s["inv"], 1)
                    if i >= 2:
                        c = i - 2
                        act.wait_ge(s["q2_turned"], c + 1)
                        after(act, s["down"], c - 1)
                        nc.scalar.activation(q2t[:, sl(c % 2, F)], p_q2, ACT.Copy).then_inc(s["q2_copied"], 1)


def layer8(nc, k, x, y, a):
    G, F = 64, 96
    J = G * F // P
    norm(nc, k, x, y, 1e-5)
    with ExitStack() as mem:
        sb = lambda n, w_, dt=F32, p=P: mem.enter_context(nc.sbuf_tensor(f"{n}_{nc.next_id()}", [p, w_], dt))
        ind = sb("ind", J * P, BF16)
        wt_hm, wt_lo = sb("wt_hm", T, BF16), sb("wt_lo", T, BF16, G)
        with ExitStack() as mem2, stage(nc, "loaded logits shifted exps split turned copied chain") as (block, s):
            sb2 = lambda n, w_, dt=F32: mem2.enter_context(nc.sbuf_tensor(f"{n}_{nc.next_id()}", [P, w_], dt))
            sc, sel, top, mx = sb2("sc", NT * G), sb2("sel", NT * G), sb2("top", NT * 8), sb2("mx", NT)
            hm, lo = sb2("hm", NT * 2 * G, BF16), sb2("lo", NT * G, BF16)

            @block.gpsimd
            def _(pool):
                pool.dma_start(ind[:, :], k.ap["ind"]).then_inc(s["loaded"], 16)
                pool.wait_ge(s["loaded"], 16)

            @block.tensor
            def _(pe):
                for i in range(NT):
                    mm = nc.tensor.matmul(k.ps[i // 8][:, sl(i % 8, G)], y[:, sl(i, P)], k.w["L2_ffn_gate_w"], start=True, stop=True)
                mm.then_inc(s["logits"], 1)
                pe.wait_ge(s["split"], 1)
                for b in range(B):
                    after(pe, s["copied"], 2 * b)
                    for t in range(TB):
                        i = b * TB + t
                        nc.tensor.transpose(k.ps[2][:, 0:S // 2].bitcast(BF16)[:, sl(t, P)], hm[:, sl(i, P)], k.ident_bf)
                    for t in range(TB):
                        i = b * TB + t
                        mm = nc.tensor.transpose(k.ps[3][0:G, 0:S // 2].bitcast(BF16)[:, sl(t, P)], lo[:, sl(i, G)], k.ident_bf)
                    mm.then_inc(s["turned"], 1)

            @block.scalar
            def _(act):
                act.wait_ge(s["shifted"], 1)
                nc.scalar.activation(sc[:, :], sc[:, :], ACT.Exp).then_inc(s["exps"], 1)
                for b in range(B):
                    act.wait_ge(s["turned"], b + 1)
                    nc.scalar.activation(wt_hm[:, sl(b)], k.ps[2][:, 0:S // 2].bitcast(BF16), ACT.Copy).then_inc(s["copied"], 1)
                    nc.scalar.activation(wt_lo[:, sl(b)], k.ps[3][0:G, 0:S // 2].bitcast(BF16), ACT.Copy).then_inc(s["copied"], 1)

            @block.vector
            def _(dve):
                link = Chain(dve, s["chain"])
                tile = lambda t: t[:, :].rearrange("p (t i) -> p t i", t=NT)
                wide = mx[:, :].unsqueeze(2).broadcast_to([P, NT, G])
                dve.wait_ge(s["logits"], 1)
                for j in range(2):
                    link(nc.vector.tensor_copy(sc[:, sl(j)], k.ps[j][:, :]))
                link(nc.vector.tensor_reduce(mx[:, :], tile(sc), AX.X, ALU.max))
                nc.vector.tensor_tensor(tile(sc), tile(sc), wide, ALU.subtract).then_inc(s["shifted"], 1)
                dve.wait_ge(s["exps"], 1)
                link(nc.vector.tensor_reduce(mx[:, :], tile(sc), AX.X, ALU.add))
                link(nc.vector.reciprocal(mx[:, :], mx[:, :]))
                link(nc.vector.tensor_tensor(tile(sc), tile(sc), wide, ALU.mult))
                for i in range(NT):
                    link(nc.vector.max(top[:, sl(i, 8)], sc[:, sl(i, G)]))
                    link(nc.vector.match_replace(out=sel[:, sl(i, G)], in_to_replace=top[:, sl(i, 8)], in_values=sc[:, sl(i, G)], imm_value=-1.0))
                link(nc.vector.scalar_tensor_tensor(out=sc[:, :], in0=sel[:, :], scalar=0.0, in1=sc[:, :], op0=ALU.is_lt, op1=ALU.mult))
                link(nc.vector.tensor_reduce(mx[:, :], tile(sc), AX.X, ALU.add))
                link(nc.vector.tensor_scalar(mx[:, :], mx[:, :], 1e-20, None, ALU.add))
                link(nc.vector.reciprocal(mx[:, :], mx[:, :]))
                link(nc.vector.tensor_tensor(tile(sc), tile(sc), wide, ALU.mult))
                hi, mid = tile(hm)[:, :, 0:G], tile(hm)[:, :, G:2 * G]
                link(nc.vector.tensor_copy(hi, tile(sc)))
                link(nc.vector.tensor_tensor(tile(sc), tile(sc), hi, ALU.subtract))
                link(nc.vector.tensor_copy(mid, tile(sc)))
                link(nc.vector.tensor_tensor(tile(sc), tile(sc), mid, ALU.subtract))
                nc.vector.tensor_copy(lo[:, :], sc[:, :]).then_inc(s["split"], 1)

        def spread(pw, j, b):
            nc.tensor.matmul(pw, ind[:, sl(j, P)], wt_hm[:, sl(b)], start=True, stop=False)
            return nc.tensor.matmul(pw, ind[0:G, sl(j, P)], wt_lo[:, sl(b)], start=False, stop=True)

        experts(nc, k, x, y, a, J, 32, spread)


def layer6(nc, k, x, y, a):
    HH, GH = 8, 4
    norm(nc, k, x, y, 1e-5)
    with ExitStack() as mem:
        sb = lambda n, w_, dt=F32: mem.enter_context(nc.sbuf_tensor(f"{n}_{nc.next_id()}", [P, w_], dt))
        g, beta, nbeta, gam, ngam, rest, tot = (sb(n, NT * HH) for n in ("g", "beta", "nbeta", "gam", "ngam", "rest", "tot"))
        delta_gates(nc, k, y, g, beta, nbeta, gam, ngam, rest, tot, HH)
        q, kk, v, z = (k.big[:, j * 8 * S:(j + 1) * 8 * S] for j in range(4))
        W = GH * P
        state, free = a[:, 0:HH * P], k.big[:, 32 * S:32 * S + 4 * W]
        bufs = {n: [sb(n, W) for _ in range(2)] for n in ("ea", "at", "nn", "vv", "kt")}
        bufs["mm"] = [a[:, HH * P + j * W:][:, 0:W] for j in range(2)]
        bufs["ex"] = [free[:, sl(j, W)] for j in range(2)]
        gs = [free[:, sl(2 + j, W)] for j in range(2)]
        small = {n: sb(n, 2 * GH) for n in ("ss", "rstd")}
        for b in range(B):
            delta_project(nc, k, y, b, z, bufs["ea"] + bufs["at"])
            delta_chunks(nc, k, x, b, q, kk, v, z, state, bufs, gs, small, g, beta, nbeta, gam, ngam, rest, tot, HH, GH)
    load_big(nc, k, "big2")


def delta_gates(nc, k, y, g, beta, nbeta, gam, ngam, rest, tot, HH):
    W = NT * HH
    with ExitStack() as mem, stage(nc, "ba shifted exps lns bexp aexp g_ready sums decays chain") as (block, s):
        sb = lambda n, w_: mem.enter_context(nc.sbuf_tensor(f"{n}_{nc.next_id()}", [P, w_], F32))
        bb, aa, t1, al = sb("bb", W), sb("aa", W), sb("t1", W), sb("al", HH)

        @block.tensor
        def _(pe):
            for i in range(NT):
                mm = nc.tensor.matmul(k.ps[0][:, sl(i, 2 * HH)], y[:, sl(i, P)], k.w["L2_attn_ba"], start=True, stop=True)
            mm.then_inc(s["ba"], 1)
            pe.wait_ge(s["g_ready"], 1)
            for j, w in enumerate((k.w["upto"], k.w["after"], k.ones)):
                mm = nc.tensor.matmul(k.ps[1][:, sl(j, P)], w, g[:, :], start=True, stop=True)
            mm.then_inc(s["sums"], 1)

        @block.scalar
        def _(act):
            nc.scalar.preload_act_table_set(LN_EXP)
            nc.scalar.activation(al[:, :], k.w["L2_attn_A_log"], ACT.Exp).then_inc(s["aexp"], 1)
            act.wait_ge(s["shifted"], 1)
            nc.scalar.activation(bb[:, :], bb[:, :], ACT.Exp).then_inc(s["bexp"], 1)
            nc.scalar.activation(t1[:, :], t1[:, :], ACT.Exp).then_inc(s["exps"], 1)
            act.wait_ge(s["exps"], 1)
            nc.scalar.activation(t1[:, :], t1[:, :], ACT.Ln, bias=k.ones[:, 0:1]).then_inc(s["lns"], 1)
            act.wait_ge(s["sums"], 1)
            for j, dst in enumerate((gam, rest, tot)):
                nc.scalar.activation(dst[:, :], k.ps[1][:, sl(j, P)], ACT.Exp).then_inc(s["decays"], 1)

        @block.vector
        def _(dve):
            link = Chain(dve, s["chain"])
            tile = lambda t: t[:, :].rearrange("p (t h) -> p t h", h=HH)
            ps = k.ps[0][:, 0:2 * W].rearrange("p (t h) -> p t h", h=2 * HH)
            wide = lambda c: c.unsqueeze(1).broadcast_to([P, NT, HH])
            dve.wait_ge(s["ba"], 1)
            link(nc.vector.tensor_scalar(tile(bb), ps[:, :, 0:HH], -1.0, 80.0, ALU.mult, ALU.min))
            link(nc.vector.tensor_tensor(tile(aa), ps[:, :, HH:2 * HH], wide(k.w["L2_attn_dt_bias"]), ALU.add))
            link(nc.vector.tensor_scalar(t1[:, :], aa[:, :], -1.0, None, ALU.mult))
            nc.vector.tensor_tensor(t1[:, :], t1[:, :], aa[:, :], ALU.min).then_inc(s["shifted"], 1)
            dve.wait_ge(s["bexp"], 1)
            link(nc.vector.tensor_scalar(bb[:, :], bb[:, :], 1.0, None, ALU.add))
            link(nc.vector.reciprocal(beta[:, :], bb[:, :]))
            link(nc.vector.tensor_scalar(nbeta[:, :], beta[:, :], -1.0, None, ALU.mult))
            dve.wait_ge(s["lns"], 1)
            dve.wait_ge(s["aexp"], 1)
            link(nc.vector.tensor_scalar(al[:, :], al[:, :], 3e38, -1.0, ALU.min, ALU.mult))
            link(nc.vector.scalar_tensor_tensor(out=aa[:, :], in0=aa[:, :], scalar=0.0, in1=t1[:, :], op0=ALU.max, op1=ALU.add))
            link(nc.vector.tensor_tensor(tile(aa), tile(aa), wide(al[:, :]), ALU.mult))
            nc.vector.tensor_scalar(g[:, :], aa[:, :], -200.0, None, ALU.max).then_inc(s["g_ready"], 1)
            dve.wait_ge(s["decays"], 3)
            link(nc.vector.tensor_scalar(ngam[:, :], gam[:, :], -1.0, None, ALU.mult))


def delta_project(nc, k, y, b, z, tapped):
    TAPS = 4
    with ExitStack() as mem, stage(nc, "raw scaled conv whole z_ps z_done chain") as (block, s):
        chans = 24
        zmm = 2 * TB

        @block.tensor
        def _(pe):
            for n in range(zmm):
                t, j = divmod(n, 2)
                after(pe, s["z_done"], n - 1)
                nc.tensor.matmul(k.ps[6 + n % 2][:, :], y[:, sl(b * TB + t, P)], k.w["L2_attn_z_w"][:, sl(j)], start=True, stop=True).then_inc(s["z_ps"], 1)
            for m in range(chans):
                after(pe, s["conv"], m - 5)
                nc.tensor.matmul(k.ps[m % 6][:, :], k.w["L2_attn_qkv_w"][:, sl(m, P)], y[:, sl(b)], start=True, stop=True).then_inc(s["raw"], 1)

        @block.scalar
        def _(act):
            for n in range(zmm):
                act.wait_ge(s["z_ps"], n + 1)
                nc.scalar.activation(z[:, sl(n)], k.ps[6 + n % 2][:, :], ACT.Silu).then_inc(s["z_done"], 1)
            for m in range(chans):
                act.wait_ge(s["raw"], m + 1)
                after(act, s["whole"], m - 3)
                for dst, tap in ((k.big[:, sl(m)], 3), (tapped[m % 4][:, :], 2)):
                    ins = nc.scalar.activation(dst, k.ps[m % 6][:, :], ACT.Copy, scale=k.w["L2_attn_conv"][:, m * TAPS + tap:m * TAPS + tap + 1])
                ins.then_inc(s["scaled"], 1)
            act.wait_ge(s["z_done"], zmm)

        @block.vector
        def _(dve):
            link = Chain(dve, s["chain"])
            for m in range(chans):
                dve.wait_ge(s["scaled"], m + 1)
                for back in range(2, TAPS):
                    dst = k.big[:, m * S + back:(m + 1) * S]
                    tap = m * TAPS + 3 - back
                    ins = nc.vector.scalar_tensor_tensor(out=dst, in0=k.ps[m % 6][:, 0:S - back], scalar=k.w["L2_attn_conv"][:, tap:tap + 1],
                                                         in1=dst, op0=ALU.mult, op1=ALU.add)
                    if back < TAPS - 1:
                        link(ins)
                ins.then_inc(s["conv"], 1)
            dve.wait_ge(s["conv"], chans)

        @block.gpsimd
        def _(pool):
            for m in range(chans):
                dst = k.big[:, m * S + 1:(m + 1) * S]
                pool.wait_ge(s["scaled"], m + 1)
                pool.wait_ge(s["conv"], m + 1)
                nc.gpsimd.tensor_tensor(dst, dst, tapped[m % 4][:, 0:S - 1], ALU.add).then_inc(s["whole"], 1)
            pool.wait_ge(s["whole"], chans)


def delta_chunks(nc, k, x, b, q, kk, v, z, state, bufs, gs, small, g, beta, nbeta, gam, ngam, rest, tot, HH, GH):
    LEVELS = 7
    PAIRS, TURNS, INVERT, CARRY = 0, 4, 5, 17
    SOLVE, OUTPUT, SQUARES, NORM, TURN_O, PROJECT = 18, 19, 20, 21, 22, 23
    PHASES, PERIOD, BEHIND = 24, 20, 0
    names = ("gs pairs logs masked ed eds at apt vk_turned vk_copied ap_turned init from_state r_ready "
             "qs_copied w us_ready outs o_ready s_done inv normed o_turned o_copied proj added chain achain " + " ".join(f"{n}_{gr}" for n in ("y", "y_copied", "m_part", "mn", "mn_new") for gr in range(2)))
    with stage(nc, names) as (block, s):
        heads4 = lambda t: t.rearrange("p (h e) -> p h e", h=GH)
        each = lambda t, c, gr: t[:, (b * TB + c) * HH + gr * GH:][:, 0:GH].unsqueeze(2).broadcast_to([P, GH, P])
        one = lambda t, c, gr, h: t[:, (b * TB + c) * HH + gr * GH + h:][:, 0:1]
        bank = lambda gr, j: k.ps[4 * gr + j]
        seg = lambda t, c, gr, h: t[:, (gr * GH + h) * S + c * P:][:, 0:P]
        head = lambda n, gr, h: bufs[n][gr][:, sl(h, P)]
        buf = lambda n, gr: bufs[n][gr][:, :]
        st = lambda gr, h: state[:, sl(gr * GH + h, P)]
        wide = lambda m: m.unsqueeze(1).broadcast_to([P, GH, P])
        hs = range(GH)
        nth = lambda c, gr: 2 * c + gr + 1
        level = lambda c, lv: c * (LEVELS - 1) + lv
        m_level = lambda c, lv: c * (LEVELS - 2) + lv
        carried = lambda c, gr: 2 * (c - 1) + gr + 1

        def steps():
            for slot in range((TB - 1) * PERIOD + PHASES + BEHIND):
                for c, gr in [(c, gr) for c in range(TB) for gr in range(2)]:
                    phase = slot - c * PERIOD - gr * BEHIND
                    if 0 <= phase < PHASES:
                        lv, second = divmod(phase - INVERT, 2)
                        yield c, gr, phase, lv + 1 if INVERT <= phase < CARRY else 0, second

        @block.gpsimd
        def _(pool):
            def decays(c, gr):
                nc.gpsimd.tensor_tensor(heads4(gs[gr][:, :]), wide(k.w["after"]), each(g, c, gr), ALU.mult).then_inc(s["gs"], 1)

            for gr in range(2):
                decays(0, gr)
            for c, gr, phase, lv, second in steps():
                if phase == PAIRS:
                    pool.wait_ge(s["ed"], nth(c, gr))
                    after(pool, s["o_ready"], nth(c - 1, gr))
                    nc.gpsimd.tensor_tensor(heads4(buf("ea", gr)), heads4(buf("ex", gr)), wide(k.w["key_later"]), ALU.mult).then_inc(s["masked"], 1)
                    pool.wait_ge(s["masked"], nth(c, gr))
                    nc.gpsimd.tensor_tensor(heads4(buf("ea", gr)), heads4(buf("ea", gr)), each(nbeta, c, gr), ALU.mult).then_inc(s["eds"], 1)
                elif phase == PAIRS + 3 and c < TB - 1:
                    pool.wait_ge(s["logs"], nth(c, gr))
                    decays(c + 1, gr)

        @block.tensor
        def _(pe):
            mm4 = lambda out, left, right: [nc.tensor.matmul(out[:, sl(h, P)], left(h), right(h), start=True, stop=True) for h in hs][-1]
            turn4 = lambda out, src: [nc.tensor.transpose(out[:, sl(h, P)], src(h), k.ident) for h in hs][-1]
            for c, gr, phase, lv, second in steps():
                if phase == PAIRS:
                    pe.wait_ge(s["gs"], nth(c, gr))
                    after(pe, s["s_done"], nth(c - 1, gr))
                    for h in hs:
                        nc.tensor.matmul(bank(gr, 2)[:, sl(h, P)], gs[gr][:, sl(h, P)], k.w["upto"], start=True, stop=False)
                        mm = nc.tensor.matmul(bank(gr, 2)[:, sl(h, P)], k.ident_bf, k.cut[:, :], start=False, stop=True)
                    mm.then_inc(s["logs"], 1)
                    mm4(bank(gr, 0), lambda h: seg(kk, c, gr, h), lambda h: seg(kk, c, gr, h))
                    mm4(bank(gr, 1), lambda h: seg(kk, c, gr, h), lambda h: seg(q, c, gr, h)).then_inc(s["pairs"], 1)
                elif phase == TURNS:
                    after(pe, s["added"], nth(c - 1, gr))
                    pe.wait_ge(s["ed"], nth(c, gr))
                    turn4(bank(gr, 3), lambda h: seg(v, c, gr, h))
                    turn4(bank(gr, 2), lambda h: seg(kk, c, gr, h)).then_inc(s["vk_turned"], 1)
                    pe.wait_ge(s["apt"], nth(c, gr))
                    turn4(bank(gr, 0), lambda h: head("ea", gr, h)).then_inc(s["ap_turned"], 1)
                elif lv and not second:
                    if lv == 1:
                        pe.wait_ge(s["init"], nth(c, gr))
                        pe.wait_ge(s["vk_copied"], nth(c, gr))
                    else:
                        pe.wait_ge(s[f"mn_new_{gr}"], level(c, lv - 1))
                    mm4(bank(gr, 1), lambda h: head("ea", gr, h), lambda h: head("mm", gr, h)).then_inc(s[f"y_{gr}"], 1)
                elif lv:
                    pe.wait_ge(s[f"y_copied_{gr}"], level(c, lv))
                    if lv < LEVELS - 1:
                        mm4(bank(gr, 2), lambda h: head("nn", gr, h), lambda h: head("ex", gr, h)).then_inc(s[f"m_part_{gr}"], 1)
                    mm4(bank(gr, 3), lambda h: head("ex", gr, h), lambda h: head("nn", gr, h)).then_inc(s[f"mn_{gr}"], 1)
                elif phase == CARRY and c:
                    pe.wait_ge(s["s_done"], nth(c - 1, gr))
                    mm4(bank(gr, 0), lambda h: seg(kk, c, gr, h), lambda h: st(gr, h))
                    mm4(bank(gr, 1), lambda h: seg(q, c, gr, h), lambda h: st(gr, h)).then_inc(s["from_state"], 1)
                elif phase == SOLVE:
                    pe.wait_ge(s[f"mn_new_{gr}"], level(c, LEVELS - 1))
                    if c:
                        pe.wait_ge(s["r_ready"], carried(c, gr))
                    mm4(bank(gr, 2), lambda h: head("nn", gr, h), lambda h: head("vv", gr, h)).then_inc(s["w"], 1)
                elif phase == OUTPUT:
                    pe.wait_ge(s["us_ready"], nth(c, gr))
                    mm = mm4(bank(gr, 3), lambda h: head("at", gr, h), lambda h: head("mm", gr, h))
                    if c < TB - 1:
                        mm = mm4(bank(gr, 0), lambda h: head("kt", gr, h), lambda h: head("ex", gr, h))
                    mm.then_inc(s["outs"], 1)
                elif phase == TURN_O:
                    pe.wait_ge(s["normed"], nth(c, gr))
                    turn4(bank(gr, 3), lambda h: head("kt", gr, h)).then_inc(s["o_turned"], 1)
                elif phase == PROJECT:
                    pe.wait_ge(s["o_copied"], nth(c, gr))
                    for h in hs:
                        mm = nc.tensor.matmul(bank(gr, 3)[:, 0:P], k.w["L2_attn_out_w"][:, sl(gr * GH + h, P)], head("vv", gr, h),
                                              start=h == 0, stop=h == GH - 1)
                    mm.then_inc(s["proj"], 1)

        @block.scalar
        def _(act):
            alink = Chain(act, s["achain"])
            nc.scalar.preload_act_table_set(LN_EXP)
            for c, gr, phase, lv, second in steps():
                if phase == PAIRS:
                    act.wait_ge(s["logs"], nth(c, gr))
                    nc.scalar.activation(buf("ex", gr), bank(gr, 2)[:, :], ACT.Exp).then_inc(s["ed"], 1)
                elif phase == TURNS:
                    act.wait_ge(s["vk_turned"], nth(c, gr))
                    nc.scalar.activation(buf("vv", gr), bank(gr, 3)[:, :], ACT.Copy)
                    nc.scalar.activation(buf("kt", gr), bank(gr, 2)[:, :], ACT.Copy).then_inc(s["vk_copied"], 1)
                elif lv and not second:
                    act.wait_ge(s[f"y_{gr}"], level(c, lv))
                    nc.scalar.activation(buf("ex", gr), bank(gr, 1)[:, :], ACT.Copy).then_inc(s[f"y_copied_{gr}"], 1)
                elif phase == CARRY and c:
                    act.wait_ge(s["from_state"], carried(c, gr))
                    act.wait_ge(s[f"mn_{gr}"], level(c, LEVELS - 1))
                    for h in hs:
                        ins = nc.scalar.activation(head("ea", gr, h), bank(gr, 1)[:, sl(h, P)], ACT.Copy, scale=one(gam, c, gr, h))
                    ins.then_inc(s["qs_copied"], 1)
                elif phase == SQUARES:
                    act.wait_ge(s["o_ready"], nth(c, gr))
                    ss, rstd = small["ss"][:, sl(gr, GH)], small["rstd"][:, sl(gr, GH)]
                    for h in hs:
                        ins = nc.scalar.activation(head("mm", gr, h), head("kt", gr, h), ACT.Square, accum_out=ss[:, h:h + 1])
                    alink(ins)
                    alink(nc.scalar.activation(ss, ss, ACT.Ln, scale=1.0 / P, bias=k.eps[1e-6]))
                    nc.scalar.activation(rstd, ss, ACT.Exp, scale=-0.5).then_inc(s["inv"], 1)
                elif phase == TURN_O:
                    act.wait_ge(s["o_turned"], nth(c, gr))
                    nc.scalar.activation(buf("vv", gr), bank(gr, 3)[:, :], ACT.Copy).then_inc(s["o_copied"], 1)

        @block.vector
        def _(dve):
            link = Chain(dve, s["chain"])

            def add(c, gr):
                xs = x[:, sl(b * TB + c, P)]
                dve.wait_ge(s["proj"], nth(c, gr))
                if gr:
                    dve.wait_ge(s["added"], nth(c, 0))
                nc.vector.tensor_tensor(xs, xs, bank(gr, 3)[:, 0:P], ALU.add).then_inc(s["added"], 1)

            for c, gr, phase, lv, second in steps():
                if phase == PAIRS + 1:
                    dve.wait_ge(s["pairs"], nth(c, gr))
                    dve.wait_ge(s["ed"], nth(c, gr))
                    nc.vector.tensor_tensor(buf("at", gr), buf("ex", gr), bank(gr, 1)[:, :], ALU.mult).then_inc(s["at"], 1)
                    link(nc.vector.tensor_copy(heads4(buf("nn", gr)), wide(k.ident)))
                    link(nc.vector.tensor_copy(heads4(buf("mm", gr)), wide(k.ident)))
                elif phase == PAIRS + 2:
                    dve.wait_ge(s["eds"], nth(c, gr))
                    nc.vector.tensor_tensor(buf("ea", gr), buf("ea", gr), bank(gr, 0)[:, :], ALU.mult).then_inc(s["apt"], 1)
                elif phase == PAIRS + 3:
                    dve.wait_ge(s["apt"], nth(c, gr))
                    link(nc.vector.copy_predicated(heads4(buf("nn", gr)), wide(k.level_masks[:, sl(LEVELS, P)]), heads4(buf("ea", gr))))
                elif phase == TURNS:
                    if c:
                        add(c - 1, gr)
                    dve.wait_ge(s["ap_turned"], nth(c, gr))
                    nc.vector.copy_predicated(heads4(buf("mm", gr)), wide(k.level_masks[:, sl(0, P)]), heads4(bank(gr, 0)[:, :])).then_inc(s["init"], 1)
                elif lv and second:
                    if lv < LEVELS - 1:
                        dve.wait_ge(s[f"m_part_{gr}"], m_level(c, lv))
                        nc.vector.copy_predicated(heads4(buf("mm", gr)), wide(k.level_masks[:, sl(lv, P)]), heads4(bank(gr, 2)[:, :]))
                    dve.wait_ge(s[f"mn_{gr}"], level(c, lv))
                    nc.vector.copy_predicated(heads4(buf("nn", gr)), wide(k.level_masks[:, sl(LEVELS + lv, P)]), heads4(bank(gr, 3)[:, :])).then_inc(s[f"mn_new_{gr}"], 1)
                elif phase == CARRY and c:
                    dve.wait_ge(s["from_state"], carried(c, gr))
                    dve.wait_ge(s["vk_copied"], nth(c, gr))
                    for h in hs:
                        ins = nc.vector.scalar_tensor_tensor(out=head("vv", gr, h), in0=bank(gr, 0)[:, sl(h, P)], scalar=one(ngam, c, gr, h),
                                                             in1=head("vv", gr, h), op0=ALU.mult, op1=ALU.add)
                    ins.then_inc(s["r_ready"], 1)
                elif phase == SOLVE:
                    dve.wait_ge(s["w"], nth(c, gr))
                    link(nc.vector.tensor_tensor(heads4(buf("mm", gr)), heads4(bank(gr, 2)[:, :]), each(beta, c, gr), ALU.mult))
                    nc.vector.tensor_tensor(heads4(buf("ex", gr)), heads4(buf("mm", gr)), each(rest, c, gr), ALU.mult).then_inc(s["us_ready"], 1)
                elif phase == OUTPUT:
                    dve.wait_ge(s["outs"], nth(c, gr))
                    if c:
                        dve.wait_ge(s["qs_copied"], carried(c, gr))
                        nc.vector.tensor_tensor(buf("kt", gr), buf("ea", gr), bank(gr, 3)[:, :], ALU.add).then_inc(s["o_ready"], 1)
                    else:
                        nc.vector.tensor_copy(buf("kt", gr), bank(gr, 3)[:, :]).then_inc(s["o_ready"], 1)
                    if c == 0:
                        nc.vector.tensor_copy(state[:, gr * GH * P:(gr + 1) * GH * P], bank(gr, 0)[:, :]).then_inc(s["s_done"], 1)
                    elif c < TB - 1:
                        for h in hs:
                            ins = nc.vector.scalar_tensor_tensor(out=st(gr, h), in0=st(gr, h), scalar=one(tot, c, gr, h),
                                                                 in1=bank(gr, 0)[:, sl(h, P)], op0=ALU.mult, op1=ALU.add)
                        ins.then_inc(s["s_done"], 1)
                elif phase == NORM:
                    dve.wait_ge(s["inv"], nth(c, gr))
                    rstd = small["rstd"][:, sl(gr, GH)].unsqueeze(2).broadcast_to([P, GH, P])
                    link(nc.vector.tensor_tensor(heads4(buf("kt", gr)), heads4(buf("kt", gr)), rstd, ALU.mult))
                    link(nc.vector.tensor_tensor(heads4(buf("kt", gr)), heads4(buf("kt", gr)), wide(k.w["L2_attn_norm_w"]), ALU.mult))
                    nc.vector.tensor_tensor(buf("kt", gr), buf("kt", gr), z[:, (2 * c + gr) * S:(2 * c + gr + 1) * S], ALU.mult).then_inc(s["normed"], 1)
                elif phase == PROJECT and c == TB - 1:
                    add(c, gr)
            dve.wait_ge(s["added"], 2 * TB)


def layer9(nc, k, x, y, a):
    norm(nc, k, x, y, 1e-5)
    q, kk = k.big[:, 0:T], k.big[:, T:2 * T]
    qh = [k.big[:, (2 + j) * T:(3 + j) * T] for j in range(2)]
    project(nc, k, [(k.w["L3_attn_W" + n], y, T, dst, k.w["L3_attn_b" + n], scale) for n, dst, scale in (("q", q, -HD ** -0.5), ("k", kk, 1.0))])
    with ExitStack() as mem:
        sb = lambda n, w_, dt=F32: mem.enter_context(nc.sbuf_tensor(f"{n}_{nc.next_id()}", [P, w_], dt))
        v = a
        with stage(nc, "rows done") as (block, s):
            @block.tensor
            def _(pe):
                for b in range(B):
                    for t in range(TB):
                        mm = nc.tensor.matmul(k.ps[b][:, sl(t, P)], y[:, sl(b * TB + t, P)], k.w["L3_attn_Wv"], start=True, stop=True)
                    mm.then_inc(s["rows"], 1)

            @block.vector
            def _(dve):
                tiles = lambda t: t.rearrange("p (t e) -> p t e", t=TB)
                for b in range(B):
                    dve.wait_ge(s["rows"], b + 1)
                    nc.vector.tensor_tensor(tiles(v[:, sl(b)]), tiles(k.ps[b][:, :]), k.w["L3_attn_bv"].unsqueeze(1).broadcast_to([P, TB, P]),
                                            ALU.add).then_inc(s["done"], 1)
                dve.wait_ge(s["done"], B)

        o = y
        units = [(b, i, h) for b in range(B) for i in range(TB) for h in range(H)]
        N, PER = len(units), TB * H
        TURN, COPY, ATTEND, PW, PT = 3, 4, 6, 5, 4
        low, tot, pw, pt = sb("low", 8), sb("tot", 8), sb("pw", PW * S), sb("pt", PT * S)
        vs = [sb("vs", TB * H * 32) for _ in range(2)]
        with stage(nc, "zeroed spread heads scores least weights inverted scaled turned copied_a copied_v values out") as (block, s):
            width = lambda u: (units[u][1] + 1) * P
            weights = lambda u: pw[:, (u % PW) * S:(u % PW) * S + width(u)]
            turned = lambda u: pt[:, (u % PT) * S:(u % PT) * S + width(u)]
            one = lambda t, u: t[:, u % 8:u % 8 + 1]

            def copy(eng, u, sem, op):
                eng.wait_ge(s["turned"], u + 1)
                after(eng, s["values"], u - PT + 1)
                op(turned(u), k.ps[3 + u % 3][:, 0:width(u)]).then_inc(sem, 1)

            @block.tensor
            def _(pe):
                def copied(u):
                    pe.wait_ge(s["copied_v"] if u % 2 else s["copied_a"], u // 2 + 1)

                def turn(u):
                    pe.wait_ge(s["scaled"], u + 1)
                    if u >= 3:
                        copied(u - 3)
                    for c in range(units[u][1] + 1):
                        mm = nc.tensor.transpose(k.ps[3 + u % 3][:, sl(c, P)], weights(u)[:, sl(c, P)], k.ident)
                    mm.then_inc(s["turned"], 1)

                def attend(u):
                    b, i, h = units[u]
                    copied(u)
                    if h == 0:
                        after(pe, s["out"], u // H - 1)
                        pe.wait_ge(s["spread"], 4 * (b + 1))
                    g, j = divmod(h, 4)
                    for c in range(i + 1):
                        mm = nc.tensor.matmul(k.ps[6 + (u // H) % 2][sl(g, 32), 0:P], vs[b % 2][:, sl(c * H + h, 32)], turned(u)[:, sl(c, P)],
                                              start=c == 0 and j == 0, stop=c == i and j == 3)
                    mm.then_inc(s["values"], 1)

                for u in range(N + ATTEND):
                    if u < N:
                        b, i, h = units[u]
                        w = width(u)
                        if h == 0:
                            pe.wait_ge(s["heads"], u // H + 1)
                        after(pe, s["weights"], u - 2)
                        nc.tensor.matmul(k.ps[u % 3][:, 0:w], qh[(u // H) % 2][:, sl(h, P)], kk[:, b * S:][:, 0:w], start=True, stop=False)
                        nc.tensor.matmul(k.ps[u % 3][:, w - P:w], k.ident_bf, k.later[:, :], start=False, stop=True).then_inc(s["scores"], 1)
                    if TURN <= u < N + TURN:
                        turn(u - TURN)
                    if u >= ATTEND:
                        attend(u - ATTEND)

            @block.scalar
            def _(act):
                for u in range(N + COPY):
                    if u < N:
                        act.wait_ge(s["least"], u + 1)
                        after(act, s["turned"], u - PW + 1)
                        after(act, s["inverted"], u - 7)
                        nc.scalar.activation(weights(u), k.ps[u % 3][:, 0:width(u)], ACT.Exp, scale=-1.0, bias=one(low, u),
                                             accum_out=one(tot, u)).then_inc(s["weights"], 1)
                    if u >= COPY and (u - COPY) % 2 == 0:
                        copy(act, u - COPY, s["copied_a"], lambda dst, src: nc.scalar.activation(dst, src, ACT.Copy))

            @block.gpsimd
            def _(pool):
                def spread(b):
                    after(pool, s["values"], (b - 1) * PER)
                    for j in range(4):
                        dst = vs[b % 2][:, :].rearrange("p (t g j q e) -> p t g j q e", t=TB, g=4, j=4, q=4)
                        src = v[:, sl(b)].rearrange("p (t g j e) -> p t g j e", t=TB, g=4, j=4)
                        nc.gpsimd.tensor_copy(dst[:, :, :, j, j, :], src[:, :, :, j, :]).then_inc(s["spread"], 1)

                pool.wait_ge(s["zeroed"], 2)
                spread(0)
                for n in range(NT):
                    after(pool, s["scores"], (n - 1) * H)
                    nc.gpsimd.tensor_tensor(qh[n % 2].rearrange("p (h e) -> p h e", h=H), q[:, sl(n, P)].unsqueeze(1).broadcast_to([P, H, P]),
                                            k.w["head_cols"].unsqueeze(2).broadcast_to([P, H, P]), ALU.mult).then_inc(s["heads"], 1)
                    if n % TB == 2 and n // TB < B - 1:
                        spread(n // TB + 1)

            @block.vector
            def _(dve):
                for j in range(2):
                    nc.vector.memset(vs[j][:, :], 0.0).then_inc(s["zeroed"], 1)
                for u in range(N + ATTEND + 2):
                    if u < N:
                        dve.wait_ge(s["scores"], u + 1)
                        after(dve, s["weights"], u - 7)
                        nc.vector.tensor_reduce(one(low, u), k.ps[u % 3][:, 0:width(u)], AX.X, ALU.min).then_inc(s["least"], 1)
                    if 2 <= u < N + 2:
                        dve.wait_ge(s["weights"], u - 1)
                        nc.vector.reciprocal(one(tot, u - 2), one(tot, u - 2)).then_inc(s["inverted"], 1)
                        dve.wait_ge(s["inverted"], u - 1)
                        nc.vector.tensor_scalar(weights(u - 2), weights(u - 2), one(tot, u - 2), None, ALU.mult).then_inc(s["scaled"], 1)
                    if COPY <= u < N + COPY and (u - COPY) % 2 == 1:
                        copy(dve, u - COPY, s["copied_v"], lambda dst, src: nc.vector.tensor_copy(dst, src))
                    if u >= ATTEND + H and (u - ATTEND) % H == 1:
                        i = (u - ATTEND) // H - 1
                        dve.wait_ge(s["values"], (i + 1) * H)
                        nc.vector.tensor_copy(o[:, sl(i, P)], k.ps[6 + i % 2][:, 0:P]).then_inc(s["out"], 1)
                dve.wait_ge(s["out"], NT)

        with stage(nc, "proj done") as (block, s):
            @block.tensor
            def _(pe):
                for b in range(B):
                    nc.tensor.matmul(k.ps[4 + b][:, :], k.w["L3_attn_Wo"], o[:, sl(b)], start=True, stop=True).then_inc(s["proj"], 1)

            @block.scalar
            def _(act):
                for b in range(B):
                    act.wait_ge(s["proj"], b + 1)
                    nc.scalar.activation(a[:, sl(b)], k.ps[4 + b][:, :], ACT.Identity, bias=k.w["L3_attn_bo"]).then_inc(s["done"], 1)
                act.wait_ge(s["done"], B)
    norm(nc, k, a, y, 1e-5)
    with stage(nc, "chain") as (block, s):
        @block.vector
        def _(dve):
            link = Chain(dve, s["chain"])
            for b in range(B):
                link(nc.vector.tensor_scalar(y[:, sl(b)], y[:, sl(b)], k.w["L3_attn_gamma"], k.w["L3_attn_beta"], ALU.mult, ALU.add))
                link(nc.vector.tensor_tensor(x[:, sl(b)], x[:, sl(b)], y[:, sl(b)], ALU.add))


def layer11(nc, k, x, y, a):
    F, R, K, CAND, ROUNDS = 1536, 32, 512, 32, 6
    C = F // P
    norm(nc, k, x, y, 1e-5)
    wm, wp = k.big[:, 0:F], k.big[:, F:2 * F]
    per_step = "up act down out pooled r_ps r scores shifted exps counts reached turned count total decided".split()
    with ExitStack() as mem:
        sb = lambda n, w_, dt=F32, p=P: mem.enter_context(nc.sbuf_tensor(f"{n}_{nc.next_id()}", [p, w_], dt))
        active, new, history, both = (sb(n, C * B) for n in ("active", "new", "history", "both"))
        pooled, r1 = sb("pooled", B), sb("r1", P, F32, R)
        seen = sb("seen", 2)
        going = sb("going", 1, I32)
        h = sb("h", 2 * S)
        with stage(nc, "chain") as (block, s):
            @block.vector
            def _(dve):
                link = Chain(dve, s["chain"])
                for t in (active, history):
                    link(nc.vector.memset(t[:, :], 0.0))
                    link(nc.vector.memset(t[:, 0:K // P * B], 1.0))

        p, m, eq, cum = sb("p", F), sb("m", F), sb("eq", F), sb("cum", F)
        c1, c2, hit = sb("c1", 1), sb("c2", 1), sb("hit", 1)
        base, trial, digit = sb("base", 1, I32), sb("trial", 1, I32), sb("digit", 1, I32)

        def map_pe(pe, s, blocks):
            N = B * blocks

            def down(n):
                b, c = divmod(n, blocks)
                pe.wait_ge(s["act"], n + 1)
                if c == 0:
                    after(pe, s["out"], b - 1)
                nc.tensor.matmul(k.ps[4 + b % 2][:, :], wp[:, sl(c, P)], h[:, sl(n % 2)], start=c == 0, stop=c == blocks - 1).then_inc(s["down"], 1)

            for n in range(N):
                after(pe, s["act"], n - 3)
                nc.tensor.matmul(k.ps[n % 4][:, :], wm[:, sl(n % blocks, P)], y[:, sl(n // blocks)], start=True, stop=True).then_inc(s["up"], 1)
                if n:
                    down(n - 1)
            down(N - 1)

        def map_act(act, s, blocks):
            for n in range(B * blocks):
                b, c = divmod(n, blocks)
                act.wait_ge(s["up"], n + 1)
                after(act, s["down"], n - 1)
                nc.scalar.activation(h[:, sl(n % 2)], k.ps[n % 4][:, :], ACT.Relu, scale=active[:, c * B + b:c * B + b + 1]).then_inc(s["act"], 1)

        def map_dve(dve, s, link, blocks):
            for b in range(B):
                dve.wait_ge(s["down"], blocks * (b + 1))
                nc.vector.tensor_scalar(a[:, sl(b)], k.ps[4 + b % 2][:, :], 1.0, None, ALU.mult, ALU.add, accum_out=pooled[:, b:b + 1]).then_inc(s["out"], 1)
            dve.wait_ge(s["out"], B)
            nc.vector.tensor_scalar(pooled[:, :], pooled[:, :], 1.0 / S, None, ALU.mult).then_inc(s["pooled"], 1)

        def choose_pe(pe, s):
            pe.wait_ge(s["pooled"], 1)
            nc.tensor.matmul(k.ps[6][0:R, 0:B], k.w["L3_ffn_Wc1"], pooled[:, :], start=True, stop=True).then_inc(s["r_ps"], 1)
            pe.wait_ge(s["r"], 1)
            for j in range(3):
                mm = nc.tensor.matmul(k.ps[j][:, :], r1[:, :], k.big[0:R, 2 * F + j * S:2 * F + (j + 1) * S], start=True, stop=True)
            mm.then_inc(s["scores"], 1)
            for n in range(ROUNDS):
                pe.wait_ge(s["counts"], n + 1)
                nc.tensor.matmul(k.ps[7][:, 0:1], k.w["same_batch"], hit[:, :], start=True, stop=True).then_inc(s["reached"], 1)
            pe.wait_ge(s["counts"], ROUNDS + 1)
            for c in range(C):
                mm = nc.tensor.transpose(k.ps[3 + c // 4][:, sl(c % 4, P)], m[:, sl(c, P)], k.ident)
            mm.then_inc(s["turned"], 1)
            pe.wait_ge(s["count"], 1)
            nc.tensor.matmul(k.ps[0][:, 0:1], k.ones, seen[:, 0:1], start=True, stop=True).then_inc(s["total"], 1)

        def choose_act(act, s):
            act.wait_ge(s["shifted"], 1)
            nc.scalar.activation(p[:, :], p[:, :], ACT.Exp).then_inc(s["exps"], 1)

        def choose_dve(dve, s, link):
            dve.wait_ge(s["r_ps"], 1)
            nc.vector.tensor_scalar(r1[:, :].rearrange("r (b c) -> r b c", b=B), k.ps[6][0:R, 0:B].unsqueeze(2).broadcast_to([R, B, CAND]),
                                    0.0, None, ALU.max).then_inc(s["r"], 1)
            dve.wait_ge(s["scores"], 1)
            for j in range(3):
                link(nc.vector.tensor_copy(p[:, sl(j)], k.ps[j][:, :]))
            link(nc.vector.tensor_reduce(c1[:, :], p[:, :], AX.X, ALU.max))
            nc.vector.tensor_scalar(p[:, :], p[:, :], c1[:, :], None, ALU.subtract).then_inc(s["shifted"], 1)
            dve.wait_ge(s["exps"], 1)
            link(nc.vector.tensor_reduce(c1[:, :], p[:, :], AX.X, ALU.add))
            link(nc.vector.reciprocal(c1[:, :], c1[:, :]))
            link(nc.vector.tensor_scalar(p[:, :], p[:, :], c1[:, :], None, ALU.mult))
            link(nc.vector.memset(base[:, :], 0))
            for n in range(ROUNDS):
                link(nc.vector.tensor_tensor(trial[:, :], base[:, :], k.candidate[:, n:n + 1], ALU.bitwise_or))
                link(nc.vector.tensor_scalar(m[:, :], p[:, :], trial[:, :].bitcast(F32), None, ALU.is_ge, ALU.add, accum_out=c1[:, :]))
                nc.vector.tensor_scalar(hit[:, :], c1[:, :], float(K), None, ALU.is_ge).then_inc(s["counts"], 1)
                dve.wait_ge(s["reached"], n + 1)
                link(nc.vector.tensor_scalar(digit[:, :], k.ps[7][:, 0:1], 1.0, None, ALU.subtract))
                link(nc.vector.tensor_scalar(digit[:, :], digit[:, :], 25 - 5 * n, None, ALU.logical_shift_left))
                link(nc.vector.tensor_tensor(base[:, :], base[:, :], digit[:, :], ALU.bitwise_or))
            kth = base[:, :].bitcast(F32)
            link(nc.vector.tensor_scalar(m[:, :], p[:, :], kth, None, ALU.is_gt, ALU.add, accum_out=c1[:, :]))
            link(nc.vector.tensor_scalar(c2[:, :], c1[:, :], -1.0, float(K), ALU.mult, ALU.add))
            link(nc.vector.tensor_scalar(eq[:, :], p[:, :], kth, None, ALU.is_equal))
            link(nc.vector.tensor_tensor_scan(cum[:, :], k.ones[:, 0:1].broadcast_to([P, F]), eq[:, :], 0.0, ALU.mult, ALU.add))
            link(nc.vector.scalar_tensor_tensor(out=eq[:, :], in0=cum[:, :], scalar=c2[:, :], in1=eq[:, :], op0=ALU.is_le, op1=ALU.mult))
            nc.vector.tensor_tensor(m[:, :], m[:, :], eq[:, :], ALU.add).then_inc(s["counts"], 1)
            dve.wait_ge(s["turned"], 1)
            for j in range(3):
                link(nc.vector.tensor_copy(new[:, sl(j, 4 * B)].rearrange("p (c b) -> p c b", c=4),
                                           k.ps[3 + j][:, :].rearrange("p (c b r) -> p c b r", c=4, b=B)[:, :, :, 0]))
            link(nc.vector.tensor_tensor(both[:, :], history[:, :], new[:, :], ALU.max))
            link(nc.vector.tensor_tensor(history[:, :], both[:, :], history[:, :], ALU.subtract))
            link(nc.vector.tensor_reduce(seen[:, 0:1], history[:, :], AX.X, ALU.add))
            link(nc.vector.tensor_scalar(seen[:, 0:1], seen[:, 0:1], 1.0 / (B * K), None, ALU.mult))
            nc.vector.tensor_copy(history[:, :], both[:, :]).then_inc(s["count"], 1)
            link(nc.vector.tensor_copy(active[:, :], new[:, :]))
            link(nc.vector.tensor_copy(y[:, :], a[:, :]))
            dve.wait_ge(s["total"], 1)
            nc.vector.tensor_scalar(going[:, :], k.ps[0][:, 0:1], 0.7, None, ALU.is_ge).then_inc(s["decided"], 1)

        with stage(nc, " ".join(per_step) + " chain") as (block, s):
            @block.tensor
            def _(pe):
                pe.wait_ge(k.big_loaded, 48)
                map_pe(pe, s, K // P)
                choose_pe(pe, s)

            @block.scalar
            def _(act):
                map_act(act, s, K // P)
                choose_act(act, s)

            @block.vector
            def _(dve):
                link = Chain(dve, s["chain"])
                map_dve(dve, s, link, K // P)
                choose_dve(dve, s, link)
                dve.wait_ge(s["decided"], 1)

        with stage(nc, " ".join(f"{n}_{i}" for i in (2, 3) for n in per_step) + " chain") as (block, s):
            second, third = ({n: s[f"{n}_{i}"] for n in per_step} for i in (2, 3))
            flag = going[0:1, 0:1]

            @block.tensor
            def _(pe):
                with pe.If(pe.value_load(flag, min_val=0, max_val=1) == 1):
                    map_pe(pe, second, C)
                    choose_pe(pe, second)
                    pe.wait_ge(second["decided"], 1)
                    with pe.If(pe.value_load(flag, min_val=0, max_val=1) == 1):
                        map_pe(pe, third, C)

            @block.scalar
            def _(act):
                with act.If(act.value_load(flag, min_val=0, max_val=1) == 1):
                    map_act(act, second, C)
                    choose_act(act, second)
                    act.wait_ge(second["decided"], 1)
                    with act.If(act.value_load(flag, min_val=0, max_val=1) == 1):
                        map_act(act, third, C)

            @block.vector
            def _(dve):
                link = Chain(dve, s["chain"])
                with dve.If(dve.value_load(flag, min_val=0, max_val=1) == 1):
                    map_dve(dve, second, link, C)
                    choose_dve(dve, second, link)
                    dve.wait_ge(second["decided"], 1)
                    with dve.If(dve.value_load(flag, min_val=0, max_val=1) == 1):
                        map_dve(dve, third, link, C)
                        link(nc.vector.tensor_copy(y[:, :], a[:, :]))
                        dve.wait_ge(third["pooled"], 1)
    with stage(nc, "chain") as (block, s):
        @block.vector
        def _(dve):
            link = Chain(dve, s["chain"])
            link(nc.vector.tensor_tensor(x[:, :], x[:, :], y[:, :], ALU.add))


def program(nc, ap, out, cols, first, last):
    with ExitStack() as mem:
        sb = lambda n, w, dt=F32, p=P: mem.enter_context(nc.sbuf_tensor(n, [p, w], dt))
        k = Kit()
        k.w = {}
        stored = nc.alloc_semaphore("stored")
        k.ps = [mem.enter_context(nc.psum_tensor(f"bank{i}", [P, S], F32)) for i in range(8)]
        x, y, a = sb("x", T), sb("y", T), sb("a", T)
        pack = sb("pack", ap["pack"].shape[1])
        soon = cols["L0_attn_ln2_b"][0] + cols["L0_attn_ln2_b"][1]
        rest_loaded = nc.alloc_semaphore("rest_loaded")
        for n, (lo, w) in cols.items():
            k.w[n] = pack[:, lo:lo + w]
        k.mean, k.ones, k.heads, k.ident = k.w["mean"], k.w["ones"], k.w["head_mask"], k.w["ident"]
        k.eps = {e: k.w["eps"][:, i:i + 1] for i, e in enumerate(EPSILONS)}
        k.ap = ap
        k.big = sb("big", ap["big2"].shape[1])
        k.big_loaded = nc.alloc_semaphore("big_loaded")
        k.ctx = k.w["ctx"]
        k.mask0, k.mask2 = sb("mask0", NT * M), sb("mask2", TB * M)
        k.level_masks = sb("level_masks", ap["level_masks"].shape[1], mybir.dt.uint8)[:, :]
        masks_raw = ap["level_masks"].shape[1]
        k.cut = sb("cut", P, BF16)
        k.candidate = sb("candidate", 6, I32)
        k.later = sb("later", P, BF16)
        k.ident_bf = sb("ident_bf", P, BF16)[:, :]
        raw0, raw2 = sb("raw0", NT * M, mybir.dt.uint8), sb("raw2", TB * M, I32)
        with stage(nc, "loaded masks chain") as (block, s):
            @block.sync
            def _(sp):
                sp.dma_start(x[:, :], ap["x"]).then_inc(s["loaded"], 16)
                sp.dma_start(pack[:, 0:soon], ap["pack"][:, 0:soon]).then_inc(s["loaded"], 16)
                sp.dma_start(raw0[:, :], ap["mask0"]).then_inc(s["masks"], 16)
                sp.dma_start(raw2[:, :], ap["mask2"]).then_inc(s["masks"], 16)
                sp.dma_start(k.candidate[:, :], ap["candidate"]).then_inc(s["masks"], 16)
                sp.dma_start(y[:, 0:masks_raw].bitcast(I32), ap["level_masks"]).then_inc(s["masks"], 16)
                sp.dma_start(pack[:, soon:], ap["pack"][:, soon:]).then_inc(rest_loaded, 16)
                sp.dma_start(k.big[:, 0:ap["big0"].shape[1]], ap["big0"]).then_inc(k.big_loaded, 16)
                sp.wait_ge(s["loaded"], 32)

            @block.vector
            def _(dve):
                link = Chain(dve, s["chain"])
                dve.wait_ge(s["masks"], 64)
                link(nc.vector.tensor_copy(k.mask0[:, :], raw0[:, :]))
                link(nc.vector.tensor_copy(k.level_masks, y[:, 0:masks_raw].bitcast(I32)))
                dve.wait_ge(s["loaded"], 32)
                link(nc.vector.tensor_copy(k.ident_bf, k.ident))
                link(nc.vector.tensor_scalar(k.cut[:, :], k.w["after"], -1e30, None, ALU.mult))
                link(nc.vector.tensor_scalar(k.later[:, :], k.w["key_later"], 1e30, None, ALU.mult))
                link(nc.vector.tensor_copy(k.mask2[:, :], raw2[:, :]))
                link(nc.vector.tensor_scalar(k.mask0[:, :], k.mask0[:, :], 0.0, None, ALU.not_equal))
                link(nc.vector.tensor_scalar(k.mask2[:, :], k.mask2[:, :], 0.0, None, ALU.not_equal))
        for n in range(first, last):
            if n == max(first, 1):
                with nc.Block() as block:
                    @block.sync
                    def _(sp):
                        sp.wait_ge(rest_loaded, 16)
            LAYERS[n](nc, k, x, y, a)
        with nc.Block() as block:
            @block.sync
            def _(sp):
                sp.dma_start(out, x[:, :]).then_inc(stored, 16)
                sp.wait_ge(stored, 16)
                sp.wait_ge(k.big_loaded, 48)


def layer0(nc, k, x, y, a):
    with nc.sbuf_tensor(f"res_{nc.next_id()}", [P, T], F32) as res:
        norm(nc, k, x, y, 1e-5, inner=(1e-5, k.w["L0_attn_ln1_g"], k.w["L0_attn_ln1_b"], a))
        l0_attention(nc, k, y, a, res)
        norm(nc, k, res, y, 1e-5)
        with nc.sbuf_tensor(f"h_{nc.next_id()}", [P, T], F32) as h:
            scale_shift(nc, k, y, h, k.w["L0_attn_ln2_g"], k.w["L0_attn_ln2_b"])
            l0_lookup_mlp(nc, k, h, res, x)


def scale_shift(nc, k, src, dst, gain, bias):
    with stage(nc, "done") as (block, s):
        @block.vector
        def _(dve):
            nc.vector.tensor_scalar(dst[:, :], src[:, :], gain, bias, ALU.mult, ALU.add).then_inc(s["done"], 1)
            dve.wait_ge(s["done"], 1)


def more_parts(parts, f, vec, kblocks, rows):
    hd = np.arange(P) // HD
    parts["head_cols"] = (hd[:, None] == np.arange(H)[None]) * 1.0
    parts["head_of"] = np.eye(P)[:, :H] @ parts["head_cols"].T
    parts["head_rows"] = np.concatenate([(4 * c + np.arange(P)[:, None] // M == hd[None]) * 1.0 for c in range(4)], axis=1)
    parts["ctx"] = f("ctx_1024").reshape(B * M, D).T
    kv = f("L0_xattn_Wkv")
    for n, w in (("Wq", f("L0_xattn_Wq")), ("Wk", kv[:, :D]), ("Wv", kv[:, D:]), ("Wproj", f("L0_xattn_Wproj")), ("bproj", vec(f("L0_xattn_bproj")))):
        parts["L0_xattn_" + n] = w
    for pre, turn in (("L2_xattn_", True), ("L3_xattn_", False)):
        for n in ("Wq", "Wk", "Wv", "Wo"):
            parts[pre + n] = f(pre + n).T if turn else f(pre + n)
        for n in ("bq", "bk", "bo"):
            parts[pre + n] = vec(f(pre + n))
        parts[pre + "bv"] = rows(f(pre + "bv"))
    parts["before8"] = rows((np.arange(8)[None] < np.arange(8)[:, None]) * 1.0)
    parts["L0_ffn_gate_w"], parts["L0_ffn_gate_b"] = f("L0_ffn_gate_w"), rows(f("L0_ffn_gate_b"))
    parts["L0_ffn_b1"] = vec(f("L0_ffn_b1").reshape(-1))
    parts["L0_ffn_b2"] = np.concatenate([f("L0_ffn_b2"), np.zeros((P - 8, D))])
    parts["L1_attn_rms_weight"], parts["L1_attn_b_A"] = vec(f("L1_attn_rms_weight")), vec(f("L1_attn_b_A"))
    for n in ("w_A", "w_x", "w_sidegate", "w_output", "w_o"):
        parts["L1_attn_" + n] = f("L1_attn_" + n)
    for n in ("Wq", "Wk", "Wv"):
        parts["L1_xattn_" + n] = f("L1_xattn_" + n).T
    parts["L1_ffn_w1"], parts["L1_ffn_w2"] = f("L1_ffn_w1").T, kblocks(f("L1_ffn_w2").T)
    parts["L1_ffn_norm1_w"], parts["L1_ffn_norm2_w"] = vec(f("L1_ffn_norm1_w")), rows(f("L1_ffn_norm2_w"))
    parts["L1_ffn_act_scale"], parts["L1_ffn_act_bias"] = rows(f("L1_ffn_act_scale")), rows(f("L1_ffn_act_bias"))
    parts["L2_ffn_gate_w"] = f("L2_ffn_gate_w").T
    for n in "qk":
        parts["L3_attn_b" + n] = vec(f("L3_attn_b" + n))
    for n in ("Wq", "Wk", "Wv", "Wo"):
        parts["L3_attn_" + n] = f("L3_attn_" + n)
    parts["L3_attn_bv"] = rows(f("L3_attn_bv"))
    for n in ("bo", "gamma", "beta"):
        parts["L3_attn_" + n] = vec(f("L3_attn_" + n))
    parts["L3_ffn_Wc1"] = f("L3_ffn_Wc1").T
    parts["same_batch"] = (np.arange(P)[:, None] // 32 == np.arange(P)[None] // 32) * 1.0
    parts["upto"] = np.triu(np.ones((P, P)))
    parts["L2_attn_qkv_w"], parts["L2_attn_z_w"] = f("L2_attn_qkv_w").T, f("L2_attn_z_w").T
    parts["L2_attn_ba"] = np.concatenate([f("L2_attn_b_w").T, f("L2_attn_a_w").T], axis=1)
    parts["L2_attn_conv"] = f("L2_attn_conv_w").reshape(-1, P, 4).transpose(1, 0, 2).reshape(P, -1)
    for n in ("dt_bias", "A_log", "norm_w"):
        parts["L2_attn_" + n] = rows(f("L2_attn_" + n))
    parts["L2_attn_out_w"] = kblocks(f("L2_attn_out_w").T)


def more_arrays(arrays, f, kblocks):
    at = np.arange(P)
    low = [(at[:, None] >> (n + 1) == at[None] >> (n + 1)) & (at[:, None] >> n & 1 == 1) & (at[None] >> n & 1 == 0) for n in range(7)]
    arrays["level_masks"] = np.concatenate(low + [m.T for m in low], axis=1).astype(np.int32)
    arrays["big3"] = np.concatenate([f("L3_ffn_Wm").T, kblocks(f("L3_ffn_Wp").T), np.pad(f("L3_ffn_Wc2").T, ((0, P - 32), (0, 0)))], axis=1)
    arrays["candidate"] = np.array([[(p % 32) << (25 - 5 * n) for n in range(6)] for p in range(P)], np.int32)
    arrays["ind"] = np.tile((np.arange(64)[:, None] == np.arange(64 * 96)[None] // 96).astype(np.float32), (2, 1))
    w1, w2 = f("L0_ffn_w1"), f("L0_ffn_w2")
    wide = w1.shape[2] // 2
    arrays["big0"] = np.concatenate([w1[:, :, wide:].transpose(1, 0, 2).reshape(D, -1), w1[:, :, :wide].transpose(1, 0, 2).reshape(D, -1)]
                                    + [kblocks(w) for w in w2], axis=1)
    arrays["ind0"] = np.tile(np.repeat(np.eye(8, dtype=np.float32), P, axis=1), (3, 1))
    arrays["big2"] = np.concatenate([f("L2_ffn_" + n).reshape(-1, D).T for n in ("w_gate", "w_up")]
                                    + [kblocks(f("L2_ffn_w_down").transpose(0, 2, 1).reshape(-1, D))], axis=1)
    tiles = lambda m: np.ascontiguousarray(m.reshape(-1, P, M).transpose(1, 0, 2).reshape(P, -1))
    arrays["mask0"] = tiles(f("mask_BxSxS2_bk0"))
    arrays["mask2"] = tiles(f("mask_SxS2_ik1"))


FIRST, LAST = 0, 12
LAYERS = [layer0, layer1, layer2, layer3, layer4, layer5, layer6, layer7, layer8, layer9, layer10, layer11]


EPSILONS = (1e-5, 1e-8, 1e-6)


def layout(inputs):
    f = lambda n: np.asarray(inputs[n])
    parts = {}
    vec = lambda v: v.reshape(-1, P).T
    kblocks = lambda w: np.concatenate(np.split(w, w.shape[0] // P), axis=1)
    rows = lambda v: np.broadcast_to(v.reshape(1, -1), (P, v.size))
    hd = np.arange(P) // HD
    parts["mean"] = np.full((P, P), 1.0 / P)
    parts["ones"] = np.ones((P, P))
    parts["head_mask"] = (hd[:, None] == hd[None]) * 1.0
    parts["ident"] = np.eye(P)
    parts["after"], parts["key_later"] = np.tril(np.ones((P, P)), -1), np.triu(np.ones((P, P)), 1)
    parts["eps"] = np.tile(np.array(EPSILONS), (P, 1))
    for n in ("wq", "wk", "wv", "wo", "w1"):
        parts["L0_attn_" + n] = f("L0_attn_" + n)
    parts["L0_attn_w2"] = kblocks(f("L0_attn_w2"))
    for n in ("ln1_g", "ln1_b", "ln2_g", "ln2_b"):
        parts["L0_attn_" + n] = vec(f("L0_attn_" + n))
    more_parts(parts, f, vec, kblocks, rows)
    cols, at = {}, 0
    for n, v in parts.items():
        cols[n] = (at, v.shape[1])
        at += v.shape[1]
    pack = np.concatenate([v.astype(np.float32) for v in parts.values()], axis=1)
    arrays = {"x": np.ascontiguousarray(f("x").reshape(T, D).T), "pack": pack}
    more_arrays(arrays, f, kblocks)
    return arrays, cols


def kernel(**inputs):
    import concourse.bacc as bacc
    from concourse.bass_utils import run_bass_kernel_spmd as run

    nc = bacc.Bacc("TRN2", target_bir_lowering=False, num_devices=1)
    arrays, cols = layout(inputs)
    ap = {n: nc.dram_tensor(f"in_{n}", v.shape, mybir.dt.from_np(v.dtype), kind="ExternalInput").ap() for n, v in arrays.items()}
    out = nc.dram_tensor("out", (P, T), F32, kind="ExternalOutput").ap()
    program(nc, ap, out, cols, FIRST, LAST)
    r = run(nc, [{f"in_{n}": v for n, v in arrays.items()}], core_ids=[0])
    return np.ascontiguousarray(np.asarray(r.results[0]["out"]).T).reshape(B, S, D)
```

```python
from contextlib import ExitStack, contextmanager

import numpy as np
import concourse.bass as bass
from concourse import mybir

ALU = mybir.AluOpType
ACT = mybir.ActivationFunctionType
AX = mybir.AxisListType
F32 = mybir.dt.float32
F32R = mybir.dt.float32r
BF16 = mybir.dt.bfloat16
I32 = mybir.dt.int32

B, S, D, M = 4, 512, 128, 32
T = B * S
P = 128
NT, TB = T // P, S // P
H, HD = 16, 8
LN_EXP = "natural_log_exp_and_others"
MAGIC = 12582912.0


class Kit:
    pass


@contextmanager
def stage(nc, names):
    sems = {n: nc.alloc_semaphore(f"{n}_{nc.next_id()}") for n in names.split()}
    with nc.Block() as block:
        yield block, sems
    nc.clear_and_free_semaphores(list(sems.values()))
    nc.all_engine_barrier()


def after(eng, sem, n):
    if n > 0:
        eng.wait_ge(sem, n)


class Chain:

    def __init__(self, eng, sem):
        self.eng, self.sem, self.n = eng, sem, 0

    def __call__(self, ins):
        self.n += 1
        ins.then_inc(self.sem, 1)
        self.eng.wait_ge(self.sem, self.n)


def sl(i, n=S):
    return slice(i * n, (i + 1) * n)


def norm(nc, k, src, dst, eps, inner=None, scaled=None, onto=None):
    with ExitStack() as mem, stage(nc, "centred squared var ln inv used ratio ln2 inv2 chain") as (block, s):
        sb = lambda n, w: mem.enter_context(nc.sbuf_tensor(f"{n}_{nc.next_id()}", [P, w], F32))
        sq, rs = sb("sq", 2 * S), sb("rs", 2 * S)
        tt = sb("tt", 2 * S) if inner else None
        xc, var = k.ps[0:4], k.ps[4:8]

        @block.tensor
        def _(pe):
            for b in range(B + 1):
                if b < B:
                    nc.tensor.matmul(xc[b][:, :], k.w["centre"], src[:, sl(b)], start=True, stop=True).then_inc(s["centred"], 1)
                if b:
                    pe.wait_ge(s["squared"], b)
                    nc.tensor.matmul(var[b - 1][:, :], k.mean, sq[:, sl((b - 1) % 2)], start=True, stop=True).then_inc(s["var"], 1)

        @block.scalar
        def _(act):
            nc.scalar.preload_act_table_set(LN_EXP)
            for b in range(B + 1):
                if b < B:
                    act.wait_ge(s["centred"], b + 1)
                    after(act, s["var"], b - 1)
                    nc.scalar.activation(sq[:, sl(b % 2)], xc[b][:, :], ACT.Square).then_inc(s["squared"], 1)
                if b:
                    c = b - 1
                    r = rs[:, sl(c % 2)]
                    act.wait_ge(s["var"], c + 1)
                    after(act, s["used"], c - 1)
                    nc.scalar.activation(r, var[c][:, :], ACT.Ln, bias=k.eps[eps]).then_inc(s["ln"], 1)
                    act.wait_ge(s["ln"], c + 1)
                    nc.scalar.activation(r, r, ACT.Exp, scale=-0.5).then_inc(s["inv"], 1)
                    if inner:
                        t = tt[:, sl(c % 2)]
                        act.wait_ge(s["ratio"], c + 1)
                        nc.scalar.activation(t, t, ACT.Ln, bias=k.eps[inner[0]]).then_inc(s["ln2"], 1)
                        act.wait_ge(s["ln2"], c + 1)
                        nc.scalar.activation(t, t, ACT.Exp, scale=-0.5).then_inc(s["inv2"], 1)

        @block.vector
        def _(dve):
            link = Chain(dve, s["chain"])
            for c in range(B):
                r, t = rs[:, sl(c % 2)], tt[:, sl(c % 2)] if inner else None
                dve.wait_ge(s["inv"], c + 1)
                if scaled:
                    link(nc.vector.scalar_tensor_tensor(out=r, in0=xc[c][:, :], scalar=scaled[0], in1=r, op0=ALU.mult, op1=ALU.mult))
                    if onto is None:
                        out = nc.vector.tensor_scalar(dst[:, sl(c)], r, scaled[1], None, ALU.add)
                    else:
                        out = nc.vector.scalar_tensor_tensor(out=onto[:, sl(c)], in0=r, scalar=scaled[1], in1=onto[:, sl(c)], op0=ALU.add, op1=ALU.add)
                    out.then_inc(s["used"], 1)
                    continue
                if not inner:
                    nc.vector.tensor_tensor(dst[:, sl(c)], xc[c][:, :], r, ALU.mult).then_inc(s["used"], 1)
                    continue
                _, gain, bias, dst2 = inner
                link(nc.vector.tensor_tensor(t, r, r, ALU.mult))
                nc.vector.tensor_tensor(t, t, var[c][:, :], ALU.mult).then_inc(s["ratio"], 1)
                link(nc.vector.tensor_tensor(dst[:, sl(c)], xc[c][:, :], r, ALU.mult))
                dve.wait_ge(s["inv2"], c + 1)
                if bias is None:
                    nc.vector.scalar_tensor_tensor(out=dst2[:, sl(c)], in0=dst[:, sl(c)], scalar=gain, in1=t, op0=ALU.mult, op1=ALU.mult).then_inc(s["used"], 1)
                else:
                    link(nc.vector.tensor_tensor(t, dst[:, sl(c)], t, ALU.mult))
                    nc.vector.tensor_scalar(dst2[:, sl(c)], t, gain, bias, ALU.mult, ALU.add).then_inc(s["used"], 1)
            dve.wait_ge(s["used"], B)


def l0_attention(nc, k, y, a, res):
    names = ("k_tok v_tok q_feat kv den proj k_min k_exp k_phi v_copy q_min q_exp q_phi kv_mask log inv o_ready done chain")
    with ExitStack() as mem, stage(nc, names) as (block, s):
        sb = lambda n, w: mem.enter_context(nc.sbuf_tensor(f"{n}_{nc.next_id()}", [P, w], F32))
        km, ke, vt, qm, qe = ([sb(n, S) for _ in range(2)] for n in ("km", "ke", "vt", "qm", "qe"))
        o, rec, kvm, zm = sb("o", S), sb("rec", S), sb("kvm", P), sb("zm", P)
        pk, pv, pq, pkv, pn, pd, po = k.ps[:7]

        @block.tensor
        def _(pe):
            for b in range(B + 1):
                if b < B:
                    after(pe, s["q_phi"], b)
                    after(pe, s["v_copy"], b)
                    for ps, w, sem in ((pk, "wk", s["k_tok"]), (pv, "wv", s["v_tok"])):
                        for t in range(TB):
                            mm = nc.tensor.matmul(ps[:, sl(t, P)], a[:, sl(b * TB + t, P)], k.w["L0_attn_" + w], start=True, stop=True)
                        mm.then_inc(sem, 1)
                    nc.tensor.matmul(pq[:, :], k.w["L0_attn_wq"], a[:, sl(b)], start=True, stop=True).then_inc(s["q_feat"], 1)
                if b:
                    c = b - 1
                    pe.wait_ge(s["kv_mask"], c + 1)
                    after(pe, s["o_ready"], c)
                    nc.tensor.matmul(pd[:, :], zm[:, :], qe[c % 2][:, :], start=True, stop=True)
                    nc.tensor.matmul(pn[:, :], kvm[:, :], qe[c % 2][:, :], start=True, stop=True).then_inc(s["den"], 1)
                if b < B:
                    pe.wait_ge(s["k_phi"], b + 1)
                    pe.wait_ge(s["v_copy"], b + 1)
                    for t in range(TB):
                        nc.tensor.matmul(pkv[:, 0:P], ke[b % 2][:, sl(t, P)], vt[b % 2][:, sl(t, P)], start=t == 0, stop=t == TB - 1)
                    for t in range(TB):
                        mm = nc.tensor.matmul(pkv[:, P:P + 1], ke[b % 2][:, sl(t, P)], k.ones[:, 0:1], start=t == 0, stop=t == TB - 1)
                    mm.then_inc(s["kv"], 1)
                if b:
                    pe.wait_ge(s["o_ready"], c + 1)
                    after(pe, s["done"], c)
                    nc.tensor.matmul(po[:, :], k.w["L0_attn_wo"], o[:, :], start=True, stop=True).then_inc(s["proj"], 1)

        @block.scalar
        def _(act):
            for b in range(B + 1):
                if b < B:
                    act.wait_ge(s["v_tok"], b + 1)
                    after(act, s["kv"], b - 1)
                    nc.scalar.activation(vt[b % 2][:, :], pv[:, :], ACT.Copy).then_inc(s["v_copy"], 1)
                    act.wait_ge(s["k_min"], b + 1)
                    nc.scalar.activation(ke[b % 2][:, :], km[b % 2][:, :], ACT.Exp).then_inc(s["k_exp"], 1)
                    act.wait_ge(s["q_min"], b + 1)
                    after(act, s["den"], b - 1)
                    nc.scalar.activation(qe[b % 2][:, :], qm[b % 2][:, :], ACT.Exp).then_inc(s["q_exp"], 1)
                if b:
                    act.wait_ge(s["den"], b)
                    after(act, s["o_ready"], b - 1)
                    nc.scalar.activation(rec[:, :], pd[:, :], ACT.Ln, bias=k.eps[1e-6]).then_inc(s["log"], 1)
                    act.wait_ge(s["log"], b)
                    nc.scalar.activation(rec[:, :], rec[:, :], ACT.Exp, scale=-1.0).then_inc(s["inv"], 1)

        @block.vector
        def _(dve):
            for b in range(B + 2):
                if 1 <= b <= B:
                    dve.wait_ge(s["kv"], b)
                    after(dve, s["den"], b - 1)
                    nc.vector.tensor_tensor(kvm[:, :], k.heads, pkv[:, 0:P], ALU.mult)
                    nc.vector.tensor_scalar(zm[:, :], k.heads, pkv[:, P:P + 1], None, ALU.mult).then_inc(s["kv_mask"], 1)
                if b < B:
                    dve.wait_ge(s["k_tok"], b + 1)
                    nc.vector.tensor_scalar(km[b % 2][:, :], pk[:, :], 0.0, None, ALU.min).then_inc(s["k_min"], 1)
                    dve.wait_ge(s["q_feat"], b + 1)
                    nc.vector.tensor_scalar(qm[b % 2][:, :], pq[:, :], 0.0, None, ALU.min).then_inc(s["q_min"], 1)
                    dve.wait_ge(s["k_exp"], b + 1)
                    nc.vector.scalar_tensor_tensor(out=ke[b % 2][:, :], in0=pk[:, :], scalar=0.0, in1=ke[b % 2][:, :], op0=ALU.max, op1=ALU.add).then_inc(s["k_phi"], 1)
                    dve.wait_ge(s["q_exp"], b + 1)
                    nc.vector.scalar_tensor_tensor(out=qe[b % 2][:, :], in0=pq[:, :], scalar=0.0, in1=qe[b % 2][:, :], op0=ALU.max, op1=ALU.add).then_inc(s["q_phi"], 1)
                if b >= 2:
                    c = b - 2
                    dve.wait_ge(s["proj"], c + 1)
                    nc.vector.tensor_tensor(res[:, sl(c)], y[:, sl(c)], po[:, :], ALU.add).then_inc(s["done"], 1)
                if 1 <= b <= B:
                    c = b - 1
                    dve.wait_ge(s["inv"], c + 1)
                    after(dve, s["proj"], c)
                    nc.vector.tensor_tensor(o[:, :], rec[:, :], pn[:, :], ALU.mult).then_inc(s["o_ready"], 1)
            dve.wait_ge(s["done"], B)


def l0_lookup_mlp(nc, k, h, y, x):
    C = 4
    with ExitStack() as mem, stage(nc, "up rounded grid act down chain done") as (block, s):
        sb = lambda n, w: mem.enter_context(nc.sbuf_tensor(f"{n}_{nc.next_id()}", [P, w], F32))
        r, g = sb("r", 3 * S), sb("g", 3 * S)
        w1, w2 = k.w["L0_attn_w1"], k.w["L0_attn_w2"]

        @block.tensor
        def _(pe):
            def down(i):
                b, c = divmod(i, C)
                pe.wait_ge(s["act"], i + 1)
                if c == 0:
                    after(pe, s["done"], b - 1)
                nc.tensor.matmul(k.ps[4 + b % 2][:, :], w2[:, sl(c, P)], g[:, sl(i % 3)], start=c == 0, stop=c == C - 1).then_inc(s["down"], 1)

            for i in range(B * C):
                after(pe, s["grid"], i - 3)
                nc.tensor.matmul(k.ps[i % 4][:, :], w1[:, sl(i % C, P)], h[:, sl(i // C)], start=True, stop=True).then_inc(s["up"], 1)
                if i >= 2:
                    down(i - 2)
            down(B * C - 2)
            down(B * C - 1)

        def finish(dve, link, b):
            dve.wait_ge(s["down"], C * (b + 1))
            link(nc.vector.tensor_tensor(y[:, sl(b)], y[:, sl(b)], k.ps[4 + b % 2][:, :], ALU.add))
            nc.vector.tensor_tensor(x[:, sl(b)], x[:, sl(b)], y[:, sl(b)], ALU.add).then_inc(s["done"], 1)

        @block.vector
        def _(dve):
            link = Chain(dve, s["chain"])
            for i in range(B * C):
                b, c = divmod(i, C)
                rr = r[:, sl(i % 3)]
                dve.wait_ge(s["up"], i + 1)
                after(dve, s["act"], i - 2)
                link(nc.vector.tensor_scalar(rr, k.ps[i % 4][:, :], 10.0, MAGIC, ALU.mult, ALU.add))
                link(nc.vector.tensor_scalar(rr, rr, MAGIC, -128.0, ALU.subtract, ALU.max))
                nc.vector.tensor_scalar(rr, rr, 127.0, 0.1, ALU.min, ALU.mult).then_inc(s["grid"], 1)
                if c == 1 and b:
                    finish(dve, link, b - 1)
            finish(dve, link, B - 1)

        @block.scalar
        def _(act):
            for i in range(B * C):
                act.wait_ge(s["grid"], i + 1)
                after(act, s["down"], i - 2)
                nc.scalar.activation(g[:, sl(i % 3)], r[:, sl(i % 3)], ACT.Gelu_apprx_tanh).then_inc(s["act"], 1)


def project(nc, k, jobs):
    with stage(nc, "product copied") as (block, s):
        steps = [(w, src, dst, bias, scale, slice(c, min(c + S, n)))
                 for w, src, n, dst, bias, scale in jobs for c in range(0, n, S)]

        @block.tensor
        def _(pe):
            for i, (w, src, dst, bias, scale, c) in enumerate(steps):
                after(pe, s["copied"], i - 3)
                nc.tensor.matmul(k.ps[i % 4][0:w.shape[-1], 0:c.stop - c.start], w, src[:, c], start=True, stop=True).then_inc(s["product"], 1)

        @block.vector
        def _(dve):
            for i, (w, src, dst, bias, scale, c) in enumerate(steps):
                dve.wait_ge(s["product"], i + 1)
                nc.vector.tensor_scalar(dst[:, c], k.ps[i % 4][0:w.shape[-1], 0:c.stop - c.start],
                                        0.0 if bias is None else bias, scale, ALU.add, ALU.mult).then_inc(s["copied"], 1)


def cross_attention(nc, k, xn, x, q, pre, names, scale, biased, mask=None, fill=0.0, spare=False):
    wq, wk, wv, wo = (k.w[pre + n] for n in names)
    bq, bk, bo = (k.w[pre + n] if biased else None for n in ("bq", "bk", "bo"))
    bo = k.w[pre + "bproj"] if bo is None else bo
    with ExitStack() as mem:
        sb = lambda n, w, p=P: mem.enter_context(nc.sbuf_tensor(f"{n}_{nc.next_id()}", [p, w], F32))
        kt, kbig, vbig = sb("kt", B * M), xn, sb("vbig", B * S)
        crep = sb("crep", B * P)
        project(nc, k, [(wk, k.ctx, B * M, kt, bk, 1.0), (wq, xn, T, q, bq, scale)])
        with stage(nc, "repeated rows added spread") as (block, s):
            @block.vector
            def _(dve):
                for b in range(B):
                    nc.vector.tensor_copy(crep[:, sl(b, P)].rearrange("p (r m) -> p r m", r=4),
                                          k.ctx[:, sl(b, M)].unsqueeze(1).broadcast_to([P, 4, M])).then_inc(s["repeated"], 1)
                for b in range(B):
                    nc.vector.tensor_tensor(kbig[:, sl(b)].rearrange("p (h m) -> p h m", h=H),
                                            kt[:, sl(b, M)].unsqueeze(1).broadcast_to([P, H, M]),
                                            k.w["head_cols"].unsqueeze(2).broadcast_to([P, H, M]), ALU.mult).then_inc(s["spread"], 1)
                for b in range(B):
                    v = k.ps[b][:, 0:P]
                    dve.wait_ge(s["rows"], b + 1)
                    if biased:
                        nc.vector.tensor_tensor(crep[:, sl(b, P)], v, k.w[pre + "bv"], ALU.add).then_inc(s["added"], 1)
                        dve.wait_ge(s["added"], b + 1)
                        v = crep[:, sl(b, P)]
                    nc.vector.tensor_tensor(vbig[:, sl(b)].rearrange("p (c e) -> p c e", c=4),
                                            v.unsqueeze(1).broadcast_to([P, 4, P]),
                                            k.w["head_rows"].rearrange("p (c e) -> p c e", c=4), ALU.mult).then_inc(s["spread"], 1)
                dve.wait_ge(s["spread"], 2 * B)

            @block.tensor
            def _(pe):
                for b in range(B):
                    pe.wait_ge(s["repeated"], b + 1)
                    nc.tensor.matmul(k.ps[b][:, 0:P], crep[:, sl(b, P)], wv, start=True, stop=True).then_inc(s["rows"], 1)

        E = S + H
        keep, neg = (mask, sb("neg", mask.shape[1])) if mask is not None else (None, None)
        d, p, pt = sb("d", 2 * E), sb("p", 2 * E), sb("pt", 2 * 4 * S)
        spt, rmax, o, rec = sb("spt", 2 * S, H), sb("rmax", NT * H), sb("o", S), sb("rec", S)
        sems = "scores max_ready centred weights turned copied sums values log inv normed proj done chain"
        with stage(nc, sems) as (block, s):
            turned = k.ps[2:4]

            @block.tensor
            def _(pe):
                def attend(b, quarter):
                    if quarter == 0:
                        pe.wait_ge(s["copied"], TB * (b + 1))
                        after(pe, s["log"], b)
                    if quarter == 2:
                        after(pe, s["normed"], b)
                    for c in (2 * (quarter % 2), 2 * (quarter % 2) + 1):
                        if quarter < 2:
                            mm = nc.tensor.matmul(k.ps[5][:, :], k.w["head_rows"][:, sl(c, P)], pt[:, sl(4 * (b % 2) + c)],
                                                  start=c == 0, stop=c == 3 and not spare)
                        else:
                            mm = nc.tensor.matmul(k.ps[4][:, :], vbig[:, sl(4 * b + c, P)], pt[:, sl(4 * (b % 2) + c)], start=c == 0, stop=c == 3)
                    if spare and quarter == 1:
                        mm = nc.tensor.matmul(k.ps[5][:, :], k.w["head_of"][0:H, :], spt[:, sl(b % 2)], start=False, stop=True)
                    if quarter % 2:
                        mm.then_inc(s["values" if quarter == 3 else "sums"], 1)

                def out(b):
                    pe.wait_ge(s["normed"], b + 1)
                    after(pe, s["done"], b)
                    nc.tensor.matmul(k.ps[6][:, :], wo, o[:, :], start=True, stop=True).then_inc(s["proj"], 1)

                def turn(i):
                    pe.wait_ge(s["weights"], i + 1)
                    after(pe, s["copied"], i - 1)
                    for c in range(4):
                        mm = nc.tensor.transpose(turned[i % 2][:, sl(c, P)], p[:, (i % 2) * E + c * P:(i % 2) * E + (c + 1) * P], k.ident)
                    if spare:
                        after(pe, s["copied"], i)
                        mm = nc.tensor.transpose(k.ps[7][0:H, 0:P], p[:, (i % 2) * E + S:(i % 2 + 1) * E], k.ident)
                    mm.then_inc(s["turned"], 1)

                for i in range(NT + TB + 3):
                    if i < NT:
                        b = i // TB
                        after(pe, s["centred"], i - 1)
                        nc.tensor.matmul(k.ps[i % 2][:, :], q[:, sl(i, P)], kbig[:, sl(b)], start=True, stop=True).then_inc(s["scores"], 1)
                    if 1 <= i <= NT:
                        turn(i - 1)
                    if TB < i <= NT + TB:
                        attend(*divmod(i - 1 - TB, TB))
                    if i > 2 * TB and i % TB == 2:
                        out(i // TB - 2)

            @block.vector
            def _(dve):
                link = Chain(dve, s["chain"])
                if mask is not None:
                    link(nc.vector.tensor_scalar(neg[:, :], mask, fill, None, ALU.mult))
                    link(nc.vector.tensor_scalar(keep, mask, -1.0, 1.0, ALU.mult, ALU.add))

                def normalise(b):
                    dve.wait_ge(s["inv"], b + 1)
                    dve.wait_ge(s["values"], b + 1)
                    after(dve, s["proj"], b)
                    nc.vector.tensor_tensor(o[:, :], rec[:, :], k.ps[4][:, :], ALU.mult).then_inc(s["normed"], 1)

                def finish(b):
                    dve.wait_ge(s["proj"], b + 1)
                    nc.vector.scalar_tensor_tensor(out=x[:, sl(b)], in0=k.ps[6][:, :], scalar=bo, in1=x[:, sl(b)],
                                                   op0=ALU.add, op1=ALU.add).then_inc(s["done"], 1)

                for i in range(NT + 2 * TB):
                    if i > 2 * TB and i % TB == 1:
                        normalise(i // TB - 2)
                    if i > 2 * TB and i % TB == 3:
                        finish(i // TB - 2)
                    if i >= NT:
                        continue
                    heads = lambda a: a.rearrange("p (h m) -> p h m", h=H)
                    dd = d[:, (i % 2) * E:(i % 2) * E + S]
                    mx = rmax[:, sl(i, H)]
                    dve.wait_ge(s["scores"], i + 1)
                    after(dve, s["weights"], i - 1)
                    sc = k.ps[i % 2][:, :]
                    if mask is not None:
                        span = lambda a: a[:, sl(i % (mask.shape[1] // M), M)].unsqueeze(1).broadcast_to([P, H, M])
                        link(nc.vector.tensor_tensor(heads(dd), heads(sc), span(keep), ALU.mult))
                        link(nc.vector.tensor_tensor(heads(dd), heads(dd), span(neg), ALU.add))
                        sc = dd
                    link(nc.vector.tensor_reduce(mx, heads(sc), AX.X, ALU.max))
                    if spare:
                        link(nc.vector.tensor_scalar(mx, mx, 0.0, None, ALU.max))
                        nc.vector.tensor_scalar(d[:, (i % 2) * E + S:(i % 2 + 1) * E], mx, -1.0, None, ALU.mult)
                    nc.vector.tensor_tensor(heads(dd), heads(sc), mx.unsqueeze(2).broadcast_to([P, H, M]), ALU.subtract).then_inc(s["centred"], 1)

            @block.scalar
            def _(act):
                nc.scalar.preload_act_table_set(LN_EXP)

                def copy(i):
                    b, t = divmod(i, TB)
                    act.wait_ge(s["turned"], i + 1)
                    after(act, s["values"], b - 1)
                    dst = pt[:, (b % 2) * 4 * S:(b % 2 + 1) * 4 * S].rearrange("p (c t) -> p c t", c=4)[:, :, sl(t, P)]
                    ins = nc.scalar.activation(dst, turned[i % 2][:, :].rearrange("p (c t) -> p c t", c=4), ACT.Copy)
                    if spare:
                        ins = nc.scalar.activation(spt[:, (b % 2) * S + t * P:(b % 2) * S + (t + 1) * P], k.ps[7][0:H, 0:P], ACT.Copy)
                    ins.then_inc(s["copied"], 1)

                def invert(b):
                    act.wait_ge(s["sums"], b + 1)
                    after(act, s["normed"], b)
                    nc.scalar.activation(rec[:, :], k.ps[5][:, :], ACT.Ln).then_inc(s["log"], 1)
                    act.wait_ge(s["log"], b + 1)
                    nc.scalar.activation(rec[:, :], rec[:, :], ACT.Exp, scale=-1.0).then_inc(s["inv"], 1)

                for i in range(NT + TB):
                    if i < NT:
                        w = S + (H if spare else 0)
                        act.wait_ge(s["centred"], i + 1)
                        after(act, s["turned"], i - 1)
                        nc.scalar.activation(p[:, (i % 2) * E:(i % 2) * E + w], d[:, (i % 2) * E:(i % 2) * E + w], ACT.Exp).then_inc(s["weights"], 1)
                    if 1 <= i <= NT:
                        copy(i - 1)
                    if i > TB and i % TB == 3:
                        invert(i // TB - 1)


def load_big(nc, k, name):
    with nc.Block() as block:
        @block.sync
        def _(sp):
            sp.dma_start(k.big[:, 0:k.ap[name].shape[1]], k.ap[name]).then_inc(k.big_loaded, 16)


def layer1(nc, k, x, y, a):
    norm(nc, k, x, y, 1e-5)
    cross_attention(nc, k, y, x, a, "L0_xattn_", ("Wq", "Wk", "Wv", "Wproj"), HD ** -0.5, False,
                    mask=k.mask0[:, :], fill=-1e30, spare=True)


def layer7(nc, k, x, y, a):
    norm(nc, k, x, y, 1e-5)
    cross_attention(nc, k, y, x, a, "L2_xattn_", ("Wq", "Wk", "Wv", "Wo"), HD ** -0.5, True,
                    mask=k.mask2[:, :], fill=-10000.0)


def layer10(nc, k, x, y, a):
    load_big(nc, k, "big3")
    norm(nc, k, x, y, 1e-5)
    cross_attention(nc, k, y, x, a, "L3_xattn_", ("Wq", "Wk", "Wv", "Wo"), HD ** -0.5, True)


def top2_weights(nc, k, xn, w):
    G = 8
    with ExitStack() as mem, stage(nc, "logits shifted exps done chain") as (block, s):
        sb = lambda n, w_: mem.enter_context(nc.sbuf_tensor(f"{n}_{nc.next_id()}", [P, w_], F32))
        lg, d, gt, eq, rank, mx, tot = (sb(n, c) for n, c in (("lg", NT * G), ("d", NT * G), ("gt", NT * G * G), ("eq", NT * G * G),
                                        ("rank", NT * G), ("mx", NT), ("tot", NT)))

        @block.tensor
        def _(pe):
            for i in range(NT):
                mm = nc.tensor.matmul(k.ps[0][:, sl(i, G)], xn[:, sl(i, P)], k.w["L0_ffn_gate_w"], start=True, stop=True)
            mm.then_inc(s["logits"], 1)

        @block.scalar
        def _(act):
            act.wait_ge(s["shifted"], 1)
            nc.scalar.activation(d[:, :], d[:, :], ACT.Exp).then_inc(s["exps"], 1)

        @block.vector
        def _(dve):
            link = Chain(dve, s["chain"])
            tile = lambda a: a.rearrange("p (t i) -> p t i", i=G)
            pair = lambda a: a[:, :].rearrange("p (t i j) -> p t i j", i=G, j=G)
            full = [P, NT, G, G]
            this = tile(lg[:, :]).unsqueeze(3).broadcast_to(full)
            other = tile(lg[:, :]).unsqueeze(2).broadcast_to(full)
            before = k.w["before8"].rearrange("p (i j) -> p i j", j=G).unsqueeze(1).broadcast_to(full)
            dve.wait_ge(s["logits"], 1)
            link(nc.vector.tensor_tensor(tile(lg[:, :]), tile(k.ps[0][:, 0:NT * G]),
                                         k.w["L0_ffn_gate_b"].unsqueeze(1).broadcast_to([P, NT, G]), ALU.add))
            link(nc.vector.tensor_reduce(mx[:, :], tile(lg[:, :]), AX.X, ALU.max))
            nc.vector.tensor_tensor(tile(d[:, :]), tile(lg[:, :]), mx[:, :].unsqueeze(2).broadcast_to([P, NT, G]), ALU.subtract).then_inc(s["shifted"], 1)
            nc.vector.tensor_tensor(pair(gt), other, this, ALU.is_gt)
            link(nc.vector.tensor_tensor(pair(eq), other, this, ALU.is_equal))
            link(nc.vector.tensor_tensor(pair(eq), pair(eq), before, ALU.mult))
            link(nc.vector.tensor_tensor(gt[:, :], gt[:, :], eq[:, :], ALU.add))
            link(nc.vector.tensor_reduce(rank[:, :], gt[:, :].rearrange("p (a j) -> p a j", j=G), AX.X, ALU.add))
            dve.wait_ge(s["exps"], 1)
            link(nc.vector.scalar_tensor_tensor(out=w[:, :], in0=rank[:, :], scalar=2.0, in1=d[:, :], op0=ALU.is_lt, op1=ALU.mult))
            link(nc.vector.tensor_reduce(tot[:, :], tile(w[:, :]), AX.X, ALU.add))
            link(nc.vector.reciprocal(tot[:, :], tot[:, :]))
            nc.vector.tensor_tensor(tile(w[:, :]), tile(w[:, :]), tot[:, :].unsqueeze(2).broadcast_to([P, NT, G]), ALU.mult).then_inc(s["done"], 1)
            dve.wait_ge(s["done"], 1)


def experts(nc, k, x, y, a, J, loaded, spread, gate_bias=None, up_bias=None, before=None):
    names = "y_high y_low w_high w_low gate up spread silu gated h high low down done"
    with ExitStack() as mem2, stage(nc, names) as (block, s):
        sb2 = lambda n, w_, dt=F32: mem2.enter_context(nc.sbuf_tensor(f"{n}_{nc.next_id()}", [P, w_], dt))
        yh, yl = sb2("yh", 2 * S, F32R), sb2("yl", 2 * S, F32R)
        sg, h, hh, hl = a[:, 0:2 * S], a[:, 2 * S:4 * S], sb2("hh", 3 * S, F32R), sb2("hl", 3 * S, F32R)
        wh, wl = sb2("wh", 3 * 3 * P, F32R), sb2("wl", 3 * 3 * P, F32R)
        banks = [k.ps[0:3], k.ps[3:6]]
        units = [(pair, j, b) for pair in range(B // 2) for j in range(J) for b in (2 * pair, 2 * pair + 1)]
        N = len(units)
        part = lambda t, n, i: t[:, ((n // 2) % 3 * 3 + i) * P:][:, 0:P]

        @block.gpsimd
        def _(pool):
            pool.wait_ge(k.big_loaded, loaded)
            for m in range(N // 2):
                j = m % J
                src = k.big[:, 0:3 * J * P].rearrange("p (w j e) -> p w j e", w=3, j=J)[:, :, j, :]
                high, low = (t[:, (m % 3) * 3 * P:][:, 0:3 * P].rearrange("p (w e) -> p w e", w=3) for t in (wh, wl))
                after(pool, s["down"], 2 * m - 4)
                nc.gpsimd.tensor_copy(high, src).then_inc(s["w_high"], 1)
                pool.wait_ge(s["w_high"], m + 1)
                nc.gpsimd.tensor_tensor(low, src, high.bitcast(F32), ALU.subtract).then_inc(s["w_low"], 1)

        @block.tensor
        def _(pe):
            def three(out, w_, data, cur, start, stop):
                (dh, dl), (ph, pl) = data, w_
                nc.tensor.matmul(out, pl, dh[:, cur], start=start, stop=False)
                nc.tensor.matmul(out, ph, dl[:, cur], start=False, stop=False)
                return nc.tensor.matmul(out, ph, dh[:, cur], start=False, stop=stop)

            def down(n):
                pair, j, b = units[n]
                pe.wait_ge(s["low"], n + 1)
                if j == 0:
                    after(pe, s["done"], 2 * pair)
                if j == 0 and before:
                    before(k.ps[6 + b % 2][:, :], b)
                three(k.ps[6 + b % 2][:, :], (part(wh, n, 2), part(wl, n, 2)), (hh, hl), sl(n % 3), j == 0 and not before, j == J - 1).then_inc(s["down"], 1)

            for n in range(N + 2):
                if n < N:
                    pair, j, b = units[n]
                    pg, pu, pw = banks[n % 2]
                    pe.wait_ge(s["w_low"], n // 2 + 1)
                    pe.wait_ge(s["y_low"], b + 1)
                    after(pe, s["h"], n - 1)
                    three(pg[:, :], (part(wh, n, 0), part(wl, n, 0)), (yh, yl), sl(b % 2), True, True).then_inc(s["gate"], 1)
                    three(pu[:, :], (part(wh, n, 1), part(wl, n, 1)), (yh, yl), sl(b % 2), True, True).then_inc(s["up"], 1)
                    spread(pw[:, :], j, b).then_inc(s["spread"], 1)
                if n >= 2:
                    down(n - 2)

        @block.scalar
        def _(act):
            for n in range(N + 1):
                if n < N:
                    act.wait_ge(s["gate"], n + 1)
                    after(act, s["gated"], n - 1)
                    nc.scalar.activation(sg[:, sl(n % 2)], banks[n % 2][0][:, :], ACT.Silu, bias=gate_bias(units[n][1]) if gate_bias else 0.0).then_inc(s["silu"], 1)
                if n:
                    act.wait_ge(s["h"], n)
                    after(act, s["down"], n - 3)
                    nc.scalar.activation(hh[:, sl((n - 1) % 3)], h[:, sl((n - 1) % 2)], ACT.Copy).then_inc(s["high"], 1)

        @block.vector
        def _(dve):
            def finish(pair):
                dve.wait_ge(s["down"], 2 * J * (pair + 1))
                for b in (2 * pair, 2 * pair + 1):
                    nc.vector.tensor_tensor(x[:, sl(b)], x[:, sl(b)], k.ps[6 + b % 2][:, :], ALU.add).then_inc(s["done"], 1)

            def split(b):
                nc.vector.tensor_copy(yh[:, sl(b % 2)], y[:, sl(b)]).then_inc(s["y_high"], 1)
                dve.wait_ge(s["y_high"], b + 1)
                nc.vector.tensor_tensor(yl[:, sl(b % 2)], y[:, sl(b)], yh[:, sl(b % 2)].bitcast(F32), ALU.subtract).then_inc(s["y_low"], 1)

            for n in range(N + 1):
                cur = sl(n % 2)
                if n < N:
                    pair, j, b = units[n]
                    if j == 0 and b % 2 == 0:
                        after(dve, s["up"], n)
                        split(b)
                        split(b + 1)
                    dve.wait_ge(s["up"], n + 1)
                    dve.wait_ge(s["silu"], n + 1)
                    after(dve, s["low"], n - 1)
                    if up_bias:
                        ins = nc.vector.scalar_tensor_tensor(out=h[:, cur], in0=banks[n % 2][1][:, :], scalar=up_bias(j), in1=sg[:, cur],
                                                             op0=ALU.add, op1=ALU.mult)
                    else:
                        ins = nc.vector.tensor_tensor(h[:, cur], sg[:, cur], banks[n % 2][1][:, :], ALU.mult)
                    ins.then_inc(s["gated"], 1)
                    dve.wait_ge(s["gated"], n + 1)
                    dve.wait_ge(s["spread"], n + 1)
                    nc.vector.tensor_tensor(h[:, cur], h[:, cur], banks[n % 2][2][:, :], ALU.mult).then_inc(s["h"], 1)
                    if pair and j == 1 and b % 2 == 0:
                        finish(pair - 1)
                if n:
                    m = n - 1
                    dve.wait_ge(s["high"], m + 1)
                    after(dve, s["down"], m - 2)
                    nc.vector.tensor_tensor(hl[:, sl(m % 3)], h[:, sl(m % 2)], hh[:, sl(m % 3)].bitcast(F32), ALU.subtract).then_inc(s["low"], 1)
            finish(B // 2 - 1)


def layer2(nc, k, x, y, a):
    G, C = 8, 4
    norm(nc, k, x, y, 1e-5)
    with ExitStack() as mem:
        sb = lambda n, w_, dt=F32, p=P: mem.enter_context(nc.sbuf_tensor(f"{n}_{nc.next_id()}", [p, w_], dt))
        w, wt, w3, wt3, ind = (sb("w", NT * G), sb("wt", T, F32, G), sb("w3", NT * 3 * G, BF16), sb("wt3", T, BF16, 3 * G),
                               sb("ind", G * P, BF16, 3 * G))
        top2_weights(nc, k, y, w)
        with stage(nc, "loaded split turned copied chain") as (block, s):
            @block.gpsimd
            def _(pool):
                pool.dma_start(ind[:, :], k.ap["ind0"]).then_inc(s["loaded"], 16)
                pool.wait_ge(s["loaded"], 16)

            @block.tensor
            def _(pe):
                for b in range(B):
                    for t in range(TB):
                        nc.tensor.transpose(k.ps[b][0:G, sl(t, P)], w[:, sl(b * TB + t, G)], k.ident)
                pe.wait_ge(s["split"], 1)
                for b in range(B):
                    for t in range(TB):
                        mm = nc.tensor.transpose(k.ps[4 + b][0:3 * G, 0:S // 2].bitcast(BF16)[:, sl(t, P)], w3[:, sl(b * TB + t, 3 * G)], k.ident_bf)
                    mm.then_inc(s["turned"], 1)

            @block.vector
            def _(dve):
                link = Chain(dve, s["chain"])
                tile = lambda t, n: t[:, :].rearrange("p (t i) -> p t i", i=n)
                parts = [tile(w3, 3 * G)[:, :, n * G:(n + 1) * G] for n in range(3)]
                left = sb("left", NT * G)
                link(nc.vector.tensor_copy(parts[0], tile(w, G)))
                link(nc.vector.tensor_tensor(tile(left, G), tile(w, G), parts[0], ALU.subtract))
                link(nc.vector.tensor_copy(parts[1], tile(left, G)))
                link(nc.vector.tensor_tensor(tile(left, G), tile(left, G), parts[1], ALU.subtract))
                nc.vector.tensor_copy(parts[2], tile(left, G)).then_inc(s["split"], 1)
                for b in range(B):
                    dve.wait_ge(s["turned"], b + 1)
                    nc.vector.tensor_copy(wt[:, sl(b)], k.ps[b][0:G, :]).then_inc(s["copied"], 1)
                dve.wait_ge(s["copied"], 2 * B)

            @block.scalar
            def _(act):
                for b in range(B):
                    act.wait_ge(s["turned"], b + 1)
                    nc.scalar.activation(wt3[:, sl(b)], k.ps[4 + b][0:3 * G, 0:S // 2].bitcast(BF16), ACT.Copy).then_inc(s["copied"], 1)

        experts(nc, k, x, y, a, G * C, 16,
                spread=lambda bank, j, b: nc.tensor.matmul(bank, ind[:, sl(j // C, P)], wt3[:, sl(b)], start=True, stop=True),
                gate_bias=lambda j: k.w["L0_ffn_b1"][:, j // C * 2 * C + C + j % C:][:, 0:1],
                up_bias=lambda j: k.w["L0_ffn_b1"][:, j // C * 2 * C + j % C:][:, 0:1],
                before=lambda bank, b: nc.tensor.matmul(bank, k.w["L0_ffn_b2"][0:G, :], wt[:, sl(b)], start=True, stop=False))


def layer3(nc, k, x, y, a):
    norm(nc, k, x, y, 1e-5, inner=(1e-5, k.w["L1_attn_rms_weight"], None, a))
    with ExitStack() as mem, stage(nc, "forget value side gate sig driven scanned gated proj done chain") as (block, s):
        sb = lambda n, w_: mem.enter_context(nc.sbuf_tensor(f"{n}_{nc.next_id()}", [P, w_], F32))
        fg, sd, gt, h = sb("fg", 2 * S), sb("sd", 2 * S), sb("gt", 2 * S), sb("h", 2 * S)

        @block.tensor
        def _(pe):
            def out(b):
                pe.wait_ge(s["gated"], b + 1)
                nc.tensor.matmul(k.ps[4 + b][:, :], k.w["L1_attn_w_o"], h[:, sl(b % 2)], start=True, stop=True).then_inc(s["proj"], 1)

            for b in range(B):
                after(pe, s["driven"], b)
                for j, (n, sem) in enumerate((("w_A", s["forget"]), ("w_output", s["side"]), ("w_sidegate", s["gate"]), ("w_x", s["value"]))):
                    nc.tensor.matmul(k.ps[j][:, :], k.w["L1_attn_" + n], a[:, sl(b)], start=True, stop=True).then_inc(sem, 1)
                if b:
                    out(b - 1)
            out(B - 1)

        @block.scalar
        def _(act):
            for b in range(B):
                after(act, s["gated"], b - 1)
                for j, (sem, dst, bias) in enumerate(((s["forget"], fg, k.w["L1_attn_b_A"]), (s["side"], sd, 0.0), (s["gate"], gt, 0.0))):
                    act.wait_ge(sem, b + 1)
                    nc.scalar.activation(dst[:, sl(b % 2)], k.ps[j][:, :], ACT.Sigmoid, bias=bias).then_inc(s["sig"], 1)

        @block.vector
        def _(dve):
            link = Chain(dve, s["chain"])

            def add(b):
                dve.wait_ge(s["proj"], b + 1)
                link(nc.vector.tensor_tensor(y[:, sl(b)], y[:, sl(b)], k.ps[4 + b][:, :], ALU.add))
                link(nc.vector.tensor_tensor(x[:, sl(b)], x[:, sl(b)], y[:, sl(b)], ALU.add))

            for b in range(B):
                cur = sl(b % 2)
                dve.wait_ge(s["value"], b + 1)
                dve.wait_ge(s["sig"], 3 * b + 3)
                nc.vector.tensor_tensor(sd[:, cur], sd[:, cur], k.ps[3][:, :], ALU.mult).then_inc(s["driven"], 1)
                dve.wait_ge(s["driven"], b + 1)
                after(dve, s["proj"], b - 1)
                link(nc.vector.tensor_tensor_scan(h[:, cur], fg[:, cur], sd[:, cur], 0.0, ALU.mult, ALU.add))
                nc.vector.tensor_tensor(h[:, cur], h[:, cur], gt[:, cur], ALU.mult).then_inc(s["gated"], 1)
                if b:
                    add(b - 1)
            add(B - 1)


def layer4(nc, k, x, y, a):
    norm(nc, k, x, y, 1e-5)
    q = a
    with ExitStack() as mem:
        sb = lambda n, w_, p=P: mem.enter_context(nc.sbuf_tensor(f"{n}_{nc.next_id()}", [p, w_], F32))
        kt, v, p, pt, mx = sb("kt", B * M), sb("v", B * D, M), sb("p", NT * M), sb("pt", T, M), sb("mx", NT)
        project(nc, k, [(k.w["L1_xattn_Wk"], k.ctx, B * M, kt, None, 1.0), (k.w["L1_xattn_Wq"], y, T, q, None, D ** -0.5)])
        with stage(nc, "scores values centred exps weights turned copied out done chain vcopied") as (block, s):
            @block.tensor
            def _(pe):
                for i in range(NT):
                    mm = nc.tensor.matmul(k.ps[0][:, sl(i, M)], q[:, sl(i, P)], kt[:, sl(i // TB, M)], start=True, stop=True)
                mm.then_inc(s["scores"], 1)
                for b in range(B):
                    mm = nc.tensor.matmul(k.ps[1][0:M, sl(b, D)], k.ctx[:, sl(b, M)], k.w["L1_xattn_Wv"], start=True, stop=True)
                mm.then_inc(s["values"], 1)
                pe.wait_ge(s["weights"], 1)
                for b in range(B):
                    for t in range(TB):
                        mm = nc.tensor.transpose(k.ps[2 + b][0:M, sl(t, P)], p[:, sl(b * TB + t, M)], k.ident)
                    mm.then_inc(s["turned"], 1)
                pe.wait_ge(s["vcopied"], 1)
                for b in range(B):
                    pe.wait_ge(s["copied"], b + 1)
                    after(pe, s["done"], b - 1)
                    nc.tensor.matmul(k.ps[6 + b % 2][:, :], v[:, sl(b, D)], pt[:, sl(b)], start=True, stop=True).then_inc(s["out"], 1)

            @block.scalar
            def _(act):
                act.wait_ge(s["centred"], 1)
                nc.scalar.activation(p[:, :], p[:, :], ACT.Exp).then_inc(s["exps"], 1)
                act.wait_ge(s["values"], 1)
                nc.scalar.activation(v[:, :], k.ps[1][0:M, :], ACT.Copy).then_inc(s["vcopied"], 1)
                for b in range(B):
                    act.wait_ge(s["turned"], b + 1)
                    nc.scalar.activation(pt[:, sl(b)], k.ps[2 + b][0:M, :], ACT.Copy).then_inc(s["copied"], 1)

            @block.vector
            def _(dve):
                link = Chain(dve, s["chain"])
                tile = lambda t: t[:, :].rearrange("p (t m) -> p t m", m=M)
                wide = mx[:, :].unsqueeze(2).broadcast_to([P, NT, M])
                dve.wait_ge(s["scores"], 1)
                link(nc.vector.tensor_reduce(mx[:, :], tile(k.ps[0]), AX.X, ALU.max))
                nc.vector.tensor_tensor(tile(p), tile(k.ps[0]), wide, ALU.subtract).then_inc(s["centred"], 1)
                dve.wait_ge(s["exps"], 1)
                link(nc.vector.tensor_reduce(mx[:, :], tile(p), AX.X, ALU.add))
                link(nc.vector.reciprocal(mx[:, :], mx[:, :]))
                nc.vector.tensor_tensor(tile(p), tile(p), wide, ALU.mult).then_inc(s["weights"], 1)
                for b in range(B):
                    dve.wait_ge(s["out"], b + 1)
                    nc.vector.tensor_tensor(x[:, sl(b)], x[:, sl(b)], k.ps[6 + b % 2][:, :], ALU.add).then_inc(s["done"], 1)


def layer5(nc, k, x, y, a):
    F, C = 512, 4
    norm(nc, k, x, y, 1e-5, inner=(1e-8, k.w["L1_ffn_norm1_w"], None, a))
    w1, w2 = k.w["L1_ffn_w1"], k.w["L1_ffn_w2"]
    with ExitStack() as mem:
        sb = lambda n, w_, dt=F32: mem.enter_context(nc.sbuf_tensor(f"{n}_{nc.next_id()}", [P, w_], dt))
        q1w, q2w, tmp = sb("q1w", F, BF16), sb("q2w", F, BF16), sb("tmp", F)
        part, wmean, wscale = sb("part", 2), sb("wmean", 2), sb("wscale", 2)
        with stage(nc, "abs summed total rounded chain") as (block, s):
            @block.scalar
            def _(act):
                for j, w in enumerate((w1, w2)):
                    after(act, s["abs"], j)
                    nc.scalar.activation(tmp[:, :], w, ACT.Abs, accum_out=part[:, j:j + 1]).then_inc(s["abs"], 1)

            @block.tensor
            def _(pe):
                pe.wait_ge(s["abs"], 2)
                nc.tensor.matmul(k.ps[0][:, 0:2], k.ones, part[:, :], start=True, stop=True).then_inc(s["total"], 1)

            @block.vector
            def _(dve):
                link = Chain(dve, s["chain"])
                dve.wait_ge(s["total"], 1)
                link(nc.vector.tensor_scalar(wmean[:, :], k.ps[0][:, 0:2], 1.0 / (D * F), 1e-5, ALU.mult, ALU.max))
                link(nc.vector.reciprocal(wscale[:, :], wmean[:, :]))
                for j, (w, q) in enumerate(((w1, q1w), (w2, q2w))):
                    link(nc.vector.tensor_scalar(tmp[:, :], w, wscale[:, j:j + 1], MAGIC, ALU.mult, ALU.add))
                    link(nc.vector.tensor_scalar(tmp[:, :], tmp[:, :], MAGIC, -1.0, ALU.subtract, ALU.max))
                    link(nc.vector.tensor_scalar(q[:, :], tmp[:, :], 1.0, None, ALU.min))

        top, sc, un = sb("top", 2 * NT), sb("sc", 2 * NT), sb("un", 2 * NT)
        ss, r1 = sb("ss", NT), sb("r1", NT)
        f1, q1, q1t, o = sb("f1", S), sb("q1", 2 * S, BF16), sb("q1t", 2 * S, BF16), sb("o", S)
        q2, q2t = sb("q2", TB * F, BF16), sb("q2t", TB * F, BF16)
        W = TB * F
        r, h, hn = ([k.big[:, (2 * n + j) * W:(2 * n + j + 1) * W] for j in range(2)] for n in range(3))
        tiles = lambda t: t.rearrange("p (t e) -> p t e", t=TB)
        p_in, p_q, p_h, p_q2, p_o, p_back = k.ps[0], k.ps[2][:, 0:S // 2].bitcast(BF16), k.ps[3:5], k.ps[5:7], k.ps[7], k.ps[1]
        names = ("turned quant1 q_turned q_copied up relu squared hidden sums log inv scaled_up rounded quant2 q2_turned q2_copied "
                 "down scaled back added chain")
        with stage(nc, names) as (block, s):
            col = lambda t, j, i: t[:, j * NT + i:j * NT + i + 1]
            four = lambda t, j, b: t[:, j * NT + b * TB:j * NT + (b + 1) * TB]
            wide = lambda t, j, b: four(t, j, b).unsqueeze(2).broadcast_to([P, TB, P])

            @block.tensor
            def _(pe):
                def turn(i):
                    after(pe, s["quant1"], i)
                    for t in range(TB):
                        mm = nc.tensor.transpose(p_in[:, sl(t, P)], a[:, sl(i * TB + t, P)], k.ident)
                    mm.then_inc(s["turned"], 1)

                turn(0)
                for i in range(B + 2):
                    if i < B:
                        pe.wait_ge(s["quant1"], i + 1)
                        after(pe, s["q_copied"], i)
                        for t in range(TB):
                            mm = nc.tensor.transpose(p_q[:, sl(t, P)], q1[:, (i % 2) * S + t * P:][:, 0:P], k.ident_bf)
                        mm.then_inc(s["q_turned"], 1)
                        pe.wait_ge(s["q_copied"], i + 1)
                        for t in range(TB):
                            n = i * TB + t
                            after(pe, s["relu"], n - 1)
                            nc.tensor.matmul(p_h[n % 2][:, :], q1t[:, (i % 2) * S + t * P:][:, 0:P], q1w[:, :], start=True, stop=True).then_inc(s["up"], 1)
                        if i < B - 1:
                            turn(i + 1)
                    if i >= 2:
                        pe.wait_ge(s["scaled"], i - 1)
                        after(pe, s["added"], i - 2)
                        for t in range(TB):
                            mm = nc.tensor.transpose(p_back[:, sl(t, P)], o[:, sl(t, P)], k.ident)
                        mm.then_inc(s["back"], 1)
                    if 1 <= i <= B:
                        c = i - 1
                        pe.wait_ge(s["quant2"], c + 1)
                        for t in range(TB):
                            if t % 2 == 0:
                                after(pe, s["q2_copied"], 2 * c + t // 2 - 1)
                            for j in range(C):
                                mm = nc.tensor.transpose(p_q2[t // 2][:, :].bitcast(BF16)[:, (t % 2) * F + j * P:][:, 0:P],
                                                         q2[:, t * F + j * P:][:, 0:P], k.ident_bf)
                            if t % 2:
                                mm.then_inc(s["q2_turned"], 1)
                        after(pe, s["scaled"], c)
                        for t in range(TB):
                            pe.wait_ge(s["q2_copied"], 2 * c + t // 2 + 1)
                            for j in range(C):
                                mm = nc.tensor.matmul(p_o[:, sl(t, P)], q2t[:, t * F + j * P:][:, 0:P], q2w[:, sl(j, P)], start=j == 0, stop=j == C - 1)
                        mm.then_inc(s["down"], 1)

            @block.vector
            def _(dve):
                link = Chain(dve, s["chain"])

                def scales(j, b):
                    t, m, u = (four(n, j, b) for n in (top, sc, un))
                    link(nc.vector.tensor_scalar(t, t, 1e-5, None, ALU.max))
                    link(nc.vector.reciprocal(m, t))
                    link(nc.vector.tensor_scalar(m, m, 127.0, None, ALU.mult))
                    link(nc.vector.tensor_scalar(u, t, 1.0 / 127.0, wmean[:, j:j + 1], ALU.mult, ALU.mult))

                def output(c):
                    dve.wait_ge(s["down"], c + 1)
                    nc.vector.tensor_tensor(tiles(o[:, :]), tiles(p_o[:, :]), wide(un, 1, c), ALU.mult).then_inc(s["scaled"], 1)
                    dve.wait_ge(s["back"], c + 1)
                    nc.vector.tensor_tensor(x[:, sl(c)], x[:, sl(c)], p_back[:, :], ALU.add).then_inc(s["added"], 1)

                for i in range(B + 2):
                    if 1 <= i <= B:
                        c = i - 1
                        dve.wait_ge(s["squared"], c + 1)
                        nc.vector.tensor_scalar(h[c % 2], r[c % 2], k.w["L1_ffn_act_scale"], k.w["L1_ffn_act_bias"], ALU.mult, ALU.add).then_inc(s["hidden"], 1)
                    if i < B:
                        dve.wait_ge(s["turned"], i + 1)
                        link(nc.vector.tensor_reduce(four(top, 0, i), tiles(p_in[:, :]), AX.X, ALU.max, apply_absolute_value=True))
                        scales(0, i)
                        link(nc.vector.tensor_tensor(tiles(f1[:, :]), tiles(p_in[:, :]), wide(sc, 0, i), ALU.mult))
                        link(nc.vector.tensor_scalar(f1[:, :], f1[:, :], MAGIC, MAGIC - 128.0, ALU.add, ALU.max))
                        after(dve, s["q_turned"], i - 1)
                        nc.vector.tensor_scalar(q1[:, sl(i % 2)], f1[:, :], MAGIC + 127.0, MAGIC, ALU.min, ALU.subtract).then_inc(s["quant1"], 1)
                    if i >= 2:
                        output(i - 2)
                    if 1 <= i <= B:
                        c = i - 1
                        dve.wait_ge(s["inv"], c + 1)
                        dve.wait_ge(s["hidden"], c + 1)
                        for t in range(TB):
                            ins = nc.vector.scalar_tensor_tensor(out=hn[c % 2][:, sl(t, F)], in0=h[c % 2][:, sl(t, F)], scalar=r1[:, c * TB + t:c * TB + t + 1],
                                                                 in1=k.w["L1_ffn_norm2_w"], op0=ALU.mult, op1=ALU.mult)
                        link(ins)
                        link(nc.vector.tensor_reduce(four(top, 1, c), tiles(hn[c % 2]), AX.X, ALU.max, apply_absolute_value=True))
                        scales(1, c)
                        for t in range(TB):
                            cur = hn[c % 2][:, sl(t, F)]
                            ins = nc.vector.tensor_scalar(cur, cur, col(sc, 1, c * TB + t), MAGIC, ALU.mult, ALU.add)
                        link(ins)
                        nc.vector.tensor_scalar(hn[c % 2], hn[c % 2], MAGIC - 128.0, MAGIC + 127.0, ALU.max, ALU.min).then_inc(s["rounded"], 1)

            @block.scalar
            def _(act):
                nc.scalar.preload_act_table_set(LN_EXP)

                def copy_turned(c):
                    for half in range(2):
                        act.wait_ge(s["q2_turned"], 2 * c + half + 1)
                        after(act, s["down"], c)
                        nc.scalar.activation(q2t[:, half * 2 * F:(half + 1) * 2 * F], p_q2[half][:, :].bitcast(BF16), ACT.Copy).then_inc(s["q2_copied"], 1)

                for i in range(B + 1):
                    if i < B:
                        act.wait_ge(s["q_turned"], i + 1)
                        after(act, s["up"], (i - 1) * TB)
                        nc.scalar.activation(q1t[:, sl(i % 2)], p_q, ACT.Copy).then_inc(s["q_copied"], 1)
                        after(act, s["hidden"], i - 1)
                        for t in range(TB):
                            n = i * TB + t
                            act.wait_ge(s["up"], n + 1)
                            nc.scalar.activation(r[i % 2][:, sl(t, F)], p_h[n % 2][:, :], ACT.Relu, scale=col(un, 0, n)).then_inc(s["relu"], 1)
                        act.wait_ge(s["relu"], (i + 1) * TB)
                        nc.scalar.activation(r[i % 2], r[i % 2], ACT.Square).then_inc(s["squared"], 1)
                    if i:
                        c = i - 1
                        act.wait_ge(s["rounded"], c + 1)
                        after(act, s["q2_turned"], 2 * c)
                        nc.scalar.activation(q2[:, :], hn[c % 2], ACT.Identity, bias=k.eps[-MAGIC]).then_inc(s["quant2"], 1)
                        copy_turned(c)
                    if i < B:
                        act.wait_ge(s["hidden"], i + 1)
                        after(act, s["quant2"], i - 1)
                        for t in range(TB):
                            n = i * TB + t
                            nc.scalar.activation(hn[i % 2][:, sl(t, F)], h[i % 2][:, sl(t, F)], ACT.Square, accum_out=ss[:, n:n + 1]).then_inc(s["sums"], 1)
                        act.wait_ge(s["sums"], (i + 1) * TB)
                        cur = sl(i, TB)
                        nc.scalar.activation(ss[:, cur], ss[:, cur], ACT.Ln, scale=1.0 / F, bias=k.eps[1e-8]).then_inc(s["log"], 1)
                        act.wait_ge(s["log"], i + 1)
                        nc.scalar.activation(r1[:, cur], ss[:, cur], ACT.Exp, scale=-0.5).then_inc(s["inv"], 1)


def layer8(nc, k, x, y, a):
    G, F = 64, 96
    J = G * F // P
    norm(nc, k, x, y, 1e-5)
    with ExitStack() as mem:
        sb = lambda n, w_, dt=F32, p=P: mem.enter_context(nc.sbuf_tensor(f"{n}_{nc.next_id()}", [p, w_], dt))
        ind = sb("ind", J * P, BF16)
        wt_hm, wt_lo = sb("wt_hm", T, BF16), sb("wt_lo", T, BF16, G)
        with ExitStack() as mem2, stage(nc, "loaded logits shifted exps split turned copied chain") as (block, s):
            sb2 = lambda n, w_, dt=F32: mem2.enter_context(nc.sbuf_tensor(f"{n}_{nc.next_id()}", [P, w_], dt))
            sc, sel, top, mx = sb2("sc", NT * G), sb2("sel", NT * G), sb2("top", NT * 8), sb2("mx", NT)
            hm, lo = sb2("hm", NT * 2 * G, BF16), sb2("lo", NT * G, BF16)

            @block.gpsimd
            def _(pool):
                pool.dma_start(ind[:, :], k.ap["ind"]).then_inc(s["loaded"], 16)
                pool.wait_ge(s["loaded"], 16)

            @block.tensor
            def _(pe):
                for i in range(NT):
                    mm = nc.tensor.matmul(k.ps[i // 8][:, sl(i % 8, G)], y[:, sl(i, P)], k.w["L2_ffn_gate_w"], start=True, stop=True)
                mm.then_inc(s["logits"], 1)
                pe.wait_ge(s["split"], 1)
                for b in range(B):
                    if b == 3:
                        pe.wait_ge(s["copied"], 2)
                    for t in range(TB):
                        i = b * TB + t
                        nc.tensor.transpose(k.ps[2 + 2 * (b % 3)][:, 0:S // 2].bitcast(BF16)[:, sl(t, P)], hm[:, sl(i, P)], k.ident_bf)
                    for t in range(TB):
                        i = b * TB + t
                        mm = nc.tensor.transpose(k.ps[3 + 2 * (b % 3)][0:G, 0:S // 2].bitcast(BF16)[:, sl(t, P)], lo[:, sl(i, G)], k.ident_bf)
                    mm.then_inc(s["turned"], 1)

            @block.scalar
            def _(act):
                act.wait_ge(s["shifted"], 1)
                nc.scalar.activation(sc[:, :], sc[:, :], ACT.Exp).then_inc(s["exps"], 1)
                for b in range(B):
                    act.wait_ge(s["turned"], b + 1)
                    nc.scalar.activation(wt_hm[:, sl(b)], k.ps[2 + 2 * (b % 3)][:, 0:S // 2].bitcast(BF16), ACT.Copy).then_inc(s["copied"], 1)
                    nc.scalar.activation(wt_lo[:, sl(b)], k.ps[3 + 2 * (b % 3)][0:G, 0:S // 2].bitcast(BF16), ACT.Copy).then_inc(s["copied"], 1)

            @block.vector
            def _(dve):
                link = Chain(dve, s["chain"])
                tile = lambda t: t[:, :].rearrange("p (t i) -> p t i", t=NT)
                wide = mx[:, :].unsqueeze(2).broadcast_to([P, NT, G])
                dve.wait_ge(s["logits"], 1)
                for j in range(2):
                    link(nc.vector.tensor_copy(sc[:, sl(j)], k.ps[j][:, :]))
                link(nc.vector.tensor_reduce(mx[:, :], tile(sc), AX.X, ALU.max))
                nc.vector.tensor_tensor(tile(sc), tile(sc), wide, ALU.subtract).then_inc(s["shifted"], 1)
                dve.wait_ge(s["exps"], 1)
                link(nc.vector.tensor_reduce(mx[:, :], tile(sc), AX.X, ALU.add))
                link(nc.vector.reciprocal(mx[:, :], mx[:, :]))
                link(nc.vector.tensor_tensor(tile(sc), tile(sc), wide, ALU.mult))
                for i in range(NT):
                    ins = nc.vector.max(top[:, sl(i, 8)], sc[:, sl(i, G)])
                link(ins)
                for i in range(NT):
                    ins = nc.vector.match_replace(out=sel[:, sl(i, G)], in_to_replace=top[:, sl(i, 8)], in_values=sc[:, sl(i, G)], imm_value=-1.0)
                link(ins)
                link(nc.vector.scalar_tensor_tensor(out=sc[:, :], in0=sel[:, :], scalar=0.0, in1=sc[:, :], op0=ALU.is_lt, op1=ALU.mult))
                link(nc.vector.tensor_reduce(mx[:, :], tile(sc), AX.X, ALU.add))
                link(nc.vector.tensor_scalar(mx[:, :], mx[:, :], 1e-20, None, ALU.add))
                link(nc.vector.reciprocal(mx[:, :], mx[:, :]))
                link(nc.vector.tensor_tensor(tile(sc), tile(sc), wide, ALU.mult))
                hi, mid = tile(hm)[:, :, 0:G], tile(hm)[:, :, G:2 * G]
                link(nc.vector.tensor_copy(hi, tile(sc)))
                link(nc.vector.tensor_tensor(tile(sc), tile(sc), hi, ALU.subtract))
                link(nc.vector.tensor_copy(mid, tile(sc)))
                link(nc.vector.tensor_tensor(tile(sc), tile(sc), mid, ALU.subtract))
                nc.vector.tensor_copy(lo[:, :], sc[:, :]).then_inc(s["split"], 1)

        def spread(pw, j, b):
            nc.tensor.matmul(pw, ind[:, sl(j, P)], wt_hm[:, sl(b)], start=True, stop=False)
            return nc.tensor.matmul(pw, ind[0:G, sl(j, P)], wt_lo[:, sl(b)], start=False, stop=True)

        experts(nc, k, x, y, a, J, 32, spread)


def layer6(nc, k, x, y, a):
    HH, GH = 8, 4
    norm(nc, k, x, y, 1e-5)
    with ExitStack() as mem:
        sb = lambda n, w_, dt=F32: mem.enter_context(nc.sbuf_tensor(f"{n}_{nc.next_id()}", [P, w_], dt))
        g, beta, nbeta, gam, ngam, rest, tot = (sb(n, NT * HH) for n in ("g", "beta", "nbeta", "gam", "ngam", "rest", "tot"))
        delta_gates(nc, k, y, g, beta, nbeta, gam, ngam, rest, tot, HH)
        q, kk, v, z = (k.big[:, j * 8 * S:(j + 1) * 8 * S] for j in range(4))
        W = GH * P
        state, free = a[:, 0:HH * P], k.big[:, 32 * S:32 * S + 4 * W]
        bufs = {n: [sb(n, W) for _ in range(2)] for n in ("ea", "at", "nn", "vv", "kt")}
        bufs["mm"] = [a[:, HH * P + j * W:][:, 0:W] for j in range(2)]
        bufs["ex"] = [free[:, sl(j, W)] for j in range(2)]
        gs = [free[:, sl(2 + j, W)] for j in range(2)]
        small = {n: sb(n, 2 * GH) for n in ("ss", "rstd")}
        for b in range(B):
            delta_project(nc, k, y, b, z, bufs["ea"] + bufs["at"])
            delta_chunks(nc, k, x, b, q, kk, v, z, state, bufs, gs, small, g, beta, nbeta, gam, ngam, rest, tot, HH, GH)
    load_big(nc, k, "big2")


def delta_gates(nc, k, y, g, beta, nbeta, gam, ngam, rest, tot, HH):
    W = NT * HH
    with ExitStack() as mem, stage(nc, "ba shifted exps lns bexp aexp g_ready sums decays chain") as (block, s):
        sb = lambda n, w_: mem.enter_context(nc.sbuf_tensor(f"{n}_{nc.next_id()}", [P, w_], F32))
        bb, aa, t1, al = sb("bb", W), sb("aa", W), sb("t1", W), sb("al", HH)

        @block.tensor
        def _(pe):
            for i in range(NT):
                mm = nc.tensor.matmul(k.ps[0][:, sl(i, 2 * HH)], y[:, sl(i, P)], k.w["L2_attn_ba"], start=True, stop=True)
            mm.then_inc(s["ba"], 1)
            pe.wait_ge(s["g_ready"], 1)
            for j, w in enumerate((k.w["upto"], k.w["after"], k.ones)):
                mm = nc.tensor.matmul(k.ps[1][:, sl(j, P)], w, g[:, :], start=True, stop=True)
            mm.then_inc(s["sums"], 1)

        @block.scalar
        def _(act):
            nc.scalar.preload_act_table_set(LN_EXP)
            nc.scalar.activation(al[:, :], k.w["L2_attn_A_log"], ACT.Exp).then_inc(s["aexp"], 1)
            act.wait_ge(s["shifted"], 1)
            nc.scalar.activation(bb[:, :], bb[:, :], ACT.Exp).then_inc(s["bexp"], 1)
            nc.scalar.activation(t1[:, :], t1[:, :], ACT.Exp).then_inc(s["exps"], 1)
            act.wait_ge(s["exps"], 1)
            nc.scalar.activation(t1[:, :], t1[:, :], ACT.Ln, bias=k.ones[:, 0:1]).then_inc(s["lns"], 1)
            act.wait_ge(s["sums"], 1)
            for j, dst in enumerate((gam, rest, tot)):
                nc.scalar.activation(dst[:, :], k.ps[1][:, sl(j, P)], ACT.Exp).then_inc(s["decays"], 1)

        @block.vector
        def _(dve):
            link = Chain(dve, s["chain"])
            tile = lambda t: t[:, :].rearrange("p (t h) -> p t h", h=HH)
            ps = k.ps[0][:, 0:2 * W].rearrange("p (t h) -> p t h", h=2 * HH)
            wide = lambda c: c.unsqueeze(1).broadcast_to([P, NT, HH])
            dve.wait_ge(s["ba"], 1)
            link(nc.vector.tensor_scalar(tile(bb), ps[:, :, 0:HH], -1.0, 80.0, ALU.mult, ALU.min))
            link(nc.vector.tensor_tensor(tile(aa), ps[:, :, HH:2 * HH], wide(k.w["L2_attn_dt_bias"]), ALU.add))
            link(nc.vector.tensor_scalar(t1[:, :], aa[:, :], -1.0, None, ALU.mult))
            nc.vector.tensor_tensor(t1[:, :], t1[:, :], aa[:, :], ALU.min).then_inc(s["shifted"], 1)
            dve.wait_ge(s["bexp"], 1)
            link(nc.vector.tensor_scalar(bb[:, :], bb[:, :], 1.0, None, ALU.add))
            link(nc.vector.reciprocal(beta[:, :], bb[:, :]))
            link(nc.vector.tensor_scalar(nbeta[:, :], beta[:, :], -1.0, None, ALU.mult))
            dve.wait_ge(s["lns"], 1)
            dve.wait_ge(s["aexp"], 1)
            link(nc.vector.tensor_scalar(al[:, :], al[:, :], 3e38, -1.0, ALU.min, ALU.mult))
            link(nc.vector.scalar_tensor_tensor(out=aa[:, :], in0=aa[:, :], scalar=0.0, in1=t1[:, :], op0=ALU.max, op1=ALU.add))
            link(nc.vector.tensor_tensor(tile(aa), tile(aa), wide(al[:, :]), ALU.mult))
            nc.vector.tensor_scalar(g[:, :], aa[:, :], -200.0, None, ALU.max).then_inc(s["g_ready"], 1)
            dve.wait_ge(s["decays"], 3)
            link(nc.vector.tensor_scalar(ngam[:, :], gam[:, :], -1.0, None, ALU.mult))


def delta_project(nc, k, y, b, z, tapped):
    TAPS = 4
    with ExitStack() as mem, stage(nc, "raw scaled conv whole z_ps z_done chain") as (block, s):
        chans = 24
        zmm = 2 * TB

        @block.tensor
        def _(pe):
            for n in range(zmm):
                t, j = divmod(n, 2)
                after(pe, s["z_done"], n - 1)
                nc.tensor.matmul(k.ps[6 + n % 2][:, :], y[:, sl(b * TB + t, P)], k.w["L2_attn_z_w"][:, sl(j)], start=True, stop=True).then_inc(s["z_ps"], 1)
            for m in range(chans):
                after(pe, s["conv"], m - 5)
                nc.tensor.matmul(k.ps[m % 6][:, :], k.w["L2_attn_qkv_w"][:, sl(m, P)], y[:, sl(b)], start=True, stop=True).then_inc(s["raw"], 1)

        @block.scalar
        def _(act):
            for n in range(zmm):
                act.wait_ge(s["z_ps"], n + 1)
                nc.scalar.activation(z[:, sl(n)], k.ps[6 + n % 2][:, :], ACT.Silu).then_inc(s["z_done"], 1)
            for m in range(chans):
                act.wait_ge(s["raw"], m + 1)
                after(act, s["whole"], m - 3)
                for dst, tap in ((k.big[:, sl(m)], 3), (tapped[m % 4][:, :], 2)):
                    ins = nc.scalar.activation(dst, k.ps[m % 6][:, :], ACT.Copy, scale=k.w["L2_attn_conv"][:, m * TAPS + tap:m * TAPS + tap + 1])
                ins.then_inc(s["scaled"], 1)
            act.wait_ge(s["z_done"], zmm)

        @block.vector
        def _(dve):
            link = Chain(dve, s["chain"])
            for m in range(chans):
                dve.wait_ge(s["scaled"], m + 1)
                for back in range(2, TAPS):
                    dst = k.big[:, m * S + back:(m + 1) * S]
                    tap = m * TAPS + 3 - back
                    ins = nc.vector.scalar_tensor_tensor(out=dst, in0=k.ps[m % 6][:, 0:S - back], scalar=k.w["L2_attn_conv"][:, tap:tap + 1],
                                                         in1=dst, op0=ALU.mult, op1=ALU.add)
                    if back < TAPS - 1:
                        link(ins)
                ins.then_inc(s["conv"], 1)
            dve.wait_ge(s["conv"], chans)

        @block.gpsimd
        def _(pool):
            for m in range(chans):
                dst = k.big[:, m * S + 1:(m + 1) * S]
                pool.wait_ge(s["scaled"], m + 1)
                pool.wait_ge(s["conv"], m + 1)
                nc.gpsimd.tensor_tensor(dst, dst, tapped[m % 4][:, 0:S - 1], ALU.add).then_inc(s["whole"], 1)
            pool.wait_ge(s["whole"], chans)


def delta_chunks(nc, k, x, b, q, kk, v, z, state, bufs, gs, small, g, beta, nbeta, gam, ngam, rest, tot, HH, GH):
    LEVELS = 7
    PAIRS, TURNS, INVERT, CARRY = 0, 4, 5, 17
    SOLVE, OUTPUT, SQUARES, NORM, TURN_O, PROJECT = 18, 19, 20, 21, 22, 23
    PHASES, PERIOD = 24, 20
    names = ("gs pairs logs started z_scaled ed eds at apt vk_turned vk_copied ap_turned init from_state r_ready "
             "qs_copied w us_ready outs o_ready s_done inv normed o_turned o_copied proj added chain achain " + " ".join(f"{n}_{gr}" for n in ("y", "y_copied", "m_part", "mn", "mn_new") for gr in range(2)))
    with stage(nc, names) as (block, s):
        heads4 = lambda t: t.rearrange("p (h e) -> p h e", h=GH)
        each = lambda t, c, gr: t[:, (b * TB + c) * HH + gr * GH:][:, 0:GH].unsqueeze(2).broadcast_to([P, GH, P])
        one = lambda t, c, gr, h: t[:, (b * TB + c) * HH + gr * GH + h:][:, 0:1]
        bank = lambda gr, j: k.ps[4 * gr + j]
        seg = lambda t, c, gr, h: t[:, (gr * GH + h) * S + c * P:][:, 0:P]
        head = lambda n, gr, h: bufs[n][gr][:, sl(h, P)]
        buf = lambda n, gr: bufs[n][gr][:, :]
        st = lambda gr, h: state[:, sl(gr * GH + h, P)]
        wide = lambda m: m.unsqueeze(1).broadcast_to([P, GH, P])
        hs = range(GH)
        nth = lambda c, gr: 2 * c + gr + 1
        level = lambda c, lv: c * (LEVELS - 1) + lv
        m_level = lambda c, lv: c * (LEVELS - 2) + lv
        carried = lambda c, gr: 2 * (c - 1) + gr + 1

        def steps():
            for slot in range((TB - 1) * PERIOD + PHASES):
                for c, gr in [(c, gr) for c in range(TB) for gr in range(2)]:
                    phase = slot - c * PERIOD
                    if 0 <= phase < PHASES:
                        lv, second = divmod(phase - INVERT, 2)
                        yield c, gr, phase, lv + 1 if INVERT <= phase < CARRY else 0, second

        @block.gpsimd
        def _(pool):
            def decays(c, gr):
                nc.gpsimd.tensor_tensor(heads4(gs[gr][:, :]), wide(k.w["after"]), each(g, c, gr), ALU.mult).then_inc(s["gs"], 1)

            for gr in range(2):
                decays(0, gr)
            for c, gr, phase, lv, second in steps():
                if phase == PAIRS:
                    pool.wait_ge(s["ed"], nth(c, gr))
                    after(pool, s["o_ready"], nth(c - 1, gr))
                    nc.gpsimd.tensor_tensor(heads4(buf("ea", gr)), heads4(buf("ex", gr)), each(nbeta, c, gr), ALU.mult).then_inc(s["eds"], 1)
                elif phase == INVERT:
                    gate = heads4(z[:, (2 * c + gr) * S:(2 * c + gr + 1) * S])
                    nc.gpsimd.tensor_tensor(gate, gate, wide(k.w["L2_attn_norm_w"]), ALU.mult).then_inc(s["z_scaled"], 1)
                elif phase == PAIRS + 3 and c < TB - 1:
                    pool.wait_ge(s["logs"], nth(c, gr))
                    decays(c + 1, gr)

        @block.tensor
        def _(pe):
            mm4 = lambda out, left, right: [nc.tensor.matmul(out[:, sl(h, P)], left(h), right(h), start=True, stop=True) for h in hs][-1]
            turn4 = lambda out, src: [nc.tensor.transpose(out[:, sl(h, P)], src(h), k.ident) for h in hs][-1]
            for c, gr, phase, lv, second in steps():
                if phase == PAIRS:
                    pe.wait_ge(s["gs"], nth(c, gr))
                    after(pe, s["s_done"], nth(c - 1, gr))
                    for h in hs:
                        nc.tensor.matmul(bank(gr, 2)[:, sl(h, P)], gs[gr][:, sl(h, P)], k.w["upto"], start=True, stop=False)
                        mm = nc.tensor.matmul(bank(gr, 2)[:, sl(h, P)], k.ident_bf, k.cut[:, :], start=False, stop=True)
                    mm.then_inc(s["logs"], 1)
                    mm4(bank(gr, 0), lambda h: seg(kk, c, gr, h), lambda h: seg(kk, c, gr, h))
                    mm4(bank(gr, 1), lambda h: seg(kk, c, gr, h), lambda h: seg(q, c, gr, h)).then_inc(s["pairs"], 1)
                elif phase == TURNS:
                    after(pe, s["added"], nth(c - 1, gr))
                    pe.wait_ge(s["ed"], nth(c, gr))
                    turn4(bank(gr, 3), lambda h: seg(v, c, gr, h))
                    turn4(bank(gr, 2), lambda h: seg(kk, c, gr, h)).then_inc(s["vk_turned"], 1)
                    pe.wait_ge(s["apt"], nth(c, gr))
                    turn4(bank(gr, 0), lambda h: head("ea", gr, h)).then_inc(s["ap_turned"], 1)
                elif lv and not second:
                    if lv == 1:
                        pe.wait_ge(s["init"], nth(c, gr))
                        pe.wait_ge(s["vk_copied"], nth(c, gr))
                    else:
                        pe.wait_ge(s[f"mn_new_{gr}"], level(c, lv - 1))
                    mm4(bank(gr, 1), lambda h: head("ea", gr, h), lambda h: head("mm", gr, h)).then_inc(s[f"y_{gr}"], 1)
                elif lv:
                    pe.wait_ge(s[f"y_copied_{gr}"], level(c, lv))
                    if lv < LEVELS - 1:
                        mm4(bank(gr, 2), lambda h: head("nn", gr, h), lambda h: head("ex", gr, h)).then_inc(s[f"m_part_{gr}"], 1)
                    mm4(bank(gr, 3), lambda h: head("ex", gr, h), lambda h: head("nn", gr, h)).then_inc(s[f"mn_{gr}"], 1)
                elif phase == CARRY and c:
                    pe.wait_ge(s["s_done"], nth(c - 1, gr))
                    mm4(bank(gr, 0), lambda h: seg(kk, c, gr, h), lambda h: st(gr, h))
                    mm4(bank(gr, 1), lambda h: seg(q, c, gr, h), lambda h: st(gr, h)).then_inc(s["from_state"], 1)
                elif phase == SOLVE:
                    pe.wait_ge(s[f"mn_new_{gr}"], level(c, LEVELS - 1))
                    if c:
                        pe.wait_ge(s["r_ready"], carried(c, gr))
                    mm4(bank(gr, 2), lambda h: head("nn", gr, h), lambda h: head("vv", gr, h)).then_inc(s["w"], 1)
                elif phase == OUTPUT:
                    pe.wait_ge(s["us_ready"], nth(c, gr))
                    mm = mm4(bank(gr, 3), lambda h: head("at", gr, h), lambda h: head("mm", gr, h))
                    if c < TB - 1:
                        mm = mm4(bank(gr, 0), lambda h: head("kt", gr, h), lambda h: head("ex", gr, h))
                    mm.then_inc(s["outs"], 1)
                elif phase == TURN_O:
                    pe.wait_ge(s["normed"], nth(c, gr))
                    turn4(bank(gr, 3), lambda h: head("kt", gr, h)).then_inc(s["o_turned"], 1)
                elif phase == PROJECT:
                    pe.wait_ge(s["o_copied"], nth(c, gr))
                    for h in hs:
                        mm = nc.tensor.matmul(bank(gr, 3)[:, 0:P], k.w["L2_attn_out_w"][:, sl(gr * GH + h, P)], head("vv", gr, h),
                                              start=h == 0, stop=h == GH - 1)
                    mm.then_inc(s["proj"], 1)

        @block.scalar
        def _(act):
            alink = Chain(act, s["achain"])
            nc.scalar.preload_act_table_set(LN_EXP)
            for c, gr, phase, lv, second in steps():
                if phase == PAIRS:
                    act.wait_ge(s["logs"], nth(c, gr))
                    nc.scalar.activation(buf("ex", gr), bank(gr, 2)[:, :], ACT.Exp).then_inc(s["ed"], 1)
                elif phase == PAIRS + 1:
                    after(act, s["inv"], nth(c - 1, gr))
                    for n in ("nn", "mm"):
                        ins = nc.scalar.activation(heads4(buf(n, gr)), wide(k.ident), ACT.Copy)
                    ins.then_inc(s["started"], 1)
                elif phase == TURNS:
                    act.wait_ge(s["vk_turned"], nth(c, gr))
                    nc.scalar.activation(buf("vv", gr), bank(gr, 3)[:, :], ACT.Copy)
                    nc.scalar.activation(buf("kt", gr), bank(gr, 2)[:, :], ACT.Copy).then_inc(s["vk_copied"], 1)
                elif lv and not second:
                    act.wait_ge(s[f"y_{gr}"], level(c, lv))
                    nc.scalar.activation(buf("ex", gr), bank(gr, 1)[:, :], ACT.Copy).then_inc(s[f"y_copied_{gr}"], 1)
                elif phase == CARRY and c:
                    act.wait_ge(s["from_state"], carried(c, gr))
                    act.wait_ge(s[f"mn_{gr}"], level(c, LEVELS - 1))
                    for h in hs:
                        ins = nc.scalar.activation(head("ea", gr, h), bank(gr, 1)[:, sl(h, P)], ACT.Copy, scale=one(gam, c, gr, h))
                    ins.then_inc(s["qs_copied"], 1)
                elif phase == SQUARES:
                    act.wait_ge(s["o_ready"], nth(c, gr))
                    ss, rstd = small["ss"][:, sl(gr, GH)], small["rstd"][:, sl(gr, GH)]
                    for h in hs:
                        ins = nc.scalar.activation(head("mm", gr, h), head("kt", gr, h), ACT.Square, accum_out=ss[:, h:h + 1])
                    alink(ins)
                    alink(nc.scalar.activation(ss, ss, ACT.Ln, scale=1.0 / P, bias=k.eps[1e-6]))
                    nc.scalar.activation(rstd, ss, ACT.Exp, scale=-0.5).then_inc(s["inv"], 1)
                elif phase == TURN_O:
                    act.wait_ge(s["o_turned"], nth(c, gr))
                    nc.scalar.activation(buf("vv", gr), bank(gr, 3)[:, :], ACT.Copy).then_inc(s["o_copied"], 1)

        @block.vector
        def _(dve):
            link = Chain(dve, s["chain"])

            def add(c, gr):
                xs = x[:, sl(b * TB + c, P)]
                dve.wait_ge(s["proj"], nth(c, gr))
                if gr:
                    dve.wait_ge(s["added"], nth(c, 0))
                nc.vector.tensor_tensor(xs, xs, bank(gr, 3)[:, 0:P], ALU.add).then_inc(s["added"], 1)

            for c, gr, phase, lv, second in steps():
                if phase == PAIRS + 1:
                    dve.wait_ge(s["pairs"], nth(c, gr))
                    dve.wait_ge(s["ed"], nth(c, gr))
                    nc.vector.tensor_tensor(buf("at", gr), buf("ex", gr), bank(gr, 1)[:, :], ALU.mult).then_inc(s["at"], 1)
                elif phase == PAIRS + 2:
                    dve.wait_ge(s["eds"], nth(c, gr))
                    nc.vector.tensor_tensor(buf("ea", gr), buf("ea", gr), bank(gr, 0)[:, :], ALU.mult).then_inc(s["apt"], 1)
                elif phase == PAIRS + 3:
                    dve.wait_ge(s["apt"], nth(c, gr))
                    dve.wait_ge(s["started"], nth(c, gr))
                    link(nc.vector.copy_predicated(heads4(buf("nn", gr)), wide(k.level_masks[:, sl(LEVELS, P)]), heads4(buf("ea", gr))))
                elif phase == TURNS:
                    if c:
                        add(c - 1, gr)
                    dve.wait_ge(s["ap_turned"], nth(c, gr))
                    nc.vector.copy_predicated(heads4(buf("mm", gr)), wide(k.level_masks[:, sl(0, P)]), heads4(bank(gr, 0)[:, :])).then_inc(s["init"], 1)
                elif lv and second:
                    if lv < LEVELS - 1:
                        dve.wait_ge(s[f"m_part_{gr}"], m_level(c, lv))
                        nc.vector.copy_predicated(heads4(buf("mm", gr)), wide(k.level_masks[:, sl(lv, P)]), heads4(bank(gr, 2)[:, :]))
                    dve.wait_ge(s[f"mn_{gr}"], level(c, lv))
                    nc.vector.copy_predicated(heads4(buf("nn", gr)), wide(k.level_masks[:, sl(LEVELS + lv, P)]), heads4(bank(gr, 3)[:, :])).then_inc(s[f"mn_new_{gr}"], 1)
                elif phase == CARRY and c:
                    dve.wait_ge(s["from_state"], carried(c, gr))
                    dve.wait_ge(s["vk_copied"], nth(c, gr))
                    for h in hs:
                        ins = nc.vector.scalar_tensor_tensor(out=head("vv", gr, h), in0=bank(gr, 0)[:, sl(h, P)], scalar=one(ngam, c, gr, h),
                                                             in1=head("vv", gr, h), op0=ALU.mult, op1=ALU.add)
                    ins.then_inc(s["r_ready"], 1)
                elif phase == SOLVE:
                    dve.wait_ge(s["w"], nth(c, gr))
                    link(nc.vector.tensor_tensor(heads4(buf("mm", gr)), heads4(bank(gr, 2)[:, :]), each(beta, c, gr), ALU.mult))
                    nc.vector.tensor_tensor(heads4(buf("ex", gr)), heads4(buf("mm", gr)), each(rest, c, gr), ALU.mult).then_inc(s["us_ready"], 1)
                elif phase == OUTPUT:
                    dve.wait_ge(s["outs"], nth(c, gr))
                    if c:
                        dve.wait_ge(s["qs_copied"], carried(c, gr))
                        nc.vector.tensor_tensor(buf("kt", gr), buf("ea", gr), bank(gr, 3)[:, :], ALU.add).then_inc(s["o_ready"], 1)
                    else:
                        nc.vector.tensor_copy(buf("kt", gr), bank(gr, 3)[:, :]).then_inc(s["o_ready"], 1)
                    if c == 0:
                        nc.vector.tensor_copy(state[:, gr * GH * P:(gr + 1) * GH * P], bank(gr, 0)[:, :]).then_inc(s["s_done"], 1)
                    elif c < TB - 1:
                        for h in hs:
                            ins = nc.vector.scalar_tensor_tensor(out=st(gr, h), in0=st(gr, h), scalar=one(tot, c, gr, h),
                                                                 in1=bank(gr, 0)[:, sl(h, P)], op0=ALU.mult, op1=ALU.add)
                        ins.then_inc(s["s_done"], 1)
                elif phase == NORM:
                    dve.wait_ge(s["inv"], nth(c, gr))
                    rstd = small["rstd"][:, sl(gr, GH)].unsqueeze(2).broadcast_to([P, GH, P])
                    link(nc.vector.tensor_tensor(heads4(buf("kt", gr)), heads4(buf("kt", gr)), rstd, ALU.mult))
                    dve.wait_ge(s["z_scaled"], nth(c, gr))
                    nc.vector.tensor_tensor(buf("kt", gr), buf("kt", gr), z[:, (2 * c + gr) * S:(2 * c + gr + 1) * S], ALU.mult).then_inc(s["normed"], 1)
                elif phase == PROJECT and c == TB - 1:
                    add(c, gr)
            dve.wait_ge(s["added"], 2 * TB)


def layer9(nc, k, x, y, a):
    norm(nc, k, x, y, 1e-5)
    q, kk = k.big[:, 0:T], k.big[:, T:2 * T]
    qh = [k.big[:, (2 + j) * T:(3 + j) * T] for j in range(2)]
    project(nc, k, [(k.w["L3_attn_W" + n], y, T, dst, k.w["L3_attn_b" + n], scale) for n, dst, scale in (("q", q, -HD ** -0.5), ("k", kk, 1.0))])
    with ExitStack() as mem:
        sb = lambda n, w_, dt=F32: mem.enter_context(nc.sbuf_tensor(f"{n}_{nc.next_id()}", [P, w_], dt))
        v = a
        with stage(nc, "rows done") as (block, s):
            @block.tensor
            def _(pe):
                for b in range(B):
                    for t in range(TB):
                        mm = nc.tensor.matmul(k.ps[b][:, sl(t, P)], y[:, sl(b * TB + t, P)], k.w["L3_attn_Wv"], start=True, stop=True)
                    mm.then_inc(s["rows"], 1)

            @block.vector
            def _(dve):
                tiles = lambda t: t.rearrange("p (t e) -> p t e", t=TB)
                for b in range(B):
                    dve.wait_ge(s["rows"], b + 1)
                    nc.vector.tensor_tensor(tiles(v[:, sl(b)]), tiles(k.ps[b][:, :]), k.w["L3_attn_bv"].unsqueeze(1).broadcast_to([P, TB, P]),
                                            ALU.add).then_inc(s["done"], 1)
                dve.wait_ge(s["done"], B)

        o = y
        units = [(b, i, h) for b in range(B) for i in range(TB) for h in range(H)]
        N, PER = len(units), TB * H
        TURN, COPY, ATTEND, PW, PT = 4, 5, 7, 6, 4
        low, tot, pw, pt = sb("low", 8), sb("tot", 8), sb("pw", PW * S), sb("pt", PT * S)
        vs = [sb("vs", TB * H * 32) for _ in range(2)]
        with stage(nc, "zeroed spread heads scores least weights inverted scaled turned copied_a copied_v values out") as (block, s):
            width = lambda u: (units[u][1] + 1) * P
            weights = lambda u: pw[:, (u % PW) * S:(u % PW) * S + width(u)]
            turned = lambda u: pt[:, (u % PT) * S:(u % PT) * S + width(u)]
            one = lambda t, u: t[:, u % 8:u % 8 + 1]

            def copy(eng, u, sem, op):
                eng.wait_ge(s["turned"], u + 1)
                after(eng, s["values"], u - PT + 1)
                op(turned(u), k.ps[3 + u % 3][:, 0:width(u)]).then_inc(sem, 1)

            @block.tensor
            def _(pe):
                def copied(u):
                    pe.wait_ge(s["copied_v"] if u % 2 else s["copied_a"], u // 2 + 1)

                def turn(u):
                    pe.wait_ge(s["scaled"], u + 1)
                    if u >= 3:
                        copied(u - 3)
                    for c in range(units[u][1] + 1):
                        mm = nc.tensor.transpose(k.ps[3 + u % 3][:, sl(c, P)], weights(u)[:, sl(c, P)], k.ident)
                    mm.then_inc(s["turned"], 1)

                def attend(u):
                    b, i, h = units[u]
                    copied(u)
                    if h == 0:
                        after(pe, s["out"], u // H - 1)
                        pe.wait_ge(s["spread"], 4 * (b + 1))
                    g, j = divmod(h, 4)
                    for c in range(i + 1):
                        mm = nc.tensor.matmul(k.ps[6 + (u // H) % 2][sl(g, 32), 0:P], vs[b % 2][:, sl(c * H + h, 32)], turned(u)[:, sl(c, P)],
                                              start=c == 0 and j == 0, stop=c == i and j == 3)
                    mm.then_inc(s["values"], 1)

                for u in range(N + ATTEND):
                    if u < N:
                        b, i, h = units[u]
                        w = width(u)
                        if h == 0:
                            pe.wait_ge(s["heads"], u // H + 1)
                        after(pe, s["weights"], u - 2)
                        nc.tensor.matmul(k.ps[u % 3][:, 0:w], qh[(u // H) % 2][:, sl(h, P)], kk[:, b * S:][:, 0:w], start=True, stop=False)
                        nc.tensor.matmul(k.ps[u % 3][:, w - P:w], k.ident_bf, k.later[:, :], start=False, stop=True).then_inc(s["scores"], 1)
                    if TURN <= u < N + TURN:
                        turn(u - TURN)
                    if u >= ATTEND:
                        attend(u - ATTEND)

            @block.scalar
            def _(act):
                for u in range(N + COPY):
                    if u < N:
                        act.wait_ge(s["least"], u + 1)
                        after(act, s["turned"], u - PW + 1)
                        after(act, s["inverted"], u - 7)
                        nc.scalar.activation(weights(u), k.ps[u % 3][:, 0:width(u)], ACT.Exp, scale=-1.0, bias=one(low, u),
                                             accum_out=one(tot, u)).then_inc(s["weights"], 1)
                    if u >= COPY and (u - COPY) % 2 == 0:
                        copy(act, u - COPY, s["copied_a"], lambda dst, src: nc.scalar.activation(dst, src, ACT.Copy))

            @block.gpsimd
            def _(pool):
                def spread(b):
                    after(pool, s["values"], (b - 1) * PER)
                    for j in range(4):
                        dst = vs[b % 2][:, :].rearrange("p (t g j q e) -> p t g j q e", t=TB, g=4, j=4, q=4)
                        src = v[:, sl(b)].rearrange("p (t g j e) -> p t g j e", t=TB, g=4, j=4)
                        nc.gpsimd.tensor_copy(dst[:, :, :, j, j, :], src[:, :, :, j, :]).then_inc(s["spread"], 1)

                pool.wait_ge(s["zeroed"], 2)
                spread(0)
                for n in range(NT):
                    after(pool, s["scores"], (n - 1) * H)
                    nc.gpsimd.tensor_tensor(qh[n % 2].rearrange("p (h e) -> p h e", h=H), q[:, sl(n, P)].unsqueeze(1).broadcast_to([P, H, P]),
                                            k.w["head_cols"].unsqueeze(2).broadcast_to([P, H, P]), ALU.mult).then_inc(s["heads"], 1)
                    if n % TB == 2 and n // TB < B - 1:
                        spread(n // TB + 1)

            @block.vector
            def _(dve):
                for j in range(2):
                    nc.vector.memset(vs[j][:, :], 0.0).then_inc(s["zeroed"], 1)
                for u in range(N + ATTEND + 2):
                    if u < N:
                        dve.wait_ge(s["scores"], u + 1)
                        after(dve, s["weights"], u - 7)
                        nc.vector.tensor_reduce(one(low, u), k.ps[u % 3][:, 0:width(u)], AX.X, ALU.min).then_inc(s["least"], 1)
                    if 2 <= u < N + 2:
                        dve.wait_ge(s["weights"], u - 1)
                        nc.vector.reciprocal(one(tot, u - 2), one(tot, u - 2)).then_inc(s["inverted"], 1)
                        dve.wait_ge(s["inverted"], u - 1)
                        nc.vector.tensor_scalar(weights(u - 2), weights(u - 2), one(tot, u - 2), None, ALU.mult).then_inc(s["scaled"], 1)
                    if COPY <= u < N + COPY and (u - COPY) % 2 == 1:
                        copy(dve, u - COPY, s["copied_v"], lambda dst, src: nc.vector.tensor_copy(dst, src))
                    if u >= ATTEND + H and (u - ATTEND) % H == 1:
                        i = (u - ATTEND) // H - 1
                        dve.wait_ge(s["values"], (i + 1) * H)
                        nc.vector.tensor_copy(o[:, sl(i, P)], k.ps[6 + i % 2][:, 0:P]).then_inc(s["out"], 1)
                dve.wait_ge(s["out"], NT)

        with stage(nc, "proj done") as (block, s):
            @block.tensor
            def _(pe):
                for b in range(B):
                    nc.tensor.matmul(k.ps[4 + b][:, :], k.w["L3_attn_Wo"], o[:, sl(b)], start=True, stop=True).then_inc(s["proj"], 1)

            @block.scalar
            def _(act):
                for b in range(B):
                    act.wait_ge(s["proj"], b + 1)
                    nc.scalar.activation(a[:, sl(b)], k.ps[4 + b][:, :], ACT.Identity, bias=k.w["L3_attn_bo"]).then_inc(s["done"], 1)
                act.wait_ge(s["done"], B)
    norm(nc, k, a, y, 1e-5, scaled=(k.w["L3_attn_gamma"], k.w["L3_attn_beta"]), onto=x)


def layer11(nc, k, x, y, a):
    F, R, K, CAND, ROUNDS = 1536, 32, 512, 32, 6
    C = F // P
    norm(nc, k, x, y, 1e-5)
    wm, wp = k.big[:, 0:F], k.big[:, F:2 * F]
    per_step = "up act down out pooled r_ps r scores shifted exps counts reached turned count total decided".split()
    with ExitStack() as mem:
        sb = lambda n, w_, dt=F32, p=P: mem.enter_context(nc.sbuf_tensor(f"{n}_{nc.next_id()}", [p, w_], dt))
        active, new, history, both = (sb(n, C * B) for n in ("active", "new", "history", "both"))
        pooled, r1 = sb("pooled", B), sb("r1", P, F32, R)
        seen = sb("seen", 2)
        going = sb("going", 1, I32)
        h = sb("h", 2 * S)
        with stage(nc, "chain") as (block, s):
            @block.vector
            def _(dve):
                link = Chain(dve, s["chain"])
                for t in (active, history):
                    link(nc.vector.memset(t[:, :], 0.0))
                    link(nc.vector.memset(t[:, 0:K // P * B], 1.0))

        p, m, eq, cum = sb("p", F), sb("m", F), sb("eq", F), sb("cum", F)
        c1, c2, hit = sb("c1", 1), sb("c2", 1), sb("hit", 1)
        base, trial, digit = sb("base", 1, I32), sb("trial", 1, I32), sb("digit", 1, I32)

        def map_pe(pe, s, blocks):
            N = B * blocks

            def down(n):
                b, c = divmod(n, blocks)
                pe.wait_ge(s["act"], n + 1)
                if c == 0:
                    after(pe, s["out"], b - 1)
                nc.tensor.matmul(k.ps[4 + b % 2][:, :], wp[:, sl(c, P)], h[:, sl(n % 2)], start=c == 0, stop=c == blocks - 1).then_inc(s["down"], 1)

            for n in range(N):
                after(pe, s["act"], n - 3)
                nc.tensor.matmul(k.ps[n % 4][:, :], wm[:, sl(n % blocks, P)], y[:, sl(n // blocks)], start=True, stop=True).then_inc(s["up"], 1)
                if n:
                    down(n - 1)
            down(N - 1)

        def map_act(act, s, blocks):
            for n in range(B * blocks):
                b, c = divmod(n, blocks)
                act.wait_ge(s["up"], n + 1)
                after(act, s["down"], n - 1)
                nc.scalar.activation(h[:, sl(n % 2)], k.ps[n % 4][:, :], ACT.Relu, scale=active[:, c * B + b:c * B + b + 1]).then_inc(s["act"], 1)

        def map_dve(dve, s, link, blocks):
            for b in range(B):
                dve.wait_ge(s["down"], blocks * (b + 1))
                nc.vector.tensor_scalar(a[:, sl(b)], k.ps[4 + b % 2][:, :], 1.0, None, ALU.mult, ALU.add, accum_out=pooled[:, b:b + 1]).then_inc(s["out"], 1)
            dve.wait_ge(s["out"], B)
            nc.vector.tensor_scalar(pooled[:, :], pooled[:, :], 1.0 / S, None, ALU.mult).then_inc(s["pooled"], 1)

        def choose_pe(pe, s):
            pe.wait_ge(s["pooled"], 1)
            nc.tensor.matmul(k.ps[6][0:R, 0:B], k.w["L3_ffn_Wc1"], pooled[:, :], start=True, stop=True).then_inc(s["r_ps"], 1)
            pe.wait_ge(s["r"], 1)
            for j in range(3):
                mm = nc.tensor.matmul(k.ps[j][:, :], r1[:, :], k.big[0:R, 2 * F + j * S:2 * F + (j + 1) * S], start=True, stop=True)
            mm.then_inc(s["scores"], 1)
            for n in range(ROUNDS):
                pe.wait_ge(s["counts"], n + 1)
                nc.tensor.matmul(k.ps[7][:, 0:1], k.w["same_batch"], hit[:, :], start=True, stop=True).then_inc(s["reached"], 1)
            pe.wait_ge(s["counts"], ROUNDS + 1)
            for c in range(C):
                mm = nc.tensor.transpose(k.ps[3 + c // 4][:, sl(c % 4, P)], m[:, sl(c, P)], k.ident)
            mm.then_inc(s["turned"], 1)
            pe.wait_ge(s["count"], 1)
            nc.tensor.matmul(k.ps[0][:, 0:1], k.ones, seen[:, 0:1], start=True, stop=True).then_inc(s["total"], 1)

        def choose_act(act, s):
            act.wait_ge(s["shifted"], 1)
            nc.scalar.activation(p[:, :], p[:, :], ACT.Exp).then_inc(s["exps"], 1)

        def choose_dve(dve, s, link):
            dve.wait_ge(s["r_ps"], 1)
            nc.vector.tensor_scalar(r1[:, :].rearrange("r (b c) -> r b c", b=B), k.ps[6][0:R, 0:B].unsqueeze(2).broadcast_to([R, B, CAND]),
                                    0.0, None, ALU.max).then_inc(s["r"], 1)
            dve.wait_ge(s["scores"], 1)
            for j in range(3):
                link(nc.vector.tensor_copy(p[:, sl(j)], k.ps[j][:, :]))
            link(nc.vector.tensor_reduce(c1[:, :], p[:, :], AX.X, ALU.max))
            nc.vector.tensor_scalar(p[:, :], p[:, :], c1[:, :], None, ALU.subtract).then_inc(s["shifted"], 1)
            dve.wait_ge(s["exps"], 1)
            link(nc.vector.tensor_reduce(c1[:, :], p[:, :], AX.X, ALU.add))
            link(nc.vector.reciprocal(c1[:, :], c1[:, :]))
            link(nc.vector.tensor_scalar(p[:, :], p[:, :], c1[:, :], None, ALU.mult))
            link(nc.vector.memset(base[:, :], 0))
            for n in range(ROUNDS):
                link(nc.vector.tensor_tensor(trial[:, :], base[:, :], k.candidate[:, n:n + 1], ALU.bitwise_or))
                link(nc.vector.tensor_scalar(m[:, :], p[:, :], trial[:, :].bitcast(F32), None, ALU.is_ge, ALU.add, accum_out=c1[:, :]))
                nc.vector.tensor_scalar(hit[:, :], c1[:, :], float(K), None, ALU.is_ge).then_inc(s["counts"], 1)
                dve.wait_ge(s["reached"], n + 1)
                link(nc.vector.tensor_scalar(digit[:, :], k.ps[7][:, 0:1], 1.0, None, ALU.subtract))
                link(nc.vector.tensor_scalar(digit[:, :], digit[:, :], 25 - 5 * n, None, ALU.logical_shift_left))
                link(nc.vector.tensor_tensor(base[:, :], base[:, :], digit[:, :], ALU.bitwise_or))
            kth = base[:, :].bitcast(F32)
            link(nc.vector.tensor_scalar(m[:, :], p[:, :], kth, None, ALU.is_gt, ALU.add, accum_out=c1[:, :]))
            link(nc.vector.tensor_scalar(c2[:, :], c1[:, :], -1.0, float(K), ALU.mult, ALU.add))
            link(nc.vector.tensor_scalar(eq[:, :], p[:, :], kth, None, ALU.is_equal))
            link(nc.vector.tensor_tensor_scan(cum[:, :], k.ones[:, 0:1].broadcast_to([P, F]), eq[:, :], 0.0, ALU.mult, ALU.add))
            link(nc.vector.scalar_tensor_tensor(out=eq[:, :], in0=cum[:, :], scalar=c2[:, :], in1=eq[:, :], op0=ALU.is_le, op1=ALU.mult))
            nc.vector.tensor_tensor(m[:, :], m[:, :], eq[:, :], ALU.add).then_inc(s["counts"], 1)
            dve.wait_ge(s["turned"], 1)
            for j in range(3):
                link(nc.vector.tensor_copy(new[:, sl(j, 4 * B)].rearrange("p (c b) -> p c b", c=4),
                                           k.ps[3 + j][:, :].rearrange("p (c b r) -> p c b r", c=4, b=B)[:, :, :, 0]))
            link(nc.vector.tensor_tensor(both[:, :], history[:, :], new[:, :], ALU.max))
            link(nc.vector.tensor_tensor(history[:, :], both[:, :], history[:, :], ALU.subtract))
            link(nc.vector.tensor_reduce(seen[:, 0:1], history[:, :], AX.X, ALU.add))
            link(nc.vector.tensor_scalar(seen[:, 0:1], seen[:, 0:1], 1.0 / (B * K), None, ALU.mult))
            nc.vector.tensor_copy(history[:, :], both[:, :]).then_inc(s["count"], 1)
            link(nc.vector.tensor_copy(active[:, :], new[:, :]))
            link(nc.vector.tensor_copy(y[:, :], a[:, :]))
            dve.wait_ge(s["total"], 1)
            nc.vector.tensor_scalar(going[:, :], k.ps[0][:, 0:1], 0.7, None, ALU.is_ge).then_inc(s["decided"], 1)

        with stage(nc, " ".join(per_step) + " chain") as (block, s):
            @block.tensor
            def _(pe):
                pe.wait_ge(k.big_loaded, 48)
                map_pe(pe, s, K // P)
                choose_pe(pe, s)

            @block.scalar
            def _(act):
                map_act(act, s, K // P)
                choose_act(act, s)

            @block.vector
            def _(dve):
                link = Chain(dve, s["chain"])
                map_dve(dve, s, link, K // P)
                choose_dve(dve, s, link)
                dve.wait_ge(s["decided"], 1)

        with stage(nc, " ".join(f"{n}_{i}" for i in (2, 3) for n in per_step) + " chain") as (block, s):
            second, third = ({n: s[f"{n}_{i}"] for n in per_step} for i in (2, 3))
            flag = going[0:1, 0:1]

            @block.tensor
            def _(pe):
                with pe.If(pe.value_load(flag, min_val=0, max_val=1) == 1):
                    map_pe(pe, second, C)
                    choose_pe(pe, second)
                    pe.wait_ge(second["decided"], 1)
                    with pe.If(pe.value_load(flag, min_val=0, max_val=1) == 1):
                        map_pe(pe, third, C)

            @block.scalar
            def _(act):
                with act.If(act.value_load(flag, min_val=0, max_val=1) == 1):
                    map_act(act, second, C)
                    choose_act(act, second)
                    act.wait_ge(second["decided"], 1)
                    with act.If(act.value_load(flag, min_val=0, max_val=1) == 1):
                        map_act(act, third, C)

            @block.vector
            def _(dve):
                link = Chain(dve, s["chain"])
                with dve.If(dve.value_load(flag, min_val=0, max_val=1) == 1):
                    map_dve(dve, second, link, C)
                    choose_dve(dve, second, link)
                    dve.wait_ge(second["decided"], 1)
                    with dve.If(dve.value_load(flag, min_val=0, max_val=1) == 1):
                        map_dve(dve, third, link, C)
                        link(nc.vector.tensor_copy(y[:, :], a[:, :]))
                        dve.wait_ge(third["pooled"], 1)
    with stage(nc, "chain") as (block, s):
        @block.vector
        def _(dve):
            link = Chain(dve, s["chain"])
            link(nc.vector.tensor_tensor(x[:, :], x[:, :], y[:, :], ALU.add))


def program(nc, ap, out, cols, first, last):
    with ExitStack() as mem:
        sb = lambda n, w, dt=F32, p=P: mem.enter_context(nc.sbuf_tensor(n, [p, w], dt))
        k = Kit()
        k.w = {}
        stored = nc.alloc_semaphore("stored")
        k.ps = [mem.enter_context(nc.psum_tensor(f"bank{i}", [P, S], F32)) for i in range(8)]
        x, y, a = sb("x", T), sb("y", T), sb("a", T)
        pack = sb("pack", ap["pack"].shape[1])
        soon = cols["L0_attn_ln2_b"][0] + cols["L0_attn_ln2_b"][1]
        rest_loaded = nc.alloc_semaphore("rest_loaded")
        for n, (lo, w) in cols.items():
            k.w[n] = pack[:, lo:lo + w]
        k.mean, k.ones, k.heads, k.ident = k.w["mean"], k.w["ones"], k.w["head_mask"], k.w["ident"]
        k.eps = {e: k.w["eps"][:, i:i + 1] for i, e in enumerate(EPSILONS)}
        k.ap = ap
        k.big = sb("big", ap["big2"].shape[1])
        k.big_loaded = nc.alloc_semaphore("big_loaded")
        k.ctx = k.w["ctx"]
        k.mask0, k.mask2 = sb("mask0", NT * M), sb("mask2", TB * M)
        k.level_masks = sb("level_masks", ap["level_masks"].shape[1], mybir.dt.uint8)[:, :]
        masks_raw = ap["level_masks"].shape[1]
        k.cut = sb("cut", P, BF16)
        k.candidate = sb("candidate", 6, I32)
        k.later = sb("later", P, BF16)
        k.ident_bf = sb("ident_bf", P, BF16)[:, :]
        raw0, raw2 = sb("raw0", NT * M, mybir.dt.uint8), sb("raw2", TB * M, I32)
        with stage(nc, "loaded masks chain") as (block, s):
            @block.sync
            def _(sp):
                sp.dma_start(x[:, :], ap["x"]).then_inc(s["loaded"], 16)
                sp.dma_start(pack[:, 0:soon], ap["pack"][:, 0:soon]).then_inc(s["loaded"], 16)
                sp.dma_start(raw0[:, :], ap["mask0"]).then_inc(s["masks"], 16)
                sp.dma_start(raw2[:, :], ap["mask2"]).then_inc(s["masks"], 16)
                sp.dma_start(k.candidate[:, :], ap["candidate"]).then_inc(s["masks"], 16)
                sp.dma_start(y[:, 0:masks_raw].bitcast(I32), ap["level_masks"]).then_inc(s["masks"], 16)
                sp.dma_start(pack[:, soon:], ap["pack"][:, soon:]).then_inc(rest_loaded, 16)
                sp.dma_start(k.big[:, 0:ap["big0"].shape[1]], ap["big0"]).then_inc(k.big_loaded, 16)
                sp.wait_ge(s["loaded"], 32)

            @block.vector
            def _(dve):
                link = Chain(dve, s["chain"])
                dve.wait_ge(s["masks"], 64)
                link(nc.vector.tensor_copy(k.mask0[:, :], raw0[:, :]))
                link(nc.vector.tensor_copy(k.level_masks, y[:, 0:masks_raw].bitcast(I32)))
                dve.wait_ge(s["loaded"], 32)
                link(nc.vector.tensor_copy(k.ident_bf, k.ident))
                link(nc.vector.tensor_scalar(k.cut[:, :], k.w["after"], -1e30, None, ALU.mult))
                link(nc.vector.tensor_scalar(k.later[:, :], k.w["key_later"], 1e30, None, ALU.mult))
                link(nc.vector.tensor_copy(k.mask2[:, :], raw2[:, :]))
                link(nc.vector.tensor_scalar(k.mask0[:, :], k.mask0[:, :], 0.0, None, ALU.not_equal))
                link(nc.vector.tensor_scalar(k.mask2[:, :], k.mask2[:, :], 0.0, None, ALU.not_equal))
        for n in range(first, last):
            if n == max(first, 1):
                with nc.Block() as block:
                    @block.sync
                    def _(sp):
                        sp.wait_ge(rest_loaded, 16)
            LAYERS[n](nc, k, x, y, a)
        with nc.Block() as block:
            @block.sync
            def _(sp):
                sp.dma_start(out, x[:, :]).then_inc(stored, 16)
                sp.wait_ge(stored, 16)
                sp.wait_ge(k.big_loaded, 48)


def layer0(nc, k, x, y, a):
    with nc.sbuf_tensor(f"res_{nc.next_id()}", [P, T], F32) as res:
        norm(nc, k, x, y, 1e-5, inner=(1e-5, k.w["L0_attn_ln1_g"], k.w["L0_attn_ln1_b"], a))
        l0_attention(nc, k, y, a, res)
        norm(nc, k, res, y, 1e-5, scaled=(k.w["L0_attn_ln2_g"], k.w["L0_attn_ln2_b"]))
        l0_lookup_mlp(nc, k, y, res, x)


def more_parts(parts, f, vec, kblocks, rows):
    hd = np.arange(P) // HD
    parts["head_cols"] = (hd[:, None] == np.arange(H)[None]) * 1.0
    parts["head_of"] = np.eye(P)[:, :H] @ parts["head_cols"].T
    parts["head_rows"] = np.concatenate([(4 * c + np.arange(P)[:, None] // M == hd[None]) * 1.0 for c in range(4)], axis=1)
    parts["ctx"] = f("ctx_1024").reshape(B * M, D).T
    kv = f("L0_xattn_Wkv")
    for n, w in (("Wq", f("L0_xattn_Wq")), ("Wk", kv[:, :D]), ("Wv", kv[:, D:]), ("Wproj", f("L0_xattn_Wproj")), ("bproj", vec(f("L0_xattn_bproj")))):
        parts["L0_xattn_" + n] = w
    for pre, turn in (("L2_xattn_", True), ("L3_xattn_", False)):
        for n in ("Wq", "Wk", "Wv", "Wo"):
            parts[pre + n] = f(pre + n).T if turn else f(pre + n)
        for n in ("bq", "bk", "bo"):
            parts[pre + n] = vec(f(pre + n))
        parts[pre + "bv"] = rows(f(pre + "bv"))
    parts["before8"] = rows((np.arange(8)[None] < np.arange(8)[:, None]) * 1.0)
    parts["L0_ffn_gate_w"], parts["L0_ffn_gate_b"] = f("L0_ffn_gate_w"), rows(f("L0_ffn_gate_b"))
    parts["L0_ffn_b1"] = vec(f("L0_ffn_b1").reshape(-1))
    parts["L0_ffn_b2"] = np.concatenate([f("L0_ffn_b2"), np.zeros((P - 8, D))])
    parts["L1_attn_rms_weight"], parts["L1_attn_b_A"] = vec(f("L1_attn_rms_weight")), vec(f("L1_attn_b_A"))
    for n in ("w_A", "w_x", "w_sidegate", "w_output", "w_o"):
        parts["L1_attn_" + n] = f("L1_attn_" + n)
    for n in ("Wq", "Wk", "Wv"):
        parts["L1_xattn_" + n] = f("L1_xattn_" + n).T
    parts["L1_ffn_w1"], parts["L1_ffn_w2"] = f("L1_ffn_w1").T, kblocks(f("L1_ffn_w2").T)
    parts["L1_ffn_norm1_w"], parts["L1_ffn_norm2_w"] = vec(f("L1_ffn_norm1_w")), rows(f("L1_ffn_norm2_w"))
    parts["L1_ffn_act_scale"], parts["L1_ffn_act_bias"] = rows(f("L1_ffn_act_scale")), rows(f("L1_ffn_act_bias"))
    parts["L2_ffn_gate_w"] = f("L2_ffn_gate_w").T
    for n in "qk":
        parts["L3_attn_b" + n] = vec(f("L3_attn_b" + n))
    for n in ("Wq", "Wk", "Wv", "Wo"):
        parts["L3_attn_" + n] = f("L3_attn_" + n)
    parts["L3_attn_bv"] = rows(f("L3_attn_bv"))
    for n in ("bo", "gamma", "beta"):
        parts["L3_attn_" + n] = vec(f("L3_attn_" + n))
    parts["L3_ffn_Wc1"] = f("L3_ffn_Wc1").T
    parts["same_batch"] = (np.arange(P)[:, None] // 32 == np.arange(P)[None] // 32) * 1.0
    parts["upto"] = np.triu(np.ones((P, P)))
    parts["L2_attn_qkv_w"], parts["L2_attn_z_w"] = f("L2_attn_qkv_w").T, f("L2_attn_z_w").T
    parts["L2_attn_ba"] = np.concatenate([f("L2_attn_b_w").T, f("L2_attn_a_w").T], axis=1)
    parts["L2_attn_conv"] = f("L2_attn_conv_w").reshape(-1, P, 4).transpose(1, 0, 2).reshape(P, -1)
    for n in ("dt_bias", "A_log", "norm_w"):
        parts["L2_attn_" + n] = rows(f("L2_attn_" + n))
    parts["L2_attn_out_w"] = kblocks(f("L2_attn_out_w").T)


def more_arrays(arrays, f, kblocks):
    at = np.arange(P)
    low = [(at[:, None] >> (n + 1) == at[None] >> (n + 1)) & (at[:, None] >> n & 1 == 1) & (at[None] >> n & 1 == 0) for n in range(7)]
    arrays["level_masks"] = np.concatenate(low + [m.T for m in low], axis=1).astype(np.int32)
    arrays["big3"] = np.concatenate([f("L3_ffn_Wm").T, kblocks(f("L3_ffn_Wp").T), np.pad(f("L3_ffn_Wc2").T, ((0, P - 32), (0, 0)))], axis=1)
    arrays["candidate"] = np.array([[(p % 32) << (25 - 5 * n) for n in range(6)] for p in range(P)], np.int32)
    arrays["ind"] = np.tile((np.arange(64)[:, None] == np.arange(64 * 96)[None] // 96).astype(np.float32), (2, 1))
    w1, w2 = f("L0_ffn_w1"), f("L0_ffn_w2")
    wide = w1.shape[2] // 2
    arrays["big0"] = np.concatenate([w1[:, :, wide:].transpose(1, 0, 2).reshape(D, -1), w1[:, :, :wide].transpose(1, 0, 2).reshape(D, -1)]
                                    + [kblocks(w) for w in w2], axis=1)
    arrays["ind0"] = np.tile(np.repeat(np.eye(8, dtype=np.float32), P, axis=1), (3, 1))
    arrays["big2"] = np.concatenate([f("L2_ffn_" + n).reshape(-1, D).T for n in ("w_gate", "w_up")]
                                    + [kblocks(f("L2_ffn_w_down").transpose(0, 2, 1).reshape(-1, D))], axis=1)
    tiles = lambda m: np.ascontiguousarray(m.reshape(-1, P, M).transpose(1, 0, 2).reshape(P, -1))
    arrays["mask0"] = tiles(f("mask_BxSxS2_bk0"))
    arrays["mask2"] = tiles(f("mask_SxS2_ik1"))


FIRST, LAST = 0, 12
LAYERS = [layer0, layer1, layer2, layer3, layer4, layer5, layer6, layer7, layer8, layer9, layer10, layer11]


EPSILONS = (1e-5, 1e-8, 1e-6, -MAGIC)


def layout(inputs):
    f = lambda n: np.asarray(inputs[n])
    parts = {}
    vec = lambda v: v.reshape(-1, P).T
    kblocks = lambda w: np.concatenate(np.split(w, w.shape[0] // P), axis=1)
    rows = lambda v: np.broadcast_to(v.reshape(1, -1), (P, v.size))
    hd = np.arange(P) // HD
    parts["centre"] = np.eye(P) - 1.0 / P
    parts["mean"] = np.full((P, P), 1.0 / P)
    parts["ones"] = np.ones((P, P))
    parts["head_mask"] = (hd[:, None] == hd[None]) * 1.0
    parts["ident"] = np.eye(P)
    parts["after"], parts["key_later"] = np.tril(np.ones((P, P)), -1), np.triu(np.ones((P, P)), 1)
    parts["eps"] = np.tile(np.array(EPSILONS), (P, 1))
    for n in ("wq", "wk", "wv", "wo", "w1"):
        parts["L0_attn_" + n] = f("L0_attn_" + n)
    parts["L0_attn_w2"] = kblocks(f("L0_attn_w2"))
    for n in ("ln1_g", "ln1_b", "ln2_g", "ln2_b"):
        parts["L0_attn_" + n] = vec(f("L0_attn_" + n))
    more_parts(parts, f, vec, kblocks, rows)
    cols, at = {}, 0
    for n, v in parts.items():
        cols[n] = (at, v.shape[1])
        at += v.shape[1]
    pack = np.concatenate([v.astype(np.float32) for v in parts.values()], axis=1)
    arrays = {"x": np.ascontiguousarray(f("x").reshape(T, D).T), "pack": pack}
    more_arrays(arrays, f, kblocks)
    return arrays, cols


def kernel(**inputs):
    import concourse.bacc as bacc
    from concourse.bass_utils import run_bass_kernel_spmd as run

    nc = bacc.Bacc("TRN2", target_bir_lowering=False, num_devices=1)
    arrays, cols = layout(inputs)
    ap = {n: nc.dram_tensor(f"in_{n}", v.shape, mybir.dt.from_np(v.dtype), kind="ExternalInput").ap() for n, v in arrays.items()}
    out = nc.dram_tensor("out", (P, T), F32, kind="ExternalOutput").ap()
    program(nc, ap, out, cols, FIRST, LAST)
    r = run(nc, [{f"in_{n}": v for n, v in arrays.items()}], core_ids=[0])
    return np.ascontiguousarray(np.asarray(r.results[0]["out"]).T).reshape(B, S, D)
```
